# Optimizing a Trainium2 kernel written in Bass

```python
import numpy as np
import jax
import jax.numpy as jnp

def _softmax(x, axis=-1):
    return jax.nn.softmax(x, axis=axis)

def _gelu(x):
    return jax.nn.gelu(x, approximate=True)

def _silu(x):
    return jax.nn.silu(x)

def _sigmoid(x):
    return jax.nn.sigmoid(x)

def _layernorm(x, axis=-1, eps=1e-05):
    m = jnp.mean(x, axis=axis, keepdims=True)
    v = jnp.var(x, axis=axis, keepdims=True)
    return (x - m) / jnp.sqrt(v + eps)

def _scatter_add(tgt, idx, src, axis=0):
    return tgt.at[idx].add(src)

def _segment_sum(src, seg, n):
    return jax.ops.segment_sum(src, seg, n)
kernel_name = 'mk_lm_tower_d4_tok_ids512_r4_7ccc0a'

def setup_inputs(seed: int=0):
    np.random.seed(seed)
    _w = jnp.asarray

    def _rec_inputs():
        import jax
        import jax.numpy as jnp
        _rk = jax.random.key(seed)
        x = jax.random.randint(jax.random.fold_in(_rk, 1), (8, 512), 0, 8000, jnp.int32)
        return x
    x = _rec_inputs()

    def _L0_tok_setup():
        import jax, jax.numpy as jnp
        import numpy as np
        VOCAB = 8000
        EMB = 128
        K = 3
        B, T = (8, 1024)
        key = jax.random.key(seed)
        k_ids, k_w = jax.random.split(key)
        token_ids = jax.random.randint(k_ids, (B, T), 0, VOCAB, dtype=jnp.int64)
        conv_w = jax.random.normal(k_w, (EMB, VOCAB, K), dtype=jnp.float32) * 0.02
        return {'token_ids': token_ids, 'conv_w': conv_w}
    _L0_tok_all = _L0_tok_setup()
    _L0_tok_in = {k: v for k, v in _L0_tok_all.items() if k in ('conv_w',)}
    del _L0_tok_all

    def _L0_attn_setup():
        import jax, jax.numpy as jnp
        import numpy as np
        D_MODEL, N_HEADS, D_VALUE = (128, 8, 64)
        D_HEAD = D_MODEL // N_HEADS

        def _elu_feature_map(t):
            return jax.nn.elu(t) + 1.0
        key = jax.random.key(seed)
        ks = jax.random.split(key, 5)
        B, T = (2, 512)
        x = jax.random.normal(ks[0], (B, T, D_MODEL), dtype=jnp.float32)
        scale = 0.02
        W_q = jax.random.normal(ks[1], (N_HEADS * D_HEAD, D_MODEL), dtype=jnp.float32) * scale
        W_k = jax.random.normal(ks[2], (N_HEADS * D_HEAD, D_MODEL), dtype=jnp.float32) * scale
        W_v = jax.random.normal(ks[3], (N_HEADS * D_VALUE, D_MODEL), dtype=jnp.float32) * scale
        W_out = jax.random.normal(ks[4], (D_MODEL, N_HEADS * D_VALUE), dtype=jnp.float32) * scale
        return {'x': x, 'W_q': W_q, 'W_k': W_k, 'W_v': W_v, 'W_out': W_out}
    _L0_attn_all = _L0_attn_setup()
    _L0_attn_in = {k: v for k, v in _L0_attn_all.items() if k in ('W_q', 'W_k', 'W_v', 'W_out')}
    del _L0_attn_all

    def _L0_ffn_setup():
        import jax, jax.numpy as jnp
        import numpy as np
        B, S, D, F, E = (8, 1024, 128, 512, 8)
        INIT_LAMBDA = 0.2
        LN_EPS = 1e-05
        LN_MERGE = 0.03
        key = jax.random.key(seed)
        ks = jax.random.split(key, 12)
        n = lambda k, shp, s=1.0: jax.random.normal(k, shp, dtype=jnp.float32) * s
        return {'hidden_states': n(ks[0], (B, S, D)), 'gfc1_w': n(ks[1], (D, D), 0.01), 'gfc1_b': jnp.zeros((D,), jnp.float32), 'gfc2_w': n(ks[2], (E, D), 0.01), 'gfc2_b': jnp.full((E,), INIT_LAMBDA, dtype=jnp.float32), 'W1': n(ks[3], (F, D), 0.02), 'b1': jnp.zeros((F,), jnp.float32), 'W2': n(ks[4], (D, F), 0.02), 'b2': jnp.zeros((D,), jnp.float32), 'ln_g': jnp.ones((D,), jnp.float32), 'ln_b': jnp.zeros((D,), jnp.float32), 'tv_W1': n(ks[5], (E, F, D), 0.02), 'tv_b1': n(ks[6], (E, F), 0.02), 'tv_W2': n(ks[7], (E, D, F), 0.02), 'tv_b2': n(ks[8], (E, D), 0.02), 'tv_ln_g': n(ks[9], (E, D), 0.02), 'tv_ln_b': n(ks[10], (E, D), 0.02)}
    _L0_ffn_all = _L0_ffn_setup()
    _L0_ffn_in = {k: v for k, v in _L0_ffn_all.items() if k in ('gfc1_w', 'gfc1_b', 'gfc2_w', 'gfc2_b', 'W1', 'b1', 'W2', 'b2', 'ln_g', 'ln_b', 'tv_W1', 'tv_b1', 'tv_W2', 'tv_b2', 'tv_ln_g', 'tv_ln_b')}
    del _L0_ffn_all

    def _L1_attn_setup():
        import jax, jax.numpy as jnp
        import numpy as np
        SIZE = 128
        NUM_HEADS = 8
        HEAD_SIZE = SIZE // NUM_HEADS
        EPS = 1e-05

        def _retention(x, W_Q, W_K, W_V):
            B, T, D = x.shape
            H, dh = (NUM_HEADS, HEAD_SIZE)
            q = (x @ W_Q).reshape(B, T, H, dh).transpose(0, 2, 1, 3)
            k = (x @ W_K).reshape(B, T, H, dh).transpose(0, 2, 1, 3)
            v = (x @ W_V).reshape(B, T, H, dh).transpose(0, 2, 1, 3)
            gammas = 1.0 - jnp.exp2(-5.0 - jnp.arange(H, dtype=jnp.float32))
            idx = jnp.arange(T)
            diff = (idx[:, None] - idx[None, :]).astype(jnp.float32)
            causal = diff >= 0
            decay = jnp.where(causal[None], jnp.exp(diff[None] * jnp.log(gammas)[:, None, None]), 0.0)
            scores = jnp.einsum('bhtd,bhsd->bhts', q, k) / jnp.sqrt(jnp.float32(dh))
            out = jnp.einsum('bhts,bhsd->bhtd', scores * decay[None], v)
            return out.transpose(0, 2, 1, 3).reshape(B, T, D)

        def _group_norm(y, weight, bias):
            B, T, D = y.shape
            g = y.reshape(B * T, NUM_HEADS, HEAD_SIZE)
            mean = jnp.mean(g, axis=-1, keepdims=True)
            var = jnp.var(g, axis=-1, keepdims=True)
            g = (g - mean) / jnp.sqrt(var + EPS)
            g = g.reshape(B * T, D) * weight + bias
            return g.reshape(B, T, D)
        key = jax.random.key(seed)
        ks = jax.random.split(key, 8)
        B, T, D = (2, 512, SIZE)
        mk = lambda k: jax.random.normal(k, (D, D), dtype=jnp.float32) / D
        return {'x': jax.random.normal(ks[0], (B, T, D), dtype=jnp.float32), 'W_Q': mk(ks[1]), 'W_K': mk(ks[2]), 'W_V': mk(ks[3]), 'W_G': mk(ks[4]), 'W_O': mk(ks[5]), 'gn_weight': jnp.ones((D,), dtype=jnp.float32), 'gn_bias': jnp.zeros((D,), dtype=jnp.float32)}
    _L1_attn_all = _L1_attn_setup()
    _L1_attn_in = {k: v for k, v in _L1_attn_all.items() if k in ('W_Q', 'W_K', 'W_V', 'W_G', 'W_O', 'gn_weight', 'gn_bias')}
    del _L1_attn_all

    def _L1_ffn_setup():
        import jax, jax.numpy as jnp
        import numpy as np
        EPS = 1e-06
        SINKHORN_ITERS = 8
        TEMPERATURE = 1.0
        B, N, D = (4, 2048, 128)
        E, OUT = (8, 128)
        H = 1

        def _sinkhorn(logits):
            t = jnp.log(jnp.clip(logits, EPS)) / TEMPERATURE
            for _ in range(SINKHORN_ITERS):
                t = t - jax.nn.logsumexp(t, axis=-2, keepdims=True)
                t = t - jax.nn.logsumexp(t, axis=-1, keepdims=True)
            return jnp.exp(t)
        key = jax.random.key(seed)
        k1, k2, k3 = jax.random.split(key, 3)
        x = jax.random.normal(k1, (B, N, D), dtype=jnp.float32)
        gate_weight = jax.random.normal(k2, (H, D, E), dtype=jnp.float32)
        experts = jax.random.normal(k3, (E, D, OUT), dtype=jnp.float32) * 0.02
        return {'x': x, 'gate_weight': gate_weight, 'experts': experts}
    _L1_ffn_all = _L1_ffn_setup()
    _L1_ffn_in = {k: v for k, v in _L1_ffn_all.items() if k in ('gate_weight', 'experts')}
    del _L1_ffn_all

    def _L2_attn_setup():
        import jax, jax.numpy as jnp
        import numpy as np
        EPS = 1e-07
        key = jax.random.key(seed)
        ks = jax.random.split(key, 4)
        B, L, D, U = (4, 256, 128, 64)
        scale_w = (2.0 / (D + U)) ** 0.5
        x = jax.random.normal(ks[0], (B, L, D), dtype=jnp.float32)
        Wx = jax.random.normal(ks[1], (D, U), dtype=jnp.float32) * scale_w
        Wt = jax.random.normal(ks[2], (D, U), dtype=jnp.float32) * scale_w
        bt = jnp.zeros((U,), dtype=jnp.float32)
        Wa = jax.random.normal(ks[3], (U, 1), dtype=jnp.float32) * (2.0 / (U + 1)) ** 0.5
        ba = jnp.zeros((1,), dtype=jnp.float32)
        return {'x': x, 'Wx': Wx, 'Wt': Wt, 'bt': bt, 'Wa': Wa, 'ba': ba}
    _L2_attn_all = _L2_attn_setup()
    _L2_attn_in = {k: v for k, v in _L2_attn_all.items() if k in ('Wx', 'Wt', 'bt', 'Wa', 'ba')}
    del _L2_attn_all

    def _L2_ffn_setup():
        import jax, jax.numpy as jnp
        import numpy as np
        B, S, D, H, E, K = (2, 512, 128, 256, 8, 2)

        def _moe(x, router_w, w_gate, w_up, w_down):
            bsz, seq, d = x.shape
            flat = x.reshape(-1, d)
            logits = flat @ router_w.T
            topk_vals, topk_idx = jax.lax.top_k(logits, K)
            topk_w = jax.nn.softmax(topk_vals, axis=-1)
            s = flat.shape[0]
            dense_w = jnp.zeros((s, E), dtype=flat.dtype).at[jnp.arange(s)[:, None], topk_idx].add(topk_w)
            g = jnp.einsum('sd,edh->esh', flat, w_gate)
            u = jnp.einsum('sd,edh->esh', flat, w_up)
            y = jnp.einsum('esh,ehd->esd', jax.nn.silu(g) * u, w_down)
            out = jnp.einsum('esd,se->sd', y, dense_w)
            return out.reshape(bsz, seq, d)
        key = jax.random.key(seed)
        k1, k2, k3, k4, k5 = jax.random.split(key, 5)
        return {'x': jax.random.normal(k1, (B, S, D), dtype=jnp.float32), 'router_w': jax.random.normal(k2, (E, D), dtype=jnp.float32) * D ** (-0.5), 'w_gate': jax.random.normal(k3, (E, D, H), dtype=jnp.float32) * D ** (-0.5), 'w_up': jax.random.normal(k4, (E, D, H), dtype=jnp.float32) * D ** (-0.5), 'w_down': jax.random.normal(k5, (E, H, D), dtype=jnp.float32) * H ** (-0.5)}
    _L2_ffn_all = _L2_ffn_setup()
    _L2_ffn_in = {k: v for k, v in _L2_ffn_all.items() if k in ('router_w', 'w_gate', 'w_up', 'w_down')}
    del _L2_ffn_all

    def _L3_attn_setup():
        import jax, jax.numpy as jnp
        import numpy as np
        EMB_DIM = 128
        N_HEAD = 8
        HEAD_DIM = EMB_DIM // N_HEAD
        SEQ_LEN = 512
        BATCH = 4
        key = jax.random.key(seed)
        k1, k2, k3 = jax.random.split(key, 3)
        emb = jax.random.normal(k1, (SEQ_LEN, BATCH, EMB_DIM), dtype=jnp.float32)
        W = jax.random.normal(k2, (3 * EMB_DIM, EMB_DIM), dtype=jnp.float32) * 0.02
        b = jax.random.normal(k3, (3 * EMB_DIM,), dtype=jnp.float32) * 0.02
        return {'emb': emb, 'W': W, 'b': b}
    _L3_attn_all = _L3_attn_setup()
    _L3_attn_in = {k: v for k, v in _L3_attn_all.items() if k in ('W', 'b')}
    del _L3_attn_all

    def _L3_ffn_setup():
        import jax, jax.numpy as jnp
        import numpy as np
        E = 64
        K = 2
        D = 128
        H = 64
        NSH = 2
        ROUTE_SCALE = 2.5
        CAP = 256
        STD = 0.02
        key = jax.random.key(seed)
        ks = jax.random.split(key, 8)
        x = jax.random.normal(ks[0], (4, 512, D), dtype=jnp.float32)
        gate_w = jax.random.normal(ks[1], (E, D), dtype=jnp.float32) * STD
        w1 = jax.random.normal(ks[2], (E, D, H), dtype=jnp.float32) * STD
        w3 = jax.random.normal(ks[3], (E, D, H), dtype=jnp.float32) * STD
        w2 = jax.random.normal(ks[4], (E, H, D), dtype=jnp.float32) * STD
        sw1 = jax.random.normal(ks[5], (D, H * NSH), dtype=jnp.float32) * STD
        sw3 = jax.random.normal(ks[6], (D, H * NSH), dtype=jnp.float32) * STD
        sw2 = jax.random.normal(ks[7], (H * NSH, D), dtype=jnp.float32) * STD
        return {'x': x, 'gate_w': gate_w, 'w1': w1, 'w3': w3, 'w2': w2, 'sw1': sw1, 'sw3': sw3, 'sw2': sw2}
    _L3_ffn_all = _L3_ffn_setup()
    _L3_ffn_in = {k: v for k, v in _L3_ffn_all.items() if k in ('gate_w', 'w1', 'w3', 'w2', 'sw1', 'sw3', 'sw2')}
    del _L3_ffn_all
    return {'x': x, 'L0_tok_conv_w': _L0_tok_in['conv_w'], 'L0_attn_W_q': _L0_attn_in['W_q'], 'L0_attn_W_k': _L0_attn_in['W_k'], 'L0_attn_W_v': _L0_attn_in['W_v'], 'L0_attn_W_out': _L0_attn_in['W_out'], 'L0_ffn_gfc1_w': _L0_ffn_in['gfc1_w'], 'L0_ffn_gfc1_b': _L0_ffn_in['gfc1_b'], 'L0_ffn_gfc2_w': _L0_ffn_in['gfc2_w'], 'L0_ffn_gfc2_b': _L0_ffn_in['gfc2_b'], 'L0_ffn_W1': _L0_ffn_in['W1'], 'L0_ffn_b1': _L0_ffn_in['b1'], 'L0_ffn_W2': _L0_ffn_in['W2'], 'L0_ffn_b2': _L0_ffn_in['b2'], 'L0_ffn_ln_g': _L0_ffn_in['ln_g'], 'L0_ffn_ln_b': _L0_ffn_in['ln_b'], 'L0_ffn_tv_W1': _L0_ffn_in['tv_W1'], 'L0_ffn_tv_b1': _L0_ffn_in['tv_b1'], 'L0_ffn_tv_W2': _L0_ffn_in['tv_W2'], 'L0_ffn_tv_b2': _L0_ffn_in['tv_b2'], 'L0_ffn_tv_ln_g': _L0_ffn_in['tv_ln_g'], 'L0_ffn_tv_ln_b': _L0_ffn_in['tv_ln_b'], 'L1_attn_W_Q': _L1_attn_in['W_Q'], 'L1_attn_W_K': _L1_attn_in['W_K'], 'L1_attn_W_V': _L1_attn_in['W_V'], 'L1_attn_W_G': _L1_attn_in['W_G'], 'L1_attn_W_O': _L1_attn_in['W_O'], 'L1_attn_gn_weight': _L1_attn_in['gn_weight'], 'L1_attn_gn_bias': _L1_attn_in['gn_bias'], 'L1_ffn_gate_weight': _L1_ffn_in['gate_weight'], 'L1_ffn_experts': _L1_ffn_in['experts'], 'L2_attn_Wx': _L2_attn_in['Wx'], 'L2_attn_Wt': _L2_attn_in['Wt'], 'L2_attn_bt': _L2_attn_in['bt'], 'L2_attn_Wa': _L2_attn_in['Wa'], 'L2_attn_ba': _L2_attn_in['ba'], 'L2_ffn_router_w': _L2_ffn_in['router_w'], 'L2_ffn_w_gate': _L2_ffn_in['w_gate'], 'L2_ffn_w_up': _L2_ffn_in['w_up'], 'L2_ffn_w_down': _L2_ffn_in['w_down'], 'L3_attn_W': _L3_attn_in['W'], 'L3_attn_b': _L3_attn_in['b'], 'L3_ffn_gate_w': _L3_ffn_in['gate_w'], 'L3_ffn_w1': _L3_ffn_in['w1'], 'L3_ffn_w3': _L3_ffn_in['w3'], 'L3_ffn_w2': _L3_ffn_in['w2'], 'L3_ffn_sw1': _L3_ffn_in['sw1'], 'L3_ffn_sw3': _L3_ffn_in['sw3'], 'L3_ffn_sw2': _L3_ffn_in['sw2']}

def reference(x, L0_tok_conv_w, L0_attn_W_q, L0_attn_W_k, L0_attn_W_v, L0_attn_W_out, L0_ffn_gfc1_w, L0_ffn_gfc1_b, L0_ffn_gfc2_w, L0_ffn_gfc2_b, L0_ffn_W1, L0_ffn_b1, L0_ffn_W2, L0_ffn_b2, L0_ffn_ln_g, L0_ffn_ln_b, L0_ffn_tv_W1, L0_ffn_tv_b1, L0_ffn_tv_W2, L0_ffn_tv_b2, L0_ffn_tv_ln_g, L0_ffn_tv_ln_b, L1_attn_W_Q, L1_attn_W_K, L1_attn_W_V, L1_attn_W_G, L1_attn_W_O, L1_attn_gn_weight, L1_attn_gn_bias, L1_ffn_gate_weight, L1_ffn_experts, L2_attn_Wx, L2_attn_Wt, L2_attn_bt, L2_attn_Wa, L2_attn_ba, L2_ffn_router_w, L2_ffn_w_gate, L2_ffn_w_up, L2_ffn_w_down, L3_attn_W, L3_attn_b, L3_ffn_gate_w, L3_ffn_w1, L3_ffn_w3, L3_ffn_w2, L3_ffn_sw1, L3_ffn_sw3, L3_ffn_sw2):
    import jax
    import jax.numpy as jnp

    def _L0_tok_ref(token_ids, conv_w):
        import jax, jax.numpy as jnp
        import numpy as np
        VOCAB = 8000
        EMB = 128
        K = 3
        B, T = (8, 1024)
        'Equivalent to one_hot(token_ids) -> Conv1d(V->F, k=K, pad=K//2, no bias).\n\n            Because the conv input is one-hot over the vocab channel, the V-dim\n            contraction reduces to gathering one weight row per (position, tap):\n              out[b,t,f] = sum_k W[f, token[b, t+k-pad], k]   (zero outside [0,T)).\n            '
        Bn, Tn = token_ids.shape
        F_, V_, Kn = conv_w.shape
        pad = Kn // 2
        out = jnp.zeros((Bn, Tn, F_), dtype=conv_w.dtype)
        t = jnp.arange(Tn)
        for k in range(Kn):
            shift = k - pad
            src = t + shift
            valid = (src >= 0) & (src < Tn)
            src_c = jnp.clip(src, 0, Tn - 1)
            ids = token_ids[:, src_c]
            table_k = conv_w[:, :, k].T
            emb = table_k[ids]
            out = out + jnp.where(valid[None, :, None], emb, jnp.zeros((), conv_w.dtype))
        return out

    def _L0_attn_ref(x, W_q, W_k, W_v, W_out):
        import jax, jax.numpy as jnp
        import numpy as np
        D_MODEL, N_HEADS, D_VALUE = (128, 8, 64)
        D_HEAD = D_MODEL // N_HEADS

        def _elu_feature_map(t):
            return jax.nn.elu(t) + 1.0
        B, T, D = x.shape
        H, dh, dv = (N_HEADS, D_HEAD, D_VALUE)
        Q = _elu_feature_map((x @ W_q.T).reshape(B, T, H, dh)).transpose(0, 2, 1, 3)
        K = _elu_feature_map((x @ W_k.T).reshape(B, T, H, dh)).transpose(0, 2, 1, 3)
        V = (x @ W_v.T).reshape(B, T, H, dv).transpose(0, 2, 1, 3)
        KV = jnp.einsum('bhti,bhtj->bhtij', K, V)
        S = jnp.cumsum(KV, axis=2)
        z = jnp.cumsum(K, axis=2)
        num = jnp.einsum('bhti,bhtij->bhtj', Q, S)
        den = jnp.maximum(jnp.einsum('bhti,bhti->bht', Q, z), 1e-06)[..., None]
        out = (num / den).transpose(0, 2, 1, 3).reshape(B, T, H * dv)
        return out @ W_out.T

    def _L0_ffn_ref(hidden_states, gfc1_w, gfc1_b, gfc2_w, gfc2_b, W1, b1, W2, b2, ln_g, ln_b, tv_W1, tv_b1, tv_W2, tv_b2, tv_ln_g, tv_ln_b):
        import jax, jax.numpy as jnp
        import numpy as np
        B, S, D, F, E = (8, 1024, 128, 512, 8)
        INIT_LAMBDA = 0.2
        LN_EPS = 1e-05
        LN_MERGE = 0.03
        x = hidden_states
        gh = jax.nn.relu(jnp.einsum('bsd,hd->bsh', x, gfc1_w) + gfc1_b)
        g = (jnp.einsum('bsh,eh->bse', gh, gfc2_w) + gfc2_b).mean(axis=1)
        W1m = W1 + jnp.einsum('be,efd->bfd', g, tv_W1)
        b1m = b1 + g @ tv_b1
        W2m = W2 + jnp.einsum('be,edf->bdf', g, tv_W2)
        b2m = b2 + g @ tv_b2
        lng = ln_g + LN_MERGE * (tv_ln_g - ln_g).sum(axis=0)
        lnb = ln_b + LN_MERGE * (tv_ln_b - ln_b).sum(axis=0)
        h = jax.nn.relu(jnp.einsum('bsd,bfd->bsf', x, W1m) + b1m[:, None, :])
        out = jnp.einsum('bsf,bdf->bsd', h, W2m) + b2m[:, None, :]
        res = x + out
        mu = res.mean(axis=-1, keepdims=True)
        var = res.var(axis=-1, keepdims=True)
        return (res - mu) * jax.lax.rsqrt(var + LN_EPS) * lng + lnb

    def _L1_attn_ref(x, W_Q, W_K, W_V, W_G, W_O, gn_weight, gn_bias):
        import jax, jax.numpy as jnp
        import numpy as np
        SIZE = 128
        NUM_HEADS = 8
        HEAD_SIZE = SIZE // NUM_HEADS
        EPS = 1e-05

        def _retention(x, W_Q, W_K, W_V):
            B, T, D = x.shape
            H, dh = (NUM_HEADS, HEAD_SIZE)
            q = (x @ W_Q).reshape(B, T, H, dh).transpose(0, 2, 1, 3)
            k = (x @ W_K).reshape(B, T, H, dh).transpose(0, 2, 1, 3)
            v = (x @ W_V).reshape(B, T, H, dh).transpose(0, 2, 1, 3)
            gammas = 1.0 - jnp.exp2(-5.0 - jnp.arange(H, dtype=jnp.float32))
            idx = jnp.arange(T)
            diff = (idx[:, None] - idx[None, :]).astype(jnp.float32)
            causal = diff >= 0
            decay = jnp.where(causal[None], jnp.exp(diff[None] * jnp.log(gammas)[:, None, None]), 0.0)
            scores = jnp.einsum('bhtd,bhsd->bhts', q, k) / jnp.sqrt(jnp.float32(dh))
            out = jnp.einsum('bhts,bhsd->bhtd', scores * decay[None], v)
            return out.transpose(0, 2, 1, 3).reshape(B, T, D)

        def _group_norm(y, weight, bias):
            B, T, D = y.shape
            g = y.reshape(B * T, NUM_HEADS, HEAD_SIZE)
            mean = jnp.mean(g, axis=-1, keepdims=True)
            var = jnp.var(g, axis=-1, keepdims=True)
            g = (g - mean) / jnp.sqrt(var + EPS)
            g = g.reshape(B * T, D) * weight + bias
            return g.reshape(B, T, D)
        ret = _retention(x, W_Q, W_K, W_V)
        normed = _group_norm(ret, gn_weight, gn_bias)
        return jax.nn.silu(x @ W_G + normed) @ W_O

    def _L1_ffn_ref(x, gate_weight, experts):
        import jax, jax.numpy as jnp
        import numpy as np
        EPS = 1e-06
        SINKHORN_ITERS = 8
        TEMPERATURE = 1.0
        B, N, D = (4, 2048, 128)
        E, OUT = (8, 128)
        H = 1

        def _sinkhorn(logits):
            t = jnp.log(jnp.clip(logits, EPS)) / TEMPERATURE
            for _ in range(SINKHORN_ITERS):
                t = t - jax.nn.logsumexp(t, axis=-2, keepdims=True)
                t = t - jax.nn.logsumexp(t, axis=-1, keepdims=True)
            return jnp.exp(t)
        b, n, d = x.shape
        e = experts.shape[0]
        m = n // e
        xh = x[:, None, :, :]
        gate_logits = jnp.einsum('bhnd,hde->bhne', xh, gate_weight)
        gates = _sinkhorn(gate_logits)
        g_t = jnp.swapaxes(gates, -1, -2)
        vals, idx = jax.lax.top_k(g_t, m)
        gate_values = jnp.transpose(vals, (2, 0, 1, 3))[..., None]
        routed = jnp.take_along_axis(xh[:, :, None, :, :], idx[..., None], axis=3)
        routed = jnp.transpose(routed, (2, 0, 1, 3, 4))
        expert_w = experts[:, None, :, :]
        outputs = jnp.einsum('ebhmi,ehio->ebhmo', routed, expert_w)
        outputs = outputs * gate_values
        bh_idx = idx.reshape(b, 1, e * m)
        bh_vals = jnp.transpose(outputs, (1, 2, 0, 3, 4)).reshape(b, 1, e * m, outputs.shape[-1])

        def scat(i1, v1):
            return jnp.zeros((n, v1.shape[-1]), dtype=v1.dtype).at[i1].set(v1)
        routed_back = jax.vmap(jax.vmap(scat))(bh_idx, bh_vals)
        return routed_back[:, 0]

    def _L2_attn_ref(x, Wx, Wt, bt, Wa, ba):
        import jax, jax.numpy as jnp
        import numpy as np
        EPS = 1e-07
        k = x @ Wx
        q = x @ Wt
        h = jnp.tanh(q[:, :, None, :] + k[:, None, :, :] + bt)
        e = jnp.exp(jnp.einsum('bijq,qo->bij', h, Wa) + ba[0])
        s = jnp.sum(e, axis=-1, keepdims=True)
        a = e / (s + EPS)
        v = jnp.einsum('bij,bjd->bid', a, x)
        return v

    def _L2_ffn_ref(x, router_w, w_gate, w_up, w_down):
        import jax, jax.numpy as jnp
        import numpy as np
        B, S, D, H, E, K = (2, 512, 128, 256, 8, 2)

        def _moe(x, router_w, w_gate, w_up, w_down):
            bsz, seq, d = x.shape
            flat = x.reshape(-1, d)
            logits = flat @ router_w.T
            topk_vals, topk_idx = jax.lax.top_k(logits, K)
            topk_w = jax.nn.softmax(topk_vals, axis=-1)
            s = flat.shape[0]
            dense_w = jnp.zeros((s, E), dtype=flat.dtype).at[jnp.arange(s)[:, None], topk_idx].add(topk_w)
            g = jnp.einsum('sd,edh->esh', flat, w_gate)
            u = jnp.einsum('sd,edh->esh', flat, w_up)
            y = jnp.einsum('esh,ehd->esd', jax.nn.silu(g) * u, w_down)
            out = jnp.einsum('esd,se->sd', y, dense_w)
            return out.reshape(bsz, seq, d)
        return _moe(x, router_w, w_gate, w_up, w_down)

    def _L3_attn_ref(emb, W, b):
        import jax, jax.numpy as jnp
        import numpy as np
        EMB_DIM = 128
        N_HEAD = 8
        HEAD_DIM = EMB_DIM // N_HEAD
        SEQ_LEN = 512
        BATCH = 4
        L, B, E = emb.shape
        scaling = (E / N_HEAD) ** (-0.5)
        ft = jnp.einsum('lbe,oe->lbo', emb, W) + b
        ft = ft.reshape(L, B * N_HEAD, 3 * HEAD_DIM).transpose(1, 0, 2)
        q, k, v = jnp.split(ft, 3, axis=-1)
        scores = jnp.einsum('bld,bmd->blm', q, k) * scaling
        mask = scores == 0
        scores = jnp.where(mask, -jnp.inf, scores)
        attn = jax.nn.softmax(scores, axis=-1)
        attn = jnp.where(mask, jnp.zeros((), attn.dtype), attn)
        out = jnp.einsum('blm,bmd->bld', attn, v)
        out = out.transpose(1, 0, 2).reshape(L, B, E)
        return out

    def _L3_ffn_ref(x, gate_w, w1, w3, w2, sw1, sw3, sw2):
        import jax, jax.numpy as jnp
        import numpy as np
        E = 64
        K = 2
        D = 128
        H = 64
        NSH = 2
        ROUTE_SCALE = 2.5
        CAP = 256
        STD = 0.02
        bs, slen, d = x.shape
        xf = x.reshape(-1, d)
        logits = xf @ gate_w.T
        scores = jax.nn.sigmoid(logits.astype(jnp.float32))
        top_scores, top_idx = jax.lax.top_k(scores, K)
        top_scores = top_scores / (top_scores.sum(-1, keepdims=True) + 1e-20)
        top_scores = top_scores * ROUTE_SCALE
        flat_e = top_idx.reshape(-1)
        x_pairs = jnp.repeat(xf, K, axis=0)
        oh = jax.nn.one_hot(flat_e, E, dtype=jnp.int32)
        pos = jnp.take_along_axis(jnp.cumsum(oh, axis=0), flat_e[:, None], axis=1)[:, 0] - 1
        buf = jnp.zeros((E, CAP, d), dtype=xf.dtype).at[flat_e, pos].set(x_pairs, mode='drop')
        h = jax.nn.silu(jnp.einsum('ecd,edh->ech', buf, w1)) * jnp.einsum('ecd,edh->ech', buf, w3)
        y = jnp.einsum('ech,ehd->ecd', h, w2)
        valid = (pos < CAP)[:, None]
        y_pairs = jnp.where(valid, y[flat_e, jnp.minimum(pos, CAP - 1)], 0.0)
        routed = (y_pairs.reshape(-1, K, d) * top_scores[..., None].astype(xf.dtype)).sum(axis=1)
        shared = jax.nn.silu(xf @ sw1) * (xf @ sw3) @ sw2
        return (shared + routed).reshape(bs, slen, d)
    h = _L0_tok_ref(x, L0_tok_conv_w)
    h = h + _L0_attn_ref(_layernorm(h, axis=-1), L0_attn_W_q, L0_attn_W_k, L0_attn_W_v, L0_attn_W_out)
    h = h + _L0_ffn_ref(_layernorm(h, axis=-1), L0_ffn_gfc1_w, L0_ffn_gfc1_b, L0_ffn_gfc2_w, L0_ffn_gfc2_b, L0_ffn_W1, L0_ffn_b1, L0_ffn_W2, L0_ffn_b2, L0_ffn_ln_g, L0_ffn_ln_b, L0_ffn_tv_W1, L0_ffn_tv_b1, L0_ffn_tv_W2, L0_ffn_tv_b2, L0_ffn_tv_ln_g, L0_ffn_tv_ln_b)
    h = h + _L1_attn_ref(_layernorm(h, axis=-1), L1_attn_W_Q, L1_attn_W_K, L1_attn_W_V, L1_attn_W_G, L1_attn_W_O, L1_attn_gn_weight, L1_attn_gn_bias)
    h = h + _L1_ffn_ref(_layernorm(h, axis=-1), L1_ffn_gate_weight, L1_ffn_experts)
    h = h + _L2_attn_ref(_layernorm(h, axis=-1), L2_attn_Wx, L2_attn_Wt, L2_attn_bt, L2_attn_Wa, L2_attn_ba)
    h = h + _L2_ffn_ref(_layernorm(h, axis=-1), L2_ffn_router_w, L2_ffn_w_gate, L2_ffn_w_up, L2_ffn_w_down)
    h = h + _L3_attn_ref(_layernorm(h, axis=-1), L3_attn_W, L3_attn_b)
    h = h + _L3_ffn_ref(_layernorm(h, axis=-1), L3_ffn_gate_w, L3_ffn_w1, L3_ffn_w3, L3_ffn_w2, L3_ffn_sw1, L3_ffn_sw3, L3_ffn_sw2)
    return h

_drawn_inputs = setup_inputs


def setup_inputs(seed=0):
    import zlib

    import numpy as np

    out = dict(_drawn_inputs(seed))
    spreads = {'L0_ffn_gfc1_b': (0.0, 0.334),
     'L0_ffn_gfc2_b': (0.20000000298023224, 0.2),
     'L0_ffn_b1': (0.0, 0.1),
     'L0_ffn_b2': (0.0, 0.1),
     'L0_ffn_ln_g': (1.0, 0.2),
     'L0_ffn_ln_b': (0.0, 0.1),
     'L1_attn_gn_weight': (1.0, 0.2),
     'L1_attn_gn_bias': (0.0, 0.1),
     'L2_attn_bt': (0.0, 0.344)}
    factors = {'L0_ffn_gfc1_w': 5.857,
     'L0_ffn_tv_ln_g': 3.452,
     'L0_ffn_tv_ln_b': 2.953,
     'L3_attn_b': 3.013,
     'L3_ffn_gate_w': 8.0,
     'L3_ffn_w1': 8.0,
     'L3_ffn_w3': 8.0,
     'L3_ffn_w2': 8.0,
     'L3_ffn_sw1': 8.0,
     'L3_ffn_sw3': 8.0,
     'L3_ffn_sw2': 8.0}
    for name, (base, spread) in spreads.items():
        noise = np.random.default_rng([zlib.crc32(name.encode()), seed]).standard_normal(out[name].shape)
        drawn = base * np.exp(spread * noise) if base else spread * noise
        out[name] = jnp.asarray(drawn.astype(out[name].dtype))
    for name, factor in factors.items():
        out[name] = (out[name] * factor).astype(out[name].dtype)
    return out
```

```python
import numpy as np
import concourse.bass as bass
from concourse import mybir
from contextlib import ExitStack

F32 = mybir.dt.float32
I32 = mybir.dt.int32
U32 = mybir.dt.uint32
ALU = mybir.AluOpType
ACT = mybir.ActivationFunctionType
AX = mybir.AxisListType

P = 128
B, T, D = 8, 512, 128
NC_ = T // P
NT = B * NC_
NH = 8
DH = D // NH
DV = 64
VOCAB, TAPS = 8000, 3
PAIRS = B // 2
LN_EPS = 1e-5
CE, CH, CAP = 64, 64, 256
ROUTE_SCALE = 2.5


class Layer(ExitStack):

    def __init__(self, nc):
        super().__init__()
        self.nc, self.sems = nc, []

    def semaphore(self, name):
        self.sems.append(self.nc.alloc_semaphore(name))
        return self.sems[-1]

    def sb(self, name, shape, dtype=F32):
        return self.enter_context(self.nc.sbuf_tensor(name, shape, dtype))

    def end(self):
        self.close()
        self.nc.clear_and_free_semaphores(self.sems)
        self.nc.all_engine_barrier()


class Signal:

    def __init__(self, ctx, nc, name, per=0):
        self.sem = ctx.semaphore(name)
        self.per = per

    def at(self, i, k):
        return i * self.per + k


def shape_constants():
    p = np.arange(P)
    t = np.arange(T)
    head = p // DH
    decay = np.log(1.0 - 2.0 ** (-5.0 - head.astype(np.float64)))
    shift = (p[:, None] + 1 == p[None, :])
    edge = (p[:, None] == P - 1) & (p[None, :] == 0)
    out = {
        "ident": np.eye(P),
        "prev": shift, "prev_edge": edge,
        "next": shift.T, "next_edge": edge.T,
        "causal": p[:, None] <= p[None, :],
        "same_head": head[:, None] == head[None, :],
        "head_col": head[:, None] == np.arange(NH)[None, :],
        "state_mask": head[:, None] == (np.arange(NH * DV) // DV)[None, :],
        "ones": np.ones((P, T)),
        "decay_q": np.exp(decay[:, None] * t) / np.sqrt(float(DH)),
        "decay_k": np.exp(-decay[:, None] * t),
    }
    return {k: np.ascontiguousarray(v, dtype=np.float32) for k, v in out.items()}


class Memory:

    def __init__(self, ctx, nc, dram):
        self.ctx, self.nc, self.dram = ctx, nc, dram
        self.h = self.sb("h", [P, NT, D])
        self.bank = [ctx.enter_context(nc.psum_tensor(f"bank{n}", [P, T], F32)) for n in range(8)]
        self.w = {}
        self.loaded = {}
        self.load_log = []

    def sb(self, name, shape, dtype=F32):
        return self.ctx.enter_context(self.nc.sbuf_tensor(name, shape, dtype))

    def load(self, layer, name):
        src = self.dram[name]
        self.load_log.append(name)
        t = layer.enter_context(self.nc.sbuf_tensor(f"w_{name}_{len(self.load_log)}", list(src.shape), src.dtype))
        s = layer.semaphore(f"loaded_{name}_{len(self.load_log)}")
        self.w[name] = t
        self.loaded[name] = s
        return t, s, src


def token_conv(ctx, nc, m):
    gathered = [Signal(ctx, nc, f"tok_gathered{b}") for b in range(B)]
    ids_in = Signal(ctx, nc, "tok_ids_in")
    summed = Signal(ctx, nc, "tok_summed")
    copied = Signal(ctx, nc, "tok_copied")
    loads = [(n, *m.load(m.ctx, n)) for n in ("ident", "prev", "prev_edge", "next", "next_edge")]
    rest = [(n, *m.load(m.ctx, n)) for n in m.early]
    ids = m.sb("ids", [P, NT], I32)
    rows = m.big[:, 0:NT * TAPS * D].rearrange("p (n k) -> p n k", n=NT)
    with nc.Block() as block:
        @block.sync
        def _(sp):
            for _, t, s, src in loads + rest:
                sp.dma_start(t[:, :], src).then_inc(s, 16)

        @block.gpsimd
        def _(pool):
            pool.dma_start(ids[:, :], m.dram["ids"]).then_inc(ids_in.sem, 16)
            pool.wait_ge(ids_in.sem, 16)
            for n in range(NT):
                pool.indirect_dma_start(
                    out=rows[:, n, :], out_offset=None, in_=m.dram["table"],
                    in_offset=bass.IndirectOffsetOnAxis(ap=ids[:, n:n + 1].bitcast(U32), axis=0),
                ).then_inc(gathered[n // NC_].sem, 16)

        @block.tensor
        def _(pe):
            for name, _, s, _ in loads:
                pe.wait_ge(s, 16)
            for b in range(B):
                pe.wait_ge(gathered[b].sem, 16 * NC_)
                if b >= 4:
                    pe.wait_ge(copied.sem, b - 3)
                g = rows[:, b * NC_:(b + 1) * NC_, :]
                ps = m.bank[b % 4]
                out = ps[:, :].rearrange("p (c d) -> p c d", c=NC_)
                w = m.w
                nc.tensor.matmul(out[:, :, :], w["prev"][:, :], g[:, :, 0:D], start=True, stop=False)
                nc.tensor.matmul(out[:, 1:NC_, :], w["prev_edge"][:, :], g[:, 0:NC_ - 1, 0:D], start=False, stop=False, skip_group_check=True)
                nc.tensor.matmul(out[:, :, :], w["ident"][:, :], g[:, :, D:2 * D], start=False, stop=False)
                nc.tensor.matmul(out[:, 0:NC_ - 1, :], w["next_edge"][:, :], g[:, 1:NC_, 2 * D:3 * D], start=False, stop=False, skip_group_check=True)
                last = nc.tensor.matmul(out[:, :, :], w["next"][:, :], g[:, :, 2 * D:3 * D], start=False, stop=True)
                last.then_inc(summed.sem, 1)

        @block.vector
        def _(dve):
            for b in range(B):
                dve.wait_ge(summed.sem, b + 1)
                nc.vector.tensor_copy(m.h[:, b * NC_:(b + 1) * NC_, :],
                                      m.bank[b % 4][:, :].rearrange("p (c d) -> p c d", c=NC_)).then_inc(copied.sem, 1)


class Norm:

    def __init__(self, ctx, nc, m, tag, slots=2, per=2):
        self.nc, self.m = nc, m
        self.stats = [m.nstat[s] for s in range(slots)]
        self.mv = [m.nmv[s] for s in range(slots)]
        self.rstd = [m.nrstd[s] for s in range(slots)]
        self.slots = slots
        self.step = Signal(ctx, nc, tag + "_norm_step", 2 * slots)
        self.var = Signal(ctx, nc, tag + "_norm_var", slots)
        self.root = Signal(ctx, nc, tag + "_norm_root", slots)
        self.ready = Signal(ctx, nc, tag + "_norm_ready", slots)

    def vector(self, dve, i, src, out):
        nc = self.nc
        S = range(self.slots)
        for s in S:
            for c in range(NC_):
                last = nc.vector.bn_stats(self.stats[s][:, c, :], src[s][:, c, :])
            last.then_inc(self.step.sem, 1)
        for s in S:
            dve.wait_ge(self.step.sem, self.step.at(i, s + 1))
            nc.vector.memset(self.m.fence[:, s:s + 1], 0.0)
            for c in range(NC_):
                last = nc.vector.bn_aggr(self.mv[s][:, c, :], self.stats[s][:, c, :])
            last.then_inc(self.step.sem, 1)
        for s in S:
            dve.wait_ge(self.step.sem, self.step.at(i, self.slots + s + 1))
            nc.vector.tensor_scalar(self.rstd[s][:, :], self.mv[s][:, :, 1], LN_EPS, None, ALU.add).then_inc(self.var.sem, 1)
        for s in S:
            dve.wait_ge(self.root.sem, self.root.at(i, s + 1))
            for c in range(NC_):
                last = nc.vector.tensor_scalar(out[s][:, c, :], src[s][:, c, :], self.mv[s][:, c, 0:1],
                                               self.rstd[s][:, c:c + 1], ALU.subtract, ALU.mult)
            last.then_inc(self.ready.sem, 1)

    def gpsimd(self, pool, i):
        for s in range(self.slots):
            pool.wait_ge(self.var.sem, self.var.at(i, s + 1))
            self.nc.gpsimd.tensor_tensor(self.rstd[s][:, :], self.rstd[s][:, :], self.m.minus_half[:, 0:NC_],
                                         ALU.pow).then_inc(self.root.sem, 1)


def linear_attention(ctx, nc, m):
    S = range(2)
    sig = lambda name, per: Signal(ctx, nc, "la_" + name, per)
    norm = Norm(ctx, nc, m, "la")
    xt_ps, xt_sb = sig("xt_ps", 2), sig("xt_sb", 2)
    qk_ps, exp_sb, phi, phi_step = sig("qk_ps", 4), sig("exp_sb", 4), sig("phi", 4), sig("phi_step", 4)
    z_step, qz, den_ps, den_sb, qn = sig("z_step", 2), sig("qz", 2), sig("den_ps", 2), sig("den_sb", 4), sig("qn", 2)
    km_d, km_a = sig("km_d", 2), sig("km_a", 2)
    kt_ps, kt_sb = sig("kt_ps", 2), sig("kt_sb", 2)
    v_ps, v_sb = sig("v_ps", 8), sig("v_sb", 8)
    st_ps, st_sb = sig("st_ps", 6), sig("st_sb", 6)
    sc_ps, a_sb = sig("sc_ps", 16), sig("a_sb", 16)
    av_ps, ot_sb = sig("av_ps", 8), sig("ot_sb", 8)
    y_ps, h_sb = sig("y_ps", 2), sig("h_sb", 2)
    NS = NC_ - 1
    XN, XT = m.XN, m.XT
    QT, KT, EX = m.t512a, m.t512b, m.t512c
    KM, A, V, KTOK, ST, OT = m.KM, m.A, m.V, m.KTOK, m.ST, m.OT
    w = m.w

    with nc.Block() as block:
        @block.vector
        def _(dve):
            for n in ("ones", "causal", "head_col", "state_mask"):
                dve.wait_ge(m.loaded[n], 16)
            with dve.Fori(0, PAIRS) as i:
                hs = [m.h[:, bass.ds((2 * i + s) * NC_, NC_), :] for s in S]
                norm.vector(dve, i, hs, [XN[s] for s in S])
                for q in range(2):
                    for s in S:
                        n = 2 * q + s + 1
                        dve.wait_ge(exp_sb.sem, exp_sb.at(i, n))
                        nc.vector.tensor_scalar(EX[s][:, q, :], EX[s][:, q, :], 1.0, None, ALU.min).then_inc(phi_step.sem, 1)
                    for s in S:
                        n = 2 * q + s + 1
                        dve.wait_ge(phi_step.sem, phi_step.at(i, n))
                        nc.vector.scalar_tensor_tensor((QT, KT)[q][s][:, :], m.bank[4 * s + 1 + q][:, :], 1.0, EX[s][:, q, :],
                                                       ALU.add, ALU.max).then_inc(phi.sem, 1)
                for s in S:
                    dve.wait_ge(phi.sem, phi.at(i, 3 + s))
                    nc.vector.tensor_tensor_scan(EX[s][:, 0, :], w["ones"][:, :], KT[s][:, :], 0.0, ALU.mult, ALU.add).then_inc(z_step.sem, 1)
                for s in S:
                    dve.wait_ge(z_step.sem, z_step.at(i, s + 1))
                    nc.vector.tensor_tensor(EX[s][:, 1, :], EX[s][:, 0, :], QT[s][:, :], ALU.mult).then_inc(qz.sem, 1)
                for s in S:
                    for hd in range(NH // 2):
                        last = nc.vector.tensor_scalar(KM[s][:, hd, :], KT[s][:, :], w["head_col"][:, hd:hd + 1], None, ALU.mult)
                    last.then_inc(km_d.sem, 1)
                for s in S:
                    dve.wait_ge(den_ps.sem, den_ps.at(i, s + 1))
                    nc.vector.tensor_scalar(EX[s][:, 0, :], m.bank[4 * s][:, :], 1e-6, None, ALU.max).then_inc(den_sb.sem, 1)
                for s in S:
                    dve.wait_ge(den_sb.sem, den_sb.at(i, s + 1))
                    nc.vector.reciprocal(EX[s][:, 0, :], EX[s][:, 0, :]).then_inc(den_sb.sem, 1)
                for s in S:
                    dve.wait_ge(den_sb.sem, den_sb.at(i, 2 + s + 1))
                    nc.vector.tensor_tensor(QT[s][:, :], QT[s][:, :], EX[s][:, 0, :], ALU.mult).then_inc(qn.sem, 1)
                for c in range(NS):
                    for s in S:
                        dve.wait_ge(st_ps.sem, st_ps.at(i, 2 * c + s + 1))
                        nc.vector.tensor_tensor(ST[s][:, c, :], m.bank[4 * s + 3][:, :], w["state_mask"][:, :], ALU.mult).then_inc(st_sb.sem, 1)
                for g in range(NH // 2):
                    for s in S:
                        for par in range(2):
                            dve.wait_ge(sc_ps.sem, sc_ps.at(i, 4 * g + 2 * s + par + 1))
                            nc.vector.tensor_tensor(A[s][:, 2 * (g % 2) + par, :, :], m.bank[4 * s + par][:, :].rearrange("p (c t) -> p c t", c=NC_),
                                                    w["causal"][:, :].rearrange("p (o t) -> p o t", o=1).broadcast_to([P, NC_, P]),
                                                    ALU.mult).then_inc(a_sb.sem, 1)
                for s in S:
                    dve.wait_ge(y_ps.sem, y_ps.at(i, s + 1))
                    nc.vector.tensor_tensor(hs[s], hs[s], m.bank[4 * s][:, :].rearrange("p (c d) -> p c d", c=NC_), ALU.add).then_inc(h_sb.sem, 1)
                dve.wait_ge(h_sb.sem, h_sb.at(i, 2))

        @block.gpsimd
        def _(pool):
            with pool.Fori(0, PAIRS) as i:
                norm.gpsimd(pool, i)

        @block.scalar
        def _(act):
            act.wait_ge(m.loaded["head_col"], 16)
            with act.Fori(0, PAIRS) as i:
                for s in S:
                    act.wait_ge(xt_ps.sem, xt_ps.at(i, s + 1))
                    nc.scalar.copy(XT[s][:, :], m.bank[4 * s][:, :]).then_inc(xt_sb.sem, 1)
                for q in range(2):
                    for s in S:
                        act.wait_ge(qk_ps.sem, qk_ps.at(i, 2 * q + s + 1))
                        nc.scalar.activation(EX[s][:, q, :], m.bank[4 * s + 1 + q][:, :], ACT.Exp).then_inc(exp_sb.sem, 1)
                for c in range(NC_):
                    for s in S:
                        act.wait_ge(v_ps.sem, v_ps.at(i, 2 * c + s + 1))
                        nc.scalar.copy(V[s][:, c, :], m.bank[4 * s + (3 if c % 2 else 0)][:, :]).then_inc(v_sb.sem, 1)
                for s in S:
                    act.wait_ge(phi.sem, phi.at(i, 3 + s))
                    for hd in range(NH // 2, NH):
                        last = nc.scalar.activation(KM[s][:, hd, :], KT[s][:, :], ACT.Copy, scale=w["head_col"][:, hd:hd + 1])
                    last.then_inc(km_a.sem, 1)
                for s in S:
                    act.wait_ge(kt_ps.sem, kt_ps.at(i, s + 1))
                    nc.scalar.copy(KTOK[s][:, :, :], m.bank[4 * s + 1][:, 0:NS * P].rearrange("p (c k) -> p c k", c=NS)).then_inc(kt_sb.sem, 1)
                for g in range(NH // 2):
                    for s in S:
                        act.wait_ge(av_ps.sem, av_ps.at(i, 2 * g + s + 1))
                        nc.scalar.copy(OT[s][:, g, :], m.bank[4 * s + 2 + g % 2][:, :]).then_inc(ot_sb.sem, 1)

        @block.tensor
        def _(pe):
            for n in ("wq", "wk", "wv", "wout", "same_head"):
                pe.wait_ge(m.loaded[n], 16)
            with pe.Fori(0, PAIRS) as i:
                for s in S:
                    pe.wait_ge(norm.ready.sem, norm.ready.at(i, s + 1))
                    for c in range(NC_):
                        last = nc.tensor.transpose(m.bank[4 * s][:, c * P:(c + 1) * P], XN[s][:, c, :], w["ident"][:, :])
                    last.then_inc(xt_ps.sem, 1)
                for s in S:
                    pe.wait_ge(xt_sb.sem, xt_sb.at(i, s + 1))
                    nc.tensor.matmul(m.bank[4 * s + 1][:, :], w["wq"][:, :], XT[s][:, :], start=True, stop=True).then_inc(qk_ps.sem, 1)
                for s in S:
                    nc.tensor.matmul(m.bank[4 * s + 2][:, :], w["wk"][:, :], XT[s][:, :], start=True, stop=True).then_inc(qk_ps.sem, 1)
                for c in range(NC_):
                    for s in S:
                        if c >= 2:
                            pe.wait_ge(v_sb.sem, v_sb.at(i, 2 * (c - 2) + s + 1))
                        nc.tensor.matmul(m.bank[4 * s + (3 if c % 2 else 0)][:, :], XT[s][:, c * P:(c + 1) * P], w["wv"][:, :],
                                         start=True, stop=True).then_inc(v_ps.sem, 1)
                for s in S:
                    pe.wait_ge(phi.sem, phi.at(i, 3 + s))
                    for c in range(NS):
                        last = nc.tensor.transpose(m.bank[4 * s + 1][:, c * P:(c + 1) * P], KT[s][:, c * P:(c + 1) * P], w["ident"][:, :])
                    last.then_inc(kt_ps.sem, 1)
                for s in S:
                    pe.wait_ge(qz.sem, qz.at(i, s + 1))
                    pe.wait_ge(v_sb.sem, v_sb.at(i, 4 + s + 1))
                    nc.tensor.matmul(m.bank[4 * s][:, :], w["same_head"][:, :], EX[s][:, 1, :], start=True, stop=True).then_inc(den_ps.sem, 1)
                for c in range(NS):
                    for s in S:
                        if c == 0:
                            pe.wait_ge(kt_sb.sem, kt_sb.at(i, s + 1))
                            pe.wait_ge(v_sb.sem, v_sb.at(i, 6 + s + 1))
                        else:
                            pe.wait_ge(st_sb.sem, st_sb.at(i, 2 * (c - 1) + s + 1))
                        nc.tensor.matmul(m.bank[4 * s + 3][:, :], KTOK[s][:, c, :], V[s][:, c, :],
                                         start=c == 0, stop=c == NS - 1, skip_group_check=True).then_inc(st_ps.sem, 1)

                def scores(g, s):
                    if g == 0:
                        pe.wait_ge(qn.sem, qn.at(i, s + 1))
                        pe.wait_ge(km_d.sem, km_d.at(i, s + 1))
                    if g == 2:
                        pe.wait_ge(km_a.sem, km_a.at(i, s + 1))
                    for par in range(2):
                        hd = 2 * g + par
                        if g:
                            pe.wait_ge(a_sb.sem, a_sb.at(i, 4 * (g - 1) + 2 * s + par + 1))
                        for c in range(NC_):
                            last = nc.tensor.matmul(m.bank[4 * s + par][:, c * P:(c + 1) * P], KM[s][:, hd, c * P:(c + 1) * P],
                                                    QT[s][:, c * P:(c + 1) * P], start=True, stop=True)
                        last.then_inc(sc_ps.sem, 1)

                def values(g, s):
                    pe.wait_ge(a_sb.sem, a_sb.at(i, 4 * g + 2 * s + 2))
                    if g == 0:
                        pe.wait_ge(st_sb.sem, st_sb.at(i, 2 * (NS - 1) + s + 1))
                    if g >= 2:
                        pe.wait_ge(ot_sb.sem, ot_sb.at(i, 2 * (g - 2) + s + 1))
                    out = m.bank[4 * s + 2 + g % 2]
                    for c in range(NC_):
                        for par in range(2):
                            hd = 2 * g + par
                            last = nc.tensor.matmul(out[DV * par:DV * par + DV, c * P:(c + 1) * P], V[s][:, c, hd * DV:(hd + 1) * DV],
                                                    A[s][:, 2 * (g % 2) + par, c, :], start=True, stop=c == 0)
                        if c:
                            last = nc.tensor.matmul(out[:, c * P:(c + 1) * P], ST[s][:, c - 1, g * P:(g + 1) * P],
                                                    QT[s][:, c * P:(c + 1) * P], start=False, stop=True)
                    last.then_inc(av_ps.sem, 1)

                for s in S:
                    scores(0, s)
                for g in range(NH // 2):
                    for s in S:
                        if g + 1 < NH // 2:
                            scores(g + 1, s)
                        values(g, s)
                for s in S:
                    pe.wait_ge(ot_sb.sem, ot_sb.at(i, 6 + s + 1))
                    for c in range(NC_):
                        for g in range(NH // 2):
                            last = nc.tensor.matmul(m.bank[4 * s][:, c * P:(c + 1) * P], OT[s][:, g, c * P:(c + 1) * P],
                                                    w["wout"][:, g * D:(g + 1) * D], start=g == 0, stop=g == NH // 2 - 1)
                    last.then_inc(y_ps.sem, 1)


def modulated_ffn(ctx, nc, m):
    S = range(2)
    sig = lambda name, per: Signal(ctx, nc, "mf_" + name, per)
    w = m.w
    F = 512
    G4 = F // P
    late = [(n, *m.load(ctx, n)) for n in ("gfc1", "gfc1_b", "gfc2_rep", "gfc2_b", "task_b1", "b1", "ln_coef", "ln_rows",
                                            "task_b2", "gate_row", "gate_pad")]
    tv1, tv2 = m.KM[0], m.KM[1]
    tv1_in, tv2_in, w1_in, w2_in = (ctx.semaphore("loaded_" + n) for n in ("tv1", "tv2", "W1", "W2"))
    W1, W2 = m.ST[0][:, 0, :], m.ST[0][:, 1, :]
    W1M, W2M = m.t512a, m.t512b
    HH = [m.big[:, 16 * T + s * 4 * T:16 * T + (s + 1) * 4 * T].rearrange("p (g n) -> p g n", g=G4) for s in S]
    junk = [m.t512c[s][:, 0, :] for s in S]
    res = [m.XN[s] for s in S]
    GH = ctx.sb("mf_gate_hidden", [P, B])
    gcol = ctx.sb("mf_gate", [P, B])
    grow = ctx.sb("mf_gate_first", [P, B])
    b1m = ctx.sb("mf_b1m", [P, G4, B])
    lngb = ctx.sb("mf_ln", [P, 2 * D])
    gsel = [ctx.sb(f"mf_gsel{s}", [P, 48]) for s in S]
    gb2 = [ctx.sb(f"mf_gb2{s}", [P, P]) for s in S]
    norm, norm2 = Norm(ctx, nc, m, "mf"), Norm(ctx, nc, m, "mf2")
    xt_ps, xt_sb, gh_ps, gh_sb = sig("xt_ps", 2), sig("xt_sb", 2), sig("gh_ps", 2), sig("gh_sb", 2)
    gate_ps, gate_sb, small_ps, small_sb = sig("gate_ps", 0), sig("gate_sb", 0), sig("small_ps", 0), sig("small_sb", 0)
    gs_sb, xn_kept = sig("gs_sb", 2), sig("xn_kept", 32)
    XN = m.XN
    m1_ps, m1_sb, m2_ps, m2_sb = sig("m1_ps", 2), sig("m1_sb", 2), sig("m2_ps", 2), sig("m2_sb", 2)
    f_ps, f_sb, o_ps, r_sb, sc_sb, hb_sb, h_sb = (sig("f_ps", 8), sig("f_sb", 8), sig("o_ps", 2), sig("r_sb", 2), sig("sc_sb", 2),
                                                  sig("hb_sb", 2), sig("h_sb", 2))
    over = lambda v, n=NC_: v.rearrange("p (o t) -> p o t", o=1).broadcast_to([P, n, v.shape[-1]])

    with nc.Block() as block:
        @block.sync
        def _(sp):
            for _, t, sem, src in late:
                sp.dma_start(t[:, :], src).then_inc(sem, 16)
            sp.dma_start(tv1[:, :, :].rearrange("p a t -> p (a t)"), m.dram["task_W1"]).then_inc(tv1_in, 16)
            sp.dma_start(tv2[:, :, :].rearrange("p a t -> p (a t)"), m.dram["task_W2"]).then_inc(tv2_in, 16)
            sp.dma_start(W1, m.dram["W1"]).then_inc(w1_in, 16)
            sp.dma_start(W2, m.dram["W2"]).then_inc(w2_in, 16)
            with sp.Fori(0, PAIRS) as i:
                for s in S:
                    sp.wait_ge(norm.ready.sem, norm.ready.at(i, s + 1))
                    sp.dma_start(m.XNA[:, bass.ds((2 * i + s) * NC_, NC_), :], XN[s][:, :, :]).then_inc(xn_kept.sem, 16)

        @block.vector
        def _(dve):
            with dve.Fori(0, PAIRS) as i:
                hs = [m.h[:, bass.ds((2 * i + s) * NC_, NC_), :] for s in S]
                xs = [m.XNA[:, bass.ds((2 * i + s) * NC_, NC_), :] for s in S]
                norm.vector(dve, i, hs, [XN[s] for s in S])
                dve.wait_ge(xn_kept.sem, xn_kept.at(i, 32))
                dve.wait_ge(gh_sb.sem, gh_sb.at(i, 2))
            dve.wait_ge(gate_ps.sem, 1)
            dve.wait_ge(m.loaded["gfc2_b"], 16)
            nc.vector.tensor_scalar(gcol[:, :], m.bank[0][:, 0:B], 1.0 / T, w["gfc2_b"][:, 0:1], ALU.mult, ALU.add).then_inc(gate_sb.sem, 1)
            dve.wait_ge(gate_sb.sem, 1)
            dve.wait_ge(m.loaded["gate_row"], 16)
            nc.vector.tensor_scalar(grow[:, :], gcol[:, :], w["gate_row"][:, 0:1], None, ALU.mult).then_inc(gate_sb.sem, 1)
            dve.wait_ge(small_ps.sem, 1)
            dve.wait_ge(m.loaded["b1"], 16)
            nc.vector.tensor_tensor(b1m[:, :, :], m.bank[1][:, 0:G4 * B].rearrange("p (g b) -> p g b", g=G4),
                                    w["b1"][:, :].rearrange("p (g o) -> p g o", o=1).broadcast_to([P, G4, B]), ALU.add).then_inc(small_sb.sem, 1)
            nc.vector.tensor_copy(lngb[:, :], m.bank[2][:, 0:2 * D]).then_inc(small_sb.sem, 1)
            dve.wait_ge(gate_sb.sem, 2)
            dve.wait_ge(small_sb.sem, 2)
            for sem in (m.loaded["gate_pad"], w1_in, w2_in):
                dve.wait_ge(sem, 16)
            with dve.Fori(0, PAIRS) as i:
                hs = [m.h[:, bass.ds((2 * i + s) * NC_, NC_), :] for s in S]
                xs = [m.XNA[:, bass.ds((2 * i + s) * NC_, NC_), :] for s in S]
                for s in S:
                    nc.vector.tensor_scalar(gsel[s][:, :], w["gate_pad"][:, :], gcol[:, bass.ds(2 * i + s, 1)], None, ALU.mult)
                    nc.vector.tensor_scalar(gb2[s][:, :], w["ones"][:, 0:P], grow[:, bass.ds(2 * i + s, 1)], w["gate_row"][:, 1:2],
                                            ALU.mult, ALU.add).then_inc(gs_sb.sem, 1)
                for s in S:
                    dve.wait_ge(m1_ps.sem, m1_ps.at(i, s + 1))
                    nc.vector.tensor_tensor(W1M[s][:, :], m.bank[4 * s][:, :], W1, ALU.add).then_inc(m1_sb.sem, 1)
                for s in S:
                    dve.wait_ge(m2_ps.sem, m2_ps.at(i, s + 1))
                    nc.vector.tensor_tensor(W2M[s][:, :], m.bank[4 * s + 1][:, :], W2, ALU.add).then_inc(m2_sb.sem, 1)
                for s in S:
                    dve.wait_ge(o_ps.sem, o_ps.at(i, s + 1))
                    nc.vector.tensor_tensor(res[s][:, :, :], m.bank[4 * s][:, :].rearrange("p (c d) -> p c d", c=NC_), xs[s], ALU.add).then_inc(r_sb.sem, 1)
                dve.wait_ge(r_sb.sem, r_sb.at(i, 2))
                norm2.vector(dve, i, [res[s] for s in S], [res[s] for s in S])
                for s in S:
                    dve.wait_ge(norm2.ready.sem, norm2.ready.at(i, s + 1))
                    nc.vector.tensor_tensor(res[s][:, :, :], res[s][:, :, :], over(lngb[:, 0:D]), ALU.mult).then_inc(sc_sb.sem, 1)
                for s in S:
                    dve.wait_ge(sc_sb.sem, sc_sb.at(i, s + 1))
                    dve.wait_ge(hb_sb.sem, hb_sb.at(i, s + 1))
                    nc.vector.tensor_tensor(hs[s], hs[s], res[s][:, :, :], ALU.add).then_inc(h_sb.sem, 1)
                dve.wait_ge(h_sb.sem, h_sb.at(i, 2))

        @block.gpsimd
        def _(pool):
            with pool.Fori(0, PAIRS) as i:
                norm.gpsimd(pool, i)
            pool.wait_ge(small_sb.sem, 2)
            with pool.Fori(0, PAIRS) as i:
                for s in S:
                    hs = m.h[:, bass.ds((2 * i + s) * NC_, NC_), :]
                    nc.gpsimd.tensor_tensor(hs, hs, over(lngb[:, D:2 * D]), ALU.add).then_inc(hb_sb.sem, 1)
                norm2.gpsimd(pool, i)

        @block.scalar
        def _(act):
            act.wait_ge(m.loaded["gfc1_b"], 16)
            with act.Fori(0, PAIRS) as i:
                for s in S:
                    act.wait_ge(xt_ps.sem, xt_ps.at(i, s + 1))
                    nc.scalar.copy(m.XTA[:, bass.ds((2 * i + s) * T, T)], m.bank[4 * s][:, :]).then_inc(xt_sb.sem, 1)
                for s in S:
                    act.wait_ge(gh_ps.sem, gh_ps.at(i, s + 1))
                    nc.scalar.activation(junk[s], m.bank[4 * s + 1][:, :], ACT.Relu, bias=w["gfc1_b"][:, 0:1],
                                         accum_out=GH[:, bass.ds(2 * i + s, 1)]).then_inc(gh_sb.sem, 1)
            act.wait_ge(small_sb.sem, 1)
            with act.Fori(0, PAIRS) as i:
                for g in range(G4):
                    for s in S:
                        act.wait_ge(f_ps.sem, f_ps.at(i, 2 * g + s + 1))
                        nc.scalar.activation(HH[s][:, g, :], m.bank[4 * s + 2 + g % 2][:, :], ACT.Relu,
                                             bias=b1m[:, g, bass.ds(2 * i + s, 1)]).then_inc(f_sb.sem, 1)

        @block.tensor
        def _(pe):
            pe.wait_ge(m.loaded["gfc1"], 16)
            with pe.Fori(0, PAIRS) as i:
                for s in S:
                    pe.wait_ge(norm.ready.sem, norm.ready.at(i, s + 1))
                    for c in range(NC_):
                        last = nc.tensor.transpose(m.bank[4 * s][:, c * P:(c + 1) * P], XN[s][:, c, :], w["ident"][:, :])
                    last.then_inc(xt_ps.sem, 1)
                for s in S:
                    pe.wait_ge(xt_sb.sem, xt_sb.at(i, s + 1))
                    nc.tensor.matmul(m.bank[4 * s + 1][:, :], w["gfc1"][:, :], m.XTA[:, bass.ds((2 * i + s) * T, T)], start=True, stop=True).then_inc(gh_ps.sem, 1)
            for n in ("gfc2_rep", "task_b1", "ln_coef", "ln_rows", "task_b2"):
                pe.wait_ge(m.loaded[n], 16)
            pe.wait_ge(gh_sb.sem, B)
            nc.tensor.matmul(m.bank[0][:, 0:B], w["gfc2_rep"][:, :], GH[:, :], start=True, stop=True).then_inc(gate_ps.sem, 1)
            nc.tensor.matmul(m.bank[2][:, 0:2 * D], w["ln_coef"][:, :], w["ln_rows"][:, :], start=True, stop=True)
            pe.wait_ge(gate_sb.sem, 1)
            for g in range(G4):
                last = nc.tensor.matmul(m.bank[1][:, g * B:(g + 1) * B], w["task_b1"][:, g * P:(g + 1) * P], gcol[:, :], start=True, stop=True)
            last.then_inc(small_ps.sem, 1)
            pe.wait_ge(tv1_in, 16)
            pe.wait_ge(tv2_in, 16)
            pe.wait_ge(small_sb.sem, 2)
            with pe.Fori(0, PAIRS) as i:
                def merge(s, bank, tv):
                    for j in range(2):
                        for q in range(NC_):
                            last = nc.tensor.matmul(bank[32 * q:32 * q + 32, :], gsel[s][:, 16 - 16 * j:48 - 16 * j], tv[:, 2 * q + j, :],
                                                    start=j == 0, stop=j == 1)
                    return last
                for s in S:
                    pe.wait_ge(gs_sb.sem, gs_sb.at(i, s + 1))
                    merge(s, m.bank[4 * s], tv1).then_inc(m1_ps.sem, 1)
                for s in S:
                    merge(s, m.bank[4 * s + 1], tv2).then_inc(m2_ps.sem, 1)
                for g in range(G4):
                    for s in S:
                        if g == 0:
                            pe.wait_ge(m1_sb.sem, m1_sb.at(i, s + 1))
                        if g >= 2:
                            pe.wait_ge(f_sb.sem, f_sb.at(i, 2 * (g - 2) + s + 1))
                        nc.tensor.matmul(m.bank[4 * s + 2 + g % 2][:, :], W1M[s][:, g * P:(g + 1) * P], m.XTA[:, bass.ds((2 * i + s) * T, T)],
                                         start=True, stop=True).then_inc(f_ps.sem, 1)
                for s in S:
                    pe.wait_ge(m2_sb.sem, m2_sb.at(i, s + 1))
                    pe.wait_ge(f_sb.sem, f_sb.at(i, 6 + s + 1))
                    for c in range(NC_):
                        nc.tensor.matmul(m.bank[4 * s][:, c * P:(c + 1) * P], gb2[s][:, :], w["task_b2"][:, :], start=True, stop=False)
                        for g in range(G4):
                            last = nc.tensor.matmul(m.bank[4 * s][:, c * P:(c + 1) * P], HH[s][:, g, c * P:(c + 1) * P],
                                                    W2M[s][:, g * D:(g + 1) * D], start=False, stop=g == G4 - 1)
                    last.then_inc(o_ps.sem, 1)


def retention(ctx, nc, m):
    S = range(2)
    sig = lambda name, per: Signal(ctx, nc, "re_" + name, per)
    w = m.w
    late = [(n, *m.load(ctx, n)) for n in ("r_wq", "r_wk", "r_wv", "r_wg", "r_wo", "gn", "decay_q", "decay_k")]
    XN, XT, QT, KT, KM, KTOK, ST = m.XN, m.XT, m.t512a, m.t512b, m.KM, m.KTOK, m.ST
    G = [m.t512c[s][:, 0, :] for s in S]
    TH = [m.t512c[s][:, 1, :] for s in S]
    A = [m.big[:, s * 8 * T:(s + 1) * 8 * T].rearrange("p (a c t) -> p a c t", a=NH, c=NC_) for s in S]
    VP = [[m.big[:, (16 + 2 * s + par) * T:(17 + 2 * s + par) * T].rearrange("p (c n) -> p c n", c=NC_) for par in range(2)] for s in S]
    V = [m.big[:, (20 + s) * T:(21 + s) * T].rearrange("p (c n) -> p c n", c=NC_) for s in S]
    Y = [m.big[:, (22 + s) * T:(23 + s) * T] for s in S]
    SQ = [ST[s][:, 1, :] for s in S]
    group = lambda v: v.rearrange("p (n k) -> p n k", k=DH)
    wide = lambda v: v.rearrange("p (n o) -> p n o", o=1).broadcast_to([P, NC_ * NH, DH])
    gsum = [ctx.sb(f"re_gsum{s}", [P, NC_ * NH]) for s in S]
    gvar = [ctx.sb(f"re_gvar{s}", [P, NC_ * NH]) for s in S]
    norm = Norm(ctx, nc, m, "re")
    xt_ps, xt_sb, qk_ps, qk_sb = sig("xt_ps", 2), sig("xt_sb", 2), sig("qk_ps", 4), sig("qk_sb", 4)
    g_ps, g_sb, v_ps, v_sb = sig("g_ps", 2), sig("g_sb", 2), sig("v_ps", 2), sig("v_sb", 2)
    km_d, km_a, kt_ps, kt_sb = sig("km_d", 2), sig("km_a", 2), sig("kt_ps", 2), sig("kt_sb", 2)
    st_ps, st_sb, sc_ps, a_sb = sig("st_ps", 6), sig("st_sb", 6), sig("sc_ps", 16), sig("a_sb", 16)
    av_ps, ot_sb, tok_ps, y_sb = sig("av_ps", 2), sig("ot_sb", 2), sig("tok_ps", 2), sig("y_sb", 2)
    gstep, sq_sb, root_in, root, gn_sb = sig("gstep", 8), sig("sq_sb", 2), sig("root_in", 2), sig("root", 2), sig("gn_sb", 2)
    ch_ps, ch_sb, sum_sb, th_sb, z_sb, y_ps, h_sb = (sig("ch_ps", 2), sig("ch_sb", 2), sig("sum_sb", 2), sig("th_sb", 2), sig("z_sb", 2),
                                                     sig("y_ps", 2), sig("h_sb", 2))
    zeroed = sig("zeroed", 0)
    NS = NC_ - 1
    ND = 3

    with nc.Block() as block:
        @block.sync
        def _(sp):
            for _, t, sem, src in late:
                sp.dma_start(t[:, :], src).then_inc(sem, 16)

        @block.vector
        def _(dve):
            for n in ("decay_q", "decay_k"):
                dve.wait_ge(m.loaded[n], 16)
            with dve.Fori(0, PAIRS) as i:
                hs = [m.h[:, bass.ds((2 * i + s) * NC_, NC_), :] for s in S]
                norm.vector(dve, i, hs, [XN[s] for s in S])
                for q in range(2):
                    for s in S:
                        dve.wait_ge(qk_ps.sem, qk_ps.at(i, 2 * q + s + 1))
                        nc.vector.tensor_tensor((QT, KT)[q][s][:, :], m.bank[4 * s + 1 + q][:, :], w[("decay_q", "decay_k")[q]][:, :],
                                                ALU.mult).then_inc(qk_sb.sem, 1)
                for s in S:
                    dve.wait_ge(qk_sb.sem, qk_sb.at(i, 3 + s))
                    for hd in range(ND):
                        last = nc.vector.tensor_scalar(KM[s][:, hd, :], KT[s][:, :], w["head_col"][:, hd:hd + 1], None, ALU.mult)
                    last.then_inc(km_d.sem, 1)
                for c in range(NS):
                    for s in S:
                        dve.wait_ge(st_ps.sem, st_ps.at(i, 2 * c + s + 1))
                        nc.vector.tensor_tensor(ST[s][:, 0, c * P:(c + 1) * P], m.bank[4 * s + 3][:, 0:P], w["same_head"][:, :], ALU.mult).then_inc(st_sb.sem, 1)
                for g in range(NH // 2):
                    for s in S:
                        for par in range(2):
                            dve.wait_ge(sc_ps.sem, sc_ps.at(i, 4 * g + 2 * s + par + 1))
                            nc.vector.tensor_tensor(A[s][:, 2 * g + par, :, :], m.bank[4 * s + par][:, :].rearrange("p (c t) -> p c t", c=NC_),
                                                    w["causal"][:, :].rearrange("p (o t) -> p o t", o=1).broadcast_to([P, NC_, P]),
                                                    ALU.mult).then_inc(a_sb.sem, 1)
                for s in S:
                    dve.wait_ge(y_sb.sem, y_sb.at(i, s + 1))
                    nc.vector.tensor_reduce(gsum[s][:, :], group(Y[s]), AX.X, ALU.add).then_inc(gstep.sem, 1)
                for s in S:
                    dve.wait_ge(gstep.sem, gstep.at(i, s + 1))
                    nc.vector.tensor_scalar(gsum[s][:, :], gsum[s][:, :], 1.0 / DH, None, ALU.mult).then_inc(gstep.sem, 1)
                for s in S:
                    dve.wait_ge(gstep.sem, gstep.at(i, 2 + s + 1))
                    nc.vector.tensor_tensor(group(Y[s]), group(Y[s]), wide(gsum[s][:, :]), ALU.subtract).then_inc(gstep.sem, 1)
                for s in S:
                    dve.wait_ge(sq_sb.sem, sq_sb.at(i, s + 1))
                    nc.vector.tensor_reduce(gvar[s][:, :], group(SQ[s]), AX.X, ALU.add).then_inc(gstep.sem, 1)
                for s in S:
                    dve.wait_ge(gstep.sem, gstep.at(i, 6 + s + 1))
                    nc.vector.tensor_scalar(gvar[s][:, :], gvar[s][:, :], 1.0 / DH, LN_EPS, ALU.mult, ALU.add).then_inc(root_in.sem, 1)
                for s in S:
                    dve.wait_ge(root.sem, root.at(i, s + 1))
                    nc.vector.tensor_tensor(group(Y[s]), group(Y[s]), wide(gvar[s][:, :]), ALU.mult).then_inc(gn_sb.sem, 1)
                for s in S:
                    dve.wait_ge(ch_sb.sem, ch_sb.at(i, s + 1))
                    nc.vector.tensor_tensor(G[s], G[s], SQ[s], ALU.add).then_inc(sum_sb.sem, 1)
                for s in S:
                    dve.wait_ge(th_sb.sem, th_sb.at(i, s + 1))
                    nc.vector.scalar_tensor_tensor(G[s], TH[s], 1.0, G[s], ALU.add, ALU.mult).then_inc(z_sb.sem, 1)
                for s in S:
                    dve.wait_ge(y_ps.sem, y_ps.at(i, s + 1))
                    nc.vector.scalar_tensor_tensor(hs[s], m.bank[4 * s][:, :].rearrange("p (c d) -> p c d", c=NC_), 0.5, hs[s],
                                                   ALU.mult, ALU.add).then_inc(h_sb.sem, 1)
                dve.wait_ge(h_sb.sem, h_sb.at(i, 2))

        @block.gpsimd
        def _(pool):
            for s in S:
                for par in range(2):
                    nc.gpsimd.memset(VP[s][par][:, :, :], 0.0).then_inc(zeroed.sem, 1)
            pool.wait_ge(zeroed.sem, 4)
            with pool.Fori(0, PAIRS) as i:
                norm.gpsimd(pool, i)
                for s in S:
                    pool.wait_ge(root_in.sem, root_in.at(i, s + 1))
                    nc.gpsimd.tensor_tensor(gvar[s][:, :], gvar[s][:, :], m.minus_half[:, 0:NC_ * NH], ALU.pow).then_inc(root.sem, 1)

        @block.scalar
        def _(act):
            act.wait_ge(m.loaded["gn"], 16)
            act.wait_ge(zeroed.sem, 4)
            half = lambda v, par: v.rearrange("p c (g a k) -> p (c g) a k", a=2, k=DH)[:, :, par, :]
            with act.Fori(0, PAIRS) as i:
                for s in S:
                    act.wait_ge(xt_ps.sem, xt_ps.at(i, s + 1))
                    nc.scalar.copy(XT[s][:, :], m.bank[4 * s][:, :]).then_inc(xt_sb.sem, 1)
                for s in S:
                    act.wait_ge(g_ps.sem, g_ps.at(i, s + 1))
                    nc.scalar.copy(G[s], m.bank[4 * s + 3][:, :]).then_inc(g_sb.sem, 1)
                for s in S:
                    act.wait_ge(v_ps.sem, v_ps.at(i, s + 1))
                    v = m.bank[4 * s + 2][:, :].rearrange("p (c n) -> p c n", c=NC_)
                    for par in range(2):
                        nc.scalar.copy(half(VP[s][par][:, :, :], par), half(v, par))
                    nc.scalar.copy(V[s][:, :, :], v).then_inc(v_sb.sem, 1)
                for s in S:
                    act.wait_ge(kt_ps.sem, kt_ps.at(i, s + 1))
                    nc.scalar.copy(KTOK[s][:, :, :], m.bank[4 * s + 1][:, 0:NS * P].rearrange("p (c k) -> p c k", c=NS)).then_inc(kt_sb.sem, 1)
                for s in S:
                    act.wait_ge(qk_sb.sem, qk_sb.at(i, 3 + s))
                    for hd in range(ND, NH):
                        last = nc.scalar.activation(KM[s][:, hd, :], KT[s][:, :], ACT.Copy, scale=w["head_col"][:, hd:hd + 1])
                    last.then_inc(km_a.sem, 1)
                for s in S:
                    act.wait_ge(av_ps.sem, av_ps.at(i, s + 1))
                    nc.scalar.copy(SQ[s], m.bank[4 * s + 2][:, :]).then_inc(ot_sb.sem, 1)
                for s in S:
                    act.wait_ge(tok_ps.sem, tok_ps.at(i, s + 1))
                    nc.scalar.copy(Y[s], m.bank[4 * s + 3][:, :]).then_inc(y_sb.sem, 1)
                for s in S:
                    act.wait_ge(gstep.sem, gstep.at(i, 4 + s + 1))
                    nc.scalar.activation(SQ[s], Y[s], ACT.Square).then_inc(sq_sb.sem, 1)
                for s in S:
                    act.wait_ge(ch_ps.sem, ch_ps.at(i, s + 1))
                    nc.scalar.activation(SQ[s], m.bank[4 * s + 3][:, :], ACT.Identity, scale=w["gn"][:, 0:1], bias=w["gn"][:, 1:2]).then_inc(ch_sb.sem, 1)
                for s in S:
                    act.wait_ge(sum_sb.sem, sum_sb.at(i, s + 1))
                    nc.scalar.activation(TH[s], G[s], ACT.Tanh, scale=0.5).then_inc(th_sb.sem, 1)

        @block.tensor
        def _(pe):
            for n in ("r_wq", "r_wk", "r_wv", "r_wg", "r_wo"):
                pe.wait_ge(m.loaded[n], 16)
            with pe.Fori(0, PAIRS) as i:
                for s in S:
                    pe.wait_ge(norm.ready.sem, norm.ready.at(i, s + 1))
                    for c in range(NC_):
                        last = nc.tensor.transpose(m.bank[4 * s][:, c * P:(c + 1) * P], XN[s][:, c, :], w["ident"][:, :])
                    last.then_inc(xt_ps.sem, 1)
                for s in S:
                    pe.wait_ge(xt_sb.sem, xt_sb.at(i, s + 1))
                    nc.tensor.matmul(m.bank[4 * s + 1][:, :], w["r_wq"][:, :], XT[s][:, :], start=True, stop=True).then_inc(qk_ps.sem, 1)
                for s in S:
                    nc.tensor.matmul(m.bank[4 * s + 2][:, :], w["r_wk"][:, :], XT[s][:, :], start=True, stop=True).then_inc(qk_ps.sem, 1)
                for s in S:
                    nc.tensor.matmul(m.bank[4 * s + 3][:, :], w["r_wg"][:, :], XT[s][:, :], start=True, stop=True).then_inc(g_ps.sem, 1)
                for s in S:
                    pe.wait_ge(qk_sb.sem, qk_sb.at(i, 3 + s))
                    for c in range(NC_):
                        last = nc.tensor.matmul(m.bank[4 * s + 2][:, c * P:(c + 1) * P], XT[s][:, c * P:(c + 1) * P], w["r_wv"][:, :], start=True, stop=True)
                    last.then_inc(v_ps.sem, 1)
                    for c in range(NS):
                        last = nc.tensor.transpose(m.bank[4 * s + 1][:, c * P:(c + 1) * P], KT[s][:, c * P:(c + 1) * P], w["ident"][:, :])
                    last.then_inc(kt_ps.sem, 1)
                for c in range(NS):
                    for s in S:
                        if c == 0:
                            pe.wait_ge(kt_sb.sem, kt_sb.at(i, s + 1))
                            pe.wait_ge(v_sb.sem, v_sb.at(i, s + 1))
                            pe.wait_ge(g_sb.sem, g_sb.at(i, s + 1))
                        else:
                            pe.wait_ge(st_sb.sem, st_sb.at(i, 2 * (c - 1) + s + 1))
                        nc.tensor.matmul(m.bank[4 * s + 3][:, 0:P], KTOK[s][:, c, :], V[s][:, c, :],
                                         start=c == 0, stop=c == NS - 1, skip_group_check=True).then_inc(st_ps.sem, 1)
                for g in range(NH // 2):
                    for s in S:
                        if g == 0:
                            pe.wait_ge(km_d.sem, km_d.at(i, s + 1))
                        if g == ND // 2:
                            pe.wait_ge(km_a.sem, km_a.at(i, s + 1))
                        for par in range(2):
                            if g:
                                pe.wait_ge(a_sb.sem, a_sb.at(i, 4 * (g - 1) + 2 * s + par + 1))
                            for c in range(NC_):
                                last = nc.tensor.matmul(m.bank[4 * s + par][:, c * P:(c + 1) * P], KM[s][:, 2 * g + par, c * P:(c + 1) * P],
                                                        QT[s][:, c * P:(c + 1) * P], start=True, stop=True)
                            last.then_inc(sc_ps.sem, 1)
                for s in S:
                    pe.wait_ge(a_sb.sem, a_sb.at(i, 12 + 2 * s + 2))
                    pe.wait_ge(st_sb.sem, st_sb.at(i, 2 * (NS - 1) + s + 1))
                    for c in range(NC_):
                        for par in range(2):
                            for g in range(NH // 2):
                                last = nc.tensor.matmul(m.bank[4 * s + 2][32 * g:32 * g + 32, c * P:(c + 1) * P],
                                                        VP[s][par][:, c, 32 * g:32 * g + 32], A[s][:, 2 * g + par, c, :],
                                                        start=par == 0, stop=par == 1 and c == 0)
                        if c:
                            last = nc.tensor.matmul(m.bank[4 * s + 2][:, c * P:(c + 1) * P], ST[s][:, 0, (c - 1) * P:c * P],
                                                    QT[s][:, c * P:(c + 1) * P], start=False, stop=True)
                    last.then_inc(av_ps.sem, 1)
                for s in S:
                    pe.wait_ge(ot_sb.sem, ot_sb.at(i, s + 1))
                    for c in range(NC_):
                        last = nc.tensor.transpose(m.bank[4 * s + 3][:, c * P:(c + 1) * P], SQ[s][:, c * P:(c + 1) * P], w["ident"][:, :])
                    last.then_inc(tok_ps.sem, 1)
                for s in S:
                    pe.wait_ge(gn_sb.sem, gn_sb.at(i, s + 1))
                    for c in range(NC_):
                        last = nc.tensor.transpose(m.bank[4 * s + 3][:, c * P:(c + 1) * P], Y[s][:, c * P:(c + 1) * P], w["ident"][:, :])
                    last.then_inc(ch_ps.sem, 1)
                for s in S:
                    pe.wait_ge(z_sb.sem, z_sb.at(i, s + 1))
                    for c in range(NC_):
                        last = nc.tensor.matmul(m.bank[4 * s][:, c * P:(c + 1) * P], G[s][:, c * P:(c + 1) * P], w["r_wo"][:, :], start=True, stop=True)
                    last.then_inc(y_ps.sem, 1)


def balanced_experts(ctx, nc, m):
    S = range(2)
    E, M, ITERS = 8, T // 8, 8
    BE = B * E
    sig = lambda name, per: Signal(ctx, nc, "be_" + name, per)
    w = m.w
    late = [(n, *m.load(ctx, n)) for n in ("gate_w", "experts", "later_expert")]
    XN, XT, XTA = m.XN, m.XT, m.XTA
    G = m.big[:, 0:NC_ * BE]
    G4 = G.rearrange("p (c b e) -> p c b e", c=NC_, b=B)
    GR = G.rearrange("p (n e) -> p n e", e=E)
    rowsum = ctx.sb("be_rowsum", [P, NC_ * B])
    colsum = ctx.sb("be_colsum", [P, BE])
    GT, WK0, WK1, SEL, EQ, PRE = (m.big[:, (1 + n) * T:(2 + n) * T] for n in range(6))
    WK = (WK0, WK1)
    m8 = ctx.sb("be_m8", [BE, 8, 8])
    small = ctx.sb("be_small", [BE, 2])
    WT = m.big[:, 7 * T:7 * T + NC_ * BE]
    WT4 = WT.rearrange("p (c b e) -> p c b e", c=NC_, b=B)
    YW = [m.KM[s][:, 0:4, :].rearrange("p a (x d) -> p (a x) d", d=D) for s in S]
    YR = [m.t512a[s] for s in S]
    norm = Norm(ctx, nc, m, "be")
    xt_ps, xt_sb, xt_kept, lg_ps, lg_sb = sig("xt_ps", 2), sig("xt_sb", 2), sig("xt_kept", 32), sig("lg_ps", 2), sig("lg_sb", 2)
    step, col_in, col_ps = sig("step", 5), sig("col_in", 1), sig("col_ps", 1)
    gt_ps, pick, sel_in, later_ps, w_in, w_ps, w_sb = (sig("gt_ps", 0), sig("pick", 0), sig("sel_in", 0), sig("later_ps", 0),
                                                       sig("w_in", 0), sig("w_ps", 0), sig("w_sb", 0))
    zeroed = sig("zeroed", 0)
    x_sb = [sig(f"x_sb{s}", 16) for s in S]
    y_ps, yw_sb, yr_sb, h_sb = sig("y_ps", 8), sig("yw_sb", 8), sig("yr_sb", 8), sig("h_sb", 2)

    with nc.Block() as block:
        @block.sync
        def _(sp):
            for _, t, sem, src in late:
                sp.dma_start(t[:, :], src).then_inc(sem, 16)
            with sp.Fori(0, PAIRS) as i:
                for s in S:
                    sp.wait_ge(xt_sb.sem, xt_sb.at(i, s + 1))
                    sp.dma_start(XTA[:, bass.ds((2 * i + s) * T, T)], XT[s][:, :]).then_inc(xt_kept.sem, 16)
            sp.wait_ge(xt_kept.sem, 16 * B)
            sp.wait_ge(lg_sb.sem, B)
            for s in S:
                sp.dma_start(XT[s][:, :], XTA[:, s * T:(s + 1) * T]).then_inc(x_sb[s].sem, 16)
            with sp.Fori(1, PAIRS) as i:
                for s in S:
                    if s == 0:
                        sp.wait_ge(y_ps.sem, y_ps.at(i, 0))
                    sp.dma_start(XT[s][:, :], XTA[:, bass.ds((2 * i + s) * T, T)]).then_inc(x_sb[s].sem, 16)

        @block.vector
        def _(dve):
            nc.vector.memset(SEL[BE:P, :], 0.0).then_inc(zeroed.sem, 1)
            with dve.Fori(0, PAIRS) as i:
                hs = [m.h[:, bass.ds((2 * i + s) * NC_, NC_), :] for s in S]
                norm.vector(dve, i, hs, [XN[s] for s in S])
                for s in S:
                    dve.wait_ge(lg_ps.sem, lg_ps.at(i, s + 1))
                    nc.vector.tensor_scalar(G4[:, :, bass.ds(2 * i + s, 1), :].rearrange("p c o e -> p c (o e)"),
                                            m.bank[4 * s + 1][:, 0:NC_ * E].rearrange("p (c e) -> p c e", c=NC_), 1e-6, None, ALU.max).then_inc(lg_sb.sem, 1)
                dve.wait_ge(lg_sb.sem, lg_sb.at(i, 2))
                dve.wait_ge(xt_kept.sem, xt_kept.at(i, 32))
            nc.vector.tensor_copy(colsum[:, :], m.w["ones"][:, 0:BE]).then_inc(lg_sb.sem, 1)
            dve.wait_ge(lg_sb.sem, B + 1)
            with dve.Fori(0, ITERS) as k:
                dve.wait_ge(col_ps.sem, col_ps.at(k, 1))
                nc.vector.tensor_reduce(colsum[:, :], m.bank[0][:, 0:NC_ * BE].rearrange("p (c n) -> p n c", c=NC_), AX.X, ALU.add).then_inc(step.sem, 1)
                dve.wait_ge(step.sem, step.at(k, 1))
                nc.vector.reciprocal(colsum[:, :], colsum[:, :]).then_inc(step.sem, 1)
                dve.wait_ge(step.sem, step.at(k, 2))
                nc.vector.tensor_tensor(G.rearrange("p (c n) -> p c n", c=NC_), G.rearrange("p (c n) -> p c n", c=NC_),
                                        colsum[:, :].rearrange("p (o n) -> p o n", o=1).broadcast_to([P, NC_, BE]), ALU.mult).then_inc(step.sem, 1)
                dve.wait_ge(step.sem, step.at(k, 3))
                nc.vector.tensor_reduce(rowsum[:, :], GR, AX.X, ALU.add).then_inc(step.sem, 1)
                dve.wait_ge(step.sem, step.at(k, 4))
                nc.vector.reciprocal(rowsum[:, :], rowsum[:, :]).then_inc(step.sem, 1)
                dve.wait_ge(step.sem, step.at(k, 5))
                nc.vector.tensor_tensor(GR, GR, rowsum[:, :].rearrange("p (n o) -> p n o", o=1).broadcast_to([P, NC_ * B, E]), ALU.mult).then_inc(col_in.sem, 1)
            chain = [0]

            def link(ins):
                chain[0] += 1
                ins.then_inc(pick.sem, 1)
                dve.wait_ge(pick.sem, chain[0])

            dve.wait_ge(gt_ps.sem, 1)
            nc.vector.tensor_copy(WK0[0:BE, :], m.bank[1][0:BE, :])
            link(nc.vector.tensor_copy(GT[0:BE, :], m.bank[1][0:BE, :]))
            for r in range(M // 8):
                link(nc.vector.max(m8[:, r, :], WK[r % 2][0:BE, :]))
                if r < M // 8 - 1:
                    link(nc.vector.match_replace(WK[(r + 1) % 2][0:BE, :], m8[:, r, :], WK[r % 2][0:BE, :], -1.0))
            least = m8[:, M // 8 - 1, 7:8]
            above, need = small[:, 0:1], small[:, 1:2]
            dve.wait_ge(zeroed.sem, 1)
            link(nc.vector.tensor_scalar(SEL[0:BE, :], GT[0:BE, :], least, None, ALU.is_gt))
            link(nc.vector.tensor_reduce(above, SEL[0:BE, :], AX.X, ALU.add))
            nc.vector.tensor_scalar(EQ[0:BE, :], GT[0:BE, :], least, None, ALU.is_equal)
            link(nc.vector.tensor_scalar(need, above, -1.0, float(M), ALU.mult, ALU.add))
            link(nc.vector.tensor_tensor_scan(PRE[0:BE, :], w["ones"][0:BE, :], EQ[0:BE, :], 0.0, ALU.mult, ALU.add))
            link(nc.vector.scalar_tensor_tensor(PRE[0:BE, :], PRE[0:BE, :], need, EQ[0:BE, :], ALU.is_le, ALU.mult))
            nc.vector.tensor_tensor(SEL[0:BE, :], SEL[0:BE, :], PRE[0:BE, :], ALU.add).then_inc(sel_in.sem, 1)
            dve.wait_ge(sel_in.sem, 1)
            dve.wait_ge(later_ps.sem, 1)
            link(nc.vector.scalar_tensor_tensor(EQ[0:BE, :], m.bank[2][0:BE, :], 0.0, SEL[0:BE, :], ALU.is_equal, ALU.mult))
            nc.vector.tensor_tensor(SEL[0:BE, :], EQ[0:BE, :], GT[0:BE, :], ALU.mult).then_inc(w_in.sem, 1)
            dve.wait_ge(w_ps.sem, 1)
            nc.vector.tensor_copy(WT.rearrange("p (c n) -> p c n", c=NC_), m.bank[3][:, :].rearrange("p (c n) -> p c n", c=NC_)[:, :, 0:BE]).then_inc(w_sb.sem, 1)
            dve.wait_ge(w_sb.sem, 1)
            with dve.Fori(0, PAIRS) as i:
                hs = [m.h[:, bass.ds((2 * i + s) * NC_, NC_), :] for s in S]
                for c in range(NC_):
                    for s in S:
                        n = 2 * c + s + 1
                        wc = WT4[:, c, bass.ds(2 * i + s, 1), :].rearrange("p o e -> p (o e)")
                        dve.wait_ge(y_ps.sem, y_ps.at(i, n))
                        for q in range(2):
                            last = nc.vector.tensor_tensor(YW[s][:, 8 * (c % 2) + 4 * q:8 * (c % 2) + 4 * q + 4, :],
                                                           m.bank[4 * s + 2 * (c % 2) + q][:, :].rearrange("p (e d) -> p e d", d=D),
                                                           wc[:, 4 * q:4 * q + 4].rearrange("p (e o) -> p e o", o=1).broadcast_to([P, 4, D]), ALU.mult)
                        last.then_inc(yw_sb.sem, 1)
                    for s in S:
                        dve.wait_ge(yw_sb.sem, yw_sb.at(i, 2 * c + s + 1))
                        nc.vector.tensor_reduce(YR[s][:, c * D:(c + 1) * D], YW[s][:, 8 * (c % 2):8 * (c % 2) + 8, :].rearrange("p e d -> p d e"),
                                                AX.X, ALU.add).then_inc(yr_sb.sem, 1)
                for s in S:
                    dve.wait_ge(yr_sb.sem, yr_sb.at(i, 6 + s + 1))
                    nc.vector.tensor_tensor(hs[s], hs[s], YR[s][:, :].rearrange("p (c d) -> p c d", c=NC_), ALU.add).then_inc(h_sb.sem, 1)
                dve.wait_ge(h_sb.sem, h_sb.at(i, 2))

        @block.gpsimd
        def _(pool):
            with pool.Fori(0, PAIRS) as i:
                norm.gpsimd(pool, i)

        @block.scalar
        def _(act):
            with act.Fori(0, PAIRS) as i:
                for s in S:
                    act.wait_ge(xt_ps.sem, xt_ps.at(i, s + 1))
                    nc.scalar.copy(XT[s][:, :], m.bank[4 * s][:, :]).then_inc(xt_sb.sem, 1)

        @block.tensor
        def _(pe):
            for n in ("gate_w", "experts", "later_expert"):
                pe.wait_ge(m.loaded[n], 16)
            with pe.Fori(0, PAIRS) as i:
                for s in S:
                    pe.wait_ge(norm.ready.sem, norm.ready.at(i, s + 1))
                    for c in range(NC_):
                        last = nc.tensor.transpose(m.bank[4 * s][:, c * P:(c + 1) * P], XN[s][:, c, :], w["ident"][:, :])
                    last.then_inc(xt_ps.sem, 1)
                for s in S:
                    pe.wait_ge(xt_sb.sem, xt_sb.at(i, s + 1))
                    for c in range(NC_):
                        last = nc.tensor.matmul(m.bank[4 * s + 1][:, c * E:(c + 1) * E], XT[s][:, c * P:(c + 1) * P], w["gate_w"][:, :], start=True, stop=True)
                    last.then_inc(lg_ps.sem, 1)
            pe.wait_ge(lg_sb.sem, B + 1)
            with pe.Fori(0, ITERS) as k:
                nc.tensor.matmul(m.bank[0][:, 0:NC_ * BE], w["ones"][:, 0:P], G, start=True, stop=True).then_inc(col_ps.sem, 1)
                pe.wait_ge(col_in.sem, col_in.at(k, 1))
            for c in range(NC_):
                last = nc.tensor.transpose(m.bank[1][0:BE, c * P:(c + 1) * P], G[:, c * BE:(c + 1) * BE], w["ident"][:, :])
            last.then_inc(gt_ps.sem, 1)
            pe.wait_ge(zeroed.sem, 1)
            pe.wait_ge(sel_in.sem, 1)
            nc.tensor.matmul(m.bank[2][0:BE, :], w["later_expert"][:, :], SEL, start=True, stop=True).then_inc(later_ps.sem, 1)
            pe.wait_ge(w_in.sem, 1)
            for c in range(NC_):
                last = nc.tensor.transpose(m.bank[3][:, c * P:(c + 1) * P], SEL[:, c * P:(c + 1) * P], w["ident"][:, :])
            last.then_inc(w_ps.sem, 1)
            pe.wait_ge(w_sb.sem, 1)
            with pe.Fori(0, PAIRS) as i:
                for c in range(NC_):
                    for s in S:
                        if c == 0:
                            pe.wait_ge(x_sb[s].sem, x_sb[s].at(i, 16))
                        if c >= 2:
                            pe.wait_ge(yw_sb.sem, yw_sb.at(i, 2 * (c - 2) + s + 1))
                        for q in range(2):
                            last = nc.tensor.matmul(m.bank[4 * s + 2 * (c % 2) + q][:, :], XT[s][:, c * P:(c + 1) * P],
                                                    w["experts"][:, 512 * q:512 * q + 512], start=True, stop=True)
                        last.then_inc(y_ps.sem, 1)
                pe.wait_ge(yw_sb.sem, yw_sb.at(i, 8))


def additive_attention(ctx, nc, m):
    S = range(2)
    U, GQ, CG = 64, 64, 4
    KS = GQ // CG
    NBUF = 4
    sig = lambda name, per: Signal(ctx, nc, "aa_" + name, per)
    w = m.w
    late = [(n, *m.load(ctx, n)) for n in ("a_wx", "a_wt", "a_bt", "a_wa", "a_ba")]
    XN, XT = m.XN, m.XT
    XA = m.big[:, 0:NT * (D + 1)].rearrange("p (n d) -> p n d", d=D + 1)
    o = NT * (D + 1)
    KU = m.big[:, o:o + PAIRS * T]
    QU = m.big[:, o + PAIRS * T:o + 2 * PAIRS * T]
    ARG = [m.KM[n // 2][:, 4 * (n % 2):4 * (n % 2) + 4, :] for n in range(NBUF)]
    EX = [m.t512a[g] for g in range(2)]
    ET = m.t512c[0][:, :, :].rearrange("p a t -> p (a t)").rearrange("p (j r) -> p j r", j=NC_)
    ssum = ctx.sb("aa_sum", [P, 2])
    norm = Norm(ctx, nc, m, "aa")
    ones_in = sig("ones_in", 0)
    xt_ps, xt_sb, kq_ps, kq_sb, xa_kept = sig("xt_ps", 2), sig("xt_sb", 2), sig("kq_ps", 2), sig("kq_sb", 2), sig("xa_kept", 32)
    arg, th, used = sig("arg", 2 * KS), sig("th", 2 * KS), sig("used", 2 * KS)
    ex, tr_ps, et, o_ps, den, h_sb = sig("ex", 2), sig("tr_ps", 2), sig("et", 2), sig("o_ps", 1), sig("den", 2), sig("h_sb", 2)
    EPS = 1e-7

    with nc.Block() as block:
        @block.sync
        def _(sp):
            for _, t, sem, src in late:
                sp.dma_start(t[:, :], src).then_inc(sem, 16)
            sp.wait_ge(ones_in.sem, 1)
            with sp.Fori(0, PAIRS) as i:
                for s in S:
                    sp.wait_ge(norm.ready.sem, norm.ready.at(i, s + 1))
                    sp.dma_start(XA[:, bass.ds((2 * i + s) * NC_, NC_), 0:D], XN[s][:, :, :]).then_inc(xa_kept.sem, 16)

        @block.gpsimd
        def _(pool):
            nc.gpsimd.memset(XA[:, :, D:D + 1], 1.0).then_inc(ones_in.sem, 1)
            with pool.Fori(0, PAIRS) as i:
                norm.gpsimd(pool, i)

        @block.vector
        def _(dve):
            with dve.Fori(0, PAIRS) as i:
                hs = [m.h[:, bass.ds((2 * i + s) * NC_, NC_), :] for s in S]
                norm.vector(dve, i, hs, [XN[s] for s in S])
                dve.wait_ge(xa_kept.sem, xa_kept.at(i, 32))
                dve.wait_ge(kq_sb.sem, kq_sb.at(i, 2))
            with dve.Fori(0, PAIRS) as i:
                ku = KU[:, bass.ds(i * T, T)]
                with dve.Fori(0, NC_) as c:
                    n = i * NC_ + c
                    for g in range(2):
                        for k in range(KS):
                            step = g * KS + k
                            if step >= NBUF:
                                dve.wait_ge(used.sem, used.at(n, step - NBUF + 1))
                            for cc in range(CG):
                                q = QU[:, bass.ds(n * P + g * GQ + cc * KS + k, 1)]
                                last = nc.vector.tensor_scalar(ARG[step % NBUF][:, cc, :], ku, q, None, ALU.add)
                            last.then_inc(arg.sem, 1)
                    for g in range(2):
                        dve.wait_ge(tr_ps.sem, tr_ps.at(n, g + 1))
                        nc.vector.tensor_copy(ET[:, :, g * P:(g + 1) * P], m.bank[2 + g][:, :].rearrange("p (j r) -> p j r", j=NC_)).then_inc(et.sem, 1)
                    dve.wait_ge(o_ps.sem, o_ps.at(n, 1))
                    out = m.bank[4][:, :].rearrange("p (s d) -> p s d", s=2)
                    nc.vector.tensor_scalar(ssum[:, :], out[:, :, D], EPS, None, ALU.add).then_inc(den.sem, 1)
                    dve.wait_ge(den.sem, den.at(n, 1))
                    nc.vector.reciprocal(ssum[:, :], ssum[:, :]).then_inc(den.sem, 1)
                    dve.wait_ge(den.sem, den.at(n, 2))
                    for s in S:
                        h = m.h[:, bass.ds((2 * i + s) * NC_ + c, 1), :].rearrange("p o d -> p (o d)")
                        nc.vector.scalar_tensor_tensor(h, out[:, s, 0:D], ssum[:, s:s + 1], h, ALU.mult, ALU.add).then_inc(h_sb.sem, 1)
                    dve.wait_ge(h_sb.sem, h_sb.at(n, 2))

        @block.scalar
        def _(act):
            for name in ("a_bt", "a_ba"):
                act.wait_ge(m.loaded[name], 16)
            with act.Fori(0, PAIRS) as i:
                for s in S:
                    act.wait_ge(xt_ps.sem, xt_ps.at(i, s + 1))
                    nc.scalar.copy(XT[s][:, :], m.bank[4 * s][:, :]).then_inc(xt_sb.sem, 1)
                act.wait_ge(kq_ps.sem, kq_ps.at(i, 1))
                nc.scalar.copy(KU[:, bass.ds(i * T, T)], m.bank[1][:, :]).then_inc(kq_sb.sem, 1)
                act.wait_ge(kq_ps.sem, kq_ps.at(i, 2))
                nc.scalar.activation(QU[:, bass.ds(i * T, T)], m.bank[2][:, :], ACT.Identity, bias=w["a_bt"][:, 0:1]).then_inc(kq_sb.sem, 1)
            with act.Fori(0, PAIRS * NC_) as n:
                for g in range(2):
                    for k in range(KS):
                        step = g * KS + k
                        act.wait_ge(arg.sem, arg.at(n, step + 1))
                        nc.scalar.activation(ARG[step % NBUF], ARG[step % NBUF], ACT.Tanh).then_inc(th.sem, 1)
                        if g == 1 and k == 2:
                            act.wait_ge(used.sem, used.at(n, KS))
                            nc.scalar.activation(EX[0][:, :], m.bank[0][:, :], ACT.Exp, bias=w["a_ba"][:, 0:1]).then_inc(ex.sem, 1)
                act.wait_ge(used.sem, used.at(n, 2 * KS))
                nc.scalar.activation(EX[1][:, :], m.bank[1][:, :], ACT.Exp, bias=w["a_ba"][:, 0:1]).then_inc(ex.sem, 1)

        @block.tensor
        def _(pe):
            for name in ("a_wx", "a_wt", "a_wa"):
                pe.wait_ge(m.loaded[name], 16)
            with pe.Fori(0, PAIRS) as i:
                for s in S:
                    pe.wait_ge(norm.ready.sem, norm.ready.at(i, s + 1))
                    for c in range(NC_):
                        last = nc.tensor.transpose(m.bank[4 * s][:, c * P:(c + 1) * P], XN[s][:, c, :], w["ident"][:, :])
                    last.then_inc(xt_ps.sem, 1)
                pe.wait_ge(xt_sb.sem, xt_sb.at(i, 2))
                for bank, name in ((1, "a_wx"), (2, "a_wt")):
                    for s in S:
                        last = nc.tensor.matmul(m.bank[bank][U * s:U * s + U, :], w[name][:, :], XT[s][:, :], start=True, stop=True)
                    last.then_inc(kq_ps.sem, 1)
            with pe.Fori(0, PAIRS) as i:
                with pe.Fori(0, NC_) as c:
                    n = i * NC_ + c

                    def keys(g):
                        pe.wait_ge(ex.sem, ex.at(n, g + 1))
                        for j in range(NC_):
                            last = nc.tensor.transpose(m.bank[2 + g][:, j * P:(j + 1) * P], EX[g][:, j * P:(j + 1) * P], w["ident"][:, :])
                        last.then_inc(tr_ps.sem, 1)

                    for g in range(2):
                        for k in range(KS):
                            step = g * KS + k
                            pe.wait_ge(th.sem, th.at(n, step + 1))
                            for cc in range(CG):
                                last = nc.tensor.matmul(m.bank[g][32 * cc:32 * cc + 32, :], w["a_wa"][:, 30 - 2 * k:62 - 2 * k],
                                                        ARG[step % NBUF][:, cc, :], start=k == 0, stop=k == KS - 1)
                            last.then_inc(used.sem, 1)
                            if g == 1 and k == 6:
                                keys(0)
                    keys(1)
                    pe.wait_ge(et.sem, et.at(n, 2))
                    for s in S:
                        for j in range(NC_):
                            last = nc.tensor.matmul(m.bank[4][:, 256 * s:256 * s + D + 1], ET[:, j, s::2],
                                                    XA[:, bass.ds((2 * i + s) * NC_ + j, 1), :].rearrange("p o d -> p (o d)"),
                                                    start=j == 0, stop=j == NC_ - 1)
                    last.then_inc(o_ps.sem, 1)


class Top2:
    STEPS = 11

    def __init__(self, ctx, nc, m, tag, rows, E, per=1):
        self.nc, self.rows, self.E = nc, rows, E
        self.eq = ctx.sb(tag + "_t2_eq", [P, rows, E])
        self.rest = ctx.sb(tag + "_t2_rest", [P, rows, E])
        self.oh = [ctx.sb(f"{tag}_t2_oh{n}", [P, rows, E]) for n in range(2)]
        self.v = ctx.sb(tag + "_t2_v", [P, 2, rows])
        self.r = ctx.sb(tag + "_t2_r", [P, 2, rows])
        self.step = Signal(ctx, nc, tag + "_t2_step", self.STEPS)
        self.ramp = m.w["ramp"][:, 64 - E:64].rearrange("p (o e) -> p o e", o=1).broadcast_to([P, rows, E])

    def vector(self, dve, i, values):
        nc, E, rows = self.nc, self.E, self.rows
        over = lambda v: v.rearrange("p (n o) -> p n o", o=1).broadcast_to([P, rows, E])
        n = [0]

        def link(ins):
            n[0] += 1
            ins.then_inc(self.step.sem, 1)
            dve.wait_ge(self.step.sem, self.step.at(i, n[0]))

        for k in range(2):
            src = values if k == 0 else self.rest[:, :, :]
            link(nc.vector.tensor_reduce(self.v[:, k, :], src, AX.X, ALU.max))
            link(nc.vector.tensor_tensor(self.eq[:, :, :], src, over(self.v[:, k, :]), ALU.is_equal))
            link(nc.vector.tensor_tensor(self.eq[:, :, :], self.eq[:, :, :], self.ramp, ALU.mult))
            link(nc.vector.tensor_reduce(self.r[:, k, :], self.eq[:, :, :], AX.X, ALU.max))
            link(nc.vector.tensor_tensor(self.oh[k][:, :, :], self.ramp, over(self.r[:, k, :]), ALU.is_equal))
            if k == 0:
                link(nc.vector.scalar_tensor_tensor(self.rest[:, :, :], self.oh[0][:, :, :], -3e38, values, ALU.mult, ALU.add))
        assert n[0] == self.STEPS


def routed_ffn(ctx, nc, m):
    S = range(2)
    E, H = 8, 256
    HB = H // P
    UNITS = [(e, s, c) for e in range(E) for s in S for c in range(NC_)]
    NU = len(UNITS)
    sig = lambda name, per: Signal(ctx, nc, "rf_" + name, per)
    w = m.w
    late = [(n, *m.load(ctx, n)) for n in ("router", "ramp")]
    wgu = m.big[:, 0:E * 2 * H].rearrange("p (e n) -> p e n", e=E)
    wd = m.big[:, E * 2 * H:E * 2 * H + E * HB * D].rearrange("p (e a d) -> p e a d", e=E, a=HB)
    wgu_in, wd_in = ctx.semaphore("loaded_wgu"), ctx.semaphore("loaded_wd")
    XN, XT = m.XN, m.XT
    lg = ctx.sb("rf_lg", [P, 2 * NC_, E])
    e2, p1, p2 = (ctx.sb(f"rf_{n}", [P, 2 * NC_]) for n in ("e2", "p1", "p2"))
    WT = ctx.sb("rf_w", [P, 2 * NC_, E])
    TH = [m.t512a[s] for s in S]
    AC = [m.t512b[s] for s in S]
    AT = [m.t512c[s] for s in S]
    zero = m.KM[0][:, 0, 0:P]
    norm = Norm(ctx, nc, m, "rf")
    top = Top2(ctx, nc, m, "rf", 2 * NC_, E)
    xt_ps, xt_sb, lg_ps, lg_sb = sig("xt_ps", 2), sig("xt_sb", 2), sig("lg_ps", 1), sig("lg_sb", 1)
    wstep, e2_in, e2_sb, w_sb = sig("wstep", 4), sig("e2_in", 1), sig("e2_sb", 1), sig("w_sb", 1)
    gu_ps, th_sb, a1_sb, ac_sb = sig("gu_ps", NU), sig("th_sb", NU), sig("a1_sb", NU), sig("ac_sb", NU)
    tr_ps, at_sb, dn, y_ps, h_sb = sig("tr_ps", NU // 2), sig("at_sb", NU // 2), sig("dn", NU // 2), sig("y_ps", 2), sig("h_sb", 2)
    zeroed = sig("zeroed", 0)
    GU = lambda u: m.bank[u % 4]
    TR = lambda v: m.bank[4 + v % 2]
    OUT = lambda s: m.bank[6 + s]

    with nc.Block() as block:
        @block.sync
        def _(sp):
            for _, t, sem, src in late:
                sp.dma_start(t[:, :], src).then_inc(sem, 16)
            sp.dma_start(wgu.rearrange("p e n -> p (e n)"), m.dram["wgu"]).then_inc(wgu_in, 16)
            sp.dma_start(wd.rearrange("p e a d -> p (e a d)"), m.dram["wdown"]).then_inc(wd_in, 16)

        @block.gpsimd
        def _(pool):
            nc.gpsimd.memset(zero, 0.0).then_inc(zeroed.sem, 1)
            with pool.Fori(0, PAIRS) as i:
                norm.gpsimd(pool, i)

        @block.vector
        def _(dve):
            dve.wait_ge(m.loaded["ramp"], 16)
            with dve.Fori(0, PAIRS) as i:
                hs = [m.h[:, bass.ds((2 * i + s) * NC_, NC_), :] for s in S]
                norm.vector(dve, i, hs, [XN[s] for s in S])
                dve.wait_ge(lg_ps.sem, lg_ps.at(i, 1))
                nc.vector.tensor_copy(lg[:, :, :], m.bank[1][:, 0:2 * NC_ * E].rearrange("p (n e) -> p n e", e=E)).then_inc(lg_sb.sem, 1)
                dve.wait_ge(lg_sb.sem, lg_sb.at(i, 1))
                top.vector(dve, i, lg[:, :, :])
                nc.vector.tensor_tensor(e2[:, :], top.v[:, 1, :], top.v[:, 0, :], ALU.subtract).then_inc(e2_in.sem, 1)
                dve.wait_ge(e2_sb.sem, e2_sb.at(i, 1))
                nc.vector.tensor_scalar(p1[:, :], e2[:, :], 2.0, 2.0, ALU.mult, ALU.add).then_inc(wstep.sem, 1)
                dve.wait_ge(wstep.sem, wstep.at(i, 1))
                nc.vector.reciprocal(p1[:, :], p1[:, :]).then_inc(wstep.sem, 1)
                dve.wait_ge(wstep.sem, wstep.at(i, 2))
                nc.vector.tensor_tensor(p2[:, :], p1[:, :], e2[:, :], ALU.mult).then_inc(wstep.sem, 1)
                dve.wait_ge(wstep.sem, wstep.at(i, 3))
                over = lambda v: v.rearrange("p (n o) -> p n o", o=1).broadcast_to([P, 2 * NC_, E])
                nc.vector.tensor_tensor(WT[:, :, :], top.oh[0][:, :, :], over(p1[:, :]), ALU.mult)
                nc.vector.tensor_tensor(top.oh[1][:, :, :], top.oh[1][:, :, :], over(p2[:, :]), ALU.mult).then_inc(wstep.sem, 1)
                dve.wait_ge(wstep.sem, wstep.at(i, 4))
                nc.vector.tensor_tensor(WT[:, :, :], WT[:, :, :], top.oh[1][:, :, :], ALU.add).then_inc(w_sb.sem, 1)
                dve.wait_ge(w_sb.sem, w_sb.at(i, 1))

                def second(u):
                    e, s, c = UNITS[u]
                    dve.wait_ge(a1_sb.sem, a1_sb.at(i, u + 1))
                    if u >= 4:
                        dve.wait_ge(tr_ps.sem, tr_ps.at(i, (u - 4) // 2 + 1))
                    nc.vector.scalar_tensor_tensor(AC[(u // 2) % 2][:, (u % 2) * H:(u % 2 + 1) * H], TH[(u // 2) % 2][:, (u % 2) * H:(u % 2 + 1) * H],
                                                   WT[:, s * NC_ + c, e:e + 1], GU(u)[:, H:2 * H], ALU.mult, ALU.mult).then_inc(ac_sb.sem, 1)

                for u in range(NU):
                    dve.wait_ge(th_sb.sem, th_sb.at(i, u + 1))
                    th = TH[(u // 2) % 2][:, (u % 2) * H:(u % 2 + 1) * H]
                    nc.vector.scalar_tensor_tensor(th, th, 1.0, GU(u)[:, 0:H], ALU.add, ALU.mult).then_inc(a1_sb.sem, 1)
                    if u:
                        second(u - 1)
                second(NU - 1)
                for s in S:
                    dve.wait_ge(y_ps.sem, y_ps.at(i, s + 1))
                    nc.vector.tensor_tensor(hs[s], hs[s], OUT(s)[:, :].rearrange("p (c d) -> p c d", c=NC_), ALU.add).then_inc(h_sb.sem, 1)
                dve.wait_ge(h_sb.sem, h_sb.at(i, 2))

        @block.scalar
        def _(act):
            with act.Fori(0, PAIRS) as i:
                for s in S:
                    act.wait_ge(xt_ps.sem, xt_ps.at(i, s + 1))
                    nc.scalar.copy(XT[s][:, :], m.bank[4 * s][:, :]).then_inc(xt_sb.sem, 1)
                act.wait_ge(e2_in.sem, e2_in.at(i, 1))
                nc.scalar.activation(e2[:, :], e2[:, :], ACT.Exp).then_inc(e2_sb.sem, 1)

                def evac(v):
                    act.wait_ge(tr_ps.sem, tr_ps.at(i, v + 1))
                    if v >= 4:
                        act.wait_ge(dn.sem, dn.at(i, v - 3))
                    nc.scalar.copy(AT[v // 2 % 2][:, v % 2, :], TR(v)[:, :]).then_inc(at_sb.sem, 1)

                for u in range(NU):
                    act.wait_ge(gu_ps.sem, gu_ps.at(i, u + 1))
                    if u >= 4:
                        act.wait_ge(ac_sb.sem, ac_sb.at(i, u - 3))
                    nc.scalar.activation(TH[(u // 2) % 2][:, (u % 2) * H:(u % 2 + 1) * H], GU(u)[:, 0:H], ACT.Tanh, scale=0.5).then_inc(th_sb.sem, 1)
                    if u % 2 and u >= 5:
                        evac((u - 5) // 2)
                evac(NU // 2 - 2)
                evac(NU // 2 - 1)

        @block.tensor
        def _(pe):
            for name in ("router",):
                pe.wait_ge(m.loaded[name], 16)
            pe.wait_ge(wgu_in, 16)
            pe.wait_ge(wd_in, 16)
            pe.wait_ge(zeroed.sem, 1)
            with pe.Fori(0, PAIRS) as i:
                for s in S:
                    pe.wait_ge(norm.ready.sem, norm.ready.at(i, s + 1))
                    for c in range(NC_):
                        last = nc.tensor.transpose(m.bank[4 * s][:, c * P:(c + 1) * P], XN[s][:, c, :], w["ident"][:, :])
                    last.then_inc(xt_ps.sem, 1)
                for s in S:
                    pe.wait_ge(xt_sb.sem, xt_sb.at(i, s + 1))
                    for c in range(NC_):
                        n = s * NC_ + c
                        last = nc.tensor.matmul(m.bank[1][:, n * E:(n + 1) * E], XT[s][:, c * P:(c + 1) * P], w["router"][:, :], start=True, stop=True)
                last.then_inc(lg_ps.sem, 1)
                for s in S:
                    nc.tensor.matmul(OUT(s)[:, :], zero, XT[s][:, :], start=True, stop=False)
                pe.wait_ge(lg_sb.sem, lg_sb.at(i, 1))

                def down(v):
                    pe.wait_ge(at_sb.sem, at_sb.at(i, v + 1))
                    for u in (2 * v, 2 * v + 1):
                        e, s, c = UNITS[u]
                        for a in range(HB):
                            o = (u % 2) * H + a * P
                            last = nc.tensor.matmul(OUT(s)[:, c * P:(c + 1) * P], AT[v // 2 % 2][:, v % 2, o:o + P], wd[:, e, a, :],
                                                    start=False, stop=False, skip_group_check=True)
                    last.then_inc(dn.sem, 1)

                def turn(v):
                    pe.wait_ge(ac_sb.sem, ac_sb.at(i, 2 * v + 2))
                    if v >= 2:
                        pe.wait_ge(at_sb.sem, at_sb.at(i, v - 1))
                    for b in range(4):
                        last = nc.tensor.transpose(TR(v)[:, b * P:(b + 1) * P], AC[v % 2][:, b * P:(b + 1) * P], w["ident"][:, :])
                    last.then_inc(tr_ps.sem, 1)

                for u in range(NU):
                    e, s, c = UNITS[u]
                    if u >= 4:
                        pe.wait_ge(ac_sb.sem, ac_sb.at(i, u - 3))
                    nc.tensor.matmul(GU(u)[:, :], XT[s][:, c * P:(c + 1) * P], wgu[:, e, :], start=True, stop=True).then_inc(gu_ps.sem, 1)
                    if u % 2 and u >= 3:
                        turn((u - 3) // 2)
                    if u % 2 and u >= 7:
                        down((u - 7) // 2)
                turn(NU // 2 - 1)
                for v in range(NU // 2 - 3, NU // 2):
                    down(v)
                for s in S:
                    nc.tensor.matmul(OUT(s)[:, :], zero, XT[s][:, :], start=False, stop=True).then_inc(y_ps.sem, 1)


def batch_attention(ctx, nc, m):
    S = range(2)
    sig = lambda name, per: Signal(ctx, nc, "ba_" + name, per)
    w = m.w
    late = [(n, *m.load(ctx, n)) for n in ("b_w", "b_b")]
    L = B
    H4 = m.h[:, :, :].rearrange("p (l c) d -> p l c d", l=L)
    FT = m.big[:, 0:L * 3 * D].rearrange("p (l n) -> p l n", l=L)
    q_of = lambda l: FT[:, l, 0:D]
    K3, V3 = FT[:, :, D:2 * D], FT[:, :, 2 * D:3 * D]
    o = L * 3 * D
    PR = [m.big[:, o + n * L * D:o + (n + 1) * L * D].rearrange("p (m x) -> p m x", m=L) for n in range(4)]
    SC = m.t512a[0][:, :]
    MK = m.t512a[1][:, :]
    EX = m.t512b[0][:, :]
    mx = ctx.sb("ba_mx", [P, L * NH])
    O = m.KM[0][:, 0:2, :].rearrange("p a (l x) -> p (a l) x", x=D)
    XN, XT = m.XN, m.XT
    norm = Norm(ctx, nc, m, "ba")
    xt_ps, xt_sb, ft_ps, ft_sb = sig("xt_ps", 2), sig("xt_sb", 2), sig("ft_ps", L), sig("ft_sb", L)
    pr, sc, st, ex_in, ex_sb = sig("pr", L), sig("sc", L), sig("st", 7), sig("ex_in", 3), sig("ex_sb", 1)
    pv, ov, h_sb = sig("pv", L), sig("ov", L), sig("h_sb", 1)
    by_m = lambda v: v.rearrange("p (l m h) -> p l h m", l=L, m=L)
    wide_m = lambda v: v.rearrange("p (l o h) -> p l o h", l=L, o=1).broadcast_to([P, L, L, NH])
    lmh = lambda v: v.rearrange("p (l m h) -> p l m h", l=L, m=L)

    with nc.Block() as block:
        @block.sync
        def _(sp):
            for _, t, sem, src in late:
                sp.dma_start(t[:, :], src).then_inc(sem, 16)

        @block.gpsimd
        def _(pool):
            with pool.Fori(0, NC_) as c:
                norm.gpsimd(pool, c)

        @block.vector
        def _(dve):
            dve.wait_ge(m.loaded["b_b"], 16)
            with dve.Fori(0, NC_) as c:
                hs = [H4[:, 4 * s:4 * s + 4, bass.ds(c, 1), :].rearrange("p l o d -> p l (o d)") for s in S]
                norm.vector(dve, c, hs, [XN[s] for s in S])
                for l in range(L):
                    dve.wait_ge(ft_ps.sem, ft_ps.at(c, l + 1))
                    nc.vector.tensor_tensor(FT[:, l, :], m.bank[l][:, 0:3 * D], w["b_b"][:, :], ALU.add).then_inc(ft_sb.sem, 1)
                dve.wait_ge(ft_sb.sem, ft_sb.at(c, L))
                for l in range(L + 1):
                    if l < L:
                        if l >= 4:
                            dve.wait_ge(sc.sem, sc.at(c, l - 3))
                        nc.vector.tensor_tensor(PR[l % 4], K3, q_of(l).rearrange("p (o x) -> p o x", o=1).broadcast_to([P, L, D]), ALU.mult).then_inc(pr.sem, 1)
                    if l:
                        dve.wait_ge(pr.sem, pr.at(c, l))
                        nc.vector.tensor_reduce(SC[:, (l - 1) * L * NH:l * L * NH], PR[(l - 1) % 4].rearrange("p m (h x) -> p (m h) x", x=DH),
                                                AX.X, ALU.add).then_inc(sc.sem, 1)
                n = [0]

                def link(ins):
                    n[0] += 1
                    ins.then_inc(st.sem, 1)
                    dve.wait_ge(st.sem, st.at(c, n[0]))

                dve.wait_ge(sc.sem, sc.at(c, L))
                link(nc.vector.tensor_scalar(SC, SC, DH ** -0.5, None, ALU.mult))
                link(nc.vector.tensor_scalar(MK, SC, 0.0, None, ALU.is_equal))
                link(nc.vector.scalar_tensor_tensor(SC, MK, -3e38, SC, ALU.mult, ALU.add))
                link(nc.vector.tensor_reduce(mx[:, :].rearrange("p (l h) -> p l h", l=L), by_m(SC), AX.X, ALU.max))
                nc.vector.tensor_tensor(lmh(SC), lmh(SC), wide_m(mx[:, :]), ALU.subtract).then_inc(ex_in.sem, 1)
                dve.wait_ge(ex_sb.sem, ex_sb.at(c, 1))
                link(nc.vector.scalar_tensor_tensor(EX, MK, 0.0, EX, ALU.is_equal, ALU.mult))
                link(nc.vector.tensor_reduce(mx[:, :].rearrange("p (l h) -> p l h", l=L), by_m(EX), AX.X, ALU.add))
                link(nc.vector.tensor_scalar(mx[:, :], mx[:, :], 1e-30, None, ALU.max))
                nc.vector.reciprocal(mx[:, :], mx[:, :]).then_inc(ex_in.sem, 1)
                dve.wait_ge(ex_in.sem, ex_in.at(c, 2))
                nc.vector.tensor_tensor(lmh(EX), lmh(EX), wide_m(mx[:, :]), ALU.mult).then_inc(ex_in.sem, 1)
                dve.wait_ge(ex_in.sem, ex_in.at(c, 3))
                for l in range(L + 1):
                    if l < L:
                        if l >= 4:
                            dve.wait_ge(ov.sem, ov.at(c, l - 3))
                        pl = EX[:, l * L * NH:(l + 1) * L * NH].rearrange("p (n o) -> p n o", o=1).broadcast_to([P, L * NH, DH])
                        nc.vector.tensor_tensor(PR[l % 4].rearrange("p m (h x) -> p m h x", x=DH), V3.rearrange("p m (h x) -> p m h x", x=DH),
                                                pl.rearrange("p (m h) x -> p m h x", h=NH), ALU.mult).then_inc(pv.sem, 1)
                    if l:
                        dve.wait_ge(pv.sem, pv.at(c, l))
                        nc.vector.tensor_reduce(O[:, l - 1, :], PR[(l - 1) % 4].rearrange("p m x -> p x m"), AX.X, ALU.add).then_inc(ov.sem, 1)
                dve.wait_ge(ov.sem, ov.at(c, L))
                h = H4[:, :, bass.ds(c, 1), :].rearrange("p l o d -> p l (o d)")
                nc.vector.tensor_tensor(h, h, O, ALU.add).then_inc(h_sb.sem, 1)
                dve.wait_ge(h_sb.sem, h_sb.at(c, 1))

        @block.scalar
        def _(act):
            with act.Fori(0, NC_) as c:
                for s in S:
                    act.wait_ge(xt_ps.sem, xt_ps.at(c, s + 1))
                    nc.scalar.copy(XT[s][:, :], m.bank[4 * s][:, :]).then_inc(xt_sb.sem, 1)
                act.wait_ge(ex_in.sem, ex_in.at(c, 1))
                nc.scalar.activation(EX, SC, ACT.Exp).then_inc(ex_sb.sem, 1)

        @block.tensor
        def _(pe):
            pe.wait_ge(m.loaded["b_w"], 16)
            with pe.Fori(0, NC_) as c:
                for s in S:
                    pe.wait_ge(norm.ready.sem, norm.ready.at(c, s + 1))
                    for k in range(NC_):
                        last = nc.tensor.transpose(m.bank[4 * s][:, k * P:(k + 1) * P], XN[s][:, k, :], w["ident"][:, :])
                    last.then_inc(xt_ps.sem, 1)
                pe.wait_ge(xt_sb.sem, xt_sb.at(c, 2))
                for l in range(L):
                    nc.tensor.matmul(m.bank[l][:, 0:3 * D], XT[l // 4][:, (l % 4) * P:(l % 4 + 1) * P], w["b_w"][:, :], start=True, stop=True).then_inc(ft_ps.sem, 1)


def capacity_routing(ctx, nc, m):
    S = range(2)
    sig = lambda name, per: Signal(ctx, nc, "cr_" + name, per)
    w = m.w
    late = [(n, *m.load(ctx, n)) for n in ("c_gate", "ramp", "earlier", "spare", "sw1", "sw3", "sw2")]
    R8 = 2 * NC_
    XN, XT = m.XN, m.XT
    sc = ctx.sb("cr_sc", [P, R8, CE])
    M = ctx.sb("cr_m", [P, R8, CE])
    CU = ctx.sb("cr_cu", [P, R8 + 1, CE])
    base = ctx.sb("cr_base", [P, CE])
    pos, val, slot, alt = (ctx.sb("cr_" + n, [P, 2, R8]) for n in ("pos", "val", "slot", "alt"))
    sidx = ctx.sb("cr_sidx", [P, 2, R8], I32)
    vsum = ctx.sb("cr_vsum", [P, R8])
    SG = [m.t512a[s] for s in S]
    norm = Norm(ctx, nc, m, "cr")
    top = Top2(ctx, nc, m, "cr", R8, CE)
    xt_ps, xt_sb, lg_ps, ex_sb, one = sig("xt_ps", 2), sig("xt_sb", 2), sig("lg_ps", 1), sig("ex_sb", 1), sig("one", 2)
    g_ps, u_ps, th_sb, a_sb, y_ps, h_sb = sig("g_ps", 2), sig("u_ps", 2), sig("th_sb", 2), sig("a_sb", 4), sig("y_ps", 2), sig("h_sb", 2)
    cu, cu_sb, pos_ps, pst, idx_sb, kept, scattered = sig("cu", R8 + 2), sig("cu_sb", 1), sig("pos_ps", 1), sig("pst", 13), sig("idx_sb", 1), sig("kept", 2), sig("scattered", 16 * 2 * R8)
    based = sig("based", 0)
    G = lambda s: m.bank[2 + 4 * s]
    U = lambda s: m.bank[3 + 4 * s]
    OUT = lambda s: m.bank[4 * s]

    with nc.Block() as block:
        @block.sync
        def _(sp):
            for _, t, sem, src in late:
                sp.dma_start(t[:, :], src).then_inc(sem, 16)

        @block.gpsimd
        def _(pool):
            nc.gpsimd.memset(base[:, :], 0.0).then_inc(based.sem, 1)
            pool.wait_ge(m.queues_zero, 16)
            with pool.Fori(0, PAIRS) as i:
                norm.gpsimd(pool, i)
                pool.wait_ge(idx_sb.sem, idx_sb.at(i, 1))
                nc.gpsimd.tensor_tensor(m.pool_fence[:, 0:1], m.minus_half[:, 0:1], m.minus_half[:, 0:1], ALU.mult)
                for s in S:
                    for c in range(NC_):
                        for k in range(2):
                            pool.indirect_dma_start(
                                out=m.queues, out_offset=bass.IndirectOffsetOnAxis(ap=sidx[:, k, s * NC_ + c:s * NC_ + c + 1].bitcast(U32), axis=0),
                                in_=XN[s][:, c, :], in_offset=None).then_inc(scattered.sem, 16)
            pool.wait_ge(scattered.sem, 16 * 2 * NT)

        @block.vector
        def _(dve):
            dve.wait_ge(based.sem, 1)
            for n in ("ramp", "spare"):
                dve.wait_ge(m.loaded[n], 16)
            with dve.Fori(0, PAIRS) as i:
                hs = [m.h[:, bass.ds((2 * i + s) * NC_, NC_), :] for s in S]
                norm.vector(dve, i, hs, [XN[s] for s in S])
                flat = lambda v: v.rearrange("p n e -> p (n e)")
                dve.wait_ge(ex_sb.sem, ex_sb.at(i, 1))
                nc.vector.tensor_scalar(flat(sc[:, :, :]), flat(sc[:, :, :]), 1.0, None, ALU.add).then_inc(one.sem, 1)
                dve.wait_ge(one.sem, one.at(i, 1))
                nc.vector.reciprocal(flat(sc[:, :, :]), flat(sc[:, :, :])).then_inc(one.sem, 1)
                dve.wait_ge(one.sem, one.at(i, 2))
                top.vector(dve, i, sc[:, :, :])
                nc.vector.tensor_copy(CU[:, 0, :], base[:, :]).then_inc(cu.sem, 1)
                nc.vector.tensor_tensor(M[:, :, :], top.oh[0][:, :, :], top.oh[1][:, :, :], ALU.add).then_inc(cu.sem, 1)
                for n in range(R8):
                    dve.wait_ge(cu.sem, cu.at(i, n + 2))
                    last = nc.vector.tensor_tensor(CU[:, n + 1, :] if n + 1 < R8 else base[:, :], CU[:, n, :], M[:, n, :], ALU.add)
                    last.then_inc(cu.sem, 1)
                dve.wait_ge(cu.sem, cu.at(i, R8 + 2))
                nc.vector.tensor_tensor(vsum[:, :], top.v[:, 0, :], top.v[:, 1, :], ALU.add).then_inc(cu_sb.sem, 1)
                for s in S:
                    dve.wait_ge(th_sb.sem, th_sb.at(i, s + 1))
                    nc.vector.scalar_tensor_tensor(SG[s][:, :], SG[s][:, :], 1.0, G(s)[:, :], ALU.add, ALU.mult).then_inc(a_sb.sem, 1)
                for s in S:
                    dve.wait_ge(a_sb.sem, a_sb.at(i, s + 1))
                    dve.wait_ge(u_ps.sem, u_ps.at(i, s + 1))
                    nc.vector.tensor_tensor(SG[s][:, :], SG[s][:, :], U(s)[:, :], ALU.mult).then_inc(a_sb.sem, 1)
                n = [0]

                def link(ins):
                    n[0] += 1
                    ins.then_inc(pst.sem, 1)
                    dve.wait_ge(pst.sem, pst.at(i, n[0]))

                dve.wait_ge(pos_ps.sem, pos_ps.at(i, 1))
                count = m.bank[5][:, :].rearrange("p (n e) -> p n e", e=CE)
                for k in range(2):
                    link(nc.vector.tensor_tensor(top.oh[k][:, :, :], top.oh[k][:, :, :], count, ALU.mult))
                    link(nc.vector.tensor_reduce(pos[:, k, :], top.oh[k][:, :, :], AX.X, ALU.add))
                link(nc.vector.tensor_scalar(val[:, :, :], pos[:, :, :], float(CAP), None, ALU.is_lt))
                link(nc.vector.tensor_scalar(slot[:, :, :], top.r[:, :, :], -float(CAP), float(CE * CAP), ALU.mult, ALU.add))
                link(nc.vector.tensor_tensor(slot[:, :, :], slot[:, :, :], pos[:, :, :], ALU.add))
                link(nc.vector.tensor_tensor(alt[:, :, :], slot[:, :, :], w["spare"][:, :].rearrange("p (k n) -> p k n", k=2), ALU.subtract))
                link(nc.vector.tensor_tensor(alt[:, :, :], alt[:, :, :], val[:, :, :], ALU.mult))
                link(nc.vector.tensor_tensor(alt[:, :, :], alt[:, :, :], w["spare"][:, :].rearrange("p (k n) -> p k n", k=2), ALU.add))
                nc.vector.tensor_copy(sidx[:, :, :], alt[:, :, :]).then_inc(idx_sb.sem, 1)
                link(nc.vector.tensor_scalar(vsum[:, :], vsum[:, :], 1e-20, None, ALU.add))
                link(nc.vector.reciprocal(vsum[:, :], vsum[:, :]))
                link(nc.vector.scalar_tensor_tensor(top.v[:, :, :], top.v[:, :, :], ROUTE_SCALE, val[:, :, :], ALU.mult, ALU.mult))
                nc.vector.tensor_tensor(m.place[:, bass.ds(i, 1), :].rearrange("p o (k n) -> p (o k) n", k=2), slot[:, :, :], val[:, :, :], ALU.mult).then_inc(kept.sem, 1)
                nc.vector.tensor_tensor(m.share[:, bass.ds(i, 1), :].rearrange("p o (k n) -> p (o k) n", k=2), top.v[:, :, :],
                                        vsum[:, :].rearrange("p (o n) -> p o n", o=1).broadcast_to([P, 2, R8]), ALU.mult).then_inc(kept.sem, 1)
                for s in S:
                    dve.wait_ge(y_ps.sem, y_ps.at(i, s + 1))
                    nc.vector.scalar_tensor_tensor(hs[s], OUT(s)[:, :].rearrange("p (c d) -> p c d", c=NC_), 0.5, hs[s], ALU.mult, ALU.add).then_inc(h_sb.sem, 1)
                dve.wait_ge(h_sb.sem, h_sb.at(i, 2))
                dve.wait_ge(kept.sem, kept.at(i, 2))
                dve.wait_ge(idx_sb.sem, idx_sb.at(i, 1))
                dve.wait_ge(scattered.sem, scattered.at(i, 16 * 2 * R8))

        @block.scalar
        def _(act):
            with act.Fori(0, PAIRS) as i:
                for s in S:
                    act.wait_ge(xt_ps.sem, xt_ps.at(i, s + 1))
                    nc.scalar.copy(XT[s][:, :], m.bank[4 * s][:, :]).then_inc(xt_sb.sem, 1)
                act.wait_ge(lg_ps.sem, lg_ps.at(i, 1))
                nc.scalar.activation(sc[:, :, :].rearrange("p n e -> p (n e)"), m.bank[1][:, :], ACT.Exp, scale=-1.0).then_inc(ex_sb.sem, 1)
                for s in S:
                    act.wait_ge(g_ps.sem, g_ps.at(i, s + 1))
                    nc.scalar.activation(SG[s][:, :], G(s)[:, :], ACT.Tanh, scale=0.5).then_inc(th_sb.sem, 1)

        @block.tensor
        def _(pe):
            for name in ("c_gate", "earlier", "sw1", "sw3", "sw2"):
                pe.wait_ge(m.loaded[name], 16)
            with pe.Fori(0, PAIRS) as i:
                for s in S:
                    pe.wait_ge(norm.ready.sem, norm.ready.at(i, s + 1))
                    for c in range(NC_):
                        last = nc.tensor.transpose(m.bank[4 * s][:, c * P:(c + 1) * P], XN[s][:, c, :], w["ident"][:, :])
                    last.then_inc(xt_ps.sem, 1)
                for s in S:
                    pe.wait_ge(xt_sb.sem, xt_sb.at(i, s + 1))
                    for c in range(NC_):
                        n = s * NC_ + c
                        last = nc.tensor.matmul(m.bank[1][:, n * CE:(n + 1) * CE], XT[s][:, c * P:(c + 1) * P], w["c_gate"][:, :], start=True, stop=True)
                last.then_inc(lg_ps.sem, 1)
                for s in S:
                    nc.tensor.matmul(G(s)[:, :], w["sw1"][:, :], XT[s][:, :], start=True, stop=True).then_inc(g_ps.sem, 1)
                    nc.tensor.matmul(U(s)[:, :], w["sw3"][:, :], XT[s][:, :], start=True, stop=True).then_inc(u_ps.sem, 1)
                pe.wait_ge(cu_sb.sem, cu_sb.at(i, 1))
                flat = lambda v: v.rearrange("p n e -> p (n e)")
                nc.tensor.matmul(m.bank[5][:, :], w["earlier"][:, :], flat(M[:, :, :]), start=True, stop=False)
                nc.tensor.matmul(m.bank[5][:, :], w["ones"][:, 0:P], flat(CU[:, 0:R8, :]), start=False, stop=True).then_inc(pos_ps.sem, 1)
                for s in S:
                    pe.wait_ge(a_sb.sem, a_sb.at(i, s + 3))
                    for c in range(NC_):
                        last = nc.tensor.matmul(OUT(s)[:, c * P:(c + 1) * P], SG[s][:, c * P:(c + 1) * P], w["sw2"][:, :], start=True, stop=True)
                    last.then_inc(y_ps.sem, 1)


def capacity_experts(ctx, nc, m):
    UN = 4
    NI = CE // 2 // UN
    S = range(2)
    sig = lambda name, per: Signal(ctx, nc, "ce_" + name, per)
    w = m.w
    w13_in, w2_in = ctx.semaphore("loaded_w13"), ctx.semaphore("loaded_w2")
    w13 = ctx.sb("ce_w13", [P, CE, 2 * CH])
    w2 = m.big[:, 0:CE // 2 * 2 * D].rearrange("p (q n) -> p q n", n=2 * D)
    QC = CAP // P
    X = [m.KM[0][:, 2 * u:2 * u + 1, :].rearrange("p o t -> p (o t)") for u in range(UN)]
    Y = [m.KM[1][:, 2 * u:2 * u + 1, :].rearrange("p o t -> p (o t)") for u in range(UN)]
    XT = [m.XT[s] for s in S]
    TH = [m.t512a[s] for s in S]
    AA = [m.t512b[s] for s in S]
    AT = [m.t512c[s][:, 0, 0:2 * P] for s in S]
    x_in = [sig(f"x_in{u}", 16) for u in range(UN)]
    y_out = [sig(f"y_out{u}", 16) for u in range(UN)]
    x_free, xt_ps, xt_sb, gu_ps, th_sb, a_sb = (sig(n, UN) for n in ("x_free", "xt_ps", "xt_sb", "gu_ps", "th_sb", "a_sb"))
    aa_sb, at_ps, at_sb, y_ps, y_sb = (sig(n, UN) for n in ("aa_sb", "at_ps", "at_sb", "y_ps", "y_sb"))
    XP = lambda u: m.bank[u % 2]
    GU = lambda u: m.bank[2 + u % 2]
    AP_ = lambda u: m.bank[4 + u % 2]
    YP = lambda u: m.bank[6 + u % 2]
    acf = lambda v: v.rearrange("p (a c f) -> p a c f", a=2, c=QC)
    rows = lambda t, k: t[bass.ds(k * (2 * CAP), 2 * CAP), :].rearrange("(n p) d -> p n d", p=P)
    nd = lambda v: v.rearrange("p (n d) -> p n d", d=D)
    mark = ctx.sb("ce_mark", [P, UN])
    y_free = sig("y_free", UN)
    ROOM = 2

    with nc.Block() as block:
        @block.sync
        def _(sp):
            sp.dma_start(w13[:, :, :].rearrange("p e n -> p (e n)"), m.dram["w13"]).then_inc(w13_in, 16)
            sp.dma_start(w2.rearrange("p q n -> p (q n)"), m.dram["w2_pairs"]).then_inc(w2_in, 16)
            with sp.Fori(0, NI) as i:
                for u in range(UN):
                    sp.wait_ge(x_free.sem, x_free.at(i, u + 1))
                    sp.dma_start(nd(X[u]), rows(m.queues, i * UN + u)).then_inc(x_in[u].sem, 16)

        @block.gpsimd
        def _(pool):
            nc.gpsimd.memset(m.pool_fence[:, 0:1], 0.0).then_inc(x_free.sem, UN)
            nc.gpsimd.memset(m.pool_fence[:, 1:2], 0.0).then_inc(y_free.sem, UN)
            with pool.Fori(0, NI) as i:
                for u in range(UN + 2):
                    if u < UN:
                        pool.wait_ge(y_sb.sem, y_sb.at(i, u + 1))
                        pool.dma_start(rows(m.results, i * UN + u), nd(Y[u])).then_inc(y_out[u].sem, 16)
                    if u >= 2:
                        v = u - 2
                        pool.wait_ge(y_out[v].sem, y_out[v].at(i, 16))
                        nc.gpsimd.tensor_tensor(mark[:, v:v + 1], m.minus_half[:, 0:1], m.minus_half[:, 0:1], ALU.mult).then_inc(y_free.sem, 1)
            for u in range(UN):
                pool.wait_ge(y_out[u].sem, 16 * NI)

        @block.vector
        def _(dve):
            with dve.Fori(0, NI) as i:
                def last_part(u):
                    dve.wait_ge(y_ps.sem, y_ps.at(i, u + 1))
                    dve.wait_ge(y_free.sem, y_free.at(i, u + 1))
                    nc.vector.tensor_scalar(acf(Y[u]), YP(u)[:, :].rearrange("p (c a f) -> p a c f", a=2, c=QC), 0.5, None, ALU.mult).then_inc(y_sb.sem, 1)

                for u in range(UN):
                    dve.wait_ge(th_sb.sem, th_sb.at(i, u + 1))
                    gu = acf(GU(u)[:, :])
                    th = TH[u % 2][:, 0:2 * QC * CH].rearrange("p (a c f) -> p a c f", a=2, c=QC)
                    nc.vector.scalar_tensor_tensor(th, th, 1.0, gu[:, :, :, 0:CH], ALU.add, ALU.mult).then_inc(a_sb.sem, 1)
                    dve.wait_ge(a_sb.sem, a_sb.at(i, u + 1))
                    if u >= ROOM:
                        dve.wait_ge(at_ps.sem, at_ps.at(i, u - ROOM + 1))
                    nc.vector.tensor_tensor(AA[u % 2][:, 0:2 * QC * CH].rearrange("p (c a f) -> p a c f", a=2, c=QC), th, gu[:, :, :, CH:2 * CH],
                                            ALU.mult).then_inc(aa_sb.sem, 1)
                    if u >= 2:
                        last_part(u - 2)
                last_part(UN - 2)
                last_part(UN - 1)
                dve.wait_ge(at_ps.sem, at_ps.at(i, UN))

        @block.scalar
        def _(act):
            with act.Fori(0, NI) as i:
                for u in range(UN + 2):
                    if u < UN:
                        act.wait_ge(xt_ps.sem, xt_ps.at(i, u + 1))
                        if u >= ROOM:
                            act.wait_ge(gu_ps.sem, gu_ps.at(i, u - ROOM + 1))
                        nc.scalar.copy(XT[u % 2][:, :], XP(u)[:, :]).then_inc(xt_sb.sem, 1)
                    if 1 <= u <= UN:
                        v = u - 1
                        act.wait_ge(gu_ps.sem, gu_ps.at(i, v + 1))
                        if v >= ROOM:
                            act.wait_ge(aa_sb.sem, aa_sb.at(i, v - ROOM + 1))
                        nc.scalar.activation(TH[v % 2][:, 0:2 * QC * CH].rearrange("p (a f) -> p a f", f=CH),
                                             GU(v)[:, :].rearrange("p (a f) -> p a f", f=2 * CH)[:, :, 0:CH], ACT.Tanh, scale=0.5).then_inc(th_sb.sem, 1)
                    if 2 <= u:
                        v = u - 2
                        act.wait_ge(at_ps.sem, at_ps.at(i, v + 1))
                        if v >= ROOM:
                            act.wait_ge(y_ps.sem, y_ps.at(i, v - ROOM + 1))
                        nc.scalar.copy(AT[v % 2], AP_(v)[:, 0:QC * P]).then_inc(at_sb.sem, 1)
                act.wait_ge(y_ps.sem, y_ps.at(i, UN))

        @block.tensor
        def _(pe):
            pe.wait_ge(w13_in, 16)
            pe.wait_ge(w2_in, 16)
            with pe.Fori(0, NI) as i:
                for u in range(UN + 3):
                    if u < UN:
                        pe.wait_ge(x_in[u].sem, x_in[u].at(i, 16))
                        if u >= ROOM:
                            pe.wait_ge(xt_sb.sem, xt_sb.at(i, u - ROOM + 1))
                        for n in range(2 * QC):
                            last = nc.tensor.transpose(XP(u)[:, n * P:(n + 1) * P], X[u][:, n * P:(n + 1) * P], w["ident"][:, :])
                        last.then_inc(xt_ps.sem, 1)
                    if 1 <= u <= UN:
                        v = u - 1
                        pe.wait_ge(xt_sb.sem, xt_sb.at(i, v + 1))
                        if v >= ROOM:
                            pe.wait_ge(aa_sb.sem, aa_sb.at(i, v - ROOM + 1))
                        for a in range(2):
                            we = w13[:, bass.ds(2 * (i * UN + v) + a, 1), :].rearrange("p o n -> p (o n)")
                            for c in range(QC):
                                n = a * QC + c
                                last = nc.tensor.matmul(GU(v)[:, n * P:(n + 1) * P], XT[v % 2][:, n * P:(n + 1) * P], we, start=True, stop=True)
                                if n == 0:
                                    last.then_inc(x_free.sem, 1)
                        last.then_inc(gu_ps.sem, 1)
                    if 2 <= u <= UN + 1:
                        v = u - 2
                        pe.wait_ge(aa_sb.sem, aa_sb.at(i, v + 1))
                        if v >= ROOM:
                            pe.wait_ge(at_sb.sem, at_sb.at(i, v - ROOM + 1))
                        for c in range(QC):
                            last = nc.tensor.transpose(AP_(v)[:, c * P:(c + 1) * P], AA[v % 2][:, c * P:(c + 1) * P], w["ident"][:, :])
                        last.then_inc(at_ps.sem, 1)
                    if 3 <= u:
                        v = u - 3
                        pe.wait_ge(at_sb.sem, at_sb.at(i, v + 1))
                        if v >= ROOM:
                            pe.wait_ge(y_sb.sem, y_sb.at(i, v - ROOM + 1))
                        wp = w2[:, bass.ds(i * UN + v, 1), :].rearrange("p o n -> p (o n)")
                        for c in range(QC):
                            last = nc.tensor.matmul(YP(v)[:, c * 2 * D:(c + 1) * 2 * D], AT[v % 2][:, c * P:(c + 1) * P], wp, start=True, stop=True)
                        last.then_inc(y_ps.sem, 1)
                pe.wait_ge(y_sb.sem, y_sb.at(i, UN))


def capacity_combine(ctx, nc, m):
    U2 = range(2)
    sig = lambda name, per: Signal(ctx, nc, "cc_" + name, per)
    idx = [ctx.sb(f"cc_idx{u}", [P, 2, NC_], I32) for u in U2]
    share = [ctx.sb(f"cc_share{u}", [P, 2, NC_]) for u in U2]
    Y = [m.KM[u][:, 0:2, :].rearrange("p k (c d) -> p k c d", c=NC_) for u in U2]
    idx_sb, summed, first, fenced = sig("idx_sb", 4), sig("summed", 2), sig("first", 2), sig("fenced", 2)
    got = [sig(f"got{u}", 16 * 2 * NC_) for u in U2]
    stored = [sig(f"stored{u}", 16) for u in U2]

    with nc.Block() as block:
        @block.sync
        def _(sp):
            with sp.Fori(0, PAIRS) as i:
                for u in U2:
                    sp.wait_ge(summed.sem, summed.at(i, u + 1))
                    sp.dma_start(m.out[bass.ds(2 * i + u, 1), :, :].rearrange("o (c p) d -> p (o c) d", p=P),
                                 m.h[:, bass.ds((2 * i + u) * NC_, NC_), :]).then_inc(stored[u].sem, 16)
            for u in U2:
                sp.wait_ge(stored[u].sem, 16 * PAIRS)

        @block.gpsimd
        def _(pool):
            with pool.Fori(0, PAIRS) as i:
                for u in U2:
                    pool.wait_ge(idx_sb.sem, idx_sb.at(i, 2 * u + 2))
                    nc.gpsimd.tensor_tensor(m.pool_fence[:, u:u + 1], m.minus_half[:, 0:1], m.minus_half[:, 0:1], ALU.mult).then_inc(fenced.sem, 1)
                    for c in range(NC_):
                        for k in range(2):
                            pool.indirect_dma_start(
                                out=Y[u][:, k, c, :], out_offset=None, in_=m.results,
                                in_offset=bass.IndirectOffsetOnAxis(ap=idx[u][:, k, c:c + 1].bitcast(U32), axis=0)).then_inc(got[u].sem, 16)

        @block.vector
        def _(dve):
            with dve.Fori(0, PAIRS) as i:
                for u in U2:
                    kc = lambda t: t[:, bass.ds(i, 1), :].rearrange("p o (k n) -> p (o k) n", k=2)[:, :, u * NC_:(u + 1) * NC_]
                    nc.vector.tensor_copy(idx[u][:, :, :], kc(m.place)).then_inc(idx_sb.sem, 1)
                    nc.vector.tensor_copy(share[u][:, :, :], kc(m.share)).then_inc(idx_sb.sem, 1)
                for u in U2:
                    dve.wait_ge(idx_sb.sem, idx_sb.at(i, 2 * u + 2))
                    dve.wait_ge(got[u].sem, got[u].at(i, 16 * 2 * NC_))
                    for k in range(2):
                        for c in range(NC_):
                            h = m.h[:, bass.ds((2 * i + u) * NC_ + c, 1), :].rearrange("p o d -> p (o d)")
                            last = nc.vector.scalar_tensor_tensor(h, Y[u][:, k, c, :], share[u][:, k, c:c + 1], h, ALU.mult, ALU.add)
                        last.then_inc((first if k == 0 else summed).sem, 1)
                        if k == 0:
                            dve.wait_ge(first.sem, first.at(i, u + 1))
                dve.wait_ge(summed.sem, summed.at(i, 2))
                dve.wait_ge(fenced.sem, fenced.at(i, 2))


def workspace(m):
    m.big = m.sb("big", [P, 12288 + 0])
    m.nstat = [m.sb(f"nstat{s}", [P, NC_, 6]) for s in range(2)]
    m.nmv = [m.sb(f"nmv{s}", [P, NC_, 2]) for s in range(2)]
    m.nrstd = [m.sb(f"nrstd{s}", [P, NC_]) for s in range(2)]
    m.fence = m.sb("fence", [P, 2])
    m.pool_fence = m.sb("pool_fence", [P, 2])
    m.minus_half = m.sb("minus_half", [P, 64])
    m.XN = [m.sb(f"XN{s}", [P, NC_, D]) for s in range(2)]
    m.XT = [m.sb(f"XT{s}", [P, T]) for s in range(2)]
    m.t512a = [m.sb(f"t512a{s}", [P, T]) for s in range(2)]
    m.t512b = [m.sb(f"t512b{s}", [P, T]) for s in range(2)]
    m.t512c = [m.sb(f"t512c{s}", [P, 2, T]) for s in range(2)]
    m.KM = [m.sb(f"KM{s}", [P, NH, T]) for s in range(2)]
    m.A = [m.big[:, s * 4 * T:(s + 1) * 4 * T].rearrange("p (a c t) -> p a c t", a=4, c=NC_) for s in range(2)]
    o = 8 * T
    m.V = [m.big[:, o + s * 4 * T:o + (s + 1) * 4 * T].rearrange("p (c n) -> p c n", c=NC_) for s in range(2)]
    o = 16 * T
    m.OT = [m.big[:, o + s * 4 * T:o + (s + 1) * 4 * T].rearrange("p (g n) -> p g n", g=NC_) for s in range(2)]
    m.XNA = m.big[:, 0:8 * T].rearrange("p (n d) -> p n d", d=D)
    m.XTA = m.big[:, 8 * T:16 * T]
    m.KTOK = [m.sb(f"KTOK{s}", [P, 3, D]) for s in range(2)]
    m.ST = [m.sb(f"ST{s}", [P, 3, T]) for s in range(2)]


def build(nc, dram, out, upto=None):
    whole = Layer(nc)
    with whole:
        m = Memory(whole, nc, dram)
        workspace(m)
        m.out = out
        m.queues = nc.dram_tensor("queues", (CE * CAP + 16 * P, D), F32).ap()
        m.results = nc.dram_tensor("results", (CE * CAP, D), F32).ap()
        m.place = m.sb("place", [P, PAIRS, 4 * NC_])
        m.share = m.sb("share", [P, PAIRS, 4 * NC_])
        zeros = m.sb("zeros", [P, T])
        zeros_in = whole.semaphore("zeros_in")
        m.queues_zero = whole.semaphore("queues_zero")
        m.early = ["ones", "causal", "same_head", "head_col", "state_mask", "wq", "wk", "wv", "wout"]
        with nc.Block() as block:
            @block.gpsimd
            def _(pool):
                nc.gpsimd.memset(m.minus_half[:, :], -0.5)
                nc.gpsimd.memset(zeros[:, :], 0.0).then_inc(zeros_in, 1)
                pool.wait_ge(zeros_in, 1)
                pool.dma_start(m.queues.rearrange("(n p r) d -> p n (r d)", p=P, r=4),
                               zeros[:, :].rearrange("p (o x) -> p o x", o=1).broadcast_to([P, CE * CAP // T + 4, T])).then_inc(m.queues_zero, 16)
        for layer in LAYERS[:upto]:
            own = Layer(nc)
            layer(own, nc, m)
            own.end()
        if upto is not None:
            stored = whole.semaphore("stored")
            with nc.Block() as block:
                @block.sync
                def _(sp):
                    sp.dma_start(out.rearrange("b (c p) d -> p (b c) d", p=P), m.h[:, :, :]).then_inc(stored, 16)
                    sp.wait_ge(stored, 16)


LAYERS = [token_conv, linear_attention, modulated_ffn, retention, balanced_experts, additive_attention, routed_ffn,
          batch_attention, capacity_routing, capacity_experts, capacity_combine]


def laid_out(inputs):
    a = {k: np.asarray(v) for k, v in inputs.items()}
    row = lambda x: np.ascontiguousarray(x)
    out = dict(shape_constants())
    out["ids"] = row(a["x"].reshape(NT, P).T)
    out["table"] = row(a["L0_tok_conv_w"].transpose(1, 2, 0).reshape(VOCAB, TAPS * D))
    out["wq"] = row(a["L0_attn_W_q"].T)
    out["wk"] = row(a["L0_attn_W_k"].T)
    out["wv"] = row(a["L0_attn_W_v"].T)
    out["wout"] = row(a["L0_attn_W_out"].T.reshape(NC_, P, D).transpose(1, 0, 2).reshape(P, NC_ * D))
    E, R = 8, 16
    rep = lambda x: row(np.repeat(x, R, axis=-1))
    spread = lambda x: row(np.concatenate([x[:, None, :], np.zeros((E, R - 1, x.shape[1]), x.dtype)], axis=1).reshape(P, -1))
    out["gfc1"] = row(a["L0_ffn_gfc1_w"].T)
    out["gfc1_b"] = row(a["L0_ffn_gfc1_b"].reshape(P, 1))
    out["gfc2_rep"] = rep(a["L0_ffn_gfc2_w"].T)
    out["gfc2_b"] = rep(a["L0_ffn_gfc2_b"]).reshape(P, 1)
    out["task_b1"] = spread(a["L0_ffn_tv_b1"])
    out["b1"] = row(a["L0_ffn_b1"].reshape(4, P).T)
    tb2 = spread(a["L0_ffn_tv_b2"])
    tb2[1] = a["L0_ffn_b2"]
    out["task_b2"] = tb2
    zeros = np.zeros((P - 1 - E, 2 * D), np.float32)
    out["ln_rows"] = row(np.concatenate([
        np.concatenate([a["L0_ffn_ln_g"], a["L0_ffn_ln_b"]])[None],
        np.concatenate([a["L0_ffn_tv_ln_g"], a["L0_ffn_tv_ln_b"]], axis=1), zeros]))
    coef = np.zeros((P, P), np.float32)
    coef[0], coef[1:1 + E] = 1.0 - 0.03 * E, 0.03
    out["ln_coef"] = coef
    p = np.arange(P)
    out["gate_row"] = row(np.stack([p % R == 0, p == 1], axis=1).astype(np.float32))
    out["gate_pad"] = row(np.concatenate([np.zeros((P, R)), p[:, None] % R == np.arange(R)[None], np.zeros((P, R))], axis=1).astype(np.float32))
    out["task_W1"] = row(a["L0_ffn_tv_W1"].reshape(E, 512, 8, R).transpose(0, 3, 2, 1).reshape(P, 8 * 512))
    out["task_W2"] = row(a["L0_ffn_tv_W2"].reshape(E, D, 4, 8, R).transpose(0, 4, 3, 2, 1).reshape(P, 8 * 4 * D))
    out["W1"] = row(a["L0_ffn_W1"].T)
    out["W2"] = row(a["L0_ffn_W2"].reshape(D, 4, P).transpose(2, 1, 0).reshape(P, 4 * D))
    for n in "QKVGO":
        out["r_w" + n.lower()] = row(a["L1_attn_W_" + n])
    out["gn"] = row(np.stack([a["L1_attn_gn_weight"], a["L1_attn_gn_bias"]], axis=1))
    out["gate_w"] = row(a["L1_ffn_gate_weight"][0])
    out["experts"] = row(a["L1_ffn_experts"].transpose(1, 0, 2).reshape(D, 8 * D))
    q = np.arange(B * 8)
    later = (p[:, None] // 8 == q[None] // 8) & (p[:, None] > q[None])
    out["later_expert"] = row(later.astype(np.float32))
    wx, wt = a["L2_attn_Wx"], a["L2_attn_Wt"]
    out["a_wx"], out["a_wt"] = row(wx), row(wt)
    out["a_bt"] = row(np.tile(a["L2_attn_bt"], 2).reshape(P, 1))
    wa = np.zeros((P, 62), np.float32)
    wa[0:64, 30], wa[64:128, 31] = a["L2_attn_Wa"][:, 0], a["L2_attn_Wa"][:, 0]
    out["a_wa"] = wa
    out["a_ba"] = row(np.tile(a["L2_attn_ba"], P).reshape(P, 1))
    out["router"] = row(a["L2_ffn_router_w"].T)
    out["ramp"] = row(np.tile(np.arange(64, 0, -1, dtype=np.float32), (P, 1)))
    out["wgu"] = row(np.concatenate([a["L2_ffn_w_gate"], a["L2_ffn_w_up"]], axis=2).transpose(1, 0, 2).reshape(P, -1))
    out["wdown"] = row(a["L2_ffn_w_down"].reshape(8, 2, P, D).transpose(2, 0, 1, 3).reshape(P, -1))
    qkv = lambda x: x.reshape((NH, 3, DH) + x.shape[1:]).swapaxes(0, 1).reshape(x.shape)
    out["b_w"] = row(qkv(a["L3_attn_W"]).T)
    out["b_b"] = row(np.tile(qkv(a["L3_attn_b"]), (P, 1)))
    out["c_gate"] = row(a["L3_ffn_gate_w"].T)
    out["earlier"] = row((p[:, None] < p[None, :]).astype(np.float32))
    out["spare"] = row((CE * CAP + np.arange(16)[None, :] * P + p[:, None]).astype(np.float32))
    for n in ("sw1", "sw3", "sw2"):
        out[n] = row(a["L3_ffn_" + n])
    out["w13"] = row(np.concatenate([a["L3_ffn_w1"], a["L3_ffn_w3"]], axis=2).transpose(1, 0, 2).reshape(P, -1))
    w2 = a["L3_ffn_w2"].reshape(CE // 2, 2, CH, D)
    pairs = np.zeros((2, CH, CE // 2, 2, D), w2.dtype)
    for e in range(2):
        pairs[e, :, :, e] = w2[:, e].transpose(1, 0, 2)
    out["w2_pairs"] = pairs.reshape(P, -1)
    return out


def kernel(**inputs):
    import concourse.bacc as bacc
    from concourse.bass_utils import run_bass_kernel_spmd

    nc = bacc.Bacc("TRN2", target_bir_lowering=False, num_devices=1)
    arrays, dram = {}, {}
    for name, a in laid_out(inputs).items():
        arrays["in_" + name] = a
        dram[name] = nc.dram_tensor("in_" + name, a.shape, mybir.dt.from_np(a.dtype), kind="ExternalInput").ap()
    out = nc.dram_tensor("out_h", (B, T, D), F32, kind="ExternalOutput").ap()
    build(nc, dram, out)
    r = run_bass_kernel_spmd(nc, [arrays], core_ids=[0])
    return r.results[0]["out_h"]
```

```python
import numpy as np
import concourse.bass as bass
from concourse import mybir
from contextlib import ExitStack

F32 = mybir.dt.float32
I32 = mybir.dt.int32
U32 = mybir.dt.uint32
ALU = mybir.AluOpType
ACT = mybir.ActivationFunctionType
AX = mybir.AxisListType

P = 128
B, T, D = 8, 512, 128
NC_ = T // P
NT = B * NC_
NH = 8
DH = D // NH
DV = 64
VOCAB, TAPS = 8000, 3
PAIRS = B // 2
LN_EPS = 1e-5
CE, CH, CAP = 64, 64, 256
ROUTE_SCALE = 2.5


class Layer(ExitStack):

    def __init__(self, nc):
        super().__init__()
        self.nc, self.sems = nc, []

    def semaphore(self, name):
        self.sems.append(self.nc.alloc_semaphore(name))
        return self.sems[-1]

    def sb(self, name, shape, dtype=F32):
        return self.enter_context(self.nc.sbuf_tensor(name, shape, dtype))

    def end(self):
        self.close()
        self.nc.clear_and_free_semaphores(self.sems)
        self.nc.all_engine_barrier()


class Signal:

    def __init__(self, ctx, nc, name, per=0):
        self.sem = ctx.semaphore(name)
        self.per = per

    def at(self, i, k):
        return i * self.per + k


def shape_constants():
    p = np.arange(P)
    t = np.arange(T)
    head = p // DH
    decay = np.log(1.0 - 2.0 ** (-5.0 - head.astype(np.float64)))
    shift = (p[:, None] + 1 == p[None, :])
    edge = (p[:, None] == P - 1) & (p[None, :] == 0)
    out = {
        "ident": np.eye(P),
        "prev": shift, "prev_edge": edge,
        "next": shift.T, "next_edge": edge.T,
        "causal": p[:, None] <= p[None, :],
        "same_head": head[:, None] == head[None, :],
        "head_col": head[:, None] == np.arange(NH)[None, :],
        "state_mask": head[:, None] == (np.arange(NH * DV) // DV)[None, :],
        "ones": np.ones((P, T)),
        "decay_q": np.exp(decay[:, None] * t) / np.sqrt(float(DH)),
        "decay_k": np.exp(-decay[:, None] * t),
    }
    return {k: np.ascontiguousarray(v, dtype=np.float32) for k, v in out.items()}


class Memory:

    def __init__(self, ctx, nc, dram):
        self.ctx, self.nc, self.dram = ctx, nc, dram
        self.h = self.sb("h", [P, NT, D])
        self.bank = [ctx.enter_context(nc.psum_tensor(f"bank{n}", [P, T], F32)) for n in range(8)]
        self.w = {}
        self.loaded = {}
        self.load_log = []

    def sb(self, name, shape, dtype=F32):
        return self.ctx.enter_context(self.nc.sbuf_tensor(name, shape, dtype))

    def load(self, layer, name):
        src = self.dram[name]
        self.load_log.append(name)
        t = layer.enter_context(self.nc.sbuf_tensor(f"w_{name}_{len(self.load_log)}", list(src.shape), src.dtype))
        s = layer.semaphore(f"loaded_{name}_{len(self.load_log)}")
        self.w[name] = t
        self.loaded[name] = s
        return t, s, src


def token_conv(ctx, nc, m):
    gathered = [Signal(ctx, nc, f"tok_gathered{b}") for b in range(B)]
    ids_in = Signal(ctx, nc, "tok_ids_in")
    summed = Signal(ctx, nc, "tok_summed")
    copied = Signal(ctx, nc, "tok_copied")
    loads = [(n, *m.load(m.ctx, n)) for n in ("ident", "prev", "prev_edge", "next", "next_edge")]
    rest = [(n, *m.load(m.ctx, n)) for n in m.early]
    ids = m.sb("ids", [P, NT], I32)
    rows = m.big[:, 0:NT * TAPS * D].rearrange("p (n k) -> p n k", n=NT)
    with nc.Block() as block:
        @block.sync
        def _(sp):
            for _, t, s, src in loads + rest:
                sp.dma_start(t[:, :], src).then_inc(s, 16)
            sp.wait_ge(gathered[B - 1].sem, 16 * NC_)
            sp.dma_start(m.queues.rearrange("(n p r) d -> p n (r d)", p=P, r=4),
                         m.zeros[:, :].rearrange("p (o x) -> p o x", o=1).broadcast_to([P, CE * CAP // T + 4, T])).then_inc(m.queues_zero, 16)

        @block.gpsimd
        def _(pool):
            pool.dma_start(ids[:, :], m.dram["ids"]).then_inc(ids_in.sem, 16)
            pool.wait_ge(ids_in.sem, 16)
            for n in range(NT):
                pool.indirect_dma_start(
                    out=rows[:, n, :], out_offset=None, in_=m.dram["table"],
                    in_offset=bass.IndirectOffsetOnAxis(ap=ids[:, n:n + 1].bitcast(U32), axis=0),
                ).then_inc(gathered[n // NC_].sem, 16)

        @block.tensor
        def _(pe):
            for name, _, s, _ in loads:
                pe.wait_ge(s, 16)
            for b in range(B):
                pe.wait_ge(gathered[b].sem, 16 * NC_)
                if b >= 4:
                    pe.wait_ge(copied.sem, b - 3)
                g = rows[:, b * NC_:(b + 1) * NC_, :]
                ps = m.bank[b % 4]
                out = ps[:, :].rearrange("p (c d) -> p c d", c=NC_)
                w = m.w
                nc.tensor.matmul(out[:, :, :], w["prev"][:, :], g[:, :, 0:D], start=True, stop=False)
                nc.tensor.matmul(out[:, 1:NC_, :], w["prev_edge"][:, :], g[:, 0:NC_ - 1, 0:D], start=False, stop=False, skip_group_check=True)
                nc.tensor.matmul(out[:, :, :], w["ident"][:, :], g[:, :, D:2 * D], start=False, stop=False)
                nc.tensor.matmul(out[:, 0:NC_ - 1, :], w["next_edge"][:, :], g[:, 1:NC_, 2 * D:3 * D], start=False, stop=False, skip_group_check=True)
                last = nc.tensor.matmul(out[:, :, :], w["next"][:, :], g[:, :, 2 * D:3 * D], start=False, stop=True)
                last.then_inc(summed.sem, 1)

        @block.vector
        def _(dve):
            for b in range(B):
                dve.wait_ge(summed.sem, b + 1)
                nc.vector.tensor_copy(m.h[:, b * NC_:(b + 1) * NC_, :],
                                      m.bank[b % 4][:, :].rearrange("p (c d) -> p c d", c=NC_)).then_inc(copied.sem, 1)


class Norm:

    def __init__(self, ctx, nc, m, tag, slots=(0, 1)):
        self.nc, self.m = nc, m
        self.slots = slots
        n = len(slots)
        self.step = Signal(ctx, nc, tag + "_norm_step", 2 * n)
        self.var = Signal(ctx, nc, tag + "_norm_var", n)
        self.root = Signal(ctx, nc, tag + "_norm_root", n)
        self.ready = Signal(ctx, nc, tag + "_norm_ready", n)

    def vector_stats(self, dve, i, src):
        nc, m = self.nc, self.m
        for k, s in enumerate(self.slots):
            for c in range(NC_):
                last = nc.vector.bn_stats(m.nstat[s][:, c, :], src[k][:, c, :])
            last.then_inc(self.step.sem, 1)

    def vector_aggr(self, dve, i):
        nc, m, n = self.nc, self.m, len(self.slots)
        for k, s in enumerate(self.slots):
            dve.wait_ge(self.step.sem, self.step.at(i, k + 1))
            nc.vector.memset(m.fence[:, s:s + 1], 0.0)
            for c in range(NC_):
                last = nc.vector.bn_aggr(m.nmv[s][:, c, :], m.nstat[s][:, c, :])
            last.then_inc(self.step.sem, 1)
        for k, s in enumerate(self.slots):
            dve.wait_ge(self.step.sem, self.step.at(i, n + k + 1))
            nc.vector.tensor_scalar(m.nrstd[s][:, :], m.nmv[s][:, :, 1], LN_EPS, None, ALU.add).then_inc(self.var.sem, 1)

    def vector_scale(self, dve, i, src, out):
        nc, m = self.nc, self.m
        for k, s in enumerate(self.slots):
            dve.wait_ge(self.root.sem, self.root.at(i, k + 1))
            for c in range(NC_):
                last = nc.vector.tensor_scalar(out[k][:, c, :], src[k][:, c, :], m.nmv[s][:, c, 0:1],
                                               m.nrstd[s][:, c:c + 1], ALU.subtract, ALU.mult)
            last.then_inc(self.ready.sem, 1)

    def vector(self, dve, i, src, out):
        self.vector_stats(dve, i, src)
        self.vector_aggr(dve, i)
        self.vector_scale(dve, i, src, out)

    def gpsimd(self, pool, i):
        for k, s in enumerate(self.slots):
            pool.wait_ge(self.var.sem, self.var.at(i, k + 1))
            self.nc.gpsimd.tensor_tensor(self.m.nrstd[s][:, :], self.m.nrstd[s][:, :], self.m.minus_half[:, 0:NC_],
                                         ALU.pow).then_inc(self.root.sem, 1)


def linear_attention(ctx, nc, m):
    S = range(2)
    sig = lambda name, per: Signal(ctx, nc, "la_" + name, per)
    norm = Norm(ctx, nc, m, "la")
    xt_ps, xt_sb = sig("xt_ps", 2), sig("xt_sb", 2)
    qk_ps, exp_sb, phi, phi_step = sig("qk_ps", 4), sig("exp_sb", 4), sig("phi", 4), sig("phi_step", 4)
    z_step, qz, den_ps, den_sb, qn = sig("z_step", 2), sig("qz", 2), sig("den_ps", 2), sig("den_sb", 4), sig("qn", 2)
    km_d, km_a = sig("km_d", 2), sig("km_a", 2)
    kt_ps, kt_sb = sig("kt_ps", 2), sig("kt_sb", 2)
    v_ps, v_sb = sig("v_ps", 8), sig("v_sb", 8)
    st_ps, st_sb = sig("st_ps", 6), sig("st_sb", 6)
    sc_ps, a_sb = sig("sc_ps", 16), sig("a_sb", 16)
    av_ps, ot_sb = sig("av_ps", 8), sig("ot_sb", 8)
    y_ps, h_sb = sig("y_ps", 2), sig("h_sb", 2)
    NS = NC_ - 1
    XN, XT = m.XN, m.XT
    QT, KT, EX = m.t512a, m.t512b, m.t512c
    KM, A, V, KTOK, ST, OT = m.KM, m.A, m.V, m.KTOK, m.ST, m.OT
    w = m.w

    with nc.Block() as block:
        @block.vector
        def _(dve):
            for n in ("ones", "causal", "head_col", "state_mask"):
                dve.wait_ge(m.loaded[n], 16)
            with dve.Fori(0, PAIRS) as i:
                hs = [m.h[:, bass.ds((2 * i + s) * NC_, NC_), :] for s in S]
                norm.vector(dve, i, hs, [XN[s] for s in S])
                for q in range(2):
                    for s in S:
                        n = 2 * q + s + 1
                        dve.wait_ge(exp_sb.sem, exp_sb.at(i, n))
                        nc.vector.tensor_scalar(EX[s][:, q, :], EX[s][:, q, :], 1.0, None, ALU.min).then_inc(phi_step.sem, 1)
                    for s in S:
                        n = 2 * q + s + 1
                        dve.wait_ge(phi_step.sem, phi_step.at(i, n))
                        nc.vector.scalar_tensor_tensor((QT, KT)[q][s][:, :], m.bank[4 * s + 1 + q][:, :], 1.0, EX[s][:, q, :],
                                                       ALU.add, ALU.max).then_inc(phi.sem, 1)
                for s in S:
                    dve.wait_ge(phi.sem, phi.at(i, 3 + s))
                    nc.vector.tensor_tensor_scan(EX[s][:, 0, :], w["ones"][:, :], KT[s][:, :], 0.0, ALU.mult, ALU.add).then_inc(z_step.sem, 1)
                for s in S:
                    dve.wait_ge(z_step.sem, z_step.at(i, s + 1))
                    nc.vector.tensor_tensor(EX[s][:, 1, :], EX[s][:, 0, :], QT[s][:, :], ALU.mult).then_inc(qz.sem, 1)
                for s in S:
                    for hd in range(NH // 2):
                        last = nc.vector.tensor_scalar(KM[s][:, hd, :], KT[s][:, :], w["head_col"][:, hd:hd + 1], None, ALU.mult)
                    last.then_inc(km_d.sem, 1)
                for s in S:
                    dve.wait_ge(den_ps.sem, den_ps.at(i, s + 1))
                    nc.vector.tensor_scalar(EX[s][:, 0, :], m.bank[4 * s][:, :], 1e-6, None, ALU.max).then_inc(den_sb.sem, 1)
                for s in S:
                    dve.wait_ge(den_sb.sem, den_sb.at(i, s + 1))
                    nc.vector.reciprocal(EX[s][:, 0, :], EX[s][:, 0, :]).then_inc(den_sb.sem, 1)
                for s in S:
                    dve.wait_ge(den_sb.sem, den_sb.at(i, 2 + s + 1))
                    nc.vector.tensor_tensor(QT[s][:, :], QT[s][:, :], EX[s][:, 0, :], ALU.mult).then_inc(qn.sem, 1)
                for c in range(NS):
                    for s in S:
                        dve.wait_ge(st_ps.sem, st_ps.at(i, 2 * c + s + 1))
                        nc.vector.tensor_tensor(ST[s][:, c, :], m.bank[4 * s + 3][:, :], w["state_mask"][:, :], ALU.mult).then_inc(st_sb.sem, 1)
                for g in range(NH // 2):
                    for s in S:
                        for par in range(2):
                            dve.wait_ge(sc_ps.sem, sc_ps.at(i, 4 * g + 2 * s + par + 1))
                            nc.vector.tensor_tensor(A[s][:, 2 * (g % 2) + par, :, :], m.bank[4 * s + par][:, :].rearrange("p (c t) -> p c t", c=NC_),
                                                    w["causal"][:, :].rearrange("p (o t) -> p o t", o=1).broadcast_to([P, NC_, P]),
                                                    ALU.mult).then_inc(a_sb.sem, 1)
                for s in S:
                    dve.wait_ge(y_ps.sem, y_ps.at(i, s + 1))
                    nc.vector.tensor_tensor(hs[s], hs[s], m.bank[4 * s][:, :].rearrange("p (c d) -> p c d", c=NC_), ALU.add).then_inc(h_sb.sem, 1)
                dve.wait_ge(h_sb.sem, h_sb.at(i, 2))

        @block.gpsimd
        def _(pool):
            with pool.Fori(0, PAIRS) as i:
                norm.gpsimd(pool, i)

        @block.scalar
        def _(act):
            act.wait_ge(m.loaded["head_col"], 16)
            with act.Fori(0, PAIRS) as i:
                for s in S:
                    act.wait_ge(xt_ps.sem, xt_ps.at(i, s + 1))
                    nc.scalar.copy(XT[s][:, :], m.bank[4 * s][:, :]).then_inc(xt_sb.sem, 1)
                for q in range(2):
                    for s in S:
                        act.wait_ge(qk_ps.sem, qk_ps.at(i, 2 * q + s + 1))
                        nc.scalar.activation(EX[s][:, q, :], m.bank[4 * s + 1 + q][:, :], ACT.Exp).then_inc(exp_sb.sem, 1)
                for c in range(NC_):
                    for s in S:
                        act.wait_ge(v_ps.sem, v_ps.at(i, 2 * c + s + 1))
                        nc.scalar.copy(V[s][:, c, :], m.bank[4 * s + (3 if c % 2 else 0)][:, :]).then_inc(v_sb.sem, 1)
                for s in S:
                    act.wait_ge(phi.sem, phi.at(i, 3 + s))
                    for hd in range(NH // 2, NH):
                        last = nc.scalar.activation(KM[s][:, hd, :], KT[s][:, :], ACT.Copy, scale=w["head_col"][:, hd:hd + 1])
                    last.then_inc(km_a.sem, 1)
                for s in S:
                    act.wait_ge(kt_ps.sem, kt_ps.at(i, s + 1))
                    nc.scalar.copy(KTOK[s][:, :, :], m.bank[4 * s + 1][:, 0:NS * P].rearrange("p (c k) -> p c k", c=NS)).then_inc(kt_sb.sem, 1)
                for g in range(NH // 2):
                    for s in S:
                        act.wait_ge(av_ps.sem, av_ps.at(i, 2 * g + s + 1))
                        nc.scalar.copy(OT[s][:, g, :], m.bank[4 * s + 2 + g % 2][:, :]).then_inc(ot_sb.sem, 1)

        @block.tensor
        def _(pe):
            for n in ("wq", "wk", "wv", "wout", "same_head"):
                pe.wait_ge(m.loaded[n], 16)
            with pe.Fori(0, PAIRS) as i:
                for s in S:
                    pe.wait_ge(norm.ready.sem, norm.ready.at(i, s + 1))
                    for c in range(NC_):
                        last = nc.tensor.transpose(m.bank[4 * s][:, c * P:(c + 1) * P], XN[s][:, c, :], w["ident"][:, :])
                    last.then_inc(xt_ps.sem, 1)
                for s in S:
                    pe.wait_ge(xt_sb.sem, xt_sb.at(i, s + 1))
                    nc.tensor.matmul(m.bank[4 * s + 1][:, :], w["wq"][:, :], XT[s][:, :], start=True, stop=True).then_inc(qk_ps.sem, 1)
                for s in S:
                    nc.tensor.matmul(m.bank[4 * s + 2][:, :], w["wk"][:, :], XT[s][:, :], start=True, stop=True).then_inc(qk_ps.sem, 1)
                for c in range(NC_):
                    for s in S:
                        if c >= 2:
                            pe.wait_ge(v_sb.sem, v_sb.at(i, 2 * (c - 2) + s + 1))
                        nc.tensor.matmul(m.bank[4 * s + (3 if c % 2 else 0)][:, :], XT[s][:, c * P:(c + 1) * P], w["wv"][:, :],
                                         start=True, stop=True).then_inc(v_ps.sem, 1)
                for s in S:
                    pe.wait_ge(phi.sem, phi.at(i, 3 + s))
                    for c in range(NS):
                        last = nc.tensor.transpose(m.bank[4 * s + 1][:, c * P:(c + 1) * P], KT[s][:, c * P:(c + 1) * P], w["ident"][:, :])
                    last.then_inc(kt_ps.sem, 1)
                for s in S:
                    pe.wait_ge(qz.sem, qz.at(i, s + 1))
                    pe.wait_ge(v_sb.sem, v_sb.at(i, 4 + s + 1))
                    nc.tensor.matmul(m.bank[4 * s][:, :], w["same_head"][:, :], EX[s][:, 1, :], start=True, stop=True).then_inc(den_ps.sem, 1)
                for c in range(NS):
                    for s in S:
                        if c == 0:
                            pe.wait_ge(kt_sb.sem, kt_sb.at(i, s + 1))
                            pe.wait_ge(v_sb.sem, v_sb.at(i, 6 + s + 1))
                        else:
                            pe.wait_ge(st_sb.sem, st_sb.at(i, 2 * (c - 1) + s + 1))
                        nc.tensor.matmul(m.bank[4 * s + 3][:, :], KTOK[s][:, c, :], V[s][:, c, :],
                                         start=c == 0, stop=c == NS - 1, skip_group_check=True).then_inc(st_ps.sem, 1)

                def scores(g, s):
                    if g == 0:
                        pe.wait_ge(qn.sem, qn.at(i, s + 1))
                        pe.wait_ge(km_d.sem, km_d.at(i, s + 1))
                    if g == 2:
                        pe.wait_ge(km_a.sem, km_a.at(i, s + 1))
                    for par in range(2):
                        hd = 2 * g + par
                        if g:
                            pe.wait_ge(a_sb.sem, a_sb.at(i, 4 * (g - 1) + 2 * s + par + 1))
                        for c in range(NC_):
                            last = nc.tensor.matmul(m.bank[4 * s + par][:, c * P:(c + 1) * P], KM[s][:, hd, c * P:(c + 1) * P],
                                                    QT[s][:, c * P:(c + 1) * P], start=True, stop=True)
                        last.then_inc(sc_ps.sem, 1)

                def values(g, s):
                    pe.wait_ge(a_sb.sem, a_sb.at(i, 4 * g + 2 * s + 2))
                    if g == 0:
                        pe.wait_ge(st_sb.sem, st_sb.at(i, 2 * (NS - 1) + s + 1))
                    if g >= 2:
                        pe.wait_ge(ot_sb.sem, ot_sb.at(i, 2 * (g - 2) + s + 1))
                    out = m.bank[4 * s + 2 + g % 2]
                    for c in range(NC_):
                        for par in range(2):
                            hd = 2 * g + par
                            last = nc.tensor.matmul(out[DV * par:DV * par + DV, c * P:(c + 1) * P], V[s][:, c, hd * DV:(hd + 1) * DV],
                                                    A[s][:, 2 * (g % 2) + par, c, :], start=True, stop=c == 0)
                        if c:
                            last = nc.tensor.matmul(out[:, c * P:(c + 1) * P], ST[s][:, c - 1, g * P:(g + 1) * P],
                                                    QT[s][:, c * P:(c + 1) * P], start=False, stop=True)
                    last.then_inc(av_ps.sem, 1)

                for s in S:
                    scores(0, s)
                for g in range(NH // 2):
                    for s in S:
                        if g + 1 < NH // 2:
                            scores(g + 1, s)
                        values(g, s)
                for s in S:
                    pe.wait_ge(ot_sb.sem, ot_sb.at(i, 6 + s + 1))
                    for c in range(NC_):
                        for g in range(NH // 2):
                            last = nc.tensor.matmul(m.bank[4 * s][:, c * P:(c + 1) * P], OT[s][:, g, c * P:(c + 1) * P],
                                                    w["wout"][:, g * D:(g + 1) * D], start=g == 0, stop=g == NH // 2 - 1)
                    last.then_inc(y_ps.sem, 1)


def modulated_ffn(ctx, nc, m):
    S = range(2)
    sig = lambda name, per: Signal(ctx, nc, "mf_" + name, per)
    w = m.w
    F = 512
    G4 = F // P
    late = [(n, *m.load(ctx, n)) for n in ("gfc1", "gfc1_b", "gfc2_rep", "gfc2_b", "task_b1", "b1", "ln_coef", "ln_rows",
                                            "task_b2", "gate_row", "gate_pad")]
    tv1, tv2 = m.KM[0], m.KM[1]
    tv1_in, tv2_in, w1_in, w2_in = (ctx.semaphore("loaded_" + n) for n in ("tv1", "tv2", "W1", "W2"))
    W1, W2 = m.ST[0][:, 0, :], m.ST[0][:, 1, :]
    W1M, W2M = m.t512a, m.t512b
    HH = [m.big[:, 16 * T + s * 4 * T:16 * T + (s + 1) * 4 * T].rearrange("p (g n) -> p g n", g=G4) for s in S]
    junk = [m.t512c[s][:, 0, :] for s in S]
    res = [m.XN[s] for s in S]
    GH = ctx.sb("mf_gate_hidden", [P, B])
    gcol = ctx.sb("mf_gate", [P, B])
    grow = ctx.sb("mf_gate_first", [P, B])
    b1m = ctx.sb("mf_b1m", [P, G4, B])
    lngb = ctx.sb("mf_ln", [P, 2 * D])
    gsel = [ctx.sb(f"mf_gsel{s}", [P, 48]) for s in S]
    gb2 = [ctx.sb(f"mf_gb2{s}", [P, P]) for s in S]
    norm, norm2 = Norm(ctx, nc, m, "mf"), Norm(ctx, nc, m, "mf2")
    xt_ps, xt_sb, gh_ps, gh_sb = sig("xt_ps", 2), sig("xt_sb", 2), sig("gh_ps", 2), sig("gh_sb", 2)
    gate_ps, gate_sb, small_ps, small_sb = sig("gate_ps", 0), sig("gate_sb", 0), sig("small_ps", 0), sig("small_sb", 0)
    gs_sb, xn_kept = sig("gs_sb", 2), sig("xn_kept", 32)
    XN = m.XN
    m1_ps, m1_sb, m2_ps, m2_sb = sig("m1_ps", 2), sig("m1_sb", 2), sig("m2_ps", 2), sig("m2_sb", 2)
    f_ps, f_sb, o_ps, r_sb, sc_sb, hb_sb, h_sb = (sig("f_ps", 8), sig("f_sb", 8), sig("o_ps", 2), sig("r_sb", 2), sig("sc_sb", 2),
                                                  sig("hb_sb", 2), sig("h_sb", 2))
    over = lambda v, n=NC_: v.rearrange("p (o t) -> p o t", o=1).broadcast_to([P, n, v.shape[-1]])

    with nc.Block() as block:
        @block.sync
        def _(sp):
            for _, t, sem, src in late:
                sp.dma_start(t[:, :], src).then_inc(sem, 16)
            sp.dma_start(tv1[:, :, :].rearrange("p a t -> p (a t)"), m.dram["task_W1"]).then_inc(tv1_in, 16)
            sp.dma_start(tv2[:, :, :].rearrange("p a t -> p (a t)"), m.dram["task_W2"]).then_inc(tv2_in, 16)
            sp.dma_start(W1, m.dram["W1"]).then_inc(w1_in, 16)
            sp.dma_start(W2, m.dram["W2"]).then_inc(w2_in, 16)
            with sp.Fori(0, PAIRS) as i:
                for s in S:
                    sp.wait_ge(norm.ready.sem, norm.ready.at(i, s + 1))
                    sp.dma_start(m.XNA[:, bass.ds((2 * i + s) * NC_, NC_), :], XN[s][:, :, :]).then_inc(xn_kept.sem, 16)

        @block.vector
        def _(dve):
            with dve.Fori(0, PAIRS) as i:
                hs = [m.h[:, bass.ds((2 * i + s) * NC_, NC_), :] for s in S]
                xs = [m.XNA[:, bass.ds((2 * i + s) * NC_, NC_), :] for s in S]
                norm.vector(dve, i, hs, [XN[s] for s in S])
                dve.wait_ge(xn_kept.sem, xn_kept.at(i, 32))
                dve.wait_ge(gh_sb.sem, gh_sb.at(i, 2))
            dve.wait_ge(gate_ps.sem, 1)
            dve.wait_ge(m.loaded["gfc2_b"], 16)
            nc.vector.tensor_scalar(gcol[:, :], m.bank[0][:, 0:B], 1.0 / T, w["gfc2_b"][:, 0:1], ALU.mult, ALU.add).then_inc(gate_sb.sem, 1)
            dve.wait_ge(gate_sb.sem, 1)
            dve.wait_ge(m.loaded["gate_row"], 16)
            nc.vector.tensor_scalar(grow[:, :], gcol[:, :], w["gate_row"][:, 0:1], None, ALU.mult).then_inc(gate_sb.sem, 1)
            dve.wait_ge(small_ps.sem, 1)
            dve.wait_ge(m.loaded["b1"], 16)
            nc.vector.tensor_tensor(b1m[:, :, :], m.bank[1][:, 0:G4 * B].rearrange("p (g b) -> p g b", g=G4),
                                    w["b1"][:, :].rearrange("p (g o) -> p g o", o=1).broadcast_to([P, G4, B]), ALU.add).then_inc(small_sb.sem, 1)
            nc.vector.tensor_copy(lngb[:, :], m.bank[2][:, 0:2 * D]).then_inc(small_sb.sem, 1)
            dve.wait_ge(gate_sb.sem, 2)
            dve.wait_ge(small_sb.sem, 2)
            for sem in (m.loaded["gate_pad"], w1_in, w2_in):
                dve.wait_ge(sem, 16)
            with dve.Fori(0, PAIRS) as i:
                hs = [m.h[:, bass.ds((2 * i + s) * NC_, NC_), :] for s in S]
                xs = [m.XNA[:, bass.ds((2 * i + s) * NC_, NC_), :] for s in S]
                for s in S:
                    nc.vector.tensor_scalar(gsel[s][:, :], w["gate_pad"][:, :], gcol[:, bass.ds(2 * i + s, 1)], None, ALU.mult)
                    nc.vector.tensor_scalar(gb2[s][:, :], w["ones"][:, 0:P], grow[:, bass.ds(2 * i + s, 1)], w["gate_row"][:, 1:2],
                                            ALU.mult, ALU.add).then_inc(gs_sb.sem, 1)
                for s in S:
                    dve.wait_ge(m1_ps.sem, m1_ps.at(i, s + 1))
                    nc.vector.tensor_tensor(W1M[s][:, :], m.bank[4 * s][:, :], W1, ALU.add).then_inc(m1_sb.sem, 1)
                for s in S:
                    dve.wait_ge(m2_ps.sem, m2_ps.at(i, s + 1))
                    nc.vector.tensor_tensor(W2M[s][:, :], m.bank[4 * s + 1][:, :], W2, ALU.add).then_inc(m2_sb.sem, 1)
                for s in S:
                    dve.wait_ge(o_ps.sem, o_ps.at(i, s + 1))
                    nc.vector.tensor_tensor(res[s][:, :, :], m.bank[4 * s][:, :].rearrange("p (c d) -> p c d", c=NC_), xs[s], ALU.add).then_inc(r_sb.sem, 1)
                dve.wait_ge(r_sb.sem, r_sb.at(i, 2))
                norm2.vector(dve, i, [res[s] for s in S], [res[s] for s in S])
                for s in S:
                    dve.wait_ge(norm2.ready.sem, norm2.ready.at(i, s + 1))
                    nc.vector.tensor_tensor(res[s][:, :, :], res[s][:, :, :], over(lngb[:, 0:D]), ALU.mult).then_inc(sc_sb.sem, 1)
                for s in S:
                    dve.wait_ge(sc_sb.sem, sc_sb.at(i, s + 1))
                    dve.wait_ge(hb_sb.sem, hb_sb.at(i, s + 1))
                    nc.vector.tensor_tensor(hs[s], hs[s], res[s][:, :, :], ALU.add).then_inc(h_sb.sem, 1)
                dve.wait_ge(h_sb.sem, h_sb.at(i, 2))

        @block.gpsimd
        def _(pool):
            with pool.Fori(0, PAIRS) as i:
                norm.gpsimd(pool, i)
            pool.wait_ge(small_sb.sem, 2)
            with pool.Fori(0, PAIRS) as i:
                for s in S:
                    hs = m.h[:, bass.ds((2 * i + s) * NC_, NC_), :]
                    nc.gpsimd.tensor_tensor(hs, hs, over(lngb[:, D:2 * D]), ALU.add).then_inc(hb_sb.sem, 1)
                norm2.gpsimd(pool, i)

        @block.scalar
        def _(act):
            act.wait_ge(m.loaded["gfc1_b"], 16)
            with act.Fori(0, PAIRS) as i:
                for s in S:
                    act.wait_ge(xt_ps.sem, xt_ps.at(i, s + 1))
                    nc.scalar.copy(m.XTA[:, bass.ds((2 * i + s) * T, T)], m.bank[4 * s][:, :]).then_inc(xt_sb.sem, 1)
                for s in S:
                    act.wait_ge(gh_ps.sem, gh_ps.at(i, s + 1))
                    nc.scalar.activation(junk[s], m.bank[4 * s + 1][:, :], ACT.Relu, bias=w["gfc1_b"][:, 0:1],
                                         accum_out=GH[:, bass.ds(2 * i + s, 1)]).then_inc(gh_sb.sem, 1)
            act.wait_ge(small_sb.sem, 1)
            with act.Fori(0, PAIRS) as i:
                for g in range(G4):
                    for s in S:
                        act.wait_ge(f_ps.sem, f_ps.at(i, 2 * g + s + 1))
                        nc.scalar.activation(HH[s][:, g, :], m.bank[4 * s + 2 + g % 2][:, :], ACT.Relu,
                                             bias=b1m[:, g, bass.ds(2 * i + s, 1)]).then_inc(f_sb.sem, 1)

        @block.tensor
        def _(pe):
            pe.wait_ge(m.loaded["gfc1"], 16)
            with pe.Fori(0, PAIRS) as i:
                for s in S:
                    pe.wait_ge(norm.ready.sem, norm.ready.at(i, s + 1))
                    for c in range(NC_):
                        last = nc.tensor.transpose(m.bank[4 * s][:, c * P:(c + 1) * P], XN[s][:, c, :], w["ident"][:, :])
                    last.then_inc(xt_ps.sem, 1)
                for s in S:
                    pe.wait_ge(xt_sb.sem, xt_sb.at(i, s + 1))
                    nc.tensor.matmul(m.bank[4 * s + 1][:, :], w["gfc1"][:, :], m.XTA[:, bass.ds((2 * i + s) * T, T)], start=True, stop=True).then_inc(gh_ps.sem, 1)
            for n in ("gfc2_rep", "task_b1", "ln_coef", "ln_rows", "task_b2"):
                pe.wait_ge(m.loaded[n], 16)
            pe.wait_ge(gh_sb.sem, B)
            nc.tensor.matmul(m.bank[0][:, 0:B], w["gfc2_rep"][:, :], GH[:, :], start=True, stop=True).then_inc(gate_ps.sem, 1)
            nc.tensor.matmul(m.bank[2][:, 0:2 * D], w["ln_coef"][:, :], w["ln_rows"][:, :], start=True, stop=True)
            pe.wait_ge(gate_sb.sem, 1)
            for g in range(G4):
                last = nc.tensor.matmul(m.bank[1][:, g * B:(g + 1) * B], w["task_b1"][:, g * P:(g + 1) * P], gcol[:, :], start=True, stop=True)
            last.then_inc(small_ps.sem, 1)
            pe.wait_ge(tv1_in, 16)
            pe.wait_ge(tv2_in, 16)
            pe.wait_ge(small_sb.sem, 2)
            with pe.Fori(0, PAIRS) as i:
                def merge(s, bank, tv):
                    for j in range(2):
                        for q in range(NC_):
                            last = nc.tensor.matmul(bank[32 * q:32 * q + 32, :], gsel[s][:, 16 - 16 * j:48 - 16 * j], tv[:, 2 * q + j, :],
                                                    start=j == 0, stop=j == 1)
                    return last
                for s in S:
                    pe.wait_ge(gs_sb.sem, gs_sb.at(i, s + 1))
                    merge(s, m.bank[4 * s], tv1).then_inc(m1_ps.sem, 1)
                for s in S:
                    merge(s, m.bank[4 * s + 1], tv2).then_inc(m2_ps.sem, 1)
                for g in range(G4):
                    for s in S:
                        if g == 0:
                            pe.wait_ge(m1_sb.sem, m1_sb.at(i, s + 1))
                        if g >= 2:
                            pe.wait_ge(f_sb.sem, f_sb.at(i, 2 * (g - 2) + s + 1))
                        nc.tensor.matmul(m.bank[4 * s + 2 + g % 2][:, :], W1M[s][:, g * P:(g + 1) * P], m.XTA[:, bass.ds((2 * i + s) * T, T)],
                                         start=True, stop=True).then_inc(f_ps.sem, 1)
                for s in S:
                    pe.wait_ge(m2_sb.sem, m2_sb.at(i, s + 1))
                    pe.wait_ge(f_sb.sem, f_sb.at(i, 6 + s + 1))
                    for c in range(NC_):
                        nc.tensor.matmul(m.bank[4 * s][:, c * P:(c + 1) * P], gb2[s][:, :], w["task_b2"][:, :], start=True, stop=False)
                        for g in range(G4):
                            last = nc.tensor.matmul(m.bank[4 * s][:, c * P:(c + 1) * P], HH[s][:, g, c * P:(c + 1) * P],
                                                    W2M[s][:, g * D:(g + 1) * D], start=False, stop=g == G4 - 1)
                    last.then_inc(o_ps.sem, 1)


def retention(ctx, nc, m):
    S = range(2)
    sig = lambda name, per: Signal(ctx, nc, "re_" + name, per)
    w = m.w
    late = [(n, *m.load(ctx, n)) for n in ("r_wq", "r_wk", "r_wv", "r_wg", "r_wo", "gn", "decay_q", "decay_k")]
    XN, XT, QT, KT, KM, KTOK, ST = m.XN, m.XT, m.t512a, m.t512b, m.KM, m.KTOK, m.ST
    G = [m.t512c[s][:, 0, :] for s in S]
    TH = [m.t512c[s][:, 1, :] for s in S]
    A = [m.big[:, s * 8 * T:(s + 1) * 8 * T].rearrange("p (a c t) -> p a c t", a=NH, c=NC_) for s in S]
    VP = [[m.big[:, (16 + 2 * s + par) * T:(17 + 2 * s + par) * T].rearrange("p (c n) -> p c n", c=NC_) for par in range(2)] for s in S]
    V = [m.big[:, (20 + s) * T:(21 + s) * T].rearrange("p (c n) -> p c n", c=NC_) for s in S]
    Y = [m.big[:, (22 + s) * T:(23 + s) * T] for s in S]
    SQ = [ST[s][:, 1, :] for s in S]
    group = lambda v: v.rearrange("p (n k) -> p n k", k=DH)
    wide = lambda v: v.rearrange("p (n o) -> p n o", o=1).broadcast_to([P, NC_ * NH, DH])
    gsum = [ctx.sb(f"re_gsum{s}", [P, NC_ * NH]) for s in S]
    gvar = [ctx.sb(f"re_gvar{s}", [P, NC_ * NH]) for s in S]
    norm = Norm(ctx, nc, m, "re")
    xt_ps, xt_sb, qk_ps, qk_sb = sig("xt_ps", 2), sig("xt_sb", 2), sig("qk_ps", 4), sig("qk_sb", 4)
    g_ps, g_sb, v_ps, v_sb = sig("g_ps", 2), sig("g_sb", 2), sig("v_ps", 2), sig("v_sb", 2)
    km_d, km_a, kt_ps, kt_sb = sig("km_d", 2), sig("km_a", 2), sig("kt_ps", 2), sig("kt_sb", 2)
    st_ps, st_sb, sc_ps, a_sb = sig("st_ps", 6), sig("st_sb", 6), sig("sc_ps", 16), sig("a_sb", 16)
    av_ps, ot_sb, tok_ps, y_sb = sig("av_ps", 2), sig("ot_sb", 2), sig("tok_ps", 2), sig("y_sb", 2)
    gstep, sq_sb, root_in, root, gn_sb = sig("gstep", 8), sig("sq_sb", 2), sig("root_in", 2), sig("root", 2), sig("gn_sb", 2)
    ch_ps, ch_sb, sum_sb, th_sb, z_sb, y_ps, h_sb = (sig("ch_ps", 2), sig("ch_sb", 2), sig("sum_sb", 2), sig("th_sb", 2), sig("z_sb", 2),
                                                     sig("y_ps", 2), sig("h_sb", 2))
    zeroed = sig("zeroed", 0)
    NS = NC_ - 1
    ND = 3

    with nc.Block() as block:
        @block.sync
        def _(sp):
            for _, t, sem, src in late:
                sp.dma_start(t[:, :], src).then_inc(sem, 16)

        @block.vector
        def _(dve):
            for n in ("decay_q", "decay_k"):
                dve.wait_ge(m.loaded[n], 16)
            with dve.Fori(0, PAIRS) as i:
                hs = [m.h[:, bass.ds((2 * i + s) * NC_, NC_), :] for s in S]
                norm.vector(dve, i, hs, [XN[s] for s in S])
                for q in range(2):
                    for s in S:
                        dve.wait_ge(qk_ps.sem, qk_ps.at(i, 2 * q + s + 1))
                        nc.vector.tensor_tensor((QT, KT)[q][s][:, :], m.bank[4 * s + 1 + q][:, :], w[("decay_q", "decay_k")[q]][:, :],
                                                ALU.mult).then_inc(qk_sb.sem, 1)
                for s in S:
                    dve.wait_ge(qk_sb.sem, qk_sb.at(i, 3 + s))
                    for hd in range(ND):
                        last = nc.vector.tensor_scalar(KM[s][:, hd, :], KT[s][:, :], w["head_col"][:, hd:hd + 1], None, ALU.mult)
                    last.then_inc(km_d.sem, 1)
                for c in range(NS):
                    for s in S:
                        dve.wait_ge(st_ps.sem, st_ps.at(i, 2 * c + s + 1))
                        nc.vector.tensor_tensor(ST[s][:, 0, c * P:(c + 1) * P], m.bank[4 * s + 3][:, 0:P], w["same_head"][:, :], ALU.mult).then_inc(st_sb.sem, 1)
                for g in range(NH // 2):
                    for s in S:
                        for par in range(2):
                            dve.wait_ge(sc_ps.sem, sc_ps.at(i, 4 * g + 2 * s + par + 1))
                            nc.vector.tensor_tensor(A[s][:, 2 * g + par, :, :], m.bank[4 * s + par][:, :].rearrange("p (c t) -> p c t", c=NC_),
                                                    w["causal"][:, :].rearrange("p (o t) -> p o t", o=1).broadcast_to([P, NC_, P]),
                                                    ALU.mult).then_inc(a_sb.sem, 1)
                for s in S:
                    dve.wait_ge(y_sb.sem, y_sb.at(i, s + 1))
                    nc.vector.tensor_reduce(gsum[s][:, :], group(Y[s]), AX.X, ALU.add).then_inc(gstep.sem, 1)
                for s in S:
                    dve.wait_ge(gstep.sem, gstep.at(i, s + 1))
                    nc.vector.tensor_scalar(gsum[s][:, :], gsum[s][:, :], 1.0 / DH, None, ALU.mult).then_inc(gstep.sem, 1)
                for s in S:
                    dve.wait_ge(gstep.sem, gstep.at(i, 2 + s + 1))
                    nc.vector.tensor_tensor(group(Y[s]), group(Y[s]), wide(gsum[s][:, :]), ALU.subtract).then_inc(gstep.sem, 1)
                for s in S:
                    dve.wait_ge(sq_sb.sem, sq_sb.at(i, s + 1))
                    nc.vector.tensor_reduce(gvar[s][:, :], group(SQ[s]), AX.X, ALU.add).then_inc(gstep.sem, 1)
                for s in S:
                    dve.wait_ge(gstep.sem, gstep.at(i, 6 + s + 1))
                    nc.vector.tensor_scalar(gvar[s][:, :], gvar[s][:, :], 1.0 / DH, LN_EPS, ALU.mult, ALU.add).then_inc(root_in.sem, 1)
                for s in S:
                    dve.wait_ge(root.sem, root.at(i, s + 1))
                    nc.vector.tensor_tensor(group(Y[s]), group(Y[s]), wide(gvar[s][:, :]), ALU.mult).then_inc(gn_sb.sem, 1)
                for s in S:
                    dve.wait_ge(ch_sb.sem, ch_sb.at(i, s + 1))
                    nc.vector.tensor_tensor(G[s], G[s], SQ[s], ALU.add).then_inc(sum_sb.sem, 1)
                for s in S:
                    dve.wait_ge(th_sb.sem, th_sb.at(i, s + 1))
                    nc.vector.scalar_tensor_tensor(G[s], TH[s], 1.0, G[s], ALU.add, ALU.mult).then_inc(z_sb.sem, 1)
                for s in S:
                    dve.wait_ge(y_ps.sem, y_ps.at(i, s + 1))
                    nc.vector.scalar_tensor_tensor(hs[s], m.bank[4 * s][:, :].rearrange("p (c d) -> p c d", c=NC_), 0.5, hs[s],
                                                   ALU.mult, ALU.add).then_inc(h_sb.sem, 1)
                dve.wait_ge(h_sb.sem, h_sb.at(i, 2))

        @block.gpsimd
        def _(pool):
            for s in S:
                for par in range(2):
                    nc.gpsimd.memset(VP[s][par][:, :, :], 0.0).then_inc(zeroed.sem, 1)
            pool.wait_ge(zeroed.sem, 4)
            with pool.Fori(0, PAIRS) as i:
                norm.gpsimd(pool, i)
                for s in S:
                    pool.wait_ge(root_in.sem, root_in.at(i, s + 1))
                    nc.gpsimd.tensor_tensor(gvar[s][:, :], gvar[s][:, :], m.minus_half[:, 0:NC_ * NH], ALU.pow).then_inc(root.sem, 1)

        @block.scalar
        def _(act):
            act.wait_ge(m.loaded["gn"], 16)
            act.wait_ge(zeroed.sem, 4)
            half = lambda v, par: v.rearrange("p c (g a k) -> p (c g) a k", a=2, k=DH)[:, :, par, :]
            with act.Fori(0, PAIRS) as i:
                for s in S:
                    act.wait_ge(xt_ps.sem, xt_ps.at(i, s + 1))
                    nc.scalar.copy(XT[s][:, :], m.bank[4 * s][:, :]).then_inc(xt_sb.sem, 1)
                for s in S:
                    act.wait_ge(g_ps.sem, g_ps.at(i, s + 1))
                    nc.scalar.copy(G[s], m.bank[4 * s + 3][:, :]).then_inc(g_sb.sem, 1)
                for s in S:
                    act.wait_ge(v_ps.sem, v_ps.at(i, s + 1))
                    v = m.bank[4 * s + 2][:, :].rearrange("p (c n) -> p c n", c=NC_)
                    for par in range(2):
                        nc.scalar.copy(half(VP[s][par][:, :, :], par), half(v, par))
                    nc.scalar.copy(V[s][:, :, :], v).then_inc(v_sb.sem, 1)
                for s in S:
                    act.wait_ge(kt_ps.sem, kt_ps.at(i, s + 1))
                    nc.scalar.copy(KTOK[s][:, :, :], m.bank[4 * s + 1][:, 0:NS * P].rearrange("p (c k) -> p c k", c=NS)).then_inc(kt_sb.sem, 1)
                for s in S:
                    act.wait_ge(qk_sb.sem, qk_sb.at(i, 3 + s))
                    for hd in range(ND, NH):
                        last = nc.scalar.activation(KM[s][:, hd, :], KT[s][:, :], ACT.Copy, scale=w["head_col"][:, hd:hd + 1])
                    last.then_inc(km_a.sem, 1)
                for s in S:
                    act.wait_ge(av_ps.sem, av_ps.at(i, s + 1))
                    nc.scalar.copy(SQ[s], m.bank[4 * s + 2][:, :]).then_inc(ot_sb.sem, 1)
                for s in S:
                    act.wait_ge(tok_ps.sem, tok_ps.at(i, s + 1))
                    nc.scalar.copy(Y[s], m.bank[4 * s + 3][:, :]).then_inc(y_sb.sem, 1)
                for s in S:
                    act.wait_ge(gstep.sem, gstep.at(i, 4 + s + 1))
                    nc.scalar.activation(SQ[s], Y[s], ACT.Square).then_inc(sq_sb.sem, 1)
                for s in S:
                    act.wait_ge(ch_ps.sem, ch_ps.at(i, s + 1))
                    nc.scalar.activation(SQ[s], m.bank[4 * s + 3][:, :], ACT.Identity, scale=w["gn"][:, 0:1], bias=w["gn"][:, 1:2]).then_inc(ch_sb.sem, 1)
                for s in S:
                    act.wait_ge(sum_sb.sem, sum_sb.at(i, s + 1))
                    nc.scalar.activation(TH[s], G[s], ACT.Tanh, scale=0.5).then_inc(th_sb.sem, 1)

        @block.tensor
        def _(pe):
            for n in ("r_wq", "r_wk", "r_wv", "r_wg", "r_wo"):
                pe.wait_ge(m.loaded[n], 16)
            with pe.Fori(0, PAIRS) as i:
                for s in S:
                    pe.wait_ge(norm.ready.sem, norm.ready.at(i, s + 1))
                    for c in range(NC_):
                        last = nc.tensor.transpose(m.bank[4 * s][:, c * P:(c + 1) * P], XN[s][:, c, :], w["ident"][:, :])
                    last.then_inc(xt_ps.sem, 1)
                for s in S:
                    pe.wait_ge(xt_sb.sem, xt_sb.at(i, s + 1))
                    nc.tensor.matmul(m.bank[4 * s + 1][:, :], w["r_wq"][:, :], XT[s][:, :], start=True, stop=True).then_inc(qk_ps.sem, 1)
                for s in S:
                    nc.tensor.matmul(m.bank[4 * s + 2][:, :], w["r_wk"][:, :], XT[s][:, :], start=True, stop=True).then_inc(qk_ps.sem, 1)
                for s in S:
                    nc.tensor.matmul(m.bank[4 * s + 3][:, :], w["r_wg"][:, :], XT[s][:, :], start=True, stop=True).then_inc(g_ps.sem, 1)
                for s in S:
                    pe.wait_ge(qk_sb.sem, qk_sb.at(i, 3 + s))
                    for c in range(NC_):
                        last = nc.tensor.matmul(m.bank[4 * s + 2][:, c * P:(c + 1) * P], XT[s][:, c * P:(c + 1) * P], w["r_wv"][:, :], start=True, stop=True)
                    last.then_inc(v_ps.sem, 1)
                    for c in range(NS):
                        last = nc.tensor.transpose(m.bank[4 * s + 1][:, c * P:(c + 1) * P], KT[s][:, c * P:(c + 1) * P], w["ident"][:, :])
                    last.then_inc(kt_ps.sem, 1)
                for c in range(NS):
                    for s in S:
                        if c == 0:
                            pe.wait_ge(kt_sb.sem, kt_sb.at(i, s + 1))
                            pe.wait_ge(v_sb.sem, v_sb.at(i, s + 1))
                            pe.wait_ge(g_sb.sem, g_sb.at(i, s + 1))
                        else:
                            pe.wait_ge(st_sb.sem, st_sb.at(i, 2 * (c - 1) + s + 1))
                        nc.tensor.matmul(m.bank[4 * s + 3][:, 0:P], KTOK[s][:, c, :], V[s][:, c, :],
                                         start=c == 0, stop=c == NS - 1, skip_group_check=True).then_inc(st_ps.sem, 1)
                for g in range(NH // 2):
                    for s in S:
                        if g == 0:
                            pe.wait_ge(km_d.sem, km_d.at(i, s + 1))
                        if g == ND // 2:
                            pe.wait_ge(km_a.sem, km_a.at(i, s + 1))
                        for par in range(2):
                            if g:
                                pe.wait_ge(a_sb.sem, a_sb.at(i, 4 * (g - 1) + 2 * s + par + 1))
                            for c in range(NC_):
                                last = nc.tensor.matmul(m.bank[4 * s + par][:, c * P:(c + 1) * P], KM[s][:, 2 * g + par, c * P:(c + 1) * P],
                                                        QT[s][:, c * P:(c + 1) * P], start=True, stop=True)
                            last.then_inc(sc_ps.sem, 1)
                for s in S:
                    pe.wait_ge(a_sb.sem, a_sb.at(i, 12 + 2 * s + 2))
                    pe.wait_ge(st_sb.sem, st_sb.at(i, 2 * (NS - 1) + s + 1))
                    for c in range(NC_):
                        for par in range(2):
                            for g in range(NH // 2):
                                last = nc.tensor.matmul(m.bank[4 * s + 2][32 * g:32 * g + 32, c * P:(c + 1) * P],
                                                        VP[s][par][:, c, 32 * g:32 * g + 32], A[s][:, 2 * g + par, c, :],
                                                        start=par == 0, stop=par == 1 and c == 0)
                        if c:
                            last = nc.tensor.matmul(m.bank[4 * s + 2][:, c * P:(c + 1) * P], ST[s][:, 0, (c - 1) * P:c * P],
                                                    QT[s][:, c * P:(c + 1) * P], start=False, stop=True)
                    last.then_inc(av_ps.sem, 1)
                for s in S:
                    pe.wait_ge(ot_sb.sem, ot_sb.at(i, s + 1))
                    for c in range(NC_):
                        last = nc.tensor.transpose(m.bank[4 * s + 3][:, c * P:(c + 1) * P], SQ[s][:, c * P:(c + 1) * P], w["ident"][:, :])
                    last.then_inc(tok_ps.sem, 1)
                for s in S:
                    pe.wait_ge(gn_sb.sem, gn_sb.at(i, s + 1))
                    for c in range(NC_):
                        last = nc.tensor.transpose(m.bank[4 * s + 3][:, c * P:(c + 1) * P], Y[s][:, c * P:(c + 1) * P], w["ident"][:, :])
                    last.then_inc(ch_ps.sem, 1)
                for s in S:
                    pe.wait_ge(z_sb.sem, z_sb.at(i, s + 1))
                    for c in range(NC_):
                        last = nc.tensor.matmul(m.bank[4 * s][:, c * P:(c + 1) * P], G[s][:, c * P:(c + 1) * P], w["r_wo"][:, :], start=True, stop=True)
                    last.then_inc(y_ps.sem, 1)


def balanced_experts(ctx, nc, m):
    S = range(2)
    E, M, ITERS = 8, T // 8, 8
    BE = B * E
    sig = lambda name, per: Signal(ctx, nc, "be_" + name, per)
    w = m.w
    late = [(n, *m.load(ctx, n)) for n in ("gate_w", "experts", "later_expert")]
    XN, XT, XTA = m.XN, m.XT, m.XTA
    G = m.big[:, 0:NC_ * BE]
    G4 = G.rearrange("p (c b e) -> p c b e", c=NC_, b=B)
    GR = G.rearrange("p (n e) -> p n e", e=E)
    rowsum = ctx.sb("be_rowsum", [P, NC_ * B])
    colsum = ctx.sb("be_colsum", [P, BE])
    GT, WK0, WK1, SEL, EQ, PRE = (m.big[:, (1 + n) * T:(2 + n) * T] for n in range(6))
    WK = (WK0, WK1)
    m8 = ctx.sb("be_m8", [BE, 8, 8])
    small = ctx.sb("be_small", [BE, 2])
    WT = m.big[:, 7 * T:7 * T + NC_ * BE]
    WT4 = WT.rearrange("p (c b e) -> p c b e", c=NC_, b=B)
    YW = [m.KM[s][:, 0:4, :].rearrange("p a (x d) -> p (a x) d", d=D) for s in S]
    YR = [m.t512a[s] for s in S]
    norm = Norm(ctx, nc, m, "be")
    xt_ps, xt_sb, xt_kept, lg_ps, lg_sb = sig("xt_ps", 2), sig("xt_sb", 2), sig("xt_kept", 32), sig("lg_ps", 2), sig("lg_sb", 2)
    step, col_in, col_ps = sig("step", 5), sig("col_in", 1), sig("col_ps", 1)
    gt_ps, pick, sel_in, later_ps, w_in, w_ps, w_sb = (sig("gt_ps", 0), sig("pick", 0), sig("sel_in", 0), sig("later_ps", 0),
                                                       sig("w_in", 0), sig("w_ps", 0), sig("w_sb", 0))
    zeroed = sig("zeroed", 0)
    x_sb = [sig(f"x_sb{s}", 16) for s in S]
    y_ps, yw_sb, yr_sb, h_sb = sig("y_ps", 8), sig("yw_sb", 8), sig("yr_sb", 8), sig("h_sb", 2)

    with nc.Block() as block:
        @block.sync
        def _(sp):
            for _, t, sem, src in late:
                sp.dma_start(t[:, :], src).then_inc(sem, 16)
            with sp.Fori(0, PAIRS) as i:
                for s in S:
                    sp.wait_ge(xt_sb.sem, xt_sb.at(i, s + 1))
                    sp.dma_start(XTA[:, bass.ds((2 * i + s) * T, T)], XT[s][:, :]).then_inc(xt_kept.sem, 16)
            sp.wait_ge(xt_kept.sem, 16 * B)
            sp.wait_ge(lg_sb.sem, B)
            for s in S:
                sp.dma_start(XT[s][:, :], XTA[:, s * T:(s + 1) * T]).then_inc(x_sb[s].sem, 16)
            with sp.Fori(1, PAIRS) as i:
                for s in S:
                    if s == 0:
                        sp.wait_ge(y_ps.sem, y_ps.at(i, 0))
                    sp.dma_start(XT[s][:, :], XTA[:, bass.ds((2 * i + s) * T, T)]).then_inc(x_sb[s].sem, 16)

        @block.vector
        def _(dve):
            nc.vector.memset(SEL[BE:P, :], 0.0).then_inc(zeroed.sem, 1)
            with dve.Fori(0, PAIRS) as i:
                hs = [m.h[:, bass.ds((2 * i + s) * NC_, NC_), :] for s in S]
                norm.vector(dve, i, hs, [XN[s] for s in S])
                for s in S:
                    dve.wait_ge(lg_ps.sem, lg_ps.at(i, s + 1))
                    nc.vector.tensor_scalar(G4[:, :, bass.ds(2 * i + s, 1), :].rearrange("p c o e -> p c (o e)"),
                                            m.bank[4 * s + 1][:, 0:NC_ * E].rearrange("p (c e) -> p c e", c=NC_), 1e-6, None, ALU.max).then_inc(lg_sb.sem, 1)
                dve.wait_ge(lg_sb.sem, lg_sb.at(i, 2))
                dve.wait_ge(xt_kept.sem, xt_kept.at(i, 32))
            nc.vector.tensor_copy(colsum[:, :], m.w["ones"][:, 0:BE]).then_inc(lg_sb.sem, 1)
            dve.wait_ge(lg_sb.sem, B + 1)
            with dve.Fori(0, ITERS) as k:
                dve.wait_ge(col_ps.sem, col_ps.at(k, 1))
                nc.vector.tensor_reduce(colsum[:, :], m.bank[0][:, 0:NC_ * BE].rearrange("p (c n) -> p n c", c=NC_), AX.X, ALU.add).then_inc(step.sem, 1)
                dve.wait_ge(step.sem, step.at(k, 1))
                nc.vector.reciprocal(colsum[:, :], colsum[:, :]).then_inc(step.sem, 1)
                dve.wait_ge(step.sem, step.at(k, 2))
                nc.vector.tensor_tensor(G.rearrange("p (c n) -> p c n", c=NC_), G.rearrange("p (c n) -> p c n", c=NC_),
                                        colsum[:, :].rearrange("p (o n) -> p o n", o=1).broadcast_to([P, NC_, BE]), ALU.mult).then_inc(step.sem, 1)
                dve.wait_ge(step.sem, step.at(k, 3))
                nc.vector.tensor_reduce(rowsum[:, :], GR, AX.X, ALU.add).then_inc(step.sem, 1)
                dve.wait_ge(step.sem, step.at(k, 4))
                nc.vector.reciprocal(rowsum[:, :], rowsum[:, :]).then_inc(step.sem, 1)
                dve.wait_ge(step.sem, step.at(k, 5))
                nc.vector.tensor_tensor(GR, GR, rowsum[:, :].rearrange("p (n o) -> p n o", o=1).broadcast_to([P, NC_ * B, E]), ALU.mult).then_inc(col_in.sem, 1)
            chain = [0]

            def link(ins):
                chain[0] += 1
                ins.then_inc(pick.sem, 1)
                dve.wait_ge(pick.sem, chain[0])

            dve.wait_ge(gt_ps.sem, 1)
            nc.vector.tensor_copy(WK0[0:BE, :], m.bank[1][0:BE, :])
            link(nc.vector.tensor_copy(GT[0:BE, :], m.bank[1][0:BE, :]))
            for r in range(M // 8):
                link(nc.vector.max(m8[:, r, :], WK[r % 2][0:BE, :]))
                if r < M // 8 - 1:
                    link(nc.vector.match_replace(WK[(r + 1) % 2][0:BE, :], m8[:, r, :], WK[r % 2][0:BE, :], -1.0))
            least = m8[:, M // 8 - 1, 7:8]
            above, need = small[:, 0:1], small[:, 1:2]
            dve.wait_ge(zeroed.sem, 1)
            link(nc.vector.tensor_scalar(SEL[0:BE, :], GT[0:BE, :], least, None, ALU.is_gt))
            link(nc.vector.tensor_reduce(above, SEL[0:BE, :], AX.X, ALU.add))
            nc.vector.tensor_scalar(EQ[0:BE, :], GT[0:BE, :], least, None, ALU.is_equal)
            link(nc.vector.tensor_scalar(need, above, -1.0, float(M), ALU.mult, ALU.add))
            link(nc.vector.tensor_tensor_scan(PRE[0:BE, :], w["ones"][0:BE, :], EQ[0:BE, :], 0.0, ALU.mult, ALU.add))
            link(nc.vector.scalar_tensor_tensor(PRE[0:BE, :], PRE[0:BE, :], need, EQ[0:BE, :], ALU.is_le, ALU.mult))
            nc.vector.tensor_tensor(SEL[0:BE, :], SEL[0:BE, :], PRE[0:BE, :], ALU.add).then_inc(sel_in.sem, 1)
            dve.wait_ge(sel_in.sem, 1)
            dve.wait_ge(later_ps.sem, 1)
            link(nc.vector.scalar_tensor_tensor(EQ[0:BE, :], m.bank[2][0:BE, :], 0.0, SEL[0:BE, :], ALU.is_equal, ALU.mult))
            nc.vector.tensor_tensor(SEL[0:BE, :], EQ[0:BE, :], GT[0:BE, :], ALU.mult).then_inc(w_in.sem, 1)
            dve.wait_ge(w_ps.sem, 1)
            nc.vector.tensor_copy(WT.rearrange("p (c n) -> p c n", c=NC_), m.bank[3][:, :].rearrange("p (c n) -> p c n", c=NC_)[:, :, 0:BE]).then_inc(w_sb.sem, 1)
            dve.wait_ge(w_sb.sem, 1)
            with dve.Fori(0, PAIRS) as i:
                hs = [m.h[:, bass.ds((2 * i + s) * NC_, NC_), :] for s in S]
                for c in range(NC_):
                    for s in S:
                        n = 2 * c + s + 1
                        wc = WT4[:, c, bass.ds(2 * i + s, 1), :].rearrange("p o e -> p (o e)")
                        dve.wait_ge(y_ps.sem, y_ps.at(i, n))
                        for q in range(2):
                            last = nc.vector.tensor_tensor(YW[s][:, 8 * (c % 2) + 4 * q:8 * (c % 2) + 4 * q + 4, :],
                                                           m.bank[4 * s + 2 * (c % 2) + q][:, :].rearrange("p (e d) -> p e d", d=D),
                                                           wc[:, 4 * q:4 * q + 4].rearrange("p (e o) -> p e o", o=1).broadcast_to([P, 4, D]), ALU.mult)
                        last.then_inc(yw_sb.sem, 1)
                    for s in S:
                        dve.wait_ge(yw_sb.sem, yw_sb.at(i, 2 * c + s + 1))
                        nc.vector.tensor_reduce(YR[s][:, c * D:(c + 1) * D], YW[s][:, 8 * (c % 2):8 * (c % 2) + 8, :].rearrange("p e d -> p d e"),
                                                AX.X, ALU.add).then_inc(yr_sb.sem, 1)
                for s in S:
                    dve.wait_ge(yr_sb.sem, yr_sb.at(i, 6 + s + 1))
                    nc.vector.tensor_tensor(hs[s], hs[s], YR[s][:, :].rearrange("p (c d) -> p c d", c=NC_), ALU.add).then_inc(h_sb.sem, 1)
                dve.wait_ge(h_sb.sem, h_sb.at(i, 2))

        @block.gpsimd
        def _(pool):
            with pool.Fori(0, PAIRS) as i:
                norm.gpsimd(pool, i)

        @block.scalar
        def _(act):
            with act.Fori(0, PAIRS) as i:
                for s in S:
                    act.wait_ge(xt_ps.sem, xt_ps.at(i, s + 1))
                    nc.scalar.copy(XT[s][:, :], m.bank[4 * s][:, :]).then_inc(xt_sb.sem, 1)

        @block.tensor
        def _(pe):
            for n in ("gate_w", "experts", "later_expert"):
                pe.wait_ge(m.loaded[n], 16)
            with pe.Fori(0, PAIRS) as i:
                for s in S:
                    pe.wait_ge(norm.ready.sem, norm.ready.at(i, s + 1))
                    for c in range(NC_):
                        last = nc.tensor.transpose(m.bank[4 * s][:, c * P:(c + 1) * P], XN[s][:, c, :], w["ident"][:, :])
                    last.then_inc(xt_ps.sem, 1)
                for s in S:
                    pe.wait_ge(xt_sb.sem, xt_sb.at(i, s + 1))
                    for c in range(NC_):
                        last = nc.tensor.matmul(m.bank[4 * s + 1][:, c * E:(c + 1) * E], XT[s][:, c * P:(c + 1) * P], w["gate_w"][:, :], start=True, stop=True)
                    last.then_inc(lg_ps.sem, 1)
            pe.wait_ge(lg_sb.sem, B + 1)
            with pe.Fori(0, ITERS) as k:
                nc.tensor.matmul(m.bank[0][:, 0:NC_ * BE], w["ones"][:, 0:P], G, start=True, stop=True).then_inc(col_ps.sem, 1)
                pe.wait_ge(col_in.sem, col_in.at(k, 1))
            for c in range(NC_):
                last = nc.tensor.transpose(m.bank[1][0:BE, c * P:(c + 1) * P], G[:, c * BE:(c + 1) * BE], w["ident"][:, :])
            last.then_inc(gt_ps.sem, 1)
            pe.wait_ge(zeroed.sem, 1)
            pe.wait_ge(sel_in.sem, 1)
            nc.tensor.matmul(m.bank[2][0:BE, :], w["later_expert"][:, :], SEL, start=True, stop=True).then_inc(later_ps.sem, 1)
            pe.wait_ge(w_in.sem, 1)
            for c in range(NC_):
                last = nc.tensor.transpose(m.bank[3][:, c * P:(c + 1) * P], SEL[:, c * P:(c + 1) * P], w["ident"][:, :])
            last.then_inc(w_ps.sem, 1)
            pe.wait_ge(w_sb.sem, 1)
            with pe.Fori(0, PAIRS) as i:
                for c in range(NC_):
                    for s in S:
                        if c == 0:
                            pe.wait_ge(x_sb[s].sem, x_sb[s].at(i, 16))
                        if c >= 2:
                            pe.wait_ge(yw_sb.sem, yw_sb.at(i, 2 * (c - 2) + s + 1))
                        for q in range(2):
                            last = nc.tensor.matmul(m.bank[4 * s + 2 * (c % 2) + q][:, :], XT[s][:, c * P:(c + 1) * P],
                                                    w["experts"][:, 512 * q:512 * q + 512], start=True, stop=True)
                        last.then_inc(y_ps.sem, 1)
                pe.wait_ge(yw_sb.sem, yw_sb.at(i, 8))


class Top2:
    STEPS = 11

    def __init__(self, ctx, nc, m, tag, rows, E, per=1):
        self.nc, self.rows, self.E = nc, rows, E
        self.eq = ctx.sb(tag + "_t2_eq", [P, rows, E])
        self.rest = ctx.sb(tag + "_t2_rest", [P, rows, E])
        self.oh = [ctx.sb(f"{tag}_t2_oh{n}", [P, rows, E]) for n in range(2)]
        self.v = ctx.sb(tag + "_t2_v", [P, 2, rows])
        self.r = ctx.sb(tag + "_t2_r", [P, 2, rows])
        self.step = Signal(ctx, nc, tag + "_t2_step", self.STEPS)
        self.ramp = m.w["ramp"][:, 64 - E:64].rearrange("p (o e) -> p o e", o=1).broadcast_to([P, rows, E])

    def vector(self, dve, i, values):
        nc, E, rows = self.nc, self.E, self.rows
        over = lambda v: v.rearrange("p (n o) -> p n o", o=1).broadcast_to([P, rows, E])
        n = [0]

        def link(ins):
            n[0] += 1
            ins.then_inc(self.step.sem, 1)
            dve.wait_ge(self.step.sem, self.step.at(i, n[0]))

        for k in range(2):
            src = values if k == 0 else self.rest[:, :, :]
            link(nc.vector.tensor_reduce(self.v[:, k, :], src, AX.X, ALU.max))
            link(nc.vector.tensor_tensor(self.eq[:, :, :], src, over(self.v[:, k, :]), ALU.is_equal))
            link(nc.vector.tensor_tensor(self.eq[:, :, :], self.eq[:, :, :], self.ramp, ALU.mult))
            link(nc.vector.tensor_reduce(self.r[:, k, :], self.eq[:, :, :], AX.X, ALU.max))
            link(nc.vector.tensor_tensor(self.oh[k][:, :, :], self.ramp, over(self.r[:, k, :]), ALU.is_equal))
            if k == 0:
                link(nc.vector.scalar_tensor_tensor(self.rest[:, :, :], self.oh[0][:, :, :], -3e38, values, ALU.mult, ALU.add))
        assert n[0] == self.STEPS


def attention_and_experts(ctx, nc, m):
    S = range(2)
    U, GQ, CG = 64, 64, 4
    KS = GQ // CG
    CS = 2 * KS
    PS = NC_ * CS
    NBUF = 4
    EPS = 1e-7
    w = m.w
    late = [(n, *m.load(ctx, n)) for n in ("a_wx", "a_wt", "a_bt", "a_wa", "a_ba", "router", "ramp")]
    XN, XT = m.XN, m.XT

    sig = lambda name, per: Signal(ctx, nc, "aa_" + name, per)
    XA = m.big[:, 0:NT * (D + 1)].rearrange("p (n d) -> p n d", d=D + 1)
    o = NT * (D + 1)
    KU = m.big[:, o:o + PAIRS * T]
    QU = m.big[:, o + PAIRS * T:o + 2 * PAIRS * T]
    ARG = [m.KM[n // 2][:, 4 * (n % 2):4 * (n % 2) + 4, :] for n in range(NBUF)]
    EX = [m.t512a[g] for g in range(2)]
    ET = m.t512c[0][:, :, :].rearrange("p a t -> p (a t)").rearrange("p (j r) -> p j r", j=NC_)
    ssum = ctx.sb("aa_sum", [P, 2])
    norm = Norm(ctx, nc, m, "aa")
    ones_in = sig("ones_in", 0)
    xt_ps, xt_sb, kq_ps, kq_sb, xa_kept = sig("xt_ps", 2), sig("xt_sb", 2), sig("kq_ps", 2), sig("kq_sb", 2), sig("xa_kept", 32)
    arg, th, used = sig("arg", CS), sig("th", CS), sig("used", CS)
    ex, tr_ps, et, o_ps, den, ha_sb = sig("ex", 2), sig("tr_ps", 2), sig("et", 2), sig("o_ps", 1), sig("den", 2), sig("ha_sb", 2)

    E, H = 8, 256
    HB = H // P
    UNITS = [(s, e, c) for s in S for e in range(E) for c in range(NC_)]
    NU = len(UNITS)
    begin = lambda u: 25 + 3 * u // 2
    TANH, MUL, TURN, COPY, DOWN = 2, 4, 3, 5, 5
    sig = lambda name, per: Signal(ctx, nc, "rf_" + name, per)
    wgu = ctx.sb("rf_wgu", [P, E, 2 * H])
    wd = ctx.sb("rf_wd", [P, E, HB, D])
    wgu_in, wd_in = ctx.semaphore("loaded_wgu"), ctx.semaphore("loaded_wd")
    lg = ctx.sb("rf_lg", [P, 2 * NC_, E])
    e2, p1, p2 = (ctx.sb(f"rf_{n}", [P, 2 * NC_]) for n in ("e2", "p1", "p2"))
    WT = ctx.sb("rf_w", [P, 2 * NC_, E])
    half = lambda u: slice((u % 2) * H, (u % 2 + 1) * H)
    TH = lambda u: m.ST[0][:, u // 2 % 2, half(u)]
    AC = lambda v: m.t512b[v % 2]
    ATB = [m.ST[1][:, 0, :], m.ST[1][:, 1, :], m.t512c[1][:, 0, :], m.t512c[1][:, 1, :]]
    AT = lambda v: ATB[v % 4]
    zero = ctx.sb("rf_zero", [P, P])
    norms = [Norm(ctx, nc, m, f"rf{s}", slots=[s]) for s in S]
    top = Top2(ctx, nc, m, "rf", 2 * NC_, E)
    x_ps, x_sb, lg_ps, lg_sb = sig("xt_ps", 2), sig("xt_sb", 2), sig("lg_ps", 1), sig("lg_sb", 1)
    wstep, e2_in, e2_sb, w_sb = sig("wstep", 4), sig("e2_in", 1), sig("e2_sb", 1), sig("w_sb", 1)
    gu_ps, th_sb, a1_sb, ac_sb = sig("gu_ps", NU), sig("th_sb", NU), sig("a1_sb", NU), sig("ac_sb", NU)
    at_ps, at_sb, dn, y_ps, h_sb = sig("at_ps", NU // 2), sig("at_sb", NU // 2), sig("dn", NU // 2), sig("y_ps", 2), sig("h_sb", 2)
    zeroed = sig("zeroed", 0)
    GU = lambda u: m.bank[3 + u % 3]
    TR, OUT = m.bank[6], m.bank[7]

    def begun(t, lag):
        return [u for u in range(NU) if begin(u) + lag == t]

    def paired(t, lag):
        return [u // 2 for u in begun(t, lag) if u % 2]

    late_by = lambda v: 3 if UNITS[2 * v][0] else 0
    END = PS + 3

    def summed(t):
        return [v for v in range(NU // 2) if begin(2 * v + 1) + DOWN + late_by(v) == t]

    assert begin(NU - 1) + DOWN + 3 < END
    ADD = [begin(2 * 15 + 1) + DOWN + 2, END - 1]

    with nc.Block() as block:
        @block.sync
        def _(sp):
            for _, t, sem, src in late:
                sp.dma_start(t[:, :], src).then_inc(sem, 16)
            sp.dma_start(wgu[:, :, :].rearrange("p e n -> p (e n)"), m.dram["wgu"]).then_inc(wgu_in, 16)
            sp.dma_start(wd[:, :, :, :].rearrange("p e a d -> p (e a d)"), m.dram["wdown"]).then_inc(wd_in, 16)
            sp.wait_ge(ones_in.sem, 1)
            with sp.Fori(0, PAIRS) as i:
                for s in S:
                    sp.wait_ge(norm.ready.sem, norm.ready.at(i, s + 1))
                    sp.dma_start(XA[:, bass.ds((2 * i + s) * NC_, NC_), 0:D], XN[s][:, :, :]).then_inc(xa_kept.sem, 16)

        @block.gpsimd
        def _(pool):
            nc.gpsimd.memset(XA[:, :, D:D + 1], 1.0).then_inc(ones_in.sem, 1)
            nc.gpsimd.memset(zero[:, :], 0.0).then_inc(zeroed.sem, 1)
            with pool.Fori(0, PAIRS) as i:
                norm.gpsimd(pool, i)
            with pool.Fori(0, PAIRS) as j:
                for s in S:
                    norms[s].gpsimd(pool, j)

        @block.vector
        def _(dve):
            def arguments(n, step):
                if step >= NBUF or not isinstance(n, int):
                    dve.wait_ge(used.sem, used.at(n, step - NBUF + 1))
                i = pair_of[0]
                for cc in range(CG):
                    q = QU[:, bass.ds(n * P + (step // KS) * GQ + cc * KS + step % KS, 1)]
                    last = nc.vector.tensor_scalar(ARG[step % NBUF][:, cc, :], KU[:, bass.ds(i * T, T)], q, None, ALU.add)
                last.then_inc(arg.sem, 1)

            pair_of = [0]

            def weights(n, g):
                dve.wait_ge(tr_ps.sem, tr_ps.at(n, g + 1))
                nc.vector.tensor_copy(ET[:, :, g * P:(g + 1) * P], m.bank[2][:, :].rearrange("p (j r) -> p j r", j=NC_)).then_inc(et.sem, 1)

            def attended(n, tile):
                dve.wait_ge(o_ps.sem, o_ps.at(n, 1))
                out = m.bank[2][:, :].rearrange("p (s d) -> p s d", s=2)
                nc.vector.tensor_scalar(ssum[:, :], out[:, :, D], EPS, None, ALU.add).then_inc(den.sem, 1)
                dve.wait_ge(den.sem, den.at(n, 1))
                nc.vector.reciprocal(ssum[:, :], ssum[:, :]).then_inc(den.sem, 1)
                dve.wait_ge(den.sem, den.at(n, 2))
                for s in S:
                    h = m.h[:, bass.ds(tile + s * NC_, 1), :].rearrange("p o d -> p (o d)")
                    nc.vector.scalar_tensor_tensor(h, out[:, s, 0:D], ssum[:, s:s + 1], h, ALU.mult, ALU.add).then_inc(ha_sb.sem, 1)
                dve.wait_ge(ha_sb.sem, ha_sb.at(n, 2))

            def mixture(j, t):
                hs = [m.h[:, bass.ds((2 * j + s) * NC_, NC_), :] for s in S]
                for s in S:
                    if t == 12 + 4 * s:
                        norms[s].vector_stats(dve, j, [hs[s]])
                    if t == 13 + 4 * s:
                        norms[s].vector_aggr(dve, j)
                    if t == 15 + 4 * s:
                        norms[s].vector_scale(dve, j, [hs[s]], [XN[s]])
                if t == 25:
                    dve.wait_ge(lg_ps.sem, lg_ps.at(j, 1))
                    nc.vector.tensor_copy(lg[:, :, :], m.bank[5][:, 0:2 * NC_ * E].rearrange("p (n e) -> p n e", e=E)).then_inc(lg_sb.sem, 1)
                if t == 26:
                    dve.wait_ge(lg_sb.sem, lg_sb.at(j, 1))
                    top.vector(dve, j, lg[:, :, :])
                    nc.vector.tensor_tensor(e2[:, :], top.v[:, 1, :], top.v[:, 0, :], ALU.subtract).then_inc(e2_in.sem, 1)
                if t == 29:
                    dve.wait_ge(e2_sb.sem, e2_sb.at(j, 1))
                    nc.vector.tensor_scalar(p1[:, :], e2[:, :], 2.0, 2.0, ALU.mult, ALU.add).then_inc(wstep.sem, 1)
                    dve.wait_ge(wstep.sem, wstep.at(j, 1))
                    nc.vector.reciprocal(p1[:, :], p1[:, :]).then_inc(wstep.sem, 1)
                    dve.wait_ge(wstep.sem, wstep.at(j, 2))
                    nc.vector.tensor_tensor(p2[:, :], p1[:, :], e2[:, :], ALU.mult).then_inc(wstep.sem, 1)
                    dve.wait_ge(wstep.sem, wstep.at(j, 3))
                    over = lambda v: v.rearrange("p (n o) -> p n o", o=1).broadcast_to([P, 2 * NC_, E])
                    nc.vector.tensor_tensor(WT[:, :, :], top.oh[0][:, :, :], over(p1[:, :]), ALU.mult)
                    nc.vector.tensor_tensor(top.oh[1][:, :, :], top.oh[1][:, :, :], over(p2[:, :]), ALU.mult).then_inc(wstep.sem, 1)
                    dve.wait_ge(wstep.sem, wstep.at(j, 4))
                    nc.vector.tensor_tensor(WT[:, :, :], WT[:, :, :], top.oh[1][:, :, :], ALU.add).then_inc(w_sb.sem, 1)
                    dve.wait_ge(w_sb.sem, w_sb.at(j, 1))
                for u in begun(t, MUL):
                    s, e, c = UNITS[u]
                    dve.wait_ge(th_sb.sem, th_sb.at(j, u + 1))
                    nc.vector.scalar_tensor_tensor(TH(u), TH(u), 1.0, GU(u)[:, 0:H], ALU.add, ALU.mult).then_inc(a1_sb.sem, 1)
                    dve.wait_ge(a1_sb.sem, a1_sb.at(j, u + 1))
                    if u >= 4:
                        dve.wait_ge(at_ps.sem, at_ps.at(j, (u - 4) // 2 + 1))
                    nc.vector.scalar_tensor_tensor(AC(u // 2)[:, half(u)], TH(u), WT[:, s * NC_ + c, e:e + 1], GU(u)[:, H:2 * H],
                                                   ALU.mult, ALU.mult).then_inc(ac_sb.sem, 1)
                for s in S:
                    if t == ADD[s]:
                        dve.wait_ge(y_ps.sem, y_ps.at(j, s + 1))
                        nc.vector.tensor_tensor(hs[s], hs[s], OUT[:, :].rearrange("p (c d) -> p c d", c=NC_), ALU.add).then_inc(h_sb.sem, 1)
                if t == END - 1:
                    dve.wait_ge(h_sb.sem, h_sb.at(j, 2))

            def chunk(n, i, before, tile, j=None, c=0):
                pair_of[0] = i
                for step in range(CS):
                    if before and step == 7:
                        weights(n - 1, 1)
                    if before and step == 11:
                        attended(n - 1, tile)
                    if step == 23:
                        weights(n, 0)
                    arguments(n, step)
                    if j is not None:
                        mixture(j, c * CS + step)

            with dve.Fori(0, PAIRS) as i:
                hs = [m.h[:, bass.ds((2 * i + s) * NC_, NC_), :] for s in S]
                norm.vector(dve, i, hs, [XN[s] for s in S])
                dve.wait_ge(xa_kept.sem, xa_kept.at(i, 32))
                dve.wait_ge(kq_sb.sem, kq_sb.at(i, 2))
            dve.wait_ge(m.loaded["ramp"], 16)
            chunk(0, 0, False, None)
            with dve.Fori(1, NC_) as n:
                chunk(n, 0, True, n - 1)
            with dve.Fori(1, PAIRS) as i:
                for c in range(NC_):
                    chunk(i * NC_ + c, i, True, (i * (2 * NC_)) + (c - 1 if c else -NC_ - 1), i - 1, c)
                for t in range(PS, END):
                    mixture(i - 1, t)
            last = PAIRS * NC_ - 1
            weights(last, 1)
            attended(last, (PAIRS - 1) * 2 * NC_ + NC_ - 1)
            for t in range(END):
                mixture(PAIRS - 1, t)

        @block.scalar
        def _(act):
            def score_exp(n, g):
                act.wait_ge(used.sem, used.at(n, (g + 1) * KS))
                nc.scalar.activation(EX[g][:, :], m.bank[g][:, :], ACT.Exp, bias=w["a_ba"][:, 0:1]).then_inc(ex.sem, 1)

            def mixture(j, t):
                for s in S:
                    if t == 17 + 4 * s:
                        act.wait_ge(x_ps.sem, x_ps.at(j, s + 1))
                        nc.scalar.copy(XT[s][:, :], m.bank[3 + s][:, :]).then_inc(x_sb.sem, 1)
                if t == 27:
                    act.wait_ge(e2_in.sem, e2_in.at(j, 1))
                    nc.scalar.activation(e2[:, :], e2[:, :], ACT.Exp).then_inc(e2_sb.sem, 1)
                for v in paired(t, COPY):
                    act.wait_ge(at_ps.sem, at_ps.at(j, v + 1))
                    if v >= 4:
                        act.wait_ge(dn.sem, dn.at(j, v - 3))
                    nc.scalar.copy(AT(v), TR[:, :]).then_inc(at_sb.sem, 1)
                for u in begun(t, TANH):
                    act.wait_ge(gu_ps.sem, gu_ps.at(j, u + 1))
                    if u >= 4:
                        act.wait_ge(ac_sb.sem, ac_sb.at(j, u - 3))
                    nc.scalar.activation(TH(u), GU(u)[:, 0:H], ACT.Tanh, scale=0.5).then_inc(th_sb.sem, 1)

            def chunk(n, before, j=None, c=0):
                for step in range(CS):
                    act.wait_ge(arg.sem, arg.at(n, step + 1))
                    nc.scalar.activation(ARG[step % NBUF], ARG[step % NBUF], ACT.Tanh).then_inc(th.sem, 1)
                    if before and step == 2:
                        score_exp(n - 1, 1)
                    if step == KS + 2:
                        score_exp(n, 0)
                    if j is not None:
                        mixture(j, c * CS + step)

            for name in ("a_bt", "a_ba"):
                act.wait_ge(m.loaded[name], 16)
            with act.Fori(0, PAIRS) as i:
                for s in S:
                    act.wait_ge(xt_ps.sem, xt_ps.at(i, s + 1))
                    nc.scalar.copy(XT[s][:, :], m.bank[4 * s][:, :]).then_inc(xt_sb.sem, 1)
                act.wait_ge(kq_ps.sem, kq_ps.at(i, 1))
                nc.scalar.copy(KU[:, bass.ds(i * T, T)], m.bank[1][:, :]).then_inc(kq_sb.sem, 1)
                act.wait_ge(kq_ps.sem, kq_ps.at(i, 2))
                nc.scalar.activation(QU[:, bass.ds(i * T, T)], m.bank[2][:, :], ACT.Identity, bias=w["a_bt"][:, 0:1]).then_inc(kq_sb.sem, 1)
            chunk(0, False)
            with act.Fori(1, NC_) as n:
                chunk(n, True)
            with act.Fori(1, PAIRS) as i:
                for c in range(NC_):
                    chunk(i * NC_ + c, True, i - 1, c)
                for t in range(PS, END):
                    mixture(i - 1, t)
            score_exp(PAIRS * NC_ - 1, 1)
            for t in range(END):
                mixture(PAIRS - 1, t)

        @block.tensor
        def _(pe):
            def turn_scores(n, g, free):
                pe.wait_ge(ex.sem, ex.at(n, g + 1))
                if free is not None:
                    pe.wait_ge(*free)
                for j in range(NC_):
                    last = nc.tensor.transpose(m.bank[2][:, j * P:(j + 1) * P], EX[g][:, j * P:(j + 1) * P], w["ident"][:, :])
                last.then_inc(tr_ps.sem, 1)

            def attend(n, tile0):
                pe.wait_ge(et.sem, et.at(n, 2))
                for s in S:
                    for j in range(NC_):
                        last = nc.tensor.matmul(m.bank[2][:, 256 * s:256 * s + D + 1], ET[:, j, s::2],
                                                XA[:, bass.ds(tile0 + s * NC_ + j, 1), :].rearrange("p o d -> p (o d)"),
                                                start=j == 0, stop=j == NC_ - 1)
                last.then_inc(o_ps.sem, 1)

            def mixture(j, t):
                for s in S:
                    if t == 15 + 4 * s:
                        pe.wait_ge(norms[s].ready.sem, norms[s].ready.at(j, 1))
                        for c in range(NC_):
                            last = nc.tensor.transpose(m.bank[3 + s][:, c * P:(c + 1) * P], XN[s][:, c, :], w["ident"][:, :])
                        last.then_inc(x_ps.sem, 1)
                if t == 22:
                    pe.wait_ge(x_sb.sem, x_sb.at(j, 2))
                    for s in S:
                        for c in range(NC_):
                            n = s * NC_ + c
                            last = nc.tensor.matmul(m.bank[5][:, n * E:(n + 1) * E], XT[s][:, c * P:(c + 1) * P], w["router"][:, :], start=True, stop=True)
                    last.then_inc(lg_ps.sem, 1)
                for v in paired(t, TURN):
                    pe.wait_ge(ac_sb.sem, ac_sb.at(j, 2 * v + 2))
                    if v:
                        pe.wait_ge(at_sb.sem, at_sb.at(j, v))
                    for b in range(4):
                        last = nc.tensor.transpose(TR[:, b * P:(b + 1) * P], AC(v)[:, b * P:(b + 1) * P], w["ident"][:, :])
                    last.then_inc(at_ps.sem, 1)
                for v in summed(t):
                    s = UNITS[2 * v][0]
                    if v % 16 == 0:
                        if s:
                            pe.wait_ge(h_sb.sem, h_sb.at(j, 1))
                        nc.tensor.matmul(OUT[:, :], zero[:, :], XT[s][:, :], start=True, stop=False)
                    pe.wait_ge(at_sb.sem, at_sb.at(j, v + 1))
                    for u in (2 * v, 2 * v + 1):
                        s, e, c = UNITS[u]
                        for a in range(HB):
                            o = (u % 2) * H + a * P
                            last = nc.tensor.matmul(OUT[:, c * P:(c + 1) * P], AT(v)[:, o:o + P], wd[:, e, a, :],
                                                    start=False, stop=False, skip_group_check=True)
                    last.then_inc(dn.sem, 1)
                    if v % 16 == 15:
                        nc.tensor.matmul(OUT[:, :], zero[:, :], XT[s][:, :], start=False, stop=True).then_inc(y_ps.sem, 1)
                for u in begun(t, 0):
                    s, e, c = UNITS[u]
                    if u == 2:
                        pe.wait_ge(lg_sb.sem, lg_sb.at(j, 1))
                    if u >= 3:
                        pe.wait_ge(ac_sb.sem, ac_sb.at(j, u - 2))
                    nc.tensor.matmul(GU(u)[:, :], XT[s][:, c * P:(c + 1) * P], wgu[:, e, :], start=True, stop=True).then_inc(gu_ps.sem, 1)

            def chunk(n, before, tile0, j=None, c=0):
                for step in range(CS):
                    k, g = step % KS, step // KS
                    pe.wait_ge(th.sem, th.at(n, step + 1))
                    for cc in range(CG):
                        last = nc.tensor.matmul(m.bank[g][32 * cc:32 * cc + 32, :], w["a_wa"][:, 30 - 2 * k:62 - 2 * k],
                                                ARG[step % NBUF][:, cc, :], start=k == 0, stop=k == KS - 1)
                    last.then_inc(used.sem, 1)
                    if before and step == 4:
                        turn_scores(n - 1, 1, (et.sem, et.at(n - 1, 1)))
                    if before and step == 8:
                        attend(n - 1, tile0)
                    if step == KS + 4:
                        turn_scores(n, 0, (ha_sb.sem, ha_sb.at(n, 0)) if before else None)
                    if j is not None:
                        mixture(j, c * CS + step)

            for name in ("a_wx", "a_wt", "a_wa", "router"):
                pe.wait_ge(m.loaded[name], 16)
            with pe.Fori(0, PAIRS) as i:
                for s in S:
                    pe.wait_ge(norm.ready.sem, norm.ready.at(i, s + 1))
                    for c in range(NC_):
                        last = nc.tensor.transpose(m.bank[4 * s][:, c * P:(c + 1) * P], XN[s][:, c, :], w["ident"][:, :])
                    last.then_inc(xt_ps.sem, 1)
                pe.wait_ge(xt_sb.sem, xt_sb.at(i, 2))
                for bank, name in ((1, "a_wx"), (2, "a_wt")):
                    for s in S:
                        last = nc.tensor.matmul(m.bank[bank][U * s:U * s + U, :], w[name][:, :], XT[s][:, :], start=True, stop=True)
                    last.then_inc(kq_ps.sem, 1)
            pe.wait_ge(wgu_in, 16)
            pe.wait_ge(wd_in, 16)
            pe.wait_ge(zeroed.sem, 1)
            chunk(0, False, None)
            with pe.Fori(1, NC_) as n:
                chunk(n, True, 0)
            with pe.Fori(1, PAIRS) as i:
                for c in range(NC_):
                    chunk(i * NC_ + c, True, i * (2 * NC_) - (0 if c else 2 * NC_), i - 1, c)
                for t in range(PS, END):
                    mixture(i - 1, t)
            last = PAIRS * NC_ - 1
            turn_scores(last, 1, (et.sem, et.at(last, 1)))
            attend(last, (PAIRS - 1) * 2 * NC_)
            for t in range(END):
                mixture(PAIRS - 1, t)


def batch_attention(ctx, nc, m):
    S = range(2)
    sig = lambda name, per: Signal(ctx, nc, "ba_" + name, per)
    w = m.w
    late = [(n, *m.load(ctx, n)) for n in ("b_w", "b_b")]
    L = B
    H4 = m.h[:, :, :].rearrange("p (l c) d -> p l c d", l=L)
    FT = m.big[:, 0:L * 3 * D].rearrange("p (l n) -> p l n", l=L)
    q_of = lambda l: FT[:, l, 0:D]
    K3, V3 = FT[:, :, D:2 * D], FT[:, :, 2 * D:3 * D]
    o = L * 3 * D
    PR = [m.big[:, o + n * L * D:o + (n + 1) * L * D].rearrange("p (m x) -> p m x", m=L) for n in range(4)]
    SC = m.t512a[0][:, :]
    MK = m.t512a[1][:, :]
    EX = m.t512b[0][:, :]
    mx = ctx.sb("ba_mx", [P, L * NH])
    O = m.KM[0][:, 0:2, :].rearrange("p a (l x) -> p (a l) x", x=D)
    XN, XT = m.XN, m.XT
    norm = Norm(ctx, nc, m, "ba")
    xt_ps, xt_sb, ft_ps, ft_sb = sig("xt_ps", 2), sig("xt_sb", 2), sig("ft_ps", L), sig("ft_sb", L)
    pr, sc, st, ex_in, ex_sb = sig("pr", L), sig("sc", L), sig("st", 7), sig("ex_in", 3), sig("ex_sb", 1)
    pv, ov, h_sb = sig("pv", L), sig("ov", L), sig("h_sb", 1)
    by_m = lambda v: v.rearrange("p (l m h) -> p l h m", l=L, m=L)
    wide_m = lambda v: v.rearrange("p (l o h) -> p l o h", l=L, o=1).broadcast_to([P, L, L, NH])
    lmh = lambda v: v.rearrange("p (l m h) -> p l m h", l=L, m=L)

    with nc.Block() as block:
        @block.sync
        def _(sp):
            for _, t, sem, src in late:
                sp.dma_start(t[:, :], src).then_inc(sem, 16)

        @block.gpsimd
        def _(pool):
            with pool.Fori(0, NC_) as c:
                norm.gpsimd(pool, c)

        @block.vector
        def _(dve):
            dve.wait_ge(m.loaded["b_b"], 16)
            with dve.Fori(0, NC_) as c:
                hs = [H4[:, 4 * s:4 * s + 4, bass.ds(c, 1), :].rearrange("p l o d -> p l (o d)") for s in S]
                norm.vector(dve, c, hs, [XN[s] for s in S])
                for l in range(L):
                    dve.wait_ge(ft_ps.sem, ft_ps.at(c, l + 1))
                    nc.vector.tensor_tensor(FT[:, l, :], m.bank[l][:, 0:3 * D], w["b_b"][:, :], ALU.add).then_inc(ft_sb.sem, 1)
                dve.wait_ge(ft_sb.sem, ft_sb.at(c, L))
                for l in range(L + 1):
                    if l < L:
                        if l >= 4:
                            dve.wait_ge(sc.sem, sc.at(c, l - 3))
                        nc.vector.tensor_tensor(PR[l % 4], K3, q_of(l).rearrange("p (o x) -> p o x", o=1).broadcast_to([P, L, D]), ALU.mult).then_inc(pr.sem, 1)
                    if l:
                        dve.wait_ge(pr.sem, pr.at(c, l))
                        nc.vector.tensor_reduce(SC[:, (l - 1) * L * NH:l * L * NH], PR[(l - 1) % 4].rearrange("p m (h x) -> p (m h) x", x=DH),
                                                AX.X, ALU.add).then_inc(sc.sem, 1)
                n = [0]

                def link(ins):
                    n[0] += 1
                    ins.then_inc(st.sem, 1)
                    dve.wait_ge(st.sem, st.at(c, n[0]))

                dve.wait_ge(sc.sem, sc.at(c, L))
                link(nc.vector.tensor_scalar(SC, SC, DH ** -0.5, None, ALU.mult))
                link(nc.vector.tensor_scalar(MK, SC, 0.0, None, ALU.is_equal))
                link(nc.vector.scalar_tensor_tensor(SC, MK, -3e38, SC, ALU.mult, ALU.add))
                link(nc.vector.tensor_reduce(mx[:, :].rearrange("p (l h) -> p l h", l=L), by_m(SC), AX.X, ALU.max))
                nc.vector.tensor_tensor(lmh(SC), lmh(SC), wide_m(mx[:, :]), ALU.subtract).then_inc(ex_in.sem, 1)
                dve.wait_ge(ex_sb.sem, ex_sb.at(c, 1))
                link(nc.vector.scalar_tensor_tensor(EX, MK, 0.0, EX, ALU.is_equal, ALU.mult))
                link(nc.vector.tensor_reduce(mx[:, :].rearrange("p (l h) -> p l h", l=L), by_m(EX), AX.X, ALU.add))
                link(nc.vector.tensor_scalar(mx[:, :], mx[:, :], 1e-30, None, ALU.max))
                nc.vector.reciprocal(mx[:, :], mx[:, :]).then_inc(ex_in.sem, 1)
                dve.wait_ge(ex_in.sem, ex_in.at(c, 2))
                nc.vector.tensor_tensor(lmh(EX), lmh(EX), wide_m(mx[:, :]), ALU.mult).then_inc(ex_in.sem, 1)
                dve.wait_ge(ex_in.sem, ex_in.at(c, 3))
                for l in range(L + 1):
                    if l < L:
                        if l >= 4:
                            dve.wait_ge(ov.sem, ov.at(c, l - 3))
                        pl = EX[:, l * L * NH:(l + 1) * L * NH].rearrange("p (n o) -> p n o", o=1).broadcast_to([P, L * NH, DH])
                        nc.vector.tensor_tensor(PR[l % 4].rearrange("p m (h x) -> p m h x", x=DH), V3.rearrange("p m (h x) -> p m h x", x=DH),
                                                pl.rearrange("p (m h) x -> p m h x", h=NH), ALU.mult).then_inc(pv.sem, 1)
                    if l:
                        dve.wait_ge(pv.sem, pv.at(c, l))
                        nc.vector.tensor_reduce(O[:, l - 1, :], PR[(l - 1) % 4].rearrange("p m x -> p x m"), AX.X, ALU.add).then_inc(ov.sem, 1)
                dve.wait_ge(ov.sem, ov.at(c, L))
                h = H4[:, :, bass.ds(c, 1), :].rearrange("p l o d -> p l (o d)")
                nc.vector.tensor_tensor(h, h, O, ALU.add).then_inc(h_sb.sem, 1)
                dve.wait_ge(h_sb.sem, h_sb.at(c, 1))

        @block.scalar
        def _(act):
            with act.Fori(0, NC_) as c:
                for s in S:
                    act.wait_ge(xt_ps.sem, xt_ps.at(c, s + 1))
                    nc.scalar.copy(XT[s][:, :], m.bank[4 * s][:, :]).then_inc(xt_sb.sem, 1)
                act.wait_ge(ex_in.sem, ex_in.at(c, 1))
                nc.scalar.activation(EX, SC, ACT.Exp).then_inc(ex_sb.sem, 1)

        @block.tensor
        def _(pe):
            pe.wait_ge(m.loaded["b_w"], 16)
            with pe.Fori(0, NC_) as c:
                for s in S:
                    pe.wait_ge(norm.ready.sem, norm.ready.at(c, s + 1))
                    for k in range(NC_):
                        last = nc.tensor.transpose(m.bank[4 * s][:, k * P:(k + 1) * P], XN[s][:, k, :], w["ident"][:, :])
                    last.then_inc(xt_ps.sem, 1)
                pe.wait_ge(xt_sb.sem, xt_sb.at(c, 2))
                for l in range(L):
                    nc.tensor.matmul(m.bank[l][:, 0:3 * D], XT[l // 4][:, (l % 4) * P:(l % 4 + 1) * P], w["b_w"][:, :], start=True, stop=True).then_inc(ft_ps.sem, 1)


def capacity_routing(ctx, nc, m):
    S = range(2)
    sig = lambda name, per: Signal(ctx, nc, "cr_" + name, per)
    w = m.w
    late = [(n, *m.load(ctx, n)) for n in ("c_gate", "ramp", "earlier", "spare", "sw1", "sw3", "sw2")]
    R8 = 2 * NC_
    XN, XT = m.XN, m.XT
    sc = ctx.sb("cr_sc", [P, R8, CE])
    M = ctx.sb("cr_m", [P, R8, CE])
    CU = ctx.sb("cr_cu", [P, R8 + 1, CE])
    base = ctx.sb("cr_base", [P, CE])
    pos, val, slot, alt = (ctx.sb("cr_" + n, [P, 2, R8]) for n in ("pos", "val", "slot", "alt"))
    sidx = ctx.sb("cr_sidx", [P, 2, R8], I32)
    vsum = ctx.sb("cr_vsum", [P, R8])
    SG = [m.t512a[s] for s in S]
    norm = Norm(ctx, nc, m, "cr")
    top = Top2(ctx, nc, m, "cr", R8, CE)
    xt_ps, xt_sb, lg_ps, ex_sb, one = sig("xt_ps", 2), sig("xt_sb", 2), sig("lg_ps", 1), sig("ex_sb", 1), sig("one", 2)
    g_ps, u_ps, th_sb, a_sb, y_ps, h_sb = sig("g_ps", 2), sig("u_ps", 2), sig("th_sb", 2), sig("a_sb", 4), sig("y_ps", 2), sig("h_sb", 2)
    cu, cu_sb, pos_ps, pst, idx_sb, kept, scattered = sig("cu", R8 + 2), sig("cu_sb", 1), sig("pos_ps", 1), sig("pst", 13), sig("idx_sb", 1), sig("kept", 2), sig("scattered", 16 * 2 * R8)
    based = sig("based", 0)
    G = lambda s: m.bank[2 + 4 * s]
    U = lambda s: m.bank[3 + 4 * s]
    OUT = lambda s: m.bank[4 * s]

    with nc.Block() as block:
        @block.sync
        def _(sp):
            for _, t, sem, src in late:
                sp.dma_start(t[:, :], src).then_inc(sem, 16)

        @block.gpsimd
        def _(pool):
            nc.gpsimd.memset(base[:, :], 0.0).then_inc(based.sem, 1)
            pool.wait_ge(m.queues_zero, 16)
            with pool.Fori(0, PAIRS) as i:
                norm.gpsimd(pool, i)
                pool.wait_ge(idx_sb.sem, idx_sb.at(i, 1))
                nc.gpsimd.tensor_tensor(m.pool_fence[:, 0:1], m.minus_half[:, 0:1], m.minus_half[:, 0:1], ALU.mult)
                for s in S:
                    for c in range(NC_):
                        for k in range(2):
                            pool.indirect_dma_start(
                                out=m.queues, out_offset=bass.IndirectOffsetOnAxis(ap=sidx[:, k, s * NC_ + c:s * NC_ + c + 1].bitcast(U32), axis=0),
                                in_=XN[s][:, c, :], in_offset=None).then_inc(scattered.sem, 16)
            pool.wait_ge(scattered.sem, 16 * 2 * NT)

        @block.vector
        def _(dve):
            dve.wait_ge(based.sem, 1)
            for n in ("ramp", "spare"):
                dve.wait_ge(m.loaded[n], 16)
            with dve.Fori(0, PAIRS) as i:
                hs = [m.h[:, bass.ds((2 * i + s) * NC_, NC_), :] for s in S]
                norm.vector(dve, i, hs, [XN[s] for s in S])
                flat = lambda v: v.rearrange("p n e -> p (n e)")
                dve.wait_ge(ex_sb.sem, ex_sb.at(i, 1))
                nc.vector.tensor_scalar(flat(sc[:, :, :]), flat(sc[:, :, :]), 1.0, None, ALU.add).then_inc(one.sem, 1)
                dve.wait_ge(one.sem, one.at(i, 1))
                nc.vector.reciprocal(flat(sc[:, :, :]), flat(sc[:, :, :])).then_inc(one.sem, 1)
                dve.wait_ge(one.sem, one.at(i, 2))
                top.vector(dve, i, sc[:, :, :])
                nc.vector.tensor_copy(CU[:, 0, :], base[:, :]).then_inc(cu.sem, 1)
                nc.vector.tensor_tensor(M[:, :, :], top.oh[0][:, :, :], top.oh[1][:, :, :], ALU.add).then_inc(cu.sem, 1)
                for n in range(R8):
                    dve.wait_ge(cu.sem, cu.at(i, n + 2))
                    last = nc.vector.tensor_tensor(CU[:, n + 1, :] if n + 1 < R8 else base[:, :], CU[:, n, :], M[:, n, :], ALU.add)
                    last.then_inc(cu.sem, 1)
                dve.wait_ge(cu.sem, cu.at(i, R8 + 2))
                nc.vector.tensor_tensor(vsum[:, :], top.v[:, 0, :], top.v[:, 1, :], ALU.add).then_inc(cu_sb.sem, 1)
                for s in S:
                    dve.wait_ge(th_sb.sem, th_sb.at(i, s + 1))
                    nc.vector.scalar_tensor_tensor(SG[s][:, :], SG[s][:, :], 1.0, G(s)[:, :], ALU.add, ALU.mult).then_inc(a_sb.sem, 1)
                for s in S:
                    dve.wait_ge(a_sb.sem, a_sb.at(i, s + 1))
                    dve.wait_ge(u_ps.sem, u_ps.at(i, s + 1))
                    nc.vector.tensor_tensor(SG[s][:, :], SG[s][:, :], U(s)[:, :], ALU.mult).then_inc(a_sb.sem, 1)
                n = [0]

                def link(ins):
                    n[0] += 1
                    ins.then_inc(pst.sem, 1)
                    dve.wait_ge(pst.sem, pst.at(i, n[0]))

                dve.wait_ge(pos_ps.sem, pos_ps.at(i, 1))
                count = m.bank[5][:, :].rearrange("p (n e) -> p n e", e=CE)
                for k in range(2):
                    link(nc.vector.tensor_tensor(top.oh[k][:, :, :], top.oh[k][:, :, :], count, ALU.mult))
                    link(nc.vector.tensor_reduce(pos[:, k, :], top.oh[k][:, :, :], AX.X, ALU.add))
                link(nc.vector.tensor_scalar(val[:, :, :], pos[:, :, :], float(CAP), None, ALU.is_lt))
                link(nc.vector.tensor_scalar(slot[:, :, :], top.r[:, :, :], -float(CAP), float(CE * CAP), ALU.mult, ALU.add))
                link(nc.vector.tensor_tensor(slot[:, :, :], slot[:, :, :], pos[:, :, :], ALU.add))
                link(nc.vector.tensor_tensor(alt[:, :, :], slot[:, :, :], w["spare"][:, :].rearrange("p (k n) -> p k n", k=2), ALU.subtract))
                link(nc.vector.tensor_tensor(alt[:, :, :], alt[:, :, :], val[:, :, :], ALU.mult))
                link(nc.vector.tensor_tensor(alt[:, :, :], alt[:, :, :], w["spare"][:, :].rearrange("p (k n) -> p k n", k=2), ALU.add))
                nc.vector.tensor_copy(sidx[:, :, :], alt[:, :, :]).then_inc(idx_sb.sem, 1)
                link(nc.vector.tensor_scalar(vsum[:, :], vsum[:, :], 1e-20, None, ALU.add))
                link(nc.vector.reciprocal(vsum[:, :], vsum[:, :]))
                link(nc.vector.scalar_tensor_tensor(top.v[:, :, :], top.v[:, :, :], ROUTE_SCALE, val[:, :, :], ALU.mult, ALU.mult))
                nc.vector.tensor_tensor(m.place[:, bass.ds(i, 1), :].rearrange("p o (k n) -> p (o k) n", k=2), slot[:, :, :], val[:, :, :], ALU.mult).then_inc(kept.sem, 1)
                nc.vector.tensor_tensor(m.share[:, bass.ds(i, 1), :].rearrange("p o (k n) -> p (o k) n", k=2), top.v[:, :, :],
                                        vsum[:, :].rearrange("p (o n) -> p o n", o=1).broadcast_to([P, 2, R8]), ALU.mult).then_inc(kept.sem, 1)
                for s in S:
                    dve.wait_ge(y_ps.sem, y_ps.at(i, s + 1))
                    nc.vector.scalar_tensor_tensor(hs[s], OUT(s)[:, :].rearrange("p (c d) -> p c d", c=NC_), 0.5, hs[s], ALU.mult, ALU.add).then_inc(h_sb.sem, 1)
                dve.wait_ge(h_sb.sem, h_sb.at(i, 2))
                dve.wait_ge(kept.sem, kept.at(i, 2))
                dve.wait_ge(idx_sb.sem, idx_sb.at(i, 1))
                dve.wait_ge(scattered.sem, scattered.at(i, 16 * 2 * R8))

        @block.scalar
        def _(act):
            with act.Fori(0, PAIRS) as i:
                for s in S:
                    act.wait_ge(xt_ps.sem, xt_ps.at(i, s + 1))
                    nc.scalar.copy(XT[s][:, :], m.bank[4 * s][:, :]).then_inc(xt_sb.sem, 1)
                act.wait_ge(lg_ps.sem, lg_ps.at(i, 1))
                nc.scalar.activation(sc[:, :, :].rearrange("p n e -> p (n e)"), m.bank[1][:, :], ACT.Exp, scale=-1.0).then_inc(ex_sb.sem, 1)
                for s in S:
                    act.wait_ge(g_ps.sem, g_ps.at(i, s + 1))
                    nc.scalar.activation(SG[s][:, :], G(s)[:, :], ACT.Tanh, scale=0.5).then_inc(th_sb.sem, 1)

        @block.tensor
        def _(pe):
            for name in ("c_gate", "earlier", "sw1", "sw3", "sw2"):
                pe.wait_ge(m.loaded[name], 16)
            with pe.Fori(0, PAIRS) as i:
                for s in S:
                    pe.wait_ge(norm.ready.sem, norm.ready.at(i, s + 1))
                    for c in range(NC_):
                        last = nc.tensor.transpose(m.bank[4 * s][:, c * P:(c + 1) * P], XN[s][:, c, :], w["ident"][:, :])
                    last.then_inc(xt_ps.sem, 1)
                for s in S:
                    pe.wait_ge(xt_sb.sem, xt_sb.at(i, s + 1))
                    for c in range(NC_):
                        n = s * NC_ + c
                        last = nc.tensor.matmul(m.bank[1][:, n * CE:(n + 1) * CE], XT[s][:, c * P:(c + 1) * P], w["c_gate"][:, :], start=True, stop=True)
                last.then_inc(lg_ps.sem, 1)
                for s in S:
                    nc.tensor.matmul(G(s)[:, :], w["sw1"][:, :], XT[s][:, :], start=True, stop=True).then_inc(g_ps.sem, 1)
                    nc.tensor.matmul(U(s)[:, :], w["sw3"][:, :], XT[s][:, :], start=True, stop=True).then_inc(u_ps.sem, 1)
                pe.wait_ge(cu_sb.sem, cu_sb.at(i, 1))
                flat = lambda v: v.rearrange("p n e -> p (n e)")
                nc.tensor.matmul(m.bank[5][:, :], w["earlier"][:, :], flat(M[:, :, :]), start=True, stop=False)
                nc.tensor.matmul(m.bank[5][:, :], w["ones"][:, 0:P], flat(CU[:, 0:R8, :]), start=False, stop=True).then_inc(pos_ps.sem, 1)
                for s in S:
                    pe.wait_ge(a_sb.sem, a_sb.at(i, s + 3))
                    for c in range(NC_):
                        last = nc.tensor.matmul(OUT(s)[:, c * P:(c + 1) * P], SG[s][:, c * P:(c + 1) * P], w["sw2"][:, :], start=True, stop=True)
                    last.then_inc(y_ps.sem, 1)


def capacity_experts(ctx, nc, m):
    UN = 4
    NI = CE // 2 // UN
    S = range(2)
    sig = lambda name, per: Signal(ctx, nc, "ce_" + name, per)
    w = m.w
    w13_in, w2_in = ctx.semaphore("loaded_w13"), ctx.semaphore("loaded_w2")
    w13 = ctx.sb("ce_w13", [P, CE, 2 * CH])
    w2 = m.big[:, 0:CE // 2 * 2 * D].rearrange("p (q n) -> p q n", n=2 * D)
    QC = CAP // P
    X = [m.KM[0][:, 2 * u:2 * u + 1, :].rearrange("p o t -> p (o t)") for u in range(UN)]
    Y = [m.KM[1][:, 2 * u:2 * u + 1, :].rearrange("p o t -> p (o t)") for u in range(UN)]
    XT = [m.XT[s] for s in S]
    TH = [m.t512a[s] for s in S]
    AA = [m.t512b[s] for s in S]
    AT = [m.t512c[s][:, 0, 0:2 * P] for s in S]
    x_in = [sig(f"x_in{u}", 16) for u in range(UN)]
    y_out = [sig(f"y_out{u}", 16) for u in range(UN)]
    x_free, xt_ps, xt_sb, gu_ps, th_sb, a_sb = (sig(n, UN) for n in ("x_free", "xt_ps", "xt_sb", "gu_ps", "th_sb", "a_sb"))
    aa_sb, at_ps, at_sb, y_ps, y_sb = (sig(n, UN) for n in ("aa_sb", "at_ps", "at_sb", "y_ps", "y_sb"))
    XP = lambda u: m.bank[u % 2]
    GU = lambda u: m.bank[2 + u % 2]
    AP_ = lambda u: m.bank[4 + u % 2]
    YP = lambda u: m.bank[6 + u % 2]
    acf = lambda v: v.rearrange("p (a c f) -> p a c f", a=2, c=QC)
    rows = lambda t, k: t[bass.ds(k * (2 * CAP), 2 * CAP), :].rearrange("(n p) d -> p n d", p=P)
    nd = lambda v: v.rearrange("p (n d) -> p n d", d=D)
    mark = ctx.sb("ce_mark", [P, UN])
    y_free = sig("y_free", UN)
    ROOM = 2

    with nc.Block() as block:
        @block.sync
        def _(sp):
            sp.dma_start(w13[:, :, :].rearrange("p e n -> p (e n)"), m.dram["w13"]).then_inc(w13_in, 16)
            sp.dma_start(w2.rearrange("p q n -> p (q n)"), m.dram["w2_pairs"]).then_inc(w2_in, 16)
            with sp.Fori(0, NI) as i:
                for u in range(UN):
                    sp.wait_ge(x_free.sem, x_free.at(i, u + 1))
                    sp.dma_start(nd(X[u]), rows(m.queues, i * UN + u)).then_inc(x_in[u].sem, 16)

        @block.gpsimd
        def _(pool):
            nc.gpsimd.memset(m.pool_fence[:, 0:1], 0.0).then_inc(x_free.sem, UN)
            nc.gpsimd.memset(m.pool_fence[:, 1:2], 0.0).then_inc(y_free.sem, UN)
            with pool.Fori(0, NI) as i:
                for u in range(UN + 2):
                    if u < UN:
                        pool.wait_ge(y_sb.sem, y_sb.at(i, u + 1))
                        pool.dma_start(rows(m.results, i * UN + u), nd(Y[u])).then_inc(y_out[u].sem, 16)
                    if u >= 2:
                        v = u - 2
                        pool.wait_ge(y_out[v].sem, y_out[v].at(i, 16))
                        nc.gpsimd.tensor_tensor(mark[:, v:v + 1], m.minus_half[:, 0:1], m.minus_half[:, 0:1], ALU.mult).then_inc(y_free.sem, 1)
            for u in range(UN):
                pool.wait_ge(y_out[u].sem, 16 * NI)

        @block.vector
        def _(dve):
            with dve.Fori(0, NI) as i:
                def last_part(u):
                    dve.wait_ge(y_ps.sem, y_ps.at(i, u + 1))
                    dve.wait_ge(y_free.sem, y_free.at(i, u + 1))
                    nc.vector.tensor_scalar(acf(Y[u]), YP(u)[:, :].rearrange("p (c a f) -> p a c f", a=2, c=QC), 0.5, None, ALU.mult).then_inc(y_sb.sem, 1)

                for u in range(UN):
                    dve.wait_ge(th_sb.sem, th_sb.at(i, u + 1))
                    gu = acf(GU(u)[:, :])
                    th = TH[u % 2][:, 0:2 * QC * CH].rearrange("p (a c f) -> p a c f", a=2, c=QC)
                    nc.vector.scalar_tensor_tensor(th, th, 1.0, gu[:, :, :, 0:CH], ALU.add, ALU.mult).then_inc(a_sb.sem, 1)
                    dve.wait_ge(a_sb.sem, a_sb.at(i, u + 1))
                    if u >= ROOM:
                        dve.wait_ge(at_ps.sem, at_ps.at(i, u - ROOM + 1))
                    nc.vector.tensor_tensor(AA[u % 2][:, 0:2 * QC * CH].rearrange("p (c a f) -> p a c f", a=2, c=QC), th, gu[:, :, :, CH:2 * CH],
                                            ALU.mult).then_inc(aa_sb.sem, 1)
                    if u >= 2:
                        last_part(u - 2)
                last_part(UN - 2)
                last_part(UN - 1)
                dve.wait_ge(at_ps.sem, at_ps.at(i, UN))

        @block.scalar
        def _(act):
            with act.Fori(0, NI) as i:
                for u in range(UN + 2):
                    if u < UN:
                        act.wait_ge(xt_ps.sem, xt_ps.at(i, u + 1))
                        if u >= ROOM:
                            act.wait_ge(gu_ps.sem, gu_ps.at(i, u - ROOM + 1))
                        nc.scalar.copy(XT[u % 2][:, :], XP(u)[:, :]).then_inc(xt_sb.sem, 1)
                    if 1 <= u <= UN:
                        v = u - 1
                        act.wait_ge(gu_ps.sem, gu_ps.at(i, v + 1))
                        if v >= ROOM:
                            act.wait_ge(aa_sb.sem, aa_sb.at(i, v - ROOM + 1))
                        nc.scalar.activation(TH[v % 2][:, 0:2 * QC * CH].rearrange("p (a f) -> p a f", f=CH),
                                             GU(v)[:, :].rearrange("p (a f) -> p a f", f=2 * CH)[:, :, 0:CH], ACT.Tanh, scale=0.5).then_inc(th_sb.sem, 1)
                    if 2 <= u:
                        v = u - 2
                        act.wait_ge(at_ps.sem, at_ps.at(i, v + 1))
                        if v >= ROOM:
                            act.wait_ge(y_ps.sem, y_ps.at(i, v - ROOM + 1))
                        nc.scalar.copy(AT[v % 2], AP_(v)[:, 0:QC * P]).then_inc(at_sb.sem, 1)
                act.wait_ge(y_ps.sem, y_ps.at(i, UN))

        @block.tensor
        def _(pe):
            pe.wait_ge(w13_in, 16)
            pe.wait_ge(w2_in, 16)
            with pe.Fori(0, NI) as i:
                for u in range(UN + 3):
                    if u < UN:
                        pe.wait_ge(x_in[u].sem, x_in[u].at(i, 16))
                        if u >= ROOM:
                            pe.wait_ge(xt_sb.sem, xt_sb.at(i, u - ROOM + 1))
                        for n in range(2 * QC):
                            last = nc.tensor.transpose(XP(u)[:, n * P:(n + 1) * P], X[u][:, n * P:(n + 1) * P], w["ident"][:, :])
                        last.then_inc(xt_ps.sem, 1)
                    if 1 <= u <= UN:
                        v = u - 1
                        pe.wait_ge(xt_sb.sem, xt_sb.at(i, v + 1))
                        if v >= ROOM:
                            pe.wait_ge(aa_sb.sem, aa_sb.at(i, v - ROOM + 1))
                        for a in range(2):
                            we = w13[:, bass.ds(2 * (i * UN + v) + a, 1), :].rearrange("p o n -> p (o n)")
                            for c in range(QC):
                                n = a * QC + c
                                last = nc.tensor.matmul(GU(v)[:, n * P:(n + 1) * P], XT[v % 2][:, n * P:(n + 1) * P], we, start=True, stop=True)
                                if n == 0:
                                    last.then_inc(x_free.sem, 1)
                        last.then_inc(gu_ps.sem, 1)
                    if 2 <= u <= UN + 1:
                        v = u - 2
                        pe.wait_ge(aa_sb.sem, aa_sb.at(i, v + 1))
                        if v >= ROOM:
                            pe.wait_ge(at_sb.sem, at_sb.at(i, v - ROOM + 1))
                        for c in range(QC):
                            last = nc.tensor.transpose(AP_(v)[:, c * P:(c + 1) * P], AA[v % 2][:, c * P:(c + 1) * P], w["ident"][:, :])
                        last.then_inc(at_ps.sem, 1)
                    if 3 <= u:
                        v = u - 3
                        pe.wait_ge(at_sb.sem, at_sb.at(i, v + 1))
                        if v >= ROOM:
                            pe.wait_ge(y_sb.sem, y_sb.at(i, v - ROOM + 1))
                        wp = w2[:, bass.ds(i * UN + v, 1), :].rearrange("p o n -> p (o n)")
                        for c in range(QC):
                            last = nc.tensor.matmul(YP(v)[:, c * 2 * D:(c + 1) * 2 * D], AT[v % 2][:, c * P:(c + 1) * P], wp, start=True, stop=True)
                        last.then_inc(y_ps.sem, 1)
                pe.wait_ge(y_sb.sem, y_sb.at(i, UN))


def capacity_combine(ctx, nc, m):
    U2 = range(2)
    sig = lambda name, per: Signal(ctx, nc, "cc_" + name, per)
    idx = [ctx.sb(f"cc_idx{u}", [P, 2, NC_], I32) for u in U2]
    share = [ctx.sb(f"cc_share{u}", [P, 2, NC_]) for u in U2]
    Y = [m.KM[u][:, 0:2, :].rearrange("p k (c d) -> p k c d", c=NC_) for u in U2]
    idx_sb, summed, first, fenced = sig("idx_sb", 4), sig("summed", 2), sig("first", 2), sig("fenced", 2)
    got = [sig(f"got{u}", 16 * 2 * NC_) for u in U2]
    stored = [sig(f"stored{u}", 16) for u in U2]

    with nc.Block() as block:
        @block.sync
        def _(sp):
            with sp.Fori(0, PAIRS) as i:
                for u in U2:
                    sp.wait_ge(summed.sem, summed.at(i, u + 1))
                    sp.dma_start(m.out[bass.ds(2 * i + u, 1), :, :].rearrange("o (c p) d -> p (o c) d", p=P),
                                 m.h[:, bass.ds((2 * i + u) * NC_, NC_), :]).then_inc(stored[u].sem, 16)
            for u in U2:
                sp.wait_ge(stored[u].sem, 16 * PAIRS)

        @block.gpsimd
        def _(pool):
            with pool.Fori(0, PAIRS) as i:
                for u in U2:
                    pool.wait_ge(idx_sb.sem, idx_sb.at(i, 2 * u + 2))
                    nc.gpsimd.tensor_tensor(m.pool_fence[:, u:u + 1], m.minus_half[:, 0:1], m.minus_half[:, 0:1], ALU.mult).then_inc(fenced.sem, 1)
                    for c in range(NC_):
                        for k in range(2):
                            pool.indirect_dma_start(
                                out=Y[u][:, k, c, :], out_offset=None, in_=m.results,
                                in_offset=bass.IndirectOffsetOnAxis(ap=idx[u][:, k, c:c + 1].bitcast(U32), axis=0)).then_inc(got[u].sem, 16)

        @block.vector
        def _(dve):
            with dve.Fori(0, PAIRS) as i:
                for u in U2:
                    kc = lambda t: t[:, bass.ds(i, 1), :].rearrange("p o (k n) -> p (o k) n", k=2)[:, :, u * NC_:(u + 1) * NC_]
                    nc.vector.tensor_copy(idx[u][:, :, :], kc(m.place)).then_inc(idx_sb.sem, 1)
                    nc.vector.tensor_copy(share[u][:, :, :], kc(m.share)).then_inc(idx_sb.sem, 1)
                for u in U2:
                    dve.wait_ge(idx_sb.sem, idx_sb.at(i, 2 * u + 2))
                    dve.wait_ge(got[u].sem, got[u].at(i, 16 * 2 * NC_))
                    for k in range(2):
                        for c in range(NC_):
                            h = m.h[:, bass.ds((2 * i + u) * NC_ + c, 1), :].rearrange("p o d -> p (o d)")
                            last = nc.vector.scalar_tensor_tensor(h, Y[u][:, k, c, :], share[u][:, k, c:c + 1], h, ALU.mult, ALU.add)
                        last.then_inc((first if k == 0 else summed).sem, 1)
                        if k == 0:
                            dve.wait_ge(first.sem, first.at(i, u + 1))
                dve.wait_ge(summed.sem, summed.at(i, 2))
                dve.wait_ge(fenced.sem, fenced.at(i, 2))


def workspace(m):
    m.big = m.sb("big", [P, 12288 + 0])
    m.nstat = [m.sb(f"nstat{s}", [P, NC_, 6]) for s in range(2)]
    m.nmv = [m.sb(f"nmv{s}", [P, NC_, 2]) for s in range(2)]
    m.nrstd = [m.sb(f"nrstd{s}", [P, NC_]) for s in range(2)]
    m.fence = m.sb("fence", [P, 2])
    m.pool_fence = m.sb("pool_fence", [P, 2])
    m.minus_half = m.sb("minus_half", [P, 64])
    m.XN = [m.sb(f"XN{s}", [P, NC_, D]) for s in range(2)]
    m.XT = [m.sb(f"XT{s}", [P, T]) for s in range(2)]
    m.t512a = [m.sb(f"t512a{s}", [P, T]) for s in range(2)]
    m.t512b = [m.sb(f"t512b{s}", [P, T]) for s in range(2)]
    m.t512c = [m.sb(f"t512c{s}", [P, 2, T]) for s in range(2)]
    m.KM = [m.sb(f"KM{s}", [P, NH, T]) for s in range(2)]
    m.A = [m.big[:, s * 4 * T:(s + 1) * 4 * T].rearrange("p (a c t) -> p a c t", a=4, c=NC_) for s in range(2)]
    o = 8 * T
    m.V = [m.big[:, o + s * 4 * T:o + (s + 1) * 4 * T].rearrange("p (c n) -> p c n", c=NC_) for s in range(2)]
    o = 16 * T
    m.OT = [m.big[:, o + s * 4 * T:o + (s + 1) * 4 * T].rearrange("p (g n) -> p g n", g=NC_) for s in range(2)]
    m.XNA = m.big[:, 0:8 * T].rearrange("p (n d) -> p n d", d=D)
    m.XTA = m.big[:, 8 * T:16 * T]
    m.KTOK = [m.sb(f"KTOK{s}", [P, 3, D]) for s in range(2)]
    m.ST = [m.sb(f"ST{s}", [P, 3, T]) for s in range(2)]


def build(nc, dram, out, upto=None):
    whole = Layer(nc)
    with whole:
        m = Memory(whole, nc, dram)
        workspace(m)
        m.out = out
        m.queues = nc.dram_tensor("queues", (CE * CAP + 16 * P, D), F32).ap()
        m.results = nc.dram_tensor("results", (CE * CAP, D), F32).ap()
        m.place = m.sb("place", [P, PAIRS, 4 * NC_])
        m.share = m.sb("share", [P, PAIRS, 4 * NC_])
        m.zeros = m.sb("zeros", [P, T])
        m.queues_zero = whole.semaphore("queues_zero")
        m.early = ["ones", "causal", "same_head", "head_col", "state_mask", "wq", "wk", "wv", "wout"]
        with nc.Block() as block:
            @block.gpsimd
            def _(pool):
                nc.gpsimd.memset(m.minus_half[:, :], -0.5)
                nc.gpsimd.memset(m.zeros[:, :], 0.0)
        for layer in LAYERS[:upto]:
            own = Layer(nc)
            layer(own, nc, m)
            own.end()
        if upto is not None:
            stored = whole.semaphore("stored")
            with nc.Block() as block:
                @block.sync
                def _(sp):
                    sp.dma_start(out.rearrange("b (c p) d -> p (b c) d", p=P), m.h[:, :, :]).then_inc(stored, 16)
                    sp.wait_ge(stored, 16)


LAYERS = [token_conv, linear_attention, modulated_ffn, retention, balanced_experts, attention_and_experts,
          batch_attention, capacity_routing, capacity_experts, capacity_combine]


def laid_out(inputs):
    a = {k: np.asarray(v) for k, v in inputs.items()}
    row = lambda x: np.ascontiguousarray(x)
    out = dict(shape_constants())
    out["ids"] = row(a["x"].reshape(NT, P).T)
    out["table"] = row(a["L0_tok_conv_w"].transpose(1, 2, 0).reshape(VOCAB, TAPS * D))
    out["wq"] = row(a["L0_attn_W_q"].T)
    out["wk"] = row(a["L0_attn_W_k"].T)
    out["wv"] = row(a["L0_attn_W_v"].T)
    out["wout"] = row(a["L0_attn_W_out"].T.reshape(NC_, P, D).transpose(1, 0, 2).reshape(P, NC_ * D))
    E, R = 8, 16
    rep = lambda x: row(np.repeat(x, R, axis=-1))
    spread = lambda x: row(np.concatenate([x[:, None, :], np.zeros((E, R - 1, x.shape[1]), x.dtype)], axis=1).reshape(P, -1))
    out["gfc1"] = row(a["L0_ffn_gfc1_w"].T)
    out["gfc1_b"] = row(a["L0_ffn_gfc1_b"].reshape(P, 1))
    out["gfc2_rep"] = rep(a["L0_ffn_gfc2_w"].T)
    out["gfc2_b"] = rep(a["L0_ffn_gfc2_b"]).reshape(P, 1)
    out["task_b1"] = spread(a["L0_ffn_tv_b1"])
    out["b1"] = row(a["L0_ffn_b1"].reshape(4, P).T)
    tb2 = spread(a["L0_ffn_tv_b2"])
    tb2[1] = a["L0_ffn_b2"]
    out["task_b2"] = tb2
    zeros = np.zeros((P - 1 - E, 2 * D), np.float32)
    out["ln_rows"] = row(np.concatenate([
        np.concatenate([a["L0_ffn_ln_g"], a["L0_ffn_ln_b"]])[None],
        np.concatenate([a["L0_ffn_tv_ln_g"], a["L0_ffn_tv_ln_b"]], axis=1), zeros]))
    coef = np.zeros((P, P), np.float32)
    coef[0], coef[1:1 + E] = 1.0 - 0.03 * E, 0.03
    out["ln_coef"] = coef
    p = np.arange(P)
    out["gate_row"] = row(np.stack([p % R == 0, p == 1], axis=1).astype(np.float32))
    out["gate_pad"] = row(np.concatenate([np.zeros((P, R)), p[:, None] % R == np.arange(R)[None], np.zeros((P, R))], axis=1).astype(np.float32))
    out["task_W1"] = row(a["L0_ffn_tv_W1"].reshape(E, 512, 8, R).transpose(0, 3, 2, 1).reshape(P, 8 * 512))
    out["task_W2"] = row(a["L0_ffn_tv_W2"].reshape(E, D, 4, 8, R).transpose(0, 4, 3, 2, 1).reshape(P, 8 * 4 * D))
    out["W1"] = row(a["L0_ffn_W1"].T)
    out["W2"] = row(a["L0_ffn_W2"].reshape(D, 4, P).transpose(2, 1, 0).reshape(P, 4 * D))
    for n in "QKVGO":
        out["r_w" + n.lower()] = row(a["L1_attn_W_" + n])
    out["gn"] = row(np.stack([a["L1_attn_gn_weight"], a["L1_attn_gn_bias"]], axis=1))
    out["gate_w"] = row(a["L1_ffn_gate_weight"][0])
    out["experts"] = row(a["L1_ffn_experts"].transpose(1, 0, 2).reshape(D, 8 * D))
    q = np.arange(B * 8)
    later = (p[:, None] // 8 == q[None] // 8) & (p[:, None] > q[None])
    out["later_expert"] = row(later.astype(np.float32))
    wx, wt = a["L2_attn_Wx"], a["L2_attn_Wt"]
    out["a_wx"], out["a_wt"] = row(wx), row(wt)
    out["a_bt"] = row(np.tile(a["L2_attn_bt"], 2).reshape(P, 1))
    wa = np.zeros((P, 62), np.float32)
    wa[0:64, 30], wa[64:128, 31] = a["L2_attn_Wa"][:, 0], a["L2_attn_Wa"][:, 0]
    out["a_wa"] = wa
    out["a_ba"] = row(np.tile(a["L2_attn_ba"], P).reshape(P, 1))
    out["router"] = row(a["L2_ffn_router_w"].T)
    out["ramp"] = row(np.tile(np.arange(64, 0, -1, dtype=np.float32), (P, 1)))
    out["wgu"] = row(np.concatenate([a["L2_ffn_w_gate"], a["L2_ffn_w_up"]], axis=2).transpose(1, 0, 2).reshape(P, -1))
    out["wdown"] = row(a["L2_ffn_w_down"].reshape(8, 2, P, D).transpose(2, 0, 1, 3).reshape(P, -1))
    qkv = lambda x: x.reshape((NH, 3, DH) + x.shape[1:]).swapaxes(0, 1).reshape(x.shape)
    out["b_w"] = row(qkv(a["L3_attn_W"]).T)
    out["b_b"] = row(np.tile(qkv(a["L3_attn_b"]), (P, 1)))
    out["c_gate"] = row(a["L3_ffn_gate_w"].T)
    out["earlier"] = row((p[:, None] < p[None, :]).astype(np.float32))
    out["spare"] = row((CE * CAP + np.arange(16)[None, :] * P + p[:, None]).astype(np.float32))
    for n in ("sw1", "sw3", "sw2"):
        out[n] = row(a["L3_ffn_" + n])
    out["w13"] = row(np.concatenate([a["L3_ffn_w1"], a["L3_ffn_w3"]], axis=2).transpose(1, 0, 2).reshape(P, -1))
    w2 = a["L3_ffn_w2"].reshape(CE // 2, 2, CH, D)
    pairs = np.zeros((2, CH, CE // 2, 2, D), w2.dtype)
    for e in range(2):
        pairs[e, :, :, e] = w2[:, e].transpose(1, 0, 2)
    out["w2_pairs"] = pairs.reshape(P, -1)
    return out


def kernel(**inputs):
    import concourse.bacc as bacc
    from concourse.bass_utils import run_bass_kernel_spmd

    nc = bacc.Bacc("TRN2", target_bir_lowering=False, num_devices=1)
    arrays, dram = {}, {}
    for name, a in laid_out(inputs).items():
        arrays["in_" + name] = a
        dram[name] = nc.dram_tensor("in_" + name, a.shape, mybir.dt.from_np(a.dtype), kind="ExternalInput").ap()
    out = nc.dram_tensor("out_h", (B, T, D), F32, kind="ExternalOutput").ap()
    build(nc, dram, out)
    r = run_bass_kernel_spmd(nc, [arrays], core_ids=[0])
    return r.results[0]["out_h"]
```

```python
import numpy as np
import concourse.bass as bass
from concourse import mybir
from contextlib import ExitStack

F32 = mybir.dt.float32
I32 = mybir.dt.int32
U32 = mybir.dt.uint32
ALU = mybir.AluOpType
ACT = mybir.ActivationFunctionType
AX = mybir.AxisListType

P = 128
B, T, D = 8, 512, 128
NC_ = T // P
NT = B * NC_
NH = 8
DH = D // NH
DV = 64
VOCAB, TAPS = 8000, 3
PAIRS = B // 2
LN_EPS = 1e-5
CE, CH, CAP = 64, 64, 256
ROUTE_SCALE = 2.5


class Layer(ExitStack):

    def __init__(self, nc):
        super().__init__()
        self.nc, self.sems = nc, []

    def semaphore(self, name):
        self.sems.append(self.nc.alloc_semaphore(name))
        return self.sems[-1]

    def sb(self, name, shape, dtype=F32):
        return self.enter_context(self.nc.sbuf_tensor(name, shape, dtype))

    def end(self):
        self.close()
        self.nc.clear_and_free_semaphores(self.sems)
        self.nc.all_engine_barrier()


class Signal:

    def __init__(self, ctx, nc, name, per=0):
        self.sem = ctx.semaphore(name)
        self.per = per

    def at(self, i, k):
        return i * self.per + k


def shape_constants():
    p = np.arange(P)
    t = np.arange(T)
    head = p // DH
    decay = np.log(1.0 - 2.0 ** (-5.0 - head.astype(np.float64)))
    shift = (p[:, None] + 1 == p[None, :])
    edge = (p[:, None] == P - 1) & (p[None, :] == 0)
    out = {
        "ident": np.eye(P),
        "prev": shift, "prev_edge": edge,
        "next": shift.T, "next_edge": edge.T,
        "causal": p[:, None] <= p[None, :],
        "same_head": head[:, None] == head[None, :],
        "head_col": head[:, None] == np.arange(NH)[None, :],
        "state_mask": head[:, None] == (np.arange(NH * DV) // DV)[None, :],
        "ones": np.ones((P, T)),
        "decay_q": np.exp(decay[:, None] * t) / np.sqrt(float(DH)),
        "decay_k": np.exp(-decay[:, None] * t),
    }
    return {k: np.ascontiguousarray(v, dtype=np.float32) for k, v in out.items()}


class Memory:

    def __init__(self, ctx, nc, dram):
        self.ctx, self.nc, self.dram = ctx, nc, dram
        self.h_more = self.sb("h", [P, NT + 2 * NC_, D])
        self.h = self.h_more[:, 0:NT, :]
        self.bank = [ctx.enter_context(nc.psum_tensor(f"bank{n}", [P, T], F32)) for n in range(8)]
        self.w = {}
        self.loaded = {}
        self.load_log = []

    def sb(self, name, shape, dtype=F32):
        return self.ctx.enter_context(self.nc.sbuf_tensor(name, shape, dtype))

    def load(self, layer, name):
        src = self.dram[name]
        self.load_log.append(name)
        t = layer.enter_context(self.nc.sbuf_tensor(f"w_{name}_{len(self.load_log)}", list(src.shape), src.dtype))
        s = layer.semaphore(f"loaded_{name}_{len(self.load_log)}")
        self.w[name] = t
        self.loaded[name] = s
        return t, s, src


def token_conv(ctx, nc, m):
    gathered = [Signal(ctx, nc, f"tok_gathered{b}") for b in range(B)]
    ids_in = Signal(ctx, nc, "tok_ids_in")
    summed = Signal(ctx, nc, "tok_summed")
    copied = Signal(ctx, nc, "tok_copied")
    loads = [(n, *m.load(m.ctx, n)) for n in ("ident", "prev", "prev_edge", "next", "next_edge")]
    rest = [(n, *m.load(m.ctx, n)) for n in m.early]
    ids = m.sb("ids", [P, NT], I32)
    rows = m.big[:, 0:NT * TAPS * D].rearrange("p (n k) -> p n k", n=NT)
    with nc.Block() as block:
        @block.sync
        def _(sp):
            for _, t, s, src in loads + rest:
                sp.dma_start(t[:, :], src).then_inc(s, 16)
            sp.wait_ge(gathered[B - 1].sem, 16 * NC_)
            sp.dma_start(m.queues[0:CE * CAP, :].rearrange("(n p r) d -> p n (r d)", p=P, r=4),
                         m.zeros[:, :].rearrange("p (o x) -> p o x", o=1).broadcast_to([P, CE * CAP // T, T])).then_inc(m.queues_zero, 16)

        @block.gpsimd
        def _(pool):
            pool.dma_start(ids[:, :], m.dram["ids"]).then_inc(ids_in.sem, 16)
            pool.wait_ge(ids_in.sem, 16)
            for n in range(NT):
                pool.indirect_dma_start(
                    out=rows[:, n, :], out_offset=None, in_=m.dram["table"],
                    in_offset=bass.IndirectOffsetOnAxis(ap=ids[:, n:n + 1].bitcast(U32), axis=0),
                ).then_inc(gathered[n // NC_].sem, 16)

        @block.tensor
        def _(pe):
            for name, _, s, _ in loads:
                pe.wait_ge(s, 16)
            for b in range(B):
                pe.wait_ge(gathered[b].sem, 16 * NC_)
                if b >= 4:
                    pe.wait_ge(copied.sem, b - 3)
                g = rows[:, b * NC_:(b + 1) * NC_, :]
                ps = m.bank[b % 4]
                out = ps[:, :].rearrange("p (c d) -> p c d", c=NC_)
                w = m.w
                nc.tensor.matmul(out[:, :, :], w["prev"][:, :], g[:, :, 0:D], start=True, stop=False)
                nc.tensor.matmul(out[:, 1:NC_, :], w["prev_edge"][:, :], g[:, 0:NC_ - 1, 0:D], start=False, stop=False, skip_group_check=True)
                nc.tensor.matmul(out[:, :, :], w["ident"][:, :], g[:, :, D:2 * D], start=False, stop=False)
                nc.tensor.matmul(out[:, 0:NC_ - 1, :], w["next_edge"][:, :], g[:, 1:NC_, 2 * D:3 * D], start=False, stop=False, skip_group_check=True)
                last = nc.tensor.matmul(out[:, :, :], w["next"][:, :], g[:, :, 2 * D:3 * D], start=False, stop=True)
                last.then_inc(summed.sem, 1)

        @block.vector
        def _(dve):
            for b in range(B):
                dve.wait_ge(summed.sem, b + 1)
                nc.vector.tensor_copy(m.h[:, b * NC_:(b + 1) * NC_, :],
                                      m.bank[b % 4][:, :].rearrange("p (c d) -> p c d", c=NC_)).then_inc(copied.sem, 1)


def part(view, c):
    return view[c].rearrange("p o d -> p (o d)") if isinstance(view, list) else view[:, c, :]


class Norm:

    def __init__(self, ctx, nc, m, tag, slots=(0, 1), tiles=NC_):
        self.nc, self.m, self.tiles = nc, m, tiles
        self.slots = slots
        n = len(slots)
        self.step = Signal(ctx, nc, tag + "_norm_step", 2 * n)
        self.var = Signal(ctx, nc, tag + "_norm_var", n)
        self.root = Signal(ctx, nc, tag + "_norm_root", n)
        self.ready = Signal(ctx, nc, tag + "_norm_ready", n)

    def vector_stats(self, dve, i, src):
        nc, m = self.nc, self.m
        for k, s in enumerate(self.slots):
            for c in range(self.tiles):
                last = nc.vector.bn_stats(m.nstat[s][:, c, :], part(src[k], c))
            last.then_inc(self.step.sem, 1)

    def vector_aggr(self, dve, i):
        nc, m, n = self.nc, self.m, len(self.slots)
        for k, s in enumerate(self.slots):
            dve.wait_ge(self.step.sem, self.step.at(i, k + 1))
            nc.vector.memset(m.fence[:, s:s + 1], 0.0)
            for c in range(self.tiles):
                last = nc.vector.bn_aggr(m.nmv[s][:, c, :], m.nstat[s][:, c, :])
            last.then_inc(self.step.sem, 1)
        for k, s in enumerate(self.slots):
            dve.wait_ge(self.step.sem, self.step.at(i, n + k + 1))
            nc.vector.tensor_scalar(m.nrstd[s][:, 0:self.tiles], m.nmv[s][:, 0:self.tiles, 1], LN_EPS, None, ALU.add).then_inc(self.var.sem, 1)

    def vector_scale(self, dve, i, src, out):
        nc, m = self.nc, self.m
        for k, s in enumerate(self.slots):
            dve.wait_ge(self.root.sem, self.root.at(i, k + 1))
            for c in range(self.tiles):
                last = nc.vector.tensor_scalar(out[k][:, c, :], part(src[k], c), m.nmv[s][:, c, 0:1],
                                               m.nrstd[s][:, c:c + 1], ALU.subtract, ALU.mult)
            last.then_inc(self.ready.sem, 1)

    def pair(self, i):
        return [self.m.h_more[:, bass.ds((2 * i + s) * NC_, NC_), :] for s in range(2)]

    def vector(self, dve, i, src, out):
        self.vector_stats(dve, i, src)
        self.vector_aggr(dve, i)
        self.vector_scale(dve, i, src, out)

    def gpsimd(self, pool, i):
        for k, s in enumerate(self.slots):
            pool.wait_ge(self.var.sem, self.var.at(i, k + 1))
            self.nc.gpsimd.tensor_tensor(self.m.nrstd[s][:, 0:self.tiles], self.m.nrstd[s][:, 0:self.tiles], self.m.minus_half[:, 0:self.tiles],
                                         ALU.pow).then_inc(self.root.sem, 1)


def linear_attention(ctx, nc, m):
    S = range(2)
    sig = lambda name, per: Signal(ctx, nc, "la_" + name, per)
    norm = Norm(ctx, nc, m, "la")
    xt_ps, xt_sb = sig("xt_ps", 2), sig("xt_sb", 2)
    qk_ps, exp_sb, phi, phi_step = sig("qk_ps", 4), sig("exp_sb", 4), sig("phi", 4), sig("phi_step", 4)
    z_step, qz, den_ps, den_sb, qn = sig("z_step", 2), sig("qz", 2), sig("den_ps", 2), sig("den_sb", 4), sig("qn", 2)
    km_d, km_a = sig("km_d", 2), sig("km_a", 2)
    kt_ps, kt_sb = sig("kt_ps", 2), sig("kt_sb", 2)
    v_ps, v_sb = sig("v_ps", 8), sig("v_sb", 8)
    st_ps, st_sb = sig("st_ps", 6), sig("st_sb", 6)
    sc_ps, a_sb = sig("sc_ps", 16), sig("a_sb", 16)
    av_ps, ot_sb = sig("av_ps", 8), sig("ot_sb", 8)
    y_ps, h_sb = sig("y_ps", 2), sig("h_sb", 2)
    NS = NC_ - 1
    XN, XT = m.XN, m.XT
    QT, KT, EX = m.t512a, m.t512b, m.t512c
    KM, A, V, KTOK, ST, OT = m.KM, m.A, m.V, m.KTOK, m.ST, m.OT
    w = m.w

    with nc.Block() as block:
        @block.vector
        def _(dve):
            for n in ("ones", "causal", "head_col", "state_mask"):
                dve.wait_ge(m.loaded[n], 16)
            norm.vector(dve, 0, norm.pair(0), XN)
            with dve.Fori(0, PAIRS) as i:
                hs = norm.pair(i)
                for q in range(2):
                    for s in S:
                        n = 2 * q + s + 1
                        dve.wait_ge(exp_sb.sem, exp_sb.at(i, n))
                        nc.vector.tensor_scalar(EX[s][:, q, :], EX[s][:, q, :], 1.0, None, ALU.min).then_inc(phi_step.sem, 1)
                    for s in S:
                        n = 2 * q + s + 1
                        dve.wait_ge(phi_step.sem, phi_step.at(i, n))
                        nc.vector.scalar_tensor_tensor((QT, KT)[q][s][:, :], m.bank[4 * s + 1 + q][:, :], 1.0, EX[s][:, q, :],
                                                       ALU.add, ALU.max).then_inc(phi.sem, 1)
                for s in S:
                    dve.wait_ge(phi.sem, phi.at(i, 3 + s))
                    nc.vector.tensor_tensor_scan(EX[s][:, 0, :], w["ones"][:, :], KT[s][:, :], 0.0, ALU.mult, ALU.add).then_inc(z_step.sem, 1)
                for s in S:
                    dve.wait_ge(z_step.sem, z_step.at(i, s + 1))
                    nc.vector.tensor_tensor(EX[s][:, 1, :], EX[s][:, 0, :], QT[s][:, :], ALU.mult).then_inc(qz.sem, 1)
                for s in S:
                    for hd in range(NH // 2):
                        last = nc.vector.tensor_scalar(KM[s][:, hd, :], KT[s][:, :], w["head_col"][:, hd:hd + 1], None, ALU.mult)
                    last.then_inc(km_d.sem, 1)
                for s in S:
                    dve.wait_ge(den_ps.sem, den_ps.at(i, s + 1))
                    nc.vector.tensor_scalar(EX[s][:, 0, :], m.bank[4 * s][:, :], 1e-6, None, ALU.max).then_inc(den_sb.sem, 1)
                for s in S:
                    dve.wait_ge(den_sb.sem, den_sb.at(i, s + 1))
                    nc.vector.reciprocal(EX[s][:, 0, :], EX[s][:, 0, :]).then_inc(den_sb.sem, 1)
                for s in S:
                    dve.wait_ge(den_sb.sem, den_sb.at(i, 2 + s + 1))
                    nc.vector.tensor_tensor(QT[s][:, :], QT[s][:, :], EX[s][:, 0, :], ALU.mult).then_inc(qn.sem, 1)
                for c in range(NS):
                    for s in S:
                        dve.wait_ge(st_ps.sem, st_ps.at(i, 2 * c + s + 1))
                        nc.vector.tensor_tensor(ST[s][:, c, :], m.bank[4 * s + 3][:, :], w["state_mask"][:, :], ALU.mult).then_inc(st_sb.sem, 1)
                for g in range(NH // 2):
                    for s in S:
                        for par in range(2):
                            dve.wait_ge(sc_ps.sem, sc_ps.at(i, 4 * g + 2 * s + par + 1))
                            nc.vector.tensor_tensor(A[s][:, 2 * (g % 2) + par, :, :], m.bank[4 * s + par][:, :].rearrange("p (c t) -> p c t", c=NC_),
                                                    w["causal"][:, :].rearrange("p (o t) -> p o t", o=1).broadcast_to([P, NC_, P]),
                                                    ALU.mult).then_inc(a_sb.sem, 1)
                norm.vector(dve, i + 1, norm.pair(i + 1), XN)
                for s in S:
                    dve.wait_ge(y_ps.sem, y_ps.at(i, s + 1))
                    nc.vector.tensor_tensor(hs[s], hs[s], m.bank[4 * s][:, :].rearrange("p (c d) -> p c d", c=NC_), ALU.add).then_inc(h_sb.sem, 1)
                dve.wait_ge(h_sb.sem, h_sb.at(i, 2))

        @block.gpsimd
        def _(pool):
            norm.gpsimd(pool, 0)
            with pool.Fori(0, PAIRS) as i:
                norm.gpsimd(pool, i + 1)

        @block.scalar
        def _(act):
            act.wait_ge(m.loaded["head_col"], 16)
            with act.Fori(0, PAIRS) as i:
                for s in S:
                    act.wait_ge(xt_ps.sem, xt_ps.at(i, s + 1))
                    nc.scalar.copy(XT[s][:, :], m.bank[4 * s][:, :]).then_inc(xt_sb.sem, 1)
                for q in range(2):
                    for s in S:
                        act.wait_ge(qk_ps.sem, qk_ps.at(i, 2 * q + s + 1))
                        nc.scalar.activation(EX[s][:, q, :], m.bank[4 * s + 1 + q][:, :], ACT.Exp).then_inc(exp_sb.sem, 1)
                for c in range(NC_):
                    for s in S:
                        act.wait_ge(v_ps.sem, v_ps.at(i, 2 * c + s + 1))
                        nc.scalar.copy(V[s][:, c, :], m.bank[4 * s + (3 if c % 2 else 0)][:, :]).then_inc(v_sb.sem, 1)
                for s in S:
                    act.wait_ge(phi.sem, phi.at(i, 3 + s))
                    for hd in range(NH // 2, NH):
                        last = nc.scalar.activation(KM[s][:, hd, :], KT[s][:, :], ACT.Copy, scale=w["head_col"][:, hd:hd + 1])
                    last.then_inc(km_a.sem, 1)
                for s in S:
                    act.wait_ge(kt_ps.sem, kt_ps.at(i, s + 1))
                    nc.scalar.copy(KTOK[s][:, :, :], m.bank[4 * s + 1][:, 0:NS * P].rearrange("p (c k) -> p c k", c=NS)).then_inc(kt_sb.sem, 1)
                for g in range(NH // 2):
                    for s in S:
                        act.wait_ge(av_ps.sem, av_ps.at(i, 2 * g + s + 1))
                        nc.scalar.copy(OT[s][:, g, :], m.bank[4 * s + 2 + g % 2][:, :]).then_inc(ot_sb.sem, 1)

        @block.tensor
        def _(pe):
            for n in ("wq", "wk", "wv", "wout", "same_head"):
                pe.wait_ge(m.loaded[n], 16)
            with pe.Fori(0, PAIRS) as i:
                for s in S:
                    pe.wait_ge(norm.ready.sem, norm.ready.at(i, s + 1))
                    for c in range(NC_):
                        last = nc.tensor.transpose(m.bank[4 * s][:, c * P:(c + 1) * P], XN[s][:, c, :], w["ident"][:, :])
                    last.then_inc(xt_ps.sem, 1)
                for s in S:
                    pe.wait_ge(xt_sb.sem, xt_sb.at(i, s + 1))
                    nc.tensor.matmul(m.bank[4 * s + 1][:, :], w["wq"][:, :], XT[s][:, :], start=True, stop=True).then_inc(qk_ps.sem, 1)
                for s in S:
                    nc.tensor.matmul(m.bank[4 * s + 2][:, :], w["wk"][:, :], XT[s][:, :], start=True, stop=True).then_inc(qk_ps.sem, 1)
                for c in range(NC_):
                    for s in S:
                        if c >= 2:
                            pe.wait_ge(v_sb.sem, v_sb.at(i, 2 * (c - 2) + s + 1))
                        nc.tensor.matmul(m.bank[4 * s + (3 if c % 2 else 0)][:, :], XT[s][:, c * P:(c + 1) * P], w["wv"][:, :],
                                         start=True, stop=True).then_inc(v_ps.sem, 1)
                for s in S:
                    pe.wait_ge(phi.sem, phi.at(i, 3 + s))
                    for c in range(NS):
                        last = nc.tensor.transpose(m.bank[4 * s + 1][:, c * P:(c + 1) * P], KT[s][:, c * P:(c + 1) * P], w["ident"][:, :])
                    last.then_inc(kt_ps.sem, 1)
                for s in S:
                    pe.wait_ge(qz.sem, qz.at(i, s + 1))
                    pe.wait_ge(v_sb.sem, v_sb.at(i, 4 + s + 1))
                    nc.tensor.matmul(m.bank[4 * s][:, :], w["same_head"][:, :], EX[s][:, 1, :], start=True, stop=True).then_inc(den_ps.sem, 1)
                for c in range(NS):
                    for s in S:
                        if c == 0:
                            pe.wait_ge(kt_sb.sem, kt_sb.at(i, s + 1))
                            pe.wait_ge(v_sb.sem, v_sb.at(i, 6 + s + 1))
                        else:
                            pe.wait_ge(st_sb.sem, st_sb.at(i, 2 * (c - 1) + s + 1))
                        nc.tensor.matmul(m.bank[4 * s + 3][:, :], KTOK[s][:, c, :], V[s][:, c, :],
                                         start=c == 0, stop=c == NS - 1, skip_group_check=True).then_inc(st_ps.sem, 1)

                def scores(g, s):
                    if g == 0:
                        pe.wait_ge(qn.sem, qn.at(i, s + 1))
                        pe.wait_ge(km_d.sem, km_d.at(i, s + 1))
                    if g == 2:
                        pe.wait_ge(km_a.sem, km_a.at(i, s + 1))
                    for par in range(2):
                        hd = 2 * g + par
                        if g:
                            pe.wait_ge(a_sb.sem, a_sb.at(i, 4 * (g - 1) + 2 * s + par + 1))
                        for c in range(NC_):
                            last = nc.tensor.matmul(m.bank[4 * s + par][:, c * P:(c + 1) * P], KM[s][:, hd, c * P:(c + 1) * P],
                                                    QT[s][:, c * P:(c + 1) * P], start=True, stop=True)
                        last.then_inc(sc_ps.sem, 1)

                def values(g, s):
                    pe.wait_ge(a_sb.sem, a_sb.at(i, 4 * g + 2 * s + 2))
                    if g == 0:
                        pe.wait_ge(st_sb.sem, st_sb.at(i, 2 * (NS - 1) + s + 1))
                    if g >= 2:
                        pe.wait_ge(ot_sb.sem, ot_sb.at(i, 2 * (g - 2) + s + 1))
                    out = m.bank[4 * s + 2 + g % 2]
                    for c in range(NC_):
                        for par in range(2):
                            hd = 2 * g + par
                            last = nc.tensor.matmul(out[DV * par:DV * par + DV, c * P:(c + 1) * P], V[s][:, c, hd * DV:(hd + 1) * DV],
                                                    A[s][:, 2 * (g % 2) + par, c, :], start=True, stop=c == 0)
                        if c:
                            last = nc.tensor.matmul(out[:, c * P:(c + 1) * P], ST[s][:, c - 1, g * P:(g + 1) * P],
                                                    QT[s][:, c * P:(c + 1) * P], start=False, stop=True)
                    last.then_inc(av_ps.sem, 1)

                for s in S:
                    scores(0, s)
                for g in range(NH // 2):
                    for s in S:
                        if g + 1 < NH // 2:
                            scores(g + 1, s)
                        values(g, s)
                for s in S:
                    pe.wait_ge(ot_sb.sem, ot_sb.at(i, 6 + s + 1))
                    for c in range(NC_):
                        for g in range(NH // 2):
                            last = nc.tensor.matmul(m.bank[4 * s][:, c * P:(c + 1) * P], OT[s][:, g, c * P:(c + 1) * P],
                                                    w["wout"][:, g * D:(g + 1) * D], start=g == 0, stop=g == NH // 2 - 1)
                    last.then_inc(y_ps.sem, 1)
                pe.wait_ge(h_sb.sem, h_sb.at(i, 2))


def modulated_ffn(ctx, nc, m):
    S = range(2)
    sig = lambda name, per: Signal(ctx, nc, "mf_" + name, per)
    w = m.w
    F = 512
    G4 = F // P
    late = [(n, *m.load(ctx, n)) for n in ("gfc1", "gfc1_b", "gfc2_rep", "gfc2_b", "task_b1", "b1", "ln_coef", "ln_rows",
                                            "task_b2", "gate_row", "gate_pad")]
    tv1, tv2 = m.KM[0], m.KM[1]
    tv1_in, tv2_in, w1_in, w2_in = (ctx.semaphore("loaded_" + n) for n in ("tv1", "tv2", "W1", "W2"))
    W1, W2 = m.ST[0][:, 0, :], m.ST[0][:, 1, :]
    W1M, W2M = m.t512a, m.t512b
    HH = [m.big[:, 16 * T + s * 4 * T:16 * T + (s + 1) * 4 * T].rearrange("p (g n) -> p g n", g=G4) for s in S]
    junk = [m.t512c[s][:, 0, :] for s in S]
    res = [m.XN[s] for s in S]
    GH = ctx.sb("mf_gate_hidden", [P, B])
    gcol = ctx.sb("mf_gate", [P, B])
    grow = ctx.sb("mf_gate_first", [P, B])
    b1m = ctx.sb("mf_b1m", [P, G4, B])
    lngb = ctx.sb("mf_ln", [P, 2 * D])
    gsel = [ctx.sb(f"mf_gsel{s}", [P, 48]) for s in S]
    gb2 = [ctx.sb(f"mf_gb2{s}", [P, P]) for s in S]
    norm, norm2 = Norm(ctx, nc, m, "mf"), Norm(ctx, nc, m, "mf2")
    xt_ps, xt_sb, gh_ps, gh_sb = sig("xt_ps", 2), sig("xt_sb", 2), sig("gh_ps", 2), sig("gh_sb", 2)
    gate_ps, gate_sb, small_ps, small_sb = sig("gate_ps", 0), sig("gate_sb", 0), sig("small_ps", 0), sig("small_sb", 0)
    gs_sb, xn_kept = sig("gs_sb", 2), sig("xn_kept", 32)
    XN = m.XN
    m1_ps, m1_sb, m2_ps, m2_sb = sig("m1_ps", 2), sig("m1_sb", 2), sig("m2_ps", 2), sig("m2_sb", 2)
    f_ps, f_sb, o_ps, r_sb, sc_sb, hb_sb, h_sb = (sig("f_ps", 8), sig("f_sb", 8), sig("o_ps", 2), sig("r_sb", 2), sig("sc_sb", 2),
                                                  sig("hb_sb", 2), sig("h_sb", 2))
    over = lambda v, n=NC_: v.rearrange("p (o t) -> p o t", o=1).broadcast_to([P, n, v.shape[-1]])

    with nc.Block() as block:
        @block.sync
        def _(sp):
            for _, t, sem, src in late:
                sp.dma_start(t[:, :], src).then_inc(sem, 16)
            sp.dma_start(W1, m.dram["W1"]).then_inc(w1_in, 16)
            sp.dma_start(W2, m.dram["W2"]).then_inc(w2_in, 16)
            with sp.Fori(0, PAIRS) as i:
                for s in S:
                    sp.wait_ge(norm.ready.sem, norm.ready.at(i, s + 1))
                    sp.dma_start(m.XNA[:, bass.ds((2 * i + s) * NC_, NC_), :], XN[s][:, :, :]).then_inc(xn_kept.sem, 16)

        @block.vector
        def _(dve):
            norm.vector(dve, 0, norm.pair(0), XN)
            with dve.Fori(0, PAIRS) as i:
                norm.vector_stats(dve, i + 1, norm.pair(i + 1))
                norm.vector_aggr(dve, i + 1)
                dve.wait_ge(xn_kept.sem, xn_kept.at(i, 32))
                dve.wait_ge(xt_sb.sem, xt_sb.at(i, 2))
                norm.vector_scale(dve, i + 1, norm.pair(i + 1), XN)
            dve.wait_ge(gate_ps.sem, 1)
            dve.wait_ge(m.loaded["gfc2_b"], 16)
            nc.vector.tensor_scalar(gcol[:, :], m.bank[0][:, 0:B], 1.0 / T, w["gfc2_b"][:, 0:1], ALU.mult, ALU.add).then_inc(gate_sb.sem, 1)
            dve.wait_ge(gate_sb.sem, 1)
            dve.wait_ge(m.loaded["gate_row"], 16)
            nc.vector.tensor_scalar(grow[:, :], gcol[:, :], w["gate_row"][:, 0:1], None, ALU.mult).then_inc(gate_sb.sem, 1)
            dve.wait_ge(small_ps.sem, 1)
            dve.wait_ge(m.loaded["b1"], 16)
            nc.vector.tensor_tensor(b1m[:, :, :], m.bank[1][:, 0:G4 * B].rearrange("p (g b) -> p g b", g=G4),
                                    w["b1"][:, :].rearrange("p (g o) -> p g o", o=1).broadcast_to([P, G4, B]), ALU.add).then_inc(small_sb.sem, 1)
            nc.vector.tensor_copy(lngb[:, :], m.bank[2][:, 0:2 * D]).then_inc(small_sb.sem, 1)
            dve.wait_ge(gate_sb.sem, 2)
            dve.wait_ge(small_sb.sem, 2)
            for sem in (m.loaded["gate_pad"], w1_in, w2_in):
                dve.wait_ge(sem, 16)
            def merged(i):
                for s in S:
                    nc.vector.tensor_scalar(gsel[s][:, :], w["gate_pad"][:, :], gcol[:, bass.ds(2 * i + s, 1)], None, ALU.mult)
                    nc.vector.tensor_scalar(gb2[s][:, :], w["ones"][:, 0:P], grow[:, bass.ds(2 * i + s, 1)], w["gate_row"][:, 1:2],
                                            ALU.mult, ALU.add).then_inc(gs_sb.sem, 1)
                for s in S:
                    dve.wait_ge(m1_ps.sem, m1_ps.at(i, s + 1))
                    nc.vector.tensor_tensor(W1M[s][:, :], m.bank[4 * s][:, :], W1, ALU.add).then_inc(m1_sb.sem, 1)
                for s in S:
                    dve.wait_ge(m2_ps.sem, m2_ps.at(i, s + 1))
                    nc.vector.tensor_tensor(W2M[s][:, :], m.bank[4 * s + 1][:, :], W2, ALU.add).then_inc(m2_sb.sem, 1)

            def output(i, more):
                hs = [m.h[:, bass.ds((2 * i + s) * NC_, NC_), :] for s in S]
                xs = [m.XNA[:, bass.ds((2 * i + s) * NC_, NC_), :] for s in S]
                for s in S:
                    dve.wait_ge(o_ps.sem, o_ps.at(i, s + 1))
                    nc.vector.tensor_tensor(res[s][:, :, :], m.bank[4 * s][:, :].rearrange("p (c d) -> p c d", c=NC_), xs[s], ALU.add).then_inc(r_sb.sem, 1)
                dve.wait_ge(r_sb.sem, r_sb.at(i, 2))
                if more:
                    merged(i + 1)
                norm2.vector(dve, i, [res[s] for s in S], [res[s] for s in S])
                for s in S:
                    dve.wait_ge(norm2.ready.sem, norm2.ready.at(i, s + 1))
                    nc.vector.tensor_tensor(res[s][:, :, :], res[s][:, :, :], over(lngb[:, 0:D]), ALU.mult).then_inc(sc_sb.sem, 1)
                for s in S:
                    dve.wait_ge(sc_sb.sem, sc_sb.at(i, s + 1))
                    dve.wait_ge(hb_sb.sem, hb_sb.at(i, s + 1))
                    nc.vector.tensor_tensor(hs[s], hs[s], res[s][:, :, :], ALU.add).then_inc(h_sb.sem, 1)
                dve.wait_ge(h_sb.sem, h_sb.at(i, 2))

            merged(0)
            with dve.Fori(0, PAIRS - 1) as i:
                output(i, True)
            output(PAIRS - 1, False)

        @block.gpsimd
        def _(pool):
            norm.gpsimd(pool, 0)
            with pool.Fori(0, PAIRS) as i:
                norm.gpsimd(pool, i + 1)
            pool.wait_ge(small_sb.sem, 2)
            with pool.Fori(0, PAIRS) as i:
                for s in S:
                    hs = m.h[:, bass.ds((2 * i + s) * NC_, NC_), :]
                    nc.gpsimd.tensor_tensor(hs, hs, over(lngb[:, D:2 * D]), ALU.add).then_inc(hb_sb.sem, 1)
                norm2.gpsimd(pool, i)

        @block.scalar
        def _(act):
            nc.scalar.dma_start(tv1[:, :, :].rearrange("p a t -> p (a t)"), m.dram["task_W1"]).then_inc(tv1_in, 16)
            nc.scalar.dma_start(tv2[:, :, :].rearrange("p a t -> p (a t)"), m.dram["task_W2"]).then_inc(tv2_in, 16)
            act.wait_ge(m.loaded["gfc1_b"], 16)
            with act.Fori(0, PAIRS) as i:
                for s in S:
                    act.wait_ge(xt_ps.sem, xt_ps.at(i, s + 1))
                    nc.scalar.copy(m.XTA[:, bass.ds((2 * i + s) * T, T)], m.bank[4 * s][:, :]).then_inc(xt_sb.sem, 1)
                for s in S:
                    act.wait_ge(gh_ps.sem, gh_ps.at(i, s + 1))
                    nc.scalar.activation(junk[s], m.bank[4 * s + 1][:, :], ACT.Relu, bias=w["gfc1_b"][:, 0:1],
                                         accum_out=GH[:, bass.ds(2 * i + s, 1)]).then_inc(gh_sb.sem, 1)
            act.wait_ge(small_sb.sem, 1)
            with act.Fori(0, PAIRS) as i:
                for g in range(G4):
                    for s in S:
                        act.wait_ge(f_ps.sem, f_ps.at(i, 2 * g + s + 1))
                        nc.scalar.activation(HH[s][:, g, :], m.bank[4 * s + 2 + g % 2][:, :], ACT.Relu,
                                             bias=b1m[:, g, bass.ds(2 * i + s, 1)]).then_inc(f_sb.sem, 1)

        @block.tensor
        def _(pe):
            pe.wait_ge(m.loaded["gfc1"], 16)
            with pe.Fori(0, PAIRS) as i:
                for s in S:
                    pe.wait_ge(norm.ready.sem, norm.ready.at(i, s + 1))
                    for c in range(NC_):
                        last = nc.tensor.transpose(m.bank[4 * s][:, c * P:(c + 1) * P], XN[s][:, c, :], w["ident"][:, :])
                    last.then_inc(xt_ps.sem, 1)
                for s in S:
                    pe.wait_ge(xt_sb.sem, xt_sb.at(i, s + 1))
                    nc.tensor.matmul(m.bank[4 * s + 1][:, :], w["gfc1"][:, :], m.XTA[:, bass.ds((2 * i + s) * T, T)], start=True, stop=True).then_inc(gh_ps.sem, 1)
                pe.wait_ge(gh_sb.sem, gh_sb.at(i, 2))
            for n in ("gfc2_rep", "task_b1", "ln_coef", "ln_rows", "task_b2"):
                pe.wait_ge(m.loaded[n], 16)
            pe.wait_ge(gh_sb.sem, B)
            nc.tensor.matmul(m.bank[0][:, 0:B], w["gfc2_rep"][:, :], GH[:, :], start=True, stop=True).then_inc(gate_ps.sem, 1)
            nc.tensor.matmul(m.bank[2][:, 0:2 * D], w["ln_coef"][:, :], w["ln_rows"][:, :], start=True, stop=True)
            pe.wait_ge(gate_sb.sem, 1)
            for g in range(G4):
                last = nc.tensor.matmul(m.bank[1][:, g * B:(g + 1) * B], w["task_b1"][:, g * P:(g + 1) * P], gcol[:, :], start=True, stop=True)
            last.then_inc(small_ps.sem, 1)
            pe.wait_ge(tv1_in, 16)
            pe.wait_ge(tv2_in, 16)
            pe.wait_ge(small_sb.sem, 2)
            with pe.Fori(0, PAIRS) as i:
                def merge(s, bank, tv):
                    for j in range(2):
                        for q in range(NC_):
                            last = nc.tensor.matmul(bank[32 * q:32 * q + 32, :], gsel[s][:, 16 - 16 * j:48 - 16 * j], tv[:, 2 * q + j, :],
                                                    start=j == 0, stop=j == 1)
                    return last
                for s in S:
                    pe.wait_ge(gs_sb.sem, gs_sb.at(i, s + 1))
                    merge(s, m.bank[4 * s], tv1).then_inc(m1_ps.sem, 1)
                for s in S:
                    merge(s, m.bank[4 * s + 1], tv2).then_inc(m2_ps.sem, 1)
                for g in range(G4):
                    for s in S:
                        if g == 0:
                            pe.wait_ge(m1_sb.sem, m1_sb.at(i, s + 1))
                        if g >= 2:
                            pe.wait_ge(f_sb.sem, f_sb.at(i, 2 * (g - 2) + s + 1))
                        nc.tensor.matmul(m.bank[4 * s + 2 + g % 2][:, :], W1M[s][:, g * P:(g + 1) * P], m.XTA[:, bass.ds((2 * i + s) * T, T)],
                                         start=True, stop=True).then_inc(f_ps.sem, 1)
                for s in S:
                    pe.wait_ge(m2_sb.sem, m2_sb.at(i, s + 1))
                    pe.wait_ge(f_sb.sem, f_sb.at(i, 6 + s + 1))
                    for c in range(NC_):
                        nc.tensor.matmul(m.bank[4 * s][:, c * P:(c + 1) * P], gb2[s][:, :], w["task_b2"][:, :], start=True, stop=False)
                        for g in range(G4):
                            last = nc.tensor.matmul(m.bank[4 * s][:, c * P:(c + 1) * P], HH[s][:, g, c * P:(c + 1) * P],
                                                    W2M[s][:, g * D:(g + 1) * D], start=False, stop=g == G4 - 1)
                    last.then_inc(o_ps.sem, 1)


def retention(ctx, nc, m):
    S = range(2)
    sig = lambda name, per: Signal(ctx, nc, "re_" + name, per)
    rstep = sig("rstep", 2)
    w = m.w
    late = [(n, *m.load(ctx, n)) for n in ("r_wq", "r_wk", "r_wv", "r_wg", "r_wo", "gn", "decay_q", "decay_k")]
    XN, XT, QT, KT, KM, KTOK, ST = m.XN, m.XT, m.t512a, m.t512b, m.KM, m.KTOK, m.ST
    G = [m.t512c[s][:, 0, :] for s in S]
    TH = [m.t512c[s][:, 1, :] for s in S]
    A = [m.big[:, s * 8 * T:(s + 1) * 8 * T].rearrange("p (a c t) -> p a c t", a=NH, c=NC_) for s in S]
    VP = [[m.big[:, (16 + 2 * s + par) * T:(17 + 2 * s + par) * T].rearrange("p (c n) -> p c n", c=NC_) for par in range(2)] for s in S]
    V = [m.big[:, (20 + s) * T:(21 + s) * T].rearrange("p (c n) -> p c n", c=NC_) for s in S]
    Y = [m.big[:, (22 + s) * T:(23 + s) * T] for s in S]
    SQ = [ST[s][:, 1, :] for s in S]
    group = lambda v: v.rearrange("p (n k) -> p n k", k=DH)
    wide = lambda v: v.rearrange("p (n o) -> p n o", o=1).broadcast_to([P, NC_ * NH, DH])
    gsum = [ctx.sb(f"re_gsum{s}", [P, NC_ * NH]) for s in S]
    gvar = [ctx.sb(f"re_gvar{s}", [P, NC_ * NH]) for s in S]
    norm = Norm(ctx, nc, m, "re")
    xt_ps, xt_sb, qk_ps, qk_sb = sig("xt_ps", 2), sig("xt_sb", 2), sig("qk_ps", 4), sig("qk_sb", 4)
    g_ps, g_sb, v_ps, v_sb = sig("g_ps", 2), sig("g_sb", 2), sig("v_ps", 2), sig("v_sb", 2)
    km_d, km_a, kt_ps, kt_sb = sig("km_d", 2), sig("km_a", 2), sig("kt_ps", 2), sig("kt_sb", 2)
    st_ps, st_sb, sc_ps, a_sb = sig("st_ps", 6), sig("st_sb", 6), sig("sc_ps", 16), sig("a_sb", 16)
    av_ps, ot_sb, tok_ps, y_sb = sig("av_ps", 2), sig("ot_sb", 2), sig("tok_ps", 2), sig("y_sb", 2)
    gstep, sq_sb, root_in, root, gn_sb = sig("gstep", 8), sig("sq_sb", 2), sig("root_in", 2), sig("root", 2), sig("gn_sb", 2)
    ch_ps, ch_sb, sum_sb, th_sb, z_sb, y_ps, h_sb = (sig("ch_ps", 2), sig("ch_sb", 2), sig("sum_sb", 2), sig("th_sb", 2), sig("z_sb", 2),
                                                     sig("y_ps", 2), sig("h_sb", 2))
    zeroed = sig("zeroed", 0)
    NS = NC_ - 1
    ND = 3

    with nc.Block() as block:
        @block.sync
        def _(sp):
            for _, t, sem, src in late:
                sp.dma_start(t[:, :], src).then_inc(sem, 16)

        @block.vector
        def _(dve):
            for n in ("decay_q", "decay_k"):
                dve.wait_ge(m.loaded[n], 16)
            norm.vector(dve, 0, norm.pair(0), XN)
            with dve.Fori(0, PAIRS) as i:
                hs = norm.pair(i)
                for q in range(2):
                    for s in S:
                        dve.wait_ge(qk_ps.sem, qk_ps.at(i, 2 * q + s + 1))
                        nc.vector.tensor_tensor((QT, KT)[q][s][:, :], m.bank[4 * s + 1 + q][:, :], w[("decay_q", "decay_k")[q]][:, :],
                                                ALU.mult).then_inc(qk_sb.sem, 1)
                for s in S:
                    dve.wait_ge(qk_sb.sem, qk_sb.at(i, 3 + s))
                    for hd in range(ND):
                        last = nc.vector.tensor_scalar(KM[s][:, hd, :], KT[s][:, :], w["head_col"][:, hd:hd + 1], None, ALU.mult)
                    last.then_inc(km_d.sem, 1)
                for c in range(NS):
                    for s in S:
                        dve.wait_ge(st_ps.sem, st_ps.at(i, 2 * c + s + 1))
                        nc.vector.tensor_tensor(ST[s][:, 0, c * P:(c + 1) * P], m.bank[4 * s + 3][:, 0:P], w["same_head"][:, :], ALU.mult).then_inc(st_sb.sem, 1)
                for g in range(NH // 2):
                    for s in S:
                        for par in range(2):
                            dve.wait_ge(sc_ps.sem, sc_ps.at(i, 4 * g + 2 * s + par + 1))
                            nc.vector.tensor_tensor(A[s][:, 2 * g + par, :, :], m.bank[4 * s + par][:, :].rearrange("p (c t) -> p c t", c=NC_),
                                                    w["causal"][:, :].rearrange("p (o t) -> p o t", o=1).broadcast_to([P, NC_, P]),
                                                    ALU.mult).then_inc(a_sb.sem, 1)
                norm.vector(dve, i + 1, norm.pair(i + 1), XN)
                for s in S:
                    dve.wait_ge(y_sb.sem, y_sb.at(i, s + 1))
                    nc.vector.tensor_reduce(gsum[s][:, :], group(Y[s]), AX.X, ALU.add).then_inc(gstep.sem, 1)
                for s in S:
                    dve.wait_ge(gstep.sem, gstep.at(i, s + 1))
                    nc.vector.tensor_scalar(gsum[s][:, :], gsum[s][:, :], 1.0 / DH, None, ALU.mult).then_inc(gstep.sem, 1)
                for s in S:
                    dve.wait_ge(gstep.sem, gstep.at(i, 2 + s + 1))
                    nc.vector.tensor_tensor(group(Y[s]), group(Y[s]), wide(gsum[s][:, :]), ALU.subtract).then_inc(gstep.sem, 1)
                for s in S:
                    dve.wait_ge(sq_sb.sem, sq_sb.at(i, s + 1))
                    nc.vector.tensor_reduce(gvar[s][:, :], group(SQ[s]), AX.X, ALU.add).then_inc(gstep.sem, 1)
                for s in S:
                    dve.wait_ge(gstep.sem, gstep.at(i, 6 + s + 1))
                    nc.vector.tensor_scalar(gvar[s][:, :], gvar[s][:, :], 1.0 / DH, LN_EPS, ALU.mult, ALU.add).then_inc(root_in.sem, 1)
                for s in S:
                    dve.wait_ge(root.sem, root.at(i, s + 1))
                    nc.vector.reciprocal(gvar[s][:, :], gvar[s][:, :]).then_inc(rstep.sem, 1)
                for s in S:
                    dve.wait_ge(rstep.sem, rstep.at(i, s + 1))
                    nc.vector.tensor_tensor(group(Y[s]), group(Y[s]), wide(gvar[s][:, :]), ALU.mult).then_inc(gn_sb.sem, 1)
                for s in S:
                    dve.wait_ge(ch_sb.sem, ch_sb.at(i, s + 1))
                    nc.vector.tensor_tensor(G[s], G[s], SQ[s], ALU.add).then_inc(sum_sb.sem, 1)
                for s in S:
                    dve.wait_ge(th_sb.sem, th_sb.at(i, s + 1))
                    nc.vector.scalar_tensor_tensor(G[s], TH[s], 1.0, G[s], ALU.add, ALU.mult).then_inc(z_sb.sem, 1)
                for s in S:
                    dve.wait_ge(y_ps.sem, y_ps.at(i, s + 1))
                    nc.vector.scalar_tensor_tensor(hs[s], m.bank[4 * s][:, :].rearrange("p (c d) -> p c d", c=NC_), 0.5, hs[s],
                                                   ALU.mult, ALU.add).then_inc(h_sb.sem, 1)
                dve.wait_ge(h_sb.sem, h_sb.at(i, 2))

        @block.gpsimd
        def _(pool):
            for s in S:
                for par in range(2):
                    nc.gpsimd.memset(VP[s][par][:, :, :], 0.0).then_inc(zeroed.sem, 1)
            pool.wait_ge(zeroed.sem, 4)
            norm.gpsimd(pool, 0)
            with pool.Fori(0, PAIRS) as i:
                norm.gpsimd(pool, i + 1)

        @block.scalar
        def _(act):
            act.wait_ge(m.loaded["gn"], 16)
            act.wait_ge(zeroed.sem, 4)
            half = lambda v, par: v.rearrange("p c (g a k) -> p (c g) a k", a=2, k=DH)[:, :, par, :]
            with act.Fori(0, PAIRS) as i:
                for s in S:
                    act.wait_ge(xt_ps.sem, xt_ps.at(i, s + 1))
                    nc.scalar.copy(XT[s][:, :], m.bank[4 * s][:, :]).then_inc(xt_sb.sem, 1)
                for s in S:
                    act.wait_ge(g_ps.sem, g_ps.at(i, s + 1))
                    nc.scalar.copy(G[s], m.bank[4 * s + 3][:, :]).then_inc(g_sb.sem, 1)
                for s in S:
                    act.wait_ge(v_ps.sem, v_ps.at(i, s + 1))
                    v = m.bank[4 * s + 2][:, :].rearrange("p (c n) -> p c n", c=NC_)
                    for par in range(2):
                        nc.scalar.copy(half(VP[s][par][:, :, :], par), half(v, par))
                    nc.scalar.copy(V[s][:, :, :], v).then_inc(v_sb.sem, 1)
                for s in S:
                    act.wait_ge(kt_ps.sem, kt_ps.at(i, s + 1))
                    nc.scalar.copy(KTOK[s][:, :, :], m.bank[4 * s + 1][:, 0:NS * P].rearrange("p (c k) -> p c k", c=NS)).then_inc(kt_sb.sem, 1)
                for s in S:
                    act.wait_ge(qk_sb.sem, qk_sb.at(i, 3 + s))
                    for hd in range(ND, NH):
                        last = nc.scalar.activation(KM[s][:, hd, :], KT[s][:, :], ACT.Copy, scale=w["head_col"][:, hd:hd + 1])
                    last.then_inc(km_a.sem, 1)
                for s in S:
                    act.wait_ge(av_ps.sem, av_ps.at(i, s + 1))
                    nc.scalar.copy(SQ[s], m.bank[4 * s + 2][:, :]).then_inc(ot_sb.sem, 1)
                for s in S:
                    act.wait_ge(tok_ps.sem, tok_ps.at(i, s + 1))
                    nc.scalar.copy(Y[s], m.bank[4 * s + 3][:, :]).then_inc(y_sb.sem, 1)
                for s in S:
                    act.wait_ge(gstep.sem, gstep.at(i, 4 + s + 1))
                    nc.scalar.activation(SQ[s], Y[s], ACT.Square).then_inc(sq_sb.sem, 1)
                for s in S:
                    act.wait_ge(root_in.sem, root_in.at(i, s + 1))
                    nc.scalar.activation(gvar[s][:, :], gvar[s][:, :], ACT.Sqrt).then_inc(root.sem, 1)
                for s in S:
                    act.wait_ge(ch_ps.sem, ch_ps.at(i, s + 1))
                    nc.scalar.activation(SQ[s], m.bank[4 * s + 3][:, :], ACT.Identity, scale=w["gn"][:, 0:1], bias=w["gn"][:, 1:2]).then_inc(ch_sb.sem, 1)
                for s in S:
                    act.wait_ge(sum_sb.sem, sum_sb.at(i, s + 1))
                    nc.scalar.activation(TH[s], G[s], ACT.Tanh, scale=0.5).then_inc(th_sb.sem, 1)

        @block.tensor
        def _(pe):
            for n in ("r_wq", "r_wk", "r_wv", "r_wg", "r_wo"):
                pe.wait_ge(m.loaded[n], 16)
            with pe.Fori(0, PAIRS) as i:
                for s in S:
                    pe.wait_ge(norm.ready.sem, norm.ready.at(i, s + 1))
                    for c in range(NC_):
                        last = nc.tensor.transpose(m.bank[4 * s][:, c * P:(c + 1) * P], XN[s][:, c, :], w["ident"][:, :])
                    last.then_inc(xt_ps.sem, 1)
                for s in S:
                    pe.wait_ge(xt_sb.sem, xt_sb.at(i, s + 1))
                    nc.tensor.matmul(m.bank[4 * s + 1][:, :], w["r_wq"][:, :], XT[s][:, :], start=True, stop=True).then_inc(qk_ps.sem, 1)
                for s in S:
                    nc.tensor.matmul(m.bank[4 * s + 2][:, :], w["r_wk"][:, :], XT[s][:, :], start=True, stop=True).then_inc(qk_ps.sem, 1)
                for s in S:
                    nc.tensor.matmul(m.bank[4 * s + 3][:, :], w["r_wg"][:, :], XT[s][:, :], start=True, stop=True).then_inc(g_ps.sem, 1)
                for s in S:
                    pe.wait_ge(qk_sb.sem, qk_sb.at(i, 3 + s))
                    for c in range(NC_):
                        last = nc.tensor.matmul(m.bank[4 * s + 2][:, c * P:(c + 1) * P], XT[s][:, c * P:(c + 1) * P], w["r_wv"][:, :], start=True, stop=True)
                    last.then_inc(v_ps.sem, 1)
                    for c in range(NS):
                        last = nc.tensor.transpose(m.bank[4 * s + 1][:, c * P:(c + 1) * P], KT[s][:, c * P:(c + 1) * P], w["ident"][:, :])
                    last.then_inc(kt_ps.sem, 1)
                for c in range(NS):
                    for s in S:
                        if c == 0:
                            pe.wait_ge(kt_sb.sem, kt_sb.at(i, s + 1))
                            pe.wait_ge(v_sb.sem, v_sb.at(i, s + 1))
                            pe.wait_ge(g_sb.sem, g_sb.at(i, s + 1))
                        else:
                            pe.wait_ge(st_sb.sem, st_sb.at(i, 2 * (c - 1) + s + 1))
                        nc.tensor.matmul(m.bank[4 * s + 3][:, 0:P], KTOK[s][:, c, :], V[s][:, c, :],
                                         start=c == 0, stop=c == NS - 1, skip_group_check=True).then_inc(st_ps.sem, 1)
                for g in range(NH // 2):
                    for s in S:
                        if g == 0:
                            pe.wait_ge(km_d.sem, km_d.at(i, s + 1))
                        if g == ND // 2:
                            pe.wait_ge(km_a.sem, km_a.at(i, s + 1))
                        for par in range(2):
                            if g:
                                pe.wait_ge(a_sb.sem, a_sb.at(i, 4 * (g - 1) + 2 * s + par + 1))
                            for c in range(NC_):
                                last = nc.tensor.matmul(m.bank[4 * s + par][:, c * P:(c + 1) * P], KM[s][:, 2 * g + par, c * P:(c + 1) * P],
                                                        QT[s][:, c * P:(c + 1) * P], start=True, stop=True)
                            last.then_inc(sc_ps.sem, 1)
                for s in S:
                    pe.wait_ge(a_sb.sem, a_sb.at(i, 12 + 2 * s + 2))
                    pe.wait_ge(st_sb.sem, st_sb.at(i, 2 * (NS - 1) + s + 1))
                    for c in range(NC_):
                        for par in range(2):
                            for g in range(NH // 2):
                                last = nc.tensor.matmul(m.bank[4 * s + 2][32 * g:32 * g + 32, c * P:(c + 1) * P],
                                                        VP[s][par][:, c, 32 * g:32 * g + 32], A[s][:, 2 * g + par, c, :],
                                                        start=par == 0, stop=par == 1 and c == 0)
                        if c:
                            last = nc.tensor.matmul(m.bank[4 * s + 2][:, c * P:(c + 1) * P], ST[s][:, 0, (c - 1) * P:c * P],
                                                    QT[s][:, c * P:(c + 1) * P], start=False, stop=True)
                    last.then_inc(av_ps.sem, 1)
                for s in S:
                    pe.wait_ge(ot_sb.sem, ot_sb.at(i, s + 1))
                    for c in range(NC_):
                        last = nc.tensor.transpose(m.bank[4 * s + 3][:, c * P:(c + 1) * P], SQ[s][:, c * P:(c + 1) * P], w["ident"][:, :])
                    last.then_inc(tok_ps.sem, 1)
                for s in S:
                    pe.wait_ge(gn_sb.sem, gn_sb.at(i, s + 1))
                    for c in range(NC_):
                        last = nc.tensor.transpose(m.bank[4 * s + 3][:, c * P:(c + 1) * P], Y[s][:, c * P:(c + 1) * P], w["ident"][:, :])
                    last.then_inc(ch_ps.sem, 1)
                for s in S:
                    pe.wait_ge(z_sb.sem, z_sb.at(i, s + 1))
                    for c in range(NC_):
                        last = nc.tensor.matmul(m.bank[4 * s][:, c * P:(c + 1) * P], G[s][:, c * P:(c + 1) * P], w["r_wo"][:, :], start=True, stop=True)
                    last.then_inc(y_ps.sem, 1)
                pe.wait_ge(h_sb.sem, h_sb.at(i, 2))


def balanced_experts(ctx, nc, m):
    S = range(2)
    E, M, ITERS = 8, T // 8, 8
    BE = B * E
    sig = lambda name, per: Signal(ctx, nc, "be_" + name, per)
    w = m.w
    late = [(n, *m.load(ctx, n)) for n in ("gate_w", "experts", "later_expert")]
    XN, XT, XTA = m.XN, m.XT, m.XTA
    G = m.big[:, 0:NC_ * BE]
    G4 = G.rearrange("p (c b e) -> p c b e", c=NC_, b=B)
    GR = G.rearrange("p (n e) -> p n e", e=E)
    rowsum = ctx.sb("be_rowsum", [P, NC_ * B])
    colsum = ctx.sb("be_colsum", [P, BE])
    GT, WK0, WK1, SEL, EQ, PRE = (m.big[:, (1 + n) * T:(2 + n) * T] for n in range(6))
    WK = (WK0, WK1)
    m8 = ctx.sb("be_m8", [BE, 8, 8])
    small = ctx.sb("be_small", [BE, 2])
    WT = m.big[:, 7 * T:7 * T + NC_ * BE]
    WT4 = WT.rearrange("p (c b e) -> p c b e", c=NC_, b=B)
    YW = [m.KM[s][:, 0:4, :].rearrange("p a (x d) -> p (a x) d", d=D) for s in S]
    YR = [m.t512a[s] for s in S]
    norm = Norm(ctx, nc, m, "be")
    xt_ps, xt_sb, xt_kept, lg_ps, lg_sb = sig("xt_ps", 2), sig("xt_sb", 2), sig("xt_kept", 32), sig("lg_ps", 2), sig("lg_sb", 2)
    step, col_in, col_ps = sig("step", 5), sig("col_in", 1), sig("col_ps", 1)
    gt_ps, pick, sel_in, later_ps, w_in, w_ps, w_sb = (sig("gt_ps", 0), sig("pick", 0), sig("sel_in", 0), sig("later_ps", 0),
                                                       sig("w_in", 0), sig("w_ps", 0), sig("w_sb", 0))
    zeroed = sig("zeroed", 0)
    x_sb = [sig(f"x_sb{s}", 16) for s in S]
    yw_act = sig("yw_act", 8)
    y_ps, yw_sb, yr_sb, h_sb = sig("y_ps", 8), sig("yw_sb", 8), sig("yr_sb", 8), sig("h_sb", 2)

    with nc.Block() as block:
        @block.sync
        def _(sp):
            for _, t, sem, src in late:
                sp.dma_start(t[:, :], src).then_inc(sem, 16)
            with sp.Fori(0, PAIRS) as i:
                for s in S:
                    sp.wait_ge(xt_sb.sem, xt_sb.at(i, s + 1))
                    sp.dma_start(XTA[:, bass.ds((2 * i + s) * T, T)], XT[s][:, :]).then_inc(xt_kept.sem, 16)
            sp.wait_ge(xt_kept.sem, 16 * B)
            sp.wait_ge(lg_sb.sem, B)
            for s in S:
                sp.dma_start(XT[s][:, :], XTA[:, s * T:(s + 1) * T]).then_inc(x_sb[s].sem, 16)
            with sp.Fori(1, PAIRS) as i:
                for s in S:
                    if s == 0:
                        sp.wait_ge(y_ps.sem, y_ps.at(i, 0))
                    sp.dma_start(XT[s][:, :], XTA[:, bass.ds((2 * i + s) * T, T)]).then_inc(x_sb[s].sem, 16)

        @block.vector
        def _(dve):
            nc.vector.memset(SEL[BE:P, :], 0.0).then_inc(zeroed.sem, 1)
            norm.vector(dve, 0, norm.pair(0), XN)
            with dve.Fori(0, PAIRS) as i:
                norm.vector_stats(dve, i + 1, norm.pair(i + 1))
                norm.vector_aggr(dve, i + 1)
                dve.wait_ge(xt_sb.sem, xt_sb.at(i, 2))
                norm.vector_scale(dve, i + 1, norm.pair(i + 1), XN)
                for s in S:
                    dve.wait_ge(lg_ps.sem, lg_ps.at(i, s + 1))
                    nc.vector.tensor_scalar(G4[:, :, bass.ds(2 * i + s, 1), :].rearrange("p c o e -> p c (o e)"),
                                            m.bank[4 * s + 1][:, 0:NC_ * E].rearrange("p (c e) -> p c e", c=NC_), 1e-6, None, ALU.max).then_inc(lg_sb.sem, 1)
                dve.wait_ge(lg_sb.sem, lg_sb.at(i, 2))
                dve.wait_ge(xt_kept.sem, xt_kept.at(i, 32))
            nc.vector.tensor_copy(colsum[:, :], m.w["ones"][:, 0:BE]).then_inc(lg_sb.sem, 1)
            dve.wait_ge(lg_sb.sem, B + 1)
            with dve.Fori(0, ITERS) as k:
                dve.wait_ge(col_ps.sem, col_ps.at(k, 1))
                nc.vector.tensor_reduce(colsum[:, :], m.bank[0][:, 0:NC_ * BE].rearrange("p (c n) -> p n c", c=NC_), AX.X, ALU.add).then_inc(step.sem, 1)
                dve.wait_ge(step.sem, step.at(k, 1))
                nc.vector.reciprocal(colsum[:, :], colsum[:, :]).then_inc(step.sem, 1)
                dve.wait_ge(step.sem, step.at(k, 2))
                nc.vector.tensor_tensor(G.rearrange("p (c n) -> p c n", c=NC_), G.rearrange("p (c n) -> p c n", c=NC_),
                                        colsum[:, :].rearrange("p (o n) -> p o n", o=1).broadcast_to([P, NC_, BE]), ALU.mult).then_inc(step.sem, 1)
                dve.wait_ge(step.sem, step.at(k, 3))
                nc.vector.tensor_reduce(rowsum[:, :], GR, AX.X, ALU.add).then_inc(step.sem, 1)
                dve.wait_ge(step.sem, step.at(k, 4))
                nc.vector.reciprocal(rowsum[:, :], rowsum[:, :]).then_inc(step.sem, 1)
                dve.wait_ge(step.sem, step.at(k, 5))
                nc.vector.tensor_tensor(GR, GR, rowsum[:, :].rearrange("p (n o) -> p n o", o=1).broadcast_to([P, NC_ * B, E]), ALU.mult).then_inc(col_in.sem, 1)
            chain = [0]

            def link(ins):
                chain[0] += 1
                ins.then_inc(pick.sem, 1)
                dve.wait_ge(pick.sem, chain[0])

            dve.wait_ge(gt_ps.sem, 1)
            nc.vector.tensor_copy(WK0[0:BE, :], m.bank[1][0:BE, :])
            link(nc.vector.tensor_copy(GT[0:BE, :], m.bank[1][0:BE, :]))
            for r in range(M // 8):
                link(nc.vector.max(m8[:, r, :], WK[r % 2][0:BE, :]))
                if r < M // 8 - 1:
                    link(nc.vector.match_replace(WK[(r + 1) % 2][0:BE, :], m8[:, r, :], WK[r % 2][0:BE, :], -1.0))
            least = m8[:, M // 8 - 1, 7:8]
            above, need = small[:, 0:1], small[:, 1:2]
            dve.wait_ge(zeroed.sem, 1)
            link(nc.vector.tensor_scalar(SEL[0:BE, :], GT[0:BE, :], least, None, ALU.is_gt))
            link(nc.vector.tensor_reduce(above, SEL[0:BE, :], AX.X, ALU.add))
            nc.vector.tensor_scalar(EQ[0:BE, :], GT[0:BE, :], least, None, ALU.is_equal)
            link(nc.vector.tensor_scalar(need, above, -1.0, float(M), ALU.mult, ALU.add))
            link(nc.vector.tensor_tensor_scan(PRE[0:BE, :], w["ones"][0:BE, :], EQ[0:BE, :], 0.0, ALU.mult, ALU.add))
            link(nc.vector.scalar_tensor_tensor(PRE[0:BE, :], PRE[0:BE, :], need, EQ[0:BE, :], ALU.is_le, ALU.mult))
            nc.vector.tensor_tensor(SEL[0:BE, :], SEL[0:BE, :], PRE[0:BE, :], ALU.add).then_inc(sel_in.sem, 1)
            dve.wait_ge(sel_in.sem, 1)
            dve.wait_ge(later_ps.sem, 1)
            link(nc.vector.scalar_tensor_tensor(EQ[0:BE, :], m.bank[2][0:BE, :], 0.0, SEL[0:BE, :], ALU.is_equal, ALU.mult))
            nc.vector.tensor_tensor(SEL[0:BE, :], EQ[0:BE, :], GT[0:BE, :], ALU.mult).then_inc(w_in.sem, 1)
            dve.wait_ge(w_ps.sem, 1)
            nc.vector.tensor_copy(WT.rearrange("p (c n) -> p c n", c=NC_), m.bank[3][:, :].rearrange("p (c n) -> p c n", c=NC_)[:, :, 0:BE]).then_inc(w_sb.sem, 1)
            dve.wait_ge(w_sb.sem, 1)
            with dve.Fori(0, PAIRS) as i:
                hs = [m.h[:, bass.ds((2 * i + s) * NC_, NC_), :] for s in S]
                for c in range(NC_):
                    for s in S:
                        n = 2 * c + s + 1
                        wc = WT4[:, c, bass.ds(2 * i + s, 1), :].rearrange("p o e -> p (o e)")
                        dve.wait_ge(y_ps.sem, y_ps.at(i, n))
                        if c >= 2 and s == 0:
                            dve.wait_ge(yr_sb.sem, yr_sb.at(i, 2 * (c - 2) + 2))
                        nc.vector.tensor_tensor(YW[s][:, 8 * (c % 2):8 * (c % 2) + 4, :],
                                                m.bank[4 * s + 2 * (c % 2)][:, :].rearrange("p (e d) -> p e d", d=D),
                                                wc[:, 0:4].rearrange("p (e o) -> p e o", o=1).broadcast_to([P, 4, D]), ALU.mult).then_inc(yw_sb.sem, 1)
                    for s in S:
                        dve.wait_ge(yw_sb.sem, yw_sb.at(i, 2 * c + s + 1))
                        dve.wait_ge(yw_act.sem, yw_act.at(i, 2 * c + s + 1))
                        nc.vector.tensor_reduce(YR[s][:, c * D:(c + 1) * D], YW[s][:, 8 * (c % 2):8 * (c % 2) + 8, :].rearrange("p e d -> p d e"),
                                                AX.X, ALU.add).then_inc(yr_sb.sem, 1)
                for s in S:
                    dve.wait_ge(yr_sb.sem, yr_sb.at(i, 6 + s + 1))
                    nc.vector.tensor_tensor(hs[s], hs[s], YR[s][:, :].rearrange("p (c d) -> p c d", c=NC_), ALU.add).then_inc(h_sb.sem, 1)
                dve.wait_ge(h_sb.sem, h_sb.at(i, 2))

        @block.gpsimd
        def _(pool):
            norm.gpsimd(pool, 0)
            with pool.Fori(0, PAIRS) as i:
                norm.gpsimd(pool, i + 1)

        @block.scalar
        def _(act):
            with act.Fori(0, PAIRS) as i:
                for s in S:
                    act.wait_ge(xt_ps.sem, xt_ps.at(i, s + 1))
                    nc.scalar.copy(XT[s][:, :], m.bank[4 * s][:, :]).then_inc(xt_sb.sem, 1)
                act.wait_ge(xt_kept.sem, xt_kept.at(i, 32))
            act.wait_ge(w_sb.sem, 1)
            with act.Fori(0, PAIRS) as i:
                for c in range(NC_):
                    for s in S:
                        wc = WT4[:, c, bass.ds(2 * i + s, 1), :].rearrange("p o e -> p (o e)")
                        act.wait_ge(y_ps.sem, y_ps.at(i, 2 * c + s + 1))
                        if c >= 2:
                            act.wait_ge(yr_sb.sem, yr_sb.at(i, 2 * (c - 2) + s + 1))
                        for e in range(4, E):
                            last = nc.scalar.activation(YW[s][:, 8 * (c % 2) + e, :], m.bank[4 * s + 2 * (c % 2) + 1][:, (e - 4) * D:(e - 3) * D],
                                                        ACT.Copy, scale=wc[:, e:e + 1])
                        last.then_inc(yw_act.sem, 1)
                act.wait_ge(yr_sb.sem, yr_sb.at(i, 8))

        @block.tensor
        def _(pe):
            for n in ("gate_w", "experts", "later_expert"):
                pe.wait_ge(m.loaded[n], 16)
            with pe.Fori(0, PAIRS) as i:
                for s in S:
                    pe.wait_ge(norm.ready.sem, norm.ready.at(i, s + 1))
                    for c in range(NC_):
                        last = nc.tensor.transpose(m.bank[4 * s][:, c * P:(c + 1) * P], XN[s][:, c, :], w["ident"][:, :])
                    last.then_inc(xt_ps.sem, 1)
                for s in S:
                    pe.wait_ge(xt_sb.sem, xt_sb.at(i, s + 1))
                    for c in range(NC_):
                        last = nc.tensor.matmul(m.bank[4 * s + 1][:, c * E:(c + 1) * E], XT[s][:, c * P:(c + 1) * P], w["gate_w"][:, :], start=True, stop=True)
                    last.then_inc(lg_ps.sem, 1)
                pe.wait_ge(lg_sb.sem, lg_sb.at(i, 2))
            pe.wait_ge(lg_sb.sem, B + 1)
            with pe.Fori(0, ITERS) as k:
                nc.tensor.matmul(m.bank[0][:, 0:NC_ * BE], w["ones"][:, 0:P], G, start=True, stop=True).then_inc(col_ps.sem, 1)
                pe.wait_ge(col_in.sem, col_in.at(k, 1))
            for c in range(NC_):
                last = nc.tensor.transpose(m.bank[1][0:BE, c * P:(c + 1) * P], G[:, c * BE:(c + 1) * BE], w["ident"][:, :])
            last.then_inc(gt_ps.sem, 1)
            pe.wait_ge(zeroed.sem, 1)
            pe.wait_ge(sel_in.sem, 1)
            nc.tensor.matmul(m.bank[2][0:BE, :], w["later_expert"][:, :], SEL, start=True, stop=True).then_inc(later_ps.sem, 1)
            pe.wait_ge(w_in.sem, 1)
            for c in range(NC_):
                last = nc.tensor.transpose(m.bank[3][:, c * P:(c + 1) * P], SEL[:, c * P:(c + 1) * P], w["ident"][:, :])
            last.then_inc(w_ps.sem, 1)
            pe.wait_ge(w_sb.sem, 1)
            with pe.Fori(0, PAIRS) as i:
                for c in range(NC_):
                    for s in S:
                        if c == 0:
                            pe.wait_ge(x_sb[s].sem, x_sb[s].at(i, 16))
                        if c >= 2:
                            pe.wait_ge(yw_sb.sem, yw_sb.at(i, 2 * (c - 2) + s + 1))
                            pe.wait_ge(yw_act.sem, yw_act.at(i, 2 * (c - 2) + s + 1))
                        for q in range(2):
                            last = nc.tensor.matmul(m.bank[4 * s + 2 * (c % 2) + q][:, :], XT[s][:, c * P:(c + 1) * P],
                                                    w["experts"][:, 512 * q:512 * q + 512], start=True, stop=True)
                        last.then_inc(y_ps.sem, 1)
                pe.wait_ge(yw_sb.sem, yw_sb.at(i, 8))
                pe.wait_ge(yw_act.sem, yw_act.at(i, 8))


class Top2:
    STEPS = 11

    def __init__(self, ctx, nc, m, tag, rows, E, per=1):
        self.nc, self.rows, self.E = nc, rows, E
        self.eq = ctx.sb(tag + "_t2_eq", [P, rows, E])
        self.rest = ctx.sb(tag + "_t2_rest", [P, rows, E])
        self.oh = [ctx.sb(f"{tag}_t2_oh{n}", [P, rows, E]) for n in range(2)]
        self.v = ctx.sb(tag + "_t2_v", [P, 2, rows])
        self.r = ctx.sb(tag + "_t2_r", [P, 2, rows])
        self.step = Signal(ctx, nc, tag + "_t2_step", self.STEPS)
        self.ramp = m.w["ramp"][:, 64 - E:64].rearrange("p (o e) -> p o e", o=1).broadcast_to([P, rows, E])

    def vector(self, dve, i, values):
        nc, E, rows = self.nc, self.E, self.rows
        over = lambda v: v.rearrange("p (n o) -> p n o", o=1).broadcast_to([P, rows, E])
        n = [0]

        def link(ins):
            n[0] += 1
            ins.then_inc(self.step.sem, 1)
            dve.wait_ge(self.step.sem, self.step.at(i, n[0]))

        for k in range(2):
            src = values if k == 0 else self.rest[:, :, :]
            link(nc.vector.tensor_reduce(self.v[:, k, :], src, AX.X, ALU.max))
            link(nc.vector.tensor_tensor(self.eq[:, :, :], src, over(self.v[:, k, :]), ALU.is_equal))
            link(nc.vector.tensor_tensor(self.eq[:, :, :], self.eq[:, :, :], self.ramp, ALU.mult))
            link(nc.vector.tensor_reduce(self.r[:, k, :], self.eq[:, :, :], AX.X, ALU.max))
            link(nc.vector.tensor_tensor(self.oh[k][:, :, :], self.ramp, over(self.r[:, k, :]), ALU.is_equal))
            if k == 0:
                link(nc.vector.scalar_tensor_tensor(self.rest[:, :, :], self.oh[0][:, :, :], -3e38, values, ALU.mult, ALU.add))
        assert n[0] == self.STEPS


def attention_and_experts(ctx, nc, m):
    S = range(2)
    U, GQ, CG = 64, 64, 4
    KS = GQ // CG
    CS = 2 * KS
    NBUF = 4
    EPS = 1e-7
    w = m.w
    late = [(n, *m.load(ctx, n)) for n in ("a_wx", "a_wt", "a_bt", "a_wa", "a_ba", "router", "ramp")]
    XN, XT = m.XN, m.XT

    sig = lambda name, per: Signal(ctx, nc, "aa_" + name, per)
    XA = m.big[:, 0:NT * (D + 1)].rearrange("p (n d) -> p n d", d=D + 1)
    o = NT * (D + 1)
    KU = m.big[:, o:o + PAIRS * T]
    QU = m.big[:, o + PAIRS * T:o + 2 * PAIRS * T]
    ARG = [m.KM[n // 2][:, 4 * (n % 2):4 * (n % 2) + 4, :] for n in range(NBUF)]
    EX = [m.t512a[g] for g in range(2)]
    ET = m.t512c[0][:, :, :].rearrange("p a t -> p (a t)").rearrange("p (j r) -> p j r", j=NC_)
    ssum = ctx.sb("aa_sum", [P, 2])
    norm = Norm(ctx, nc, m, "aa")
    ones_in = sig("ones_in", 0)
    xt_ps, xt_sb, kq_ps, kq_sb, xa_kept = sig("xt_ps", 2), sig("xt_sb", 2), sig("kq_ps", 2), sig("kq_sb", 2), sig("xa_kept", 32)
    BIASED = (12, 22, 23)
    args_before = lambda step: step - sum(b < step for b in BIASED)
    arg, th, used = sig("arg", CS - len(BIASED)), sig("th", CS), sig("used", CS)
    ex, tr_ps, et, o_ps, den, ha_sb = sig("ex", 2), sig("tr_ps", 2), sig("et", 2), sig("o_ps", 1), sig("den", 2), sig("ha_sb", 2)

    E, H = 8, 256
    HB = H // P
    UNITS = [(e, s) for e in range(E) for s in S]
    NU = len(UNITS)
    begin = lambda u: 8 * u // 5
    TANH, MUL, TURN, COPY, DOWN = 2, 4, 3, 5, 5
    sig = lambda name, per: Signal(ctx, nc, "rf_" + name, per)
    wgu = ctx.sb("rf_wgu", [P, E, 2 * H])
    wd = ctx.sb("rf_wd", [P, E, HB, D])
    wgu_in, wd_in = ctx.semaphore("loaded_wgu"), ctx.semaphore("loaded_wd")
    lg = ctx.sb("rf_lg", [P, 2, E])
    e2, p1, p2 = (ctx.sb(f"rf_{n}", [P, 2]) for n in ("e2", "p1", "p2"))
    WT = ctx.sb("rf_w", [P, 2, E])
    XM = XN[0]
    XMT = XT
    half = lambda u: slice((u % 2) * H, (u % 2 + 1) * H)
    TH = lambda u: m.ST[0][:, u // 2 % 2, half(u)]
    AC = lambda v: m.t512b[v % 2]
    ATB = [m.ST[1][:, 0, :], m.ST[1][:, 1, :], m.t512c[1][:, 0, :], m.t512c[1][:, 1, :]]
    AT = lambda v: ATB[v % 4]
    zero = ctx.sb("rf_zero", [P, P])
    norm2 = Norm(ctx, nc, m, "rf", slots=[0], tiles=2)
    top = Top2(ctx, nc, m, "rf", 2, E)
    x_ps, x_sb, lg_ps, lg_sb = sig("xt_ps", 1), sig("xt_sb", 1), sig("lg_ps", 1), sig("lg_sb", 1)
    wstep, e2_in, e2_sb, w_sb = sig("wstep", 4), sig("e2_in", 1), sig("e2_sb", 1), sig("w_sb", 1)
    gu_ps, th_sb, a1_sb, ac_sb = sig("gu_ps", NU), sig("th_sb", NU), sig("a1_sb", NU), sig("ac_sb", NU)
    at_ps, at_sb, dn, y_ps, h_sb = sig("at_ps", NU // 2), sig("at_sb", NU // 2), sig("dn", NU // 2), sig("y_ps", 1), sig("h_sb", 1)
    zeroed = sig("zeroed", 0)
    GU = lambda u: m.bank[3 + u % 3]
    TR, OUT = m.bank[6], m.bank[7][:, 0:2 * D]

    def has(n, back):
        return not isinstance(n, int) or n >= back

    def begun(t, lag):
        return [u for u in range(NU) if begin(u) + lag == t]

    def paired(t, lag):
        return [u // 2 for u in begun(t, lag) if u % 2]

    assert begin(NU - 1) + DOWN + 2 < CS
    NORM, TURN_X, COPY_X, ROUTE, LOGITS, E2, EXP, SHARES = 13, 15, 16, 17, 21, 22, 26, 28
    COUNT = PAIRS * NC_

    def tile_of(n):
        return n // NC_ * (2 * NC_) + n % NC_

    def query(n, step, cc):
        return QU[:, bass.ds(n * P + (step // KS) * GQ + cc * KS + step % KS, 1)]

    with nc.Block() as block:
        @block.sync
        def _(sp):
            for _, t, sem, src in late:
                sp.dma_start(t[:, :], src).then_inc(sem, 16)
            sp.wait_ge(ones_in.sem, 1)
            with sp.Fori(0, PAIRS) as i:
                for s in S:
                    sp.wait_ge(norm.ready.sem, norm.ready.at(i, s + 1))
                    sp.dma_start(XA[:, bass.ds((2 * i + s) * NC_, NC_), 0:D], XN[s][:, :, :]).then_inc(xa_kept.sem, 16)
            sp.dma_start(wgu[:, :, :].rearrange("p e n -> p (e n)"), m.dram["wgu"]).then_inc(wgu_in, 16)
            sp.dma_start(wd[:, :, :, :].rearrange("p e a d -> p (e a d)"), m.dram["wdown"]).then_inc(wd_in, 16)

        @block.gpsimd
        def _(pool):
            nc.gpsimd.memset(XA[:, :, D:D + 1], 1.0).then_inc(ones_in.sem, 1)
            nc.gpsimd.memset(zero[:, :], 0.0).then_inc(zeroed.sem, 1)
            norm.gpsimd(pool, 0)
            with pool.Fori(0, PAIRS) as i:
                norm.gpsimd(pool, i + 1)
            with pool.Fori(0, COUNT) as n:
                norm2.gpsimd(pool, n)

        @block.vector
        def _(dve):
            def arguments(n, i, step):
                if step in BIASED:
                    return
                if step >= NBUF or has(n, 1):
                    dve.wait_ge(used.sem, used.at(n, step - NBUF + 1))
                for cc in range(CG):
                    q = query(n, step, cc)
                    last = nc.vector.tensor_scalar(ARG[step % NBUF][:, cc, :], KU[:, bass.ds(i * T, T)], q, None, ALU.add)
                last.then_inc(arg.sem, 1)

            def weights(n, g):
                dve.wait_ge(tr_ps.sem, tr_ps.at(n, g + 1))
                nc.vector.tensor_copy(ET[:, :, g * P:(g + 1) * P], m.bank[2][:, :].rearrange("p (j r) -> p j r", j=NC_)).then_inc(et.sem, 1)

            def attended(n, tile):
                dve.wait_ge(o_ps.sem, o_ps.at(n, 1))
                out = m.bank[2][:, :].rearrange("p (s d) -> p s d", s=2)
                nc.vector.tensor_scalar(ssum[:, :], out[:, :, D], EPS, None, ALU.add).then_inc(den.sem, 1)
                dve.wait_ge(den.sem, den.at(n, 1))
                nc.vector.reciprocal(ssum[:, :], ssum[:, :]).then_inc(den.sem, 1)
                dve.wait_ge(den.sem, den.at(n, 2))
                for s in S:
                    h = m.h[:, bass.ds(tile + s * NC_, 1), :].rearrange("p o d -> p (o d)")
                    nc.vector.scalar_tensor_tensor(h, out[:, s, 0:D], ssum[:, s:s + 1], h, ALU.mult, ALU.add).then_inc(ha_sb.sem, 1)
                dve.wait_ge(ha_sb.sem, ha_sb.at(n, 2))

            def route(j, tile, step):
                if step in (NORM, NORM + 1, NORM + 3):
                    both = [[m.h[:, bass.ds(tile + s * NC_, 1), :] for s in S]]
                if step == NORM:
                    norm2.vector_stats(dve, j, both)
                if step == NORM + 1:
                    norm2.vector_aggr(dve, j)
                if step == NORM + 3:
                    norm2.vector_scale(dve, j, both, [XM])
                if step == LOGITS:
                    dve.wait_ge(lg_ps.sem, lg_ps.at(j, 1))
                    nc.vector.tensor_copy(lg[:, :, :], m.bank[2][:, 0:2 * E].rearrange("p (n e) -> p n e", e=E)).then_inc(lg_sb.sem, 1)
                if step == E2:
                    dve.wait_ge(lg_sb.sem, lg_sb.at(j, 1))
                    top.vector(dve, j, lg[:, :, :])
                    nc.vector.tensor_tensor(e2[:, :], top.v[:, 1, :], top.v[:, 0, :], ALU.subtract).then_inc(e2_in.sem, 1)
                if step == SHARES:
                    dve.wait_ge(e2_sb.sem, e2_sb.at(j, 1))
                    nc.vector.tensor_scalar(p1[:, :], e2[:, :], 2.0, 2.0, ALU.mult, ALU.add).then_inc(wstep.sem, 1)
                    dve.wait_ge(wstep.sem, wstep.at(j, 1))
                    nc.vector.reciprocal(p1[:, :], p1[:, :]).then_inc(wstep.sem, 1)
                    dve.wait_ge(wstep.sem, wstep.at(j, 2))
                    nc.vector.tensor_tensor(p2[:, :], p1[:, :], e2[:, :], ALU.mult).then_inc(wstep.sem, 1)
                    dve.wait_ge(wstep.sem, wstep.at(j, 3))
                    over = lambda v: v.rearrange("p (n o) -> p n o", o=1).broadcast_to([P, 2, E])
                    nc.vector.tensor_tensor(WT[:, :, :], top.oh[0][:, :, :], over(p1[:, :]), ALU.mult)
                    nc.vector.tensor_tensor(top.oh[1][:, :, :], top.oh[1][:, :, :], over(p2[:, :]), ALU.mult).then_inc(wstep.sem, 1)
                    dve.wait_ge(wstep.sem, wstep.at(j, 4))
                    nc.vector.tensor_tensor(WT[:, :, :], WT[:, :, :], top.oh[1][:, :, :], ALU.add).then_inc(w_sb.sem, 1)
                    dve.wait_ge(w_sb.sem, w_sb.at(j, 1))

            def units(j, tile, step):
                for u in begun(step, MUL):
                    e, s = UNITS[u]
                    dve.wait_ge(th_sb.sem, th_sb.at(j, u + 1))
                    nc.vector.scalar_tensor_tensor(TH(u), TH(u), 1.0, GU(u)[:, 0:H], ALU.add, ALU.mult).then_inc(a1_sb.sem, 1)
                    dve.wait_ge(a1_sb.sem, a1_sb.at(j, u + 1))
                    if u >= 4:
                        dve.wait_ge(at_ps.sem, at_ps.at(j, (u - 4) // 2 + 1))
                    nc.vector.scalar_tensor_tensor(AC(u // 2)[:, half(u)], TH(u), WT[:, s, e:e + 1], GU(u)[:, H:2 * H],
                                                   ALU.mult, ALU.mult).then_inc(ac_sb.sem, 1)
                if step == CS - 1:
                    dve.wait_ge(y_ps.sem, y_ps.at(j, 1))
                    for s in S:
                        h = m.h[:, bass.ds(tile + s * NC_, 1), :].rearrange("p o d -> p (o d)")
                        last = nc.vector.tensor_tensor(h, h, OUT[:, s * D:(s + 1) * D], ALU.add)
                    last.then_inc(h_sb.sem, 1)
                    dve.wait_ge(h_sb.sem, h_sb.at(j, 1))

            def iteration(n, i, before, behind, attention=True):
                for step in range(CS):
                    if before is not None and step == 7:
                        weights(n - 1, 1)
                    if before is not None and step == 11:
                        attended(n - 1, before)
                    if attention:
                        if step == 23:
                            weights(n, 0)
                        arguments(n, i, step)
                    if behind is not None:
                        units(n - 2, behind, step)
                    if before is not None:
                        route(n - 1, before, step)

            norm.vector(dve, 0, norm.pair(0), XN)
            with dve.Fori(0, PAIRS) as i:
                norm.vector_stats(dve, i + 1, norm.pair(i + 1))
                norm.vector_aggr(dve, i + 1)
                dve.wait_ge(xa_kept.sem, xa_kept.at(i, 32))
                dve.wait_ge(xt_sb.sem, xt_sb.at(i, 2))
                norm.vector_scale(dve, i + 1, norm.pair(i + 1), XN)
            dve.wait_ge(kq_sb.sem, 2 * PAIRS)
            dve.wait_ge(norm.ready.sem, 2 * (PAIRS + 1))
            dve.wait_ge(m.loaded["ramp"], 16)
            iteration(0, 0, None, None)
            iteration(1, 0, tile_of(0), None)
            iteration(2, 0, tile_of(1), tile_of(0))
            iteration(3, 0, tile_of(2), tile_of(1))
            with dve.Fori(1, PAIRS) as i:
                for c in range(NC_):
                    tile = [i * (2 * NC_) + tile_of(c + NC_ - back) - 2 * NC_ for back in (1, 2)]
                    iteration(i * NC_ + c, i, tile[0], tile[1])
            iteration(COUNT, None, tile_of(COUNT - 1), tile_of(COUNT - 2), attention=False)
            for step in range(CS):
                units(COUNT - 1, tile_of(COUNT - 1), step)

        @block.scalar
        def _(act):
            def score_exp(n, g):
                act.wait_ge(used.sem, used.at(n, (g + 1) * KS))
                nc.scalar.activation(EX[g][:, :], m.bank[g][:, :], ACT.Exp, bias=w["a_ba"][:, 0:1]).then_inc(ex.sem, 1)

            def route(j, parity, step):
                if step == COPY_X:
                    act.wait_ge(x_ps.sem, x_ps.at(j, 1))
                    nc.scalar.copy(XMT[parity][:, 0:2 * P], m.bank[2][:, 0:2 * P]).then_inc(x_sb.sem, 1)
                if step == EXP:
                    act.wait_ge(e2_in.sem, e2_in.at(j, 1))
                    nc.scalar.activation(e2[:, :], e2[:, :], ACT.Exp).then_inc(e2_sb.sem, 1)

            def units(j, step):
                for v in paired(step, COPY):
                    act.wait_ge(at_ps.sem, at_ps.at(j, v + 1))
                    if v >= 4:
                        act.wait_ge(dn.sem, dn.at(j, v - 3))
                    nc.scalar.copy(AT(v), TR[:, :]).then_inc(at_sb.sem, 1)
                for u in begun(step, TANH):
                    act.wait_ge(gu_ps.sem, gu_ps.at(j, u + 1))
                    if u >= 4:
                        act.wait_ge(ac_sb.sem, ac_sb.at(j, u - 3))
                    nc.scalar.activation(TH(u), GU(u)[:, 0:H], ACT.Tanh, scale=0.5).then_inc(th_sb.sem, 1)

            def iteration(n, i, c, attention=True):
                for step in range(CS):
                    if attention and step in BIASED:
                        act.wait_ge(used.sem, used.at(n, step - NBUF + 1))
                        for cc in range(CG):
                            last = nc.scalar.activation(ARG[step % NBUF][:, cc, :], KU[:, bass.ds(i * T, T)], ACT.Tanh, bias=query(n, step, cc))
                        last.then_inc(th.sem, 1)
                    elif attention:
                        act.wait_ge(arg.sem, arg.at(n, args_before(step) + 1))
                        nc.scalar.activation(ARG[step % NBUF], ARG[step % NBUF], ACT.Tanh).then_inc(th.sem, 1)
                    if has(n, 1) and step == 2:
                        score_exp(n - 1, 1)
                    if attention and step == KS + 2:
                        score_exp(n, 0)
                    if has(n, 2):
                        units(n - 2, step)
                    if has(n, 1):
                        route(n - 1, (c + 1) % 2, step)

            for name in ("a_bt", "a_ba"):
                act.wait_ge(m.loaded[name], 16)
            with act.Fori(0, PAIRS) as i:
                for s in S:
                    act.wait_ge(xt_ps.sem, xt_ps.at(i, s + 1))
                    nc.scalar.copy(XT[s][:, :], m.bank[4 * s][:, :]).then_inc(xt_sb.sem, 1)
                act.wait_ge(kq_ps.sem, kq_ps.at(i, 1))
                nc.scalar.copy(KU[:, bass.ds(i * T, T)], m.bank[1][:, :]).then_inc(kq_sb.sem, 1)
                act.wait_ge(kq_ps.sem, kq_ps.at(i, 2))
                nc.scalar.activation(QU[:, bass.ds(i * T, T)], m.bank[2][:, :], ACT.Identity, bias=w["a_bt"][:, 0:1]).then_inc(kq_sb.sem, 1)
            for n in range(NC_):
                iteration(n, 0, n)
            with act.Fori(1, PAIRS) as i:
                for c in range(NC_):
                    iteration(i * NC_ + c, i, c)
            iteration(COUNT, None, 0, attention=False)
            for step in range(CS):
                units(COUNT - 1, step)

        @block.tensor
        def _(pe):
            def turn_scores(n, g, free):
                pe.wait_ge(ex.sem, ex.at(n, g + 1))
                if free is not None:
                    pe.wait_ge(*free)
                for j in range(NC_):
                    last = nc.tensor.transpose(m.bank[2][:, j * P:(j + 1) * P], EX[g][:, j * P:(j + 1) * P], w["ident"][:, :])
                last.then_inc(tr_ps.sem, 1)

            def attend(n, tile0):
                pe.wait_ge(et.sem, et.at(n, 2))
                for s in S:
                    for j in range(NC_):
                        last = nc.tensor.matmul(m.bank[2][:, 256 * s:256 * s + D + 1], ET[:, j, s::2],
                                                XA[:, bass.ds(tile0 + s * NC_ + j, 1), :].rearrange("p o d -> p (o d)"),
                                                start=j == 0, stop=j == NC_ - 1)
                last.then_inc(o_ps.sem, 1)

            def route(j, parity, step):
                if step == TURN_X:
                    pe.wait_ge(norm2.ready.sem, norm2.ready.at(j, 1))
                    for s in S:
                        last = nc.tensor.transpose(m.bank[2][:, s * P:(s + 1) * P], XM[:, s, :], w["ident"][:, :])
                    last.then_inc(x_ps.sem, 1)
                if step == ROUTE:
                    pe.wait_ge(x_sb.sem, x_sb.at(j, 1))
                    for s in S:
                        last = nc.tensor.matmul(m.bank[2][:, s * E:(s + 1) * E], XMT[parity][:, s * P:(s + 1) * P], w["router"][:, :], start=True, stop=True)
                    last.then_inc(lg_ps.sem, 1)

            def units(j, parity, step):
                for v in paired(step, TURN):
                    pe.wait_ge(ac_sb.sem, ac_sb.at(j, 2 * v + 2))
                    if v:
                        pe.wait_ge(at_sb.sem, at_sb.at(j, v))
                    for b in range(4):
                        last = nc.tensor.transpose(TR[:, b * P:(b + 1) * P], AC(v)[:, b * P:(b + 1) * P], w["ident"][:, :])
                    last.then_inc(at_ps.sem, 1)
                for v in paired(step, DOWN):
                    if v == 0:
                        nc.tensor.matmul(OUT, zero[:, :], w["ones"][:, 0:2 * D], start=True, stop=False)
                    pe.wait_ge(at_sb.sem, at_sb.at(j, v + 1))
                    for s in S:
                        for a in range(HB):
                            o = s * H + a * P
                            last = nc.tensor.matmul(OUT[:, s * D:(s + 1) * D], AT(v)[:, o:o + P], wd[:, v, a, :],
                                                    start=False, stop=False, skip_group_check=True)
                    last.then_inc(dn.sem, 1)
                    if v == E - 1:
                        nc.tensor.matmul(OUT, zero[:, :], w["ones"][:, 0:2 * D], start=False, stop=True).then_inc(y_ps.sem, 1)
                for u in begun(step, 0):
                    e, s = UNITS[u]
                    if u >= 3:
                        pe.wait_ge(ac_sb.sem, ac_sb.at(j, u - 2))
                    nc.tensor.matmul(GU(u)[:, :], XMT[parity][:, s * P:(s + 1) * P], wgu[:, e, :], start=True, stop=True).then_inc(gu_ps.sem, 1)

            def iteration(n, tile0, c, attention=True):
                for step in range(CS):
                    k, g = step % KS, step // KS
                    if attention:
                        pe.wait_ge(th.sem, th.at(n, step + 1))
                        for cc in range(CG):
                            last = nc.tensor.matmul(m.bank[g][32 * cc:32 * cc + 32, :], w["a_wa"][:, 30 - 2 * k:62 - 2 * k],
                                                    ARG[step % NBUF][:, cc, :], start=k == 0, stop=k == KS - 1)
                        last.then_inc(used.sem, 1)
                    if has(n, 1) and step == 4:
                        turn_scores(n - 1, 1, (et.sem, et.at(n - 1, 1)))
                    if has(n, 1) and step == 8:
                        attend(n - 1, tile0)
                    if attention and step == KS + 4:
                        turn_scores(n, 0, (lg_sb.sem, lg_sb.at(n, 0)) if has(n, 1) else None)
                    if has(n, 2):
                        units(n - 2, c % 2, step)
                    if has(n, 1):
                        route(n - 1, (c + 1) % 2, step)

            for name in ("a_wx", "a_wt", "a_wa", "router"):
                pe.wait_ge(m.loaded[name], 16)
            with pe.Fori(0, PAIRS) as i:
                for s in S:
                    pe.wait_ge(norm.ready.sem, norm.ready.at(i, s + 1))
                    for c in range(NC_):
                        last = nc.tensor.transpose(m.bank[4 * s][:, c * P:(c + 1) * P], XN[s][:, c, :], w["ident"][:, :])
                    last.then_inc(xt_ps.sem, 1)
                pe.wait_ge(xt_sb.sem, xt_sb.at(i, 2))
                for bank, name in ((1, "a_wx"), (2, "a_wt")):
                    for s in S:
                        last = nc.tensor.matmul(m.bank[bank][U * s:U * s + U, :], w[name][:, :], XT[s][:, :], start=True, stop=True)
                    last.then_inc(kq_ps.sem, 1)
                pe.wait_ge(kq_sb.sem, kq_sb.at(i, 2))
            iteration(0, None, 0)
            for n in range(1, NC_):
                if n == 2:
                    pe.wait_ge(wgu_in, 16)
                    pe.wait_ge(wd_in, 16)
                    pe.wait_ge(zeroed.sem, 1)
                iteration(n, 0, n)
            with pe.Fori(1, PAIRS) as i:
                for c in range(NC_):
                    iteration(i * NC_ + c, i * (2 * NC_) - (0 if c else 2 * NC_), c)
            iteration(COUNT, (PAIRS - 1) * 2 * NC_, 0, attention=False)
            for step in range(CS):
                units(COUNT - 1, (COUNT - 1) % 2, step)


def batch_attention(ctx, nc, m):
    S = range(2)
    sig = lambda name, per: Signal(ctx, nc, "ba_" + name, per)
    w = m.w
    late = [(n, *m.load(ctx, n)) for n in ("b_w", "b_b")]
    L = B
    H4 = m.h[:, :, :].rearrange("p (l c) d -> p l c d", l=L)
    FT = m.big[:, 0:L * 3 * D].rearrange("p (l n) -> p l n", l=L)
    q_of = lambda l: FT[:, l, 0:D]
    K3, V3 = FT[:, :, D:2 * D], FT[:, :, 2 * D:3 * D]
    o = L * 3 * D
    PR = [m.big[:, o + n * L * D:o + (n + 1) * L * D].rearrange("p (m x) -> p m x", m=L) for n in range(L)]
    ON_POOL = (3, 5, 7)
    ON_VECTOR = [l for l in range(L) if l not in ON_POOL]
    ON_PE = (0, 1, 3, 4, 5, 7)
    REST = [l for l in range(L) if l not in ON_PE]
    SC = m.t512a[0][:, :]
    MK = m.t512a[1][:, :]
    EX = m.t512b[0][:, :]
    mx = ctx.sb("ba_mx", [P, L * NH])
    O = m.KM[0][:, 0:2, :].rearrange("p a (l x) -> p (a l) x", x=D)
    XN, XT = m.XN, m.XT
    norm = Norm(ctx, nc, m, "ba")
    xt_ps, xt_sb, ft_ps, ft_sb = sig("xt_ps", 2), sig("xt_sb", 2), sig("ft_ps", L), sig("ft_sb", L)
    pr_pool, pv_pool, sum_ps = sig("pr_pool", 3), sig("pv_pool", 3), sig("sum_ps", len(ON_PE))
    pr, sc, st, ex_in, ex_sb = sig("pr", len(ON_VECTOR)), sig("sc", L), sig("st", 6), sig("ex_in", 3), sig("ex_sb", 1)
    pv, ov, h_sb = sig("pv", len(ON_VECTOR)), sig("ov", len(REST)), sig("h_sb", L)
    by_m = lambda v: v.rearrange("p (l m h) -> p l h m", l=L, m=L)
    wide_m = lambda v: v.rearrange("p (l o h) -> p l o h", l=L, o=1).broadcast_to([P, L, L, NH])
    lmh = lambda v: v.rearrange("p (l m h) -> p l m h", l=L, m=L)

    def next_chunk(c):
        more = m.h_more[:, :, :].rearrange("p (l c) d -> p l c d", c=NC_)
        if isinstance(c, int):
            return [more[:, 4 * s:4 * s + 4, c, :] for s in S]
        more = m.h_more[:, 1:1 + L * NC_, :].rearrange("p (l c) d -> p l c d", c=NC_)
        return [more[:, 4 * s:4 * s + 4, bass.ds(c - 1, 1), :].rearrange("p l o d -> p l (o d)") for s in S]

    def times_q(engine, l):
        return engine.tensor_tensor(PR[l], K3, q_of(l).rearrange("p (o x) -> p o x", o=1).broadcast_to([P, L, D]), ALU.mult)

    def times_v(engine, l):
        pl = EX[:, l * L * NH:(l + 1) * L * NH].rearrange("p (n o) -> p n o", o=1).broadcast_to([P, L * NH, DH])
        return engine.tensor_tensor(PR[l].rearrange("p m (h x) -> p m h x", x=DH), V3.rearrange("p m (h x) -> p m h x", x=DH),
                                    pl.rearrange("p (m h) x -> p m h x", h=NH), ALU.mult)

    with nc.Block() as block:
        @block.sync
        def _(sp):
            for _, t, sem, src in late:
                sp.dma_start(t[:, :], src).then_inc(sem, 16)

        @block.gpsimd
        def _(pool):
            norm.gpsimd(pool, 0)
            with pool.Fori(0, NC_) as c:
                pool.wait_ge(ft_sb.sem, ft_sb.at(c, L))
                for l in ON_POOL:
                    times_q(nc.gpsimd, l).then_inc(pr_pool.sem, 1)
                pool.wait_ge(ex_in.sem, ex_in.at(c, 3))
                for l in ON_POOL:
                    times_v(nc.gpsimd, l).then_inc(pv_pool.sem, 1)
                norm.gpsimd(pool, c + 1)

        @block.vector
        def _(dve):
            dve.wait_ge(m.loaded["b_b"], 16)
            norm.vector(dve, 0, next_chunk(0), XN)
            with dve.Fori(0, NC_) as c:
                for l in range(L):
                    dve.wait_ge(ft_ps.sem, ft_ps.at(c, l + 1))
                    nc.vector.tensor_tensor(FT[:, l, :], m.bank[l][:, 0:3 * D], w["b_b"][:, :], ALU.add).then_inc(ft_sb.sem, 1)
                dve.wait_ge(ft_sb.sem, ft_sb.at(c, L))
                for n in range(len(ON_VECTOR)):
                    times_q(nc.vector, ON_VECTOR[n]).then_inc(pr.sem, 1)
                for l in range(L):
                    if l in ON_POOL:
                        dve.wait_ge(pr_pool.sem, pr_pool.at(c, ON_POOL.index(l) + 1))
                    else:
                        dve.wait_ge(pr.sem, pr.at(c, ON_VECTOR.index(l) + 1))
                    nc.vector.tensor_reduce(SC[:, l * L * NH:(l + 1) * L * NH], PR[l].rearrange("p m (h x) -> p (m h) x", x=DH),
                                            AX.X, ALU.add).then_inc(sc.sem, 1)
                n = [0]

                def link(ins):
                    n[0] += 1
                    ins.then_inc(st.sem, 1)
                    dve.wait_ge(st.sem, st.at(c, n[0]))

                dve.wait_ge(sc.sem, sc.at(c, L))
                link(nc.vector.tensor_scalar(MK, SC, 0.0, None, ALU.is_equal))
                link(nc.vector.scalar_tensor_tensor(SC, MK, -3e38, SC, ALU.mult, ALU.add))
                link(nc.vector.tensor_reduce(mx[:, :].rearrange("p (l h) -> p l h", l=L), by_m(SC), AX.X, ALU.max))
                nc.vector.tensor_tensor(lmh(SC), lmh(SC), wide_m(mx[:, :]), ALU.subtract).then_inc(ex_in.sem, 1)
                dve.wait_ge(ex_sb.sem, ex_sb.at(c, 1))
                link(nc.vector.scalar_tensor_tensor(EX, MK, 0.0, EX, ALU.is_equal, ALU.mult))
                link(nc.vector.tensor_reduce(mx[:, :].rearrange("p (l h) -> p l h", l=L), by_m(EX), AX.X, ALU.add))
                link(nc.vector.tensor_scalar(mx[:, :], mx[:, :], 1e-30, None, ALU.max))
                nc.vector.reciprocal(mx[:, :], mx[:, :]).then_inc(ex_in.sem, 1)
                dve.wait_ge(ex_in.sem, ex_in.at(c, 2))
                nc.vector.tensor_tensor(lmh(EX), lmh(EX), wide_m(mx[:, :]), ALU.mult).then_inc(ex_in.sem, 1)
                dve.wait_ge(ex_in.sem, ex_in.at(c, 3))
                for l in ON_VECTOR:
                    times_v(nc.vector, l).then_inc(pv.sem, 1)
                norm.vector(dve, c + 1, next_chunk(c + 1), XN)
                for l in REST:
                    dve.wait_ge(pv.sem, pv.at(c, ON_VECTOR.index(l) + 1))
                    nc.vector.tensor_reduce(O[:, l, :], PR[l].rearrange("p m x -> p x m"), AX.X, ALU.add).then_inc(ov.sem, 1)
                for n, l in enumerate(ON_PE):
                    h = H4[:, l:l + 1, bass.ds(c, 1), :].rearrange("p l o d -> p (l o d)")
                    dve.wait_ge(sum_ps.sem, sum_ps.at(c, n + 1))
                    nc.vector.tensor_tensor(h, h, m.bank[n][:, 0:D], ALU.add).then_inc(h_sb.sem, 1)
                for n, l in enumerate(REST):
                    h = H4[:, l:l + 1, bass.ds(c, 1), :].rearrange("p l o d -> p (l o d)")
                    dve.wait_ge(ov.sem, ov.at(c, n + 1))
                    nc.vector.tensor_tensor(h, h, O[:, l, :], ALU.add).then_inc(h_sb.sem, 1)
                dve.wait_ge(h_sb.sem, h_sb.at(c, L))

        @block.scalar
        def _(act):
            with act.Fori(0, NC_) as c:
                for s in S:
                    act.wait_ge(xt_ps.sem, xt_ps.at(c, s + 1))
                    nc.scalar.copy(XT[s][:, :], m.bank[4 * s][:, :]).then_inc(xt_sb.sem, 1)
                act.wait_ge(ex_in.sem, ex_in.at(c, 1))
                nc.scalar.activation(EX, SC, ACT.Exp, scale=DH ** -0.5).then_inc(ex_sb.sem, 1)

        @block.tensor
        def _(pe):
            pe.wait_ge(m.loaded["b_w"], 16)
            with pe.Fori(0, NC_) as c:
                for s in S:
                    pe.wait_ge(norm.ready.sem, norm.ready.at(c, s + 1))
                    for k in range(NC_):
                        last = nc.tensor.transpose(m.bank[4 * s][:, k * P:(k + 1) * P], XN[s][:, k, :], w["ident"][:, :])
                    last.then_inc(xt_ps.sem, 1)
                pe.wait_ge(xt_sb.sem, xt_sb.at(c, 2))
                for l in range(L):
                    nc.tensor.matmul(m.bank[l][:, 0:3 * D], XT[l // 4][:, (l % 4) * P:(l % 4 + 1) * P], w["b_w"][:, :], start=True, stop=True).then_inc(ft_ps.sem, 1)
                for n, l in enumerate(ON_PE):
                    if l in ON_POOL:
                        pe.wait_ge(pv_pool.sem, pv_pool.at(c, ON_POOL.index(l) + 1))
                    else:
                        pe.wait_ge(pv.sem, pv.at(c, ON_VECTOR.index(l) + 1))
                    for k in range(L):
                        last = nc.tensor.matmul(m.bank[n][:, 0:D], w["ident"][:, :], PR[l][:, k, :], start=k == 0, stop=k == L - 1)
                    last.then_inc(sum_ps.sem, 1)
                pe.wait_ge(h_sb.sem, h_sb.at(c, L))


def capacity_mixture(ctx, nc, m):
    m.w13 = ctx.sb("w13", [P, CE, 2 * CH])
    m.w13_in, m.w2_in = ctx.semaphore("loaded_w13"), ctx.semaphore("loaded_w2")
    m.w2 = m.big[:, NT * D:NT * D + CE // 2 * 2 * D].rearrange("p (q n) -> p q n", n=2 * D)
    m.place = ctx.sb("place", [P, PAIRS, 4 * NC_])
    m.share = ctx.sb("share", [P, PAIRS, 4 * NC_])
    capacity_routing(ctx, nc, m)
    capacity_experts(ctx, nc, m)
    capacity_combine(ctx, nc, m)


def capacity_routing(ctx, nc, m):
    S = range(2)
    sig = lambda name, per: Signal(ctx, nc, "cr_" + name, per)
    w = m.w
    late = [(n, *m.load(ctx, n)) for n in ("c_gate", "ramp", "earlier", "spare", "sw1", "sw3", "sw2")]
    R8 = 2 * NC_
    XN, XT = m.XN, m.XT
    sc = ctx.sb("cr_sc", [P, R8, CE])
    M = ctx.sb("cr_m", [P, R8, CE])
    CU = ctx.sb("cr_cu", [P, R8 + 1, CE])
    base = ctx.sb("cr_base", [P, CE])
    pos, val, slot, alt = (ctx.sb("cr_" + n, [P, 2, R8]) for n in ("pos", "val", "slot", "alt"))
    sidx = ctx.sb("cr_sidx", [P, PAIRS, 2 * R8], I32)
    XNA = m.big[:, 0:NT * D].rearrange("p (n d) -> p n d", d=D)
    vsum = ctx.sb("cr_vsum", [P, R8])
    SG = [m.t512a[s] for s in S]
    norm = Norm(ctx, nc, m, "cr")
    top = Top2(ctx, nc, m, "cr", R8, CE)
    xt_ps, xt_sb, lg_ps, ex_sb, one = sig("xt_ps", 2), sig("xt_sb", 2), sig("lg_ps", 1), sig("ex_sb", 1), sig("one", 2)
    g_ps, u_ps, th_sb, a_sb, y_ps, h_sb = sig("g_ps", 2), sig("u_ps", 2), sig("th_sb", 2), sig("a_sb", 4), sig("y_ps", 2), sig("h_sb", 2)
    cu, cu_sb, pos_ps, pst, idx_sb, kept, scattered = sig("cu", R8 + 2), sig("cu_sb", 1), sig("pos_ps", 1), sig("pst", 13), sig("idx_sb", 1), sig("kept", 2), sig("scattered", 0)
    based, xn_kept = sig("based", 0), sig("xn_kept", 32)
    G = lambda s: m.bank[2 + 4 * s]
    U = lambda s: m.bank[3 + 4 * s]
    OUT = lambda s: m.bank[4 * s]

    with nc.Block() as block:
        @block.sync
        def _(sp):
            for _, t, sem, src in late:
                sp.dma_start(t[:, :], src).then_inc(sem, 16)
            sp.dma_start(m.w13[:, :, :].rearrange("p e n -> p (e n)"), m.dram["w13"]).then_inc(m.w13_in, 16)
            sp.dma_start(m.w2.rearrange("p q n -> p (q n)"), m.dram["w2_pairs"]).then_inc(m.w2_in, 16)
            with sp.Fori(0, PAIRS) as i:
                for s in S:
                    sp.wait_ge(norm.ready.sem, norm.ready.at(i, s + 1))
                    sp.dma_start(XNA[:, bass.ds((2 * i + s) * NC_, NC_), :], XN[s][:, :, :]).then_inc(xn_kept.sem, 16)

        @block.gpsimd
        def _(pool):
            nc.gpsimd.memset(base[:, :], 0.0).then_inc(based.sem, 1)
            pool.wait_ge(m.queues_zero, 16)
            norm.gpsimd(pool, 0)
            for i in range(PAIRS):
                norm.gpsimd(pool, i + 1)
                pool.wait_ge(xn_kept.sem, 32 * (i + 1))
                pool.wait_ge(idx_sb.sem, i + 1)
                for s in S:
                    for c in range(NC_):
                        for k in range(2):
                            q = k * R8 + s * NC_ + c
                            pool.indirect_dma_start(
                                out=m.queues, out_offset=bass.IndirectOffsetOnAxis(ap=sidx[:, i, q:q + 1].bitcast(U32), axis=0),
                                in_=XNA[:, (2 * i + s) * NC_ + c, :], in_offset=None).then_inc(scattered.sem, 16)
            pool.wait_ge(scattered.sem, 16 * 2 * NT)

        @block.vector
        def _(dve):
            dve.wait_ge(based.sem, 1)
            for n in ("ramp", "spare"):
                dve.wait_ge(m.loaded[n], 16)
            norm.vector(dve, 0, norm.pair(0), XN)
            with dve.Fori(0, PAIRS) as i:
                hs = norm.pair(i)
                flat = lambda v: v.rearrange("p n e -> p (n e)")
                dve.wait_ge(ex_sb.sem, ex_sb.at(i, 1))
                nc.vector.tensor_scalar(flat(sc[:, :, :]), flat(sc[:, :, :]), 1.0, None, ALU.add).then_inc(one.sem, 1)
                dve.wait_ge(one.sem, one.at(i, 1))
                nc.vector.reciprocal(flat(sc[:, :, :]), flat(sc[:, :, :])).then_inc(one.sem, 1)
                dve.wait_ge(one.sem, one.at(i, 2))
                top.vector(dve, i, sc[:, :, :])
                nc.vector.tensor_copy(CU[:, 0, :], base[:, :]).then_inc(cu.sem, 1)
                nc.vector.tensor_tensor(M[:, :, :], top.oh[0][:, :, :], top.oh[1][:, :, :], ALU.add).then_inc(cu.sem, 1)
                for n in range(R8):
                    dve.wait_ge(cu.sem, cu.at(i, n + 2))
                    last = nc.vector.tensor_tensor(CU[:, n + 1, :] if n + 1 < R8 else base[:, :], CU[:, n, :], M[:, n, :], ALU.add)
                    last.then_inc(cu.sem, 1)
                dve.wait_ge(cu.sem, cu.at(i, R8 + 2))
                nc.vector.tensor_tensor(vsum[:, :], top.v[:, 0, :], top.v[:, 1, :], ALU.add).then_inc(cu_sb.sem, 1)
                for s in S:
                    dve.wait_ge(th_sb.sem, th_sb.at(i, s + 1))
                    nc.vector.scalar_tensor_tensor(SG[s][:, :], SG[s][:, :], 1.0, G(s)[:, :], ALU.add, ALU.mult).then_inc(a_sb.sem, 1)
                for s in S:
                    dve.wait_ge(a_sb.sem, a_sb.at(i, s + 1))
                    dve.wait_ge(u_ps.sem, u_ps.at(i, s + 1))
                    nc.vector.tensor_tensor(SG[s][:, :], SG[s][:, :], U(s)[:, :], ALU.mult).then_inc(a_sb.sem, 1)
                n = [0]

                def link(ins):
                    n[0] += 1
                    ins.then_inc(pst.sem, 1)
                    dve.wait_ge(pst.sem, pst.at(i, n[0]))

                norm.vector_stats(dve, i + 1, norm.pair(i + 1))
                norm.vector_aggr(dve, i + 1)
                dve.wait_ge(pos_ps.sem, pos_ps.at(i, 1))
                count = m.bank[5][:, :].rearrange("p (n e) -> p n e", e=CE)
                for k in range(2):
                    link(nc.vector.tensor_tensor(top.oh[k][:, :, :], top.oh[k][:, :, :], count, ALU.mult))
                    link(nc.vector.tensor_reduce(pos[:, k, :], top.oh[k][:, :, :], AX.X, ALU.add))
                link(nc.vector.tensor_scalar(val[:, :, :], pos[:, :, :], float(CAP), None, ALU.is_lt))
                link(nc.vector.tensor_scalar(slot[:, :, :], top.r[:, :, :], -float(CAP), float(CE * CAP), ALU.mult, ALU.add))
                link(nc.vector.tensor_tensor(slot[:, :, :], slot[:, :, :], pos[:, :, :], ALU.add))
                link(nc.vector.tensor_tensor(alt[:, :, :], slot[:, :, :], w["spare"][:, bass.ds(i * (2 * R8), 2 * R8)].rearrange("p (k n) -> p k n", k=2), ALU.subtract))
                link(nc.vector.tensor_tensor(alt[:, :, :], alt[:, :, :], val[:, :, :], ALU.mult))
                link(nc.vector.tensor_tensor(alt[:, :, :], alt[:, :, :], w["spare"][:, bass.ds(i * (2 * R8), 2 * R8)].rearrange("p (k n) -> p k n", k=2), ALU.add))
                nc.vector.tensor_copy(sidx[:, bass.ds(i, 1), :].rearrange("p o (k n) -> p (o k) n", k=2), alt[:, :, :]).then_inc(idx_sb.sem, 1)
                link(nc.vector.tensor_scalar(vsum[:, :], vsum[:, :], 1e-20, None, ALU.add))
                link(nc.vector.reciprocal(vsum[:, :], vsum[:, :]))
                link(nc.vector.scalar_tensor_tensor(top.v[:, :, :], top.v[:, :, :], ROUTE_SCALE, val[:, :, :], ALU.mult, ALU.mult))
                nc.vector.tensor_tensor(m.place[:, bass.ds(i, 1), :].rearrange("p o (k n) -> p (o k) n", k=2), slot[:, :, :], val[:, :, :], ALU.mult).then_inc(kept.sem, 1)
                nc.vector.tensor_tensor(m.share[:, bass.ds(i, 1), :].rearrange("p o (k n) -> p (o k) n", k=2), top.v[:, :, :],
                                        vsum[:, :].rearrange("p (o n) -> p o n", o=1).broadcast_to([P, 2, R8]), ALU.mult).then_inc(kept.sem, 1)
                dve.wait_ge(xn_kept.sem, xn_kept.at(i, 32))
                norm.vector_scale(dve, i + 1, norm.pair(i + 1), XN)
                for s in S:
                    dve.wait_ge(y_ps.sem, y_ps.at(i, s + 1))
                    nc.vector.scalar_tensor_tensor(hs[s], OUT(s)[:, :].rearrange("p (c d) -> p c d", c=NC_), 0.5, hs[s], ALU.mult, ALU.add).then_inc(h_sb.sem, 1)
                dve.wait_ge(h_sb.sem, h_sb.at(i, 2))
                dve.wait_ge(kept.sem, kept.at(i, 2))
                dve.wait_ge(idx_sb.sem, idx_sb.at(i, 1))

        @block.scalar
        def _(act):
            with act.Fori(0, PAIRS) as i:
                for s in S:
                    act.wait_ge(xt_ps.sem, xt_ps.at(i, s + 1))
                    nc.scalar.copy(XT[s][:, :], m.bank[4 * s][:, :]).then_inc(xt_sb.sem, 1)
                act.wait_ge(lg_ps.sem, lg_ps.at(i, 1))
                nc.scalar.activation(sc[:, :, :].rearrange("p n e -> p (n e)"), m.bank[1][:, :], ACT.Exp, scale=-1.0).then_inc(ex_sb.sem, 1)
                for s in S:
                    act.wait_ge(g_ps.sem, g_ps.at(i, s + 1))
                    nc.scalar.activation(SG[s][:, :], G(s)[:, :], ACT.Tanh, scale=0.5).then_inc(th_sb.sem, 1)

        @block.tensor
        def _(pe):
            for name in ("c_gate", "earlier", "sw1", "sw3", "sw2"):
                pe.wait_ge(m.loaded[name], 16)
            with pe.Fori(0, PAIRS) as i:
                for s in S:
                    pe.wait_ge(norm.ready.sem, norm.ready.at(i, s + 1))
                    for c in range(NC_):
                        last = nc.tensor.transpose(m.bank[4 * s][:, c * P:(c + 1) * P], XN[s][:, c, :], w["ident"][:, :])
                    last.then_inc(xt_ps.sem, 1)
                for s in S:
                    pe.wait_ge(xt_sb.sem, xt_sb.at(i, s + 1))
                    for c in range(NC_):
                        n = s * NC_ + c
                        last = nc.tensor.matmul(m.bank[1][:, n * CE:(n + 1) * CE], XT[s][:, c * P:(c + 1) * P], w["c_gate"][:, :], start=True, stop=True)
                last.then_inc(lg_ps.sem, 1)
                for s in S:
                    nc.tensor.matmul(G(s)[:, :], w["sw1"][:, :], XT[s][:, :], start=True, stop=True).then_inc(g_ps.sem, 1)
                    nc.tensor.matmul(U(s)[:, :], w["sw3"][:, :], XT[s][:, :], start=True, stop=True).then_inc(u_ps.sem, 1)
                pe.wait_ge(cu_sb.sem, cu_sb.at(i, 1))
                flat = lambda v: v.rearrange("p n e -> p (n e)")
                nc.tensor.matmul(m.bank[5][:, :], w["earlier"][:, :], flat(M[:, :, :]), start=True, stop=False)
                nc.tensor.matmul(m.bank[5][:, :], w["ones"][:, 0:P], flat(CU[:, 0:R8, :]), start=False, stop=True).then_inc(pos_ps.sem, 1)
                for s in S:
                    pe.wait_ge(a_sb.sem, a_sb.at(i, s + 3))
                    for c in range(NC_):
                        last = nc.tensor.matmul(OUT(s)[:, c * P:(c + 1) * P], SG[s][:, c * P:(c + 1) * P], w["sw2"][:, :], start=True, stop=True)
                    last.then_inc(y_ps.sem, 1)
                pe.wait_ge(h_sb.sem, h_sb.at(i, 2))


def capacity_experts(ctx, nc, m):
    UN = 8
    NI = CE // 2 // UN
    S = range(2)
    sig = lambda name, per: Signal(ctx, nc, "ce_" + name, per)
    w = m.w
    w13, w2 = m.w13, m.w2
    QC = CAP // P
    X = [m.KM[0][:, u, :] for u in range(UN)]
    Y = [m.KM[1][:, u, :] for u in range(UN)]
    XT = [m.XT[s] for s in S]
    TH = [m.t512a[s] for s in S]
    AA = [m.t512b[s] for s in S]
    AT = [m.t512c[s][:, 0, 0:2 * P] for s in S]
    x_in = [sig(f"x_in{u}", 16) for u in range(UN)]
    y_out = [sig(f"y_out{u}", 16) for u in range(UN)]
    x_free, xt_ps, xt_sb, gu_ps, th_sb, a_sb = (sig(n, UN) for n in ("x_free", "xt_ps", "xt_sb", "gu_ps", "th_sb", "a_sb"))
    aa_sb, at_ps, at_sb, y_ps, y_sb = (sig(n, UN) for n in ("aa_sb", "at_ps", "at_sb", "y_ps", "y_sb"))
    XP = lambda u: m.bank[u % 2]
    GU = lambda u: m.bank[2 + u % 2]
    AP_ = lambda u: m.bank[4 + u % 2]
    YP = lambda u: m.bank[6 + u % 2]
    acf = lambda v: v.rearrange("p (a c f) -> p a c f", a=2, c=QC)
    rows = lambda t, k: t[bass.ds(k * (2 * CAP), 2 * CAP), :].rearrange("(n p) d -> p n d", p=P)
    nd = lambda v: v.rearrange("p (n d) -> p n d", d=D)
    mark = ctx.sb("ce_mark", [P, UN])
    y_free = sig("y_free", UN)
    ROOM = 2

    with nc.Block() as block:
        @block.sync
        def _(sp):
            with sp.Fori(0, NI) as i:
                for u in range(UN):
                    sp.wait_ge(x_free.sem, x_free.at(i, u + 1))
                    sp.dma_start(nd(X[u]), rows(m.queues, i * UN + u)).then_inc(x_in[u].sem, 16)

        @block.gpsimd
        def _(pool):
            nc.gpsimd.memset(m.pool_fence[:, 0:1], 0.0).then_inc(x_free.sem, UN)
            nc.gpsimd.memset(m.pool_fence[:, 1:2], 0.0).then_inc(y_free.sem, UN)
            with pool.Fori(0, NI) as i:
                for u in range(UN + 2):
                    if u < UN:
                        pool.wait_ge(y_sb.sem, y_sb.at(i, u + 1))
                        pool.dma_start(rows(m.results, i * UN + u), nd(Y[u])).then_inc(y_out[u].sem, 16)
                    if u >= 2:
                        v = u - 2
                        pool.wait_ge(y_out[v].sem, y_out[v].at(i, 16))
                        nc.gpsimd.tensor_tensor(mark[:, v:v + 1], m.minus_half[:, 0:1], m.minus_half[:, 0:1], ALU.mult).then_inc(y_free.sem, 1)
            for u in range(UN):
                pool.wait_ge(y_out[u].sem, 16 * NI)

        @block.vector
        def _(dve):
            with dve.Fori(0, NI) as i:
                def last_part(u):
                    dve.wait_ge(y_ps.sem, y_ps.at(i, u + 1))
                    dve.wait_ge(y_free.sem, y_free.at(i, u + 1))
                    nc.vector.tensor_scalar(acf(Y[u]), YP(u)[:, :].rearrange("p (c a f) -> p a c f", a=2, c=QC), 0.5, None, ALU.mult).then_inc(y_sb.sem, 1)

                for u in range(UN):
                    dve.wait_ge(th_sb.sem, th_sb.at(i, u + 1))
                    gu = acf(GU(u)[:, :])
                    th = TH[u % 2][:, 0:2 * QC * CH].rearrange("p (a c f) -> p a c f", a=2, c=QC)
                    nc.vector.scalar_tensor_tensor(th, th, 1.0, gu[:, :, :, 0:CH], ALU.add, ALU.mult).then_inc(a_sb.sem, 1)
                    dve.wait_ge(a_sb.sem, a_sb.at(i, u + 1))
                    if u >= ROOM:
                        dve.wait_ge(at_ps.sem, at_ps.at(i, u - ROOM + 1))
                    nc.vector.tensor_tensor(AA[u % 2][:, 0:2 * QC * CH].rearrange("p (c a f) -> p a c f", a=2, c=QC), th, gu[:, :, :, CH:2 * CH],
                                            ALU.mult).then_inc(aa_sb.sem, 1)
                    if u >= 2:
                        last_part(u - 2)
                last_part(UN - 2)
                last_part(UN - 1)
                dve.wait_ge(at_ps.sem, at_ps.at(i, UN))

        @block.scalar
        def _(act):
            with act.Fori(0, NI) as i:
                for u in range(UN + 2):
                    if u < UN:
                        act.wait_ge(xt_ps.sem, xt_ps.at(i, u + 1))
                        if u >= ROOM:
                            act.wait_ge(gu_ps.sem, gu_ps.at(i, u - ROOM + 1))
                        nc.scalar.copy(XT[u % 2][:, :], XP(u)[:, :]).then_inc(xt_sb.sem, 1)
                    if 1 <= u <= UN:
                        v = u - 1
                        act.wait_ge(gu_ps.sem, gu_ps.at(i, v + 1))
                        if v >= ROOM:
                            act.wait_ge(aa_sb.sem, aa_sb.at(i, v - ROOM + 1))
                        nc.scalar.activation(TH[v % 2][:, 0:2 * QC * CH].rearrange("p (a f) -> p a f", f=CH),
                                             GU(v)[:, :].rearrange("p (a f) -> p a f", f=2 * CH)[:, :, 0:CH], ACT.Tanh, scale=0.5).then_inc(th_sb.sem, 1)
                    if 2 <= u:
                        v = u - 2
                        act.wait_ge(at_ps.sem, at_ps.at(i, v + 1))
                        if v >= ROOM:
                            act.wait_ge(y_ps.sem, y_ps.at(i, v - ROOM + 1))
                        nc.scalar.copy(AT[v % 2], AP_(v)[:, 0:QC * P]).then_inc(at_sb.sem, 1)
                act.wait_ge(y_ps.sem, y_ps.at(i, UN))

        @block.tensor
        def _(pe):
            pe.wait_ge(m.w13_in, 16)
            pe.wait_ge(m.w2_in, 16)
            with pe.Fori(0, NI) as i:
                for u in range(UN + 3):
                    if u < UN:
                        pe.wait_ge(x_in[u].sem, x_in[u].at(i, 16))
                        if u >= ROOM:
                            pe.wait_ge(xt_sb.sem, xt_sb.at(i, u - ROOM + 1))
                        for n in range(2 * QC):
                            last = nc.tensor.transpose(XP(u)[:, n * P:(n + 1) * P], X[u][:, n * P:(n + 1) * P], w["ident"][:, :])
                        last.then_inc(xt_ps.sem, 1)
                    if 1 <= u <= UN:
                        v = u - 1
                        pe.wait_ge(xt_sb.sem, xt_sb.at(i, v + 1))
                        if v >= ROOM:
                            pe.wait_ge(aa_sb.sem, aa_sb.at(i, v - ROOM + 1))
                        for a in range(2):
                            we = w13[:, bass.ds(2 * (i * UN + v) + a, 1), :].rearrange("p o n -> p (o n)")
                            for c in range(QC):
                                n = a * QC + c
                                last = nc.tensor.matmul(GU(v)[:, n * P:(n + 1) * P], XT[v % 2][:, n * P:(n + 1) * P], we, start=True, stop=True)
                                if n == 0:
                                    last.then_inc(x_free.sem, 1)
                        last.then_inc(gu_ps.sem, 1)
                    if 2 <= u <= UN + 1:
                        v = u - 2
                        pe.wait_ge(aa_sb.sem, aa_sb.at(i, v + 1))
                        if v >= ROOM:
                            pe.wait_ge(at_sb.sem, at_sb.at(i, v - ROOM + 1))
                        for c in range(QC):
                            last = nc.tensor.transpose(AP_(v)[:, c * P:(c + 1) * P], AA[v % 2][:, c * P:(c + 1) * P], w["ident"][:, :])
                        last.then_inc(at_ps.sem, 1)
                    if 3 <= u:
                        v = u - 3
                        pe.wait_ge(at_sb.sem, at_sb.at(i, v + 1))
                        if v >= ROOM:
                            pe.wait_ge(y_sb.sem, y_sb.at(i, v - ROOM + 1))
                        wp = w2[:, bass.ds(i * UN + v, 1), :].rearrange("p o n -> p (o n)")
                        for c in range(QC):
                            last = nc.tensor.matmul(YP(v)[:, c * 2 * D:(c + 1) * 2 * D], AT[v % 2][:, c * P:(c + 1) * P], wp, start=True, stop=True)
                        last.then_inc(y_ps.sem, 1)
                pe.wait_ge(y_sb.sem, y_sb.at(i, UN))


def capacity_combine(ctx, nc, m):
    R8 = 2 * NC_
    sig = lambda name: Signal(ctx, nc, "cc_" + name)
    idx = ctx.sb("cc_idx", [P, PAIRS, 2 * R8], I32)
    Y = [m.KM[b // 2 % 2][:, 4 * (b % 2):4 * (b % 2) + 2, :].rearrange("p k (c d) -> p k c d", c=NC_) for b in range(4)]
    idx_sb, summed, first = sig("idx_sb"), sig("summed"), sig("first")
    got = [sig(f"got{b}") for b in range(B)]
    stored = sig("stored")

    with nc.Block() as block:
        @block.sync
        def _(sp):
            for b in range(B):
                sp.wait_ge(summed.sem, b + 1)
                sp.dma_start(m.out[b, :, :].rearrange("(c p) d -> p c d", p=P), m.h[:, b * NC_:(b + 1) * NC_, :]).then_inc(stored.sem, 16)
            sp.wait_ge(stored.sem, 16 * B)

        @block.gpsimd
        def _(pool):
            pool.wait_ge(idx_sb.sem, 1)
            for b in range(B):
                if b >= 4:
                    pool.wait_ge(summed.sem, b - 3)
                for c in range(NC_):
                    for k in range(2):
                        q = k * R8 + b % 2 * NC_ + c
                        pool.indirect_dma_start(
                            out=Y[b % 4][:, k, c, :], out_offset=None, in_=m.results,
                            in_offset=bass.IndirectOffsetOnAxis(ap=idx[:, b // 2, q:q + 1].bitcast(U32), axis=0)).then_inc(got[b].sem, 16)

        @block.vector
        def _(dve):
            nc.vector.tensor_copy(idx[:, :, :], m.place[:, :, :]).then_inc(idx_sb.sem, 1)
            for b in range(B):
                dve.wait_ge(got[b].sem, 16 * 2 * NC_)
                for k in range(2):
                    for c in range(NC_):
                        q = k * R8 + b % 2 * NC_ + c
                        h = m.h[:, b * NC_ + c, :]
                        last = nc.vector.scalar_tensor_tensor(h, Y[b % 4][:, k, c, :], m.share[:, b // 2, q:q + 1], h, ALU.mult, ALU.add)
                    last.then_inc((summed if k else first).sem, 1)
                    if k == 0:
                        dve.wait_ge(first.sem, b + 1)


def workspace(m):
    m.big = m.sb("big", [P, 24 * T])
    m.nstat = [m.sb(f"nstat{s}", [P, NC_, 6]) for s in range(2)]
    m.nmv = [m.sb(f"nmv{s}", [P, NC_, 2]) for s in range(2)]
    m.nrstd = [m.sb(f"nrstd{s}", [P, NC_]) for s in range(2)]
    m.fence = m.sb("fence", [P, 2])
    m.pool_fence = m.sb("pool_fence", [P, 2])
    m.minus_half = m.sb("minus_half", [P, 64])
    m.XN = [m.sb(f"XN{s}", [P, NC_, D]) for s in range(2)]
    m.XT = [m.sb(f"XT{s}", [P, T]) for s in range(2)]
    m.t512a = [m.sb(f"t512a{s}", [P, T]) for s in range(2)]
    m.t512b = [m.sb(f"t512b{s}", [P, T]) for s in range(2)]
    m.t512c = [m.sb(f"t512c{s}", [P, 2, T]) for s in range(2)]
    m.KM = [m.sb(f"KM{s}", [P, NH, T]) for s in range(2)]
    m.A = [m.big[:, s * 4 * T:(s + 1) * 4 * T].rearrange("p (a c t) -> p a c t", a=4, c=NC_) for s in range(2)]
    o = 8 * T
    m.V = [m.big[:, o + s * 4 * T:o + (s + 1) * 4 * T].rearrange("p (c n) -> p c n", c=NC_) for s in range(2)]
    o = 16 * T
    m.OT = [m.big[:, o + s * 4 * T:o + (s + 1) * 4 * T].rearrange("p (g n) -> p g n", g=NC_) for s in range(2)]
    m.XNA = m.big[:, 0:8 * T].rearrange("p (n d) -> p n d", d=D)
    m.XTA = m.big[:, 8 * T:16 * T]
    m.KTOK = [m.sb(f"KTOK{s}", [P, 3, D]) for s in range(2)]
    m.ST = [m.sb(f"ST{s}", [P, 3, T]) for s in range(2)]


def build(nc, dram, out, upto=None):
    whole = Layer(nc)
    with whole:
        m = Memory(whole, nc, dram)
        workspace(m)
        m.out = out
        m.queues = nc.dram_tensor("queues", (CE * CAP + 2 * NT * P, D), F32).ap()
        m.results = nc.dram_tensor("results", (CE * CAP, D), F32).ap()
        m.zeros = m.sb("zeros", [P, T])
        m.queues_zero = whole.semaphore("queues_zero")
        m.early = ["ones", "causal", "same_head", "head_col", "state_mask", "wq", "wk", "wv", "wout"]
        with nc.Block() as block:
            @block.gpsimd
            def _(pool):
                nc.gpsimd.memset(m.minus_half[:, :], -0.5)
                nc.gpsimd.memset(m.zeros[:, :], 0.0)
                nc.gpsimd.memset(m.h_more[:, NT:NT + 2 * NC_, :], 0.0)
        for layer in LAYERS[:upto]:
            own = Layer(nc)
            layer(own, nc, m)
            own.end()
        if upto is not None:
            stored = whole.semaphore("stored")
            with nc.Block() as block:
                @block.sync
                def _(sp):
                    sp.dma_start(out.rearrange("b (c p) d -> p (b c) d", p=P), m.h[:, :, :]).then_inc(stored, 16)
                    sp.wait_ge(stored, 16)


LAYERS = [token_conv, linear_attention, modulated_ffn, retention, balanced_experts, attention_and_experts,
          batch_attention, capacity_mixture]


def laid_out(inputs):
    a = {k: np.asarray(v) for k, v in inputs.items()}
    row = lambda x: np.ascontiguousarray(x)
    out = dict(shape_constants())
    out["ids"] = row(a["x"].reshape(NT, P).T)
    out["table"] = row(a["L0_tok_conv_w"].transpose(1, 2, 0).reshape(VOCAB, TAPS * D))
    out["wq"] = row(a["L0_attn_W_q"].T)
    out["wk"] = row(a["L0_attn_W_k"].T)
    out["wv"] = row(a["L0_attn_W_v"].T)
    out["wout"] = row(a["L0_attn_W_out"].T.reshape(NC_, P, D).transpose(1, 0, 2).reshape(P, NC_ * D))
    E, R = 8, 16
    rep = lambda x: row(np.repeat(x, R, axis=-1))
    spread = lambda x: row(np.concatenate([x[:, None, :], np.zeros((E, R - 1, x.shape[1]), x.dtype)], axis=1).reshape(P, -1))
    out["gfc1"] = row(a["L0_ffn_gfc1_w"].T)
    out["gfc1_b"] = row(a["L0_ffn_gfc1_b"].reshape(P, 1))
    out["gfc2_rep"] = rep(a["L0_ffn_gfc2_w"].T)
    out["gfc2_b"] = rep(a["L0_ffn_gfc2_b"]).reshape(P, 1)
    out["task_b1"] = spread(a["L0_ffn_tv_b1"])
    out["b1"] = row(a["L0_ffn_b1"].reshape(4, P).T)
    tb2 = spread(a["L0_ffn_tv_b2"])
    tb2[1] = a["L0_ffn_b2"]
    out["task_b2"] = tb2
    zeros = np.zeros((P - 1 - E, 2 * D), np.float32)
    out["ln_rows"] = row(np.concatenate([
        np.concatenate([a["L0_ffn_ln_g"], a["L0_ffn_ln_b"]])[None],
        np.concatenate([a["L0_ffn_tv_ln_g"], a["L0_ffn_tv_ln_b"]], axis=1), zeros]))
    coef = np.zeros((P, P), np.float32)
    coef[0], coef[1:1 + E] = 1.0 - 0.03 * E, 0.03
    out["ln_coef"] = coef
    p = np.arange(P)
    out["gate_row"] = row(np.stack([p % R == 0, p == 1], axis=1).astype(np.float32))
    out["gate_pad"] = row(np.concatenate([np.zeros((P, R)), p[:, None] % R == np.arange(R)[None], np.zeros((P, R))], axis=1).astype(np.float32))
    out["task_W1"] = row(a["L0_ffn_tv_W1"].reshape(E, 512, 8, R).transpose(0, 3, 2, 1).reshape(P, 8 * 512))
    out["task_W2"] = row(a["L0_ffn_tv_W2"].reshape(E, D, 4, 8, R).transpose(0, 4, 3, 2, 1).reshape(P, 8 * 4 * D))
    out["W1"] = row(a["L0_ffn_W1"].T)
    out["W2"] = row(a["L0_ffn_W2"].reshape(D, 4, P).transpose(2, 1, 0).reshape(P, 4 * D))
    for n in "QKVGO":
        out["r_w" + n.lower()] = row(a["L1_attn_W_" + n])
    out["gn"] = row(np.stack([a["L1_attn_gn_weight"], a["L1_attn_gn_bias"]], axis=1))
    out["gate_w"] = row(a["L1_ffn_gate_weight"][0])
    out["experts"] = row(a["L1_ffn_experts"].transpose(1, 0, 2).reshape(D, 8 * D))
    q = np.arange(B * 8)
    later = (p[:, None] // 8 == q[None] // 8) & (p[:, None] > q[None])
    out["later_expert"] = row(later.astype(np.float32))
    wx, wt = a["L2_attn_Wx"], a["L2_attn_Wt"]
    out["a_wx"], out["a_wt"] = row(wx), row(wt)
    out["a_bt"] = row(np.tile(a["L2_attn_bt"], 2).reshape(P, 1))
    wa = np.zeros((P, 62), np.float32)
    wa[0:64, 30], wa[64:128, 31] = a["L2_attn_Wa"][:, 0], a["L2_attn_Wa"][:, 0]
    out["a_wa"] = wa
    out["a_ba"] = row(np.tile(a["L2_attn_ba"], P).reshape(P, 1))
    out["router"] = row(a["L2_ffn_router_w"].T)
    out["ramp"] = row(np.tile(np.arange(64, 0, -1, dtype=np.float32), (P, 1)))
    out["wgu"] = row(np.concatenate([a["L2_ffn_w_gate"], a["L2_ffn_w_up"]], axis=2).transpose(1, 0, 2).reshape(P, -1))
    out["wdown"] = row(a["L2_ffn_w_down"].reshape(8, 2, P, D).transpose(2, 0, 1, 3).reshape(P, -1))
    qkv = lambda x: x.reshape((NH, 3, DH) + x.shape[1:]).swapaxes(0, 1).reshape(x.shape)
    out["b_w"] = row(qkv(a["L3_attn_W"]).T)
    out["b_b"] = row(np.tile(qkv(a["L3_attn_b"]), (P, 1)))
    out["c_gate"] = row(a["L3_ffn_gate_w"].T)
    out["earlier"] = row((p[:, None] < p[None, :]).astype(np.float32))
    out["spare"] = row((CE * CAP + np.arange(2 * NT)[None, :] * P + p[:, None]).astype(np.float32))
    for n in ("sw1", "sw3", "sw2"):
        out[n] = row(a["L3_ffn_" + n])
    out["w13"] = row(np.concatenate([a["L3_ffn_w1"], a["L3_ffn_w3"]], axis=2).transpose(1, 0, 2).reshape(P, -1))
    w2 = a["L3_ffn_w2"].reshape(CE // 2, 2, CH, D)
    pairs = np.zeros((2, CH, CE // 2, 2, D), w2.dtype)
    for e in range(2):
        pairs[e, :, :, e] = w2[:, e].transpose(1, 0, 2)
    out["w2_pairs"] = pairs.reshape(P, -1)
    return out


def kernel(**inputs):
    import concourse.bacc as bacc
    from concourse.bass_utils import run_bass_kernel_spmd

    nc = bacc.Bacc("TRN2", target_bir_lowering=False, num_devices=1)
    arrays, dram = {}, {}
    for name, a in laid_out(inputs).items():
        arrays["in_" + name] = a
        dram[name] = nc.dram_tensor("in_" + name, a.shape, mybir.dt.from_np(a.dtype), kind="ExternalInput").ap()
    out = nc.dram_tensor("out_h", (B, T, D), F32, kind="ExternalOutput").ap()
    build(nc, dram, out)
    r = run_bass_kernel_spmd(nc, [arrays], core_ids=[0])
    return r.results[0]["out_h"]
```
